# Optimizing a Trainium2 kernel written in Bass

```python
import numpy as np
import jax
import jax.numpy as jnp

def _softmax(x, axis=-1):
    return jax.nn.softmax(x, axis=axis)

def _gelu(x):
    return jax.nn.gelu(x, approximate=True)

def _silu(x):
    return jax.nn.silu(x)

def _sigmoid(x):
    return jax.nn.sigmoid(x)

def _layernorm(x, axis=-1, eps=1e-05):
    m = jnp.mean(x, axis=axis, keepdims=True)
    v = jnp.var(x, axis=axis, keepdims=True)
    return (x - m) / jnp.sqrt(v + eps)

def _scatter_add(tgt, idx, src, axis=0):
    return tgt.at[idx].add(src)

def _segment_sum(src, seg, n):
    return jax.ops.segment_sum(src, seg, n)
kernel_name = 'mk_prb_d4_jaxref_r8_1160b5'

def setup_inputs(seed: int=0):
    np.random.seed(seed)
    _w = jnp.asarray

    def _L0_attn_setup():
        import jax, jax.numpy as jnp
        import numpy as np
        HEADS = 16
        LN_EPS = 1e-05

        def _ln(v, w, b):
            mu = jnp.mean(v, axis=-1, keepdims=True)
            var = jnp.mean(jnp.square(v - mu), axis=-1, keepdims=True)
            return (v - mu) * jax.lax.rsqrt(var + LN_EPS) * w + b
        key = jax.random.key(seed)
        ks = jax.random.split(key, 5)
        b, t, e = (2, 256, 128)
        x = jax.random.normal(ks[0], (b, t, e), dtype=jnp.float32)
        scale = 0.02
        Wk = jax.random.normal(ks[1], (e, e), dtype=jnp.float32) * scale
        Wq = jax.random.normal(ks[2], (e, e), dtype=jnp.float32) * scale
        Wv = jax.random.normal(ks[3], (e, e), dtype=jnp.float32) * scale
        Wu = jax.random.normal(ks[4], (e, e), dtype=jnp.float32) * scale
        s = e // HEADS
        return {'x': x, 'Wk': Wk, 'Wq': Wq, 'Wv': Wv, 'Wu': Wu, 'kln_w': jnp.ones((s,), jnp.float32), 'kln_b': jnp.zeros((s,), jnp.float32), 'qln_w': jnp.ones((s,), jnp.float32), 'qln_b': jnp.zeros((s,), jnp.float32)}
    _L0_attn_in = _L0_attn_setup()

    def _L0_ffn_setup():
        import jax, jax.numpy as jnp
        import numpy as np
        DIM = 128
        DEPTH = 6
        HEADS = 16
        DIM_HEAD = 64
        WINDOW = 32
        INNER = HEADS * DIM_HEAD
        DIM_INNER = int(DIM * 4 * 2 / 3)
        QK_SCALE = 8.0

        def shift_tokens(t):
            a, s = jnp.split(t, 2, -1)
            s = jnp.pad(s, ((0, 0), (1, 0), (0, 0)))[:, :-1]
            return jnp.concatenate([a, s], -1)

        def l2norm(t):
            return t / jnp.maximum(jnp.linalg.norm(t, axis=-1, keepdims=True), 1e-12)

        def rotate_half(x):
            x1, x2 = jnp.split(x, 2, -1)
            return jnp.concatenate([-x2, x1], -1)

        def rotary_tables(n):
            half = jnp.arange(0, DIM_HEAD, 2, dtype=jnp.float32)
            inv_freq = 1.0 / 10000.0 ** (half / DIM_HEAD)
            t = jnp.arange(n, dtype=jnp.float32)
            freqs = t[:, None] * inv_freq[None, :]
            freqs = jnp.concatenate([freqs, freqs], -1)
            base_scale = (half + 0.4 * DIM_HEAD) / (1.4 * DIM_HEAD)
            power = (t - n // 2) / (WINDOW // 2)
            scale = base_scale[None, :] ** power[:, None]
            scale = jnp.concatenate([scale, scale], -1)
            return (freqs, scale)

        def local_attention(q, k, v):
            b, h, n, d = q.shape
            w = WINDOW
            nw = n // w
            bq = q.reshape(b, h, nw, w, d)
            bk = k.reshape(b, h, nw, w, d)
            bv = v.reshape(b, h, nw, w, d)

            def look(t):
                p = jnp.pad(t, ((0, 0), (0, 0), (1, 0), (0, 0), (0, 0)))
                return jnp.concatenate([p[:, :, :nw], p[:, :, 1:]], axis=3)
            bk2, bv2 = (look(bk), look(bv))
            seq = jnp.arange(n).reshape(nw, w)
            seq_p = jnp.pad(seq, ((1, 0), (0, 0)), constant_values=-1)
            jt = jnp.concatenate([seq_p[:nw], seq_p[1:]], axis=1)
            it = seq[:, :, None]
            jb = jt[:, None, :]
            mask = (it < jb) | (it > jb + w) | (jb == -1)
            sim = jnp.einsum('bhwie,bhwje->bhwij', bq, bk2) * QK_SCALE
            sim = jnp.where(mask, -jnp.finfo(sim.dtype).max, sim)
            attn = jax.nn.softmax(sim, -1)
            out = jnp.einsum('bhwij,bhwje->bhwie', attn, bv2)
            return out.reshape(b, h, n, d)

        def attn_layer(x, Wqkv, qs, ksc, Wo):
            b, n, _ = x.shape
            qkv = x @ Wqkv
            q, k, v = jnp.split(qkv, 3, -1)
            sh = lambda t: t.reshape(b, n, HEADS, DIM_HEAD).transpose(0, 2, 1, 3)
            q, k, v = (sh(q), sh(k), sh(v))
            q = l2norm(q) * qs
            k = l2norm(k) * ksc
            freqs, scale = rotary_tables(n)
            cos, sin = (jnp.cos(freqs), jnp.sin(freqs))
            q = q * cos * scale + rotate_half(q) * sin * scale
            inv = 1.0 / scale
            k = k * cos * inv + rotate_half(k) * sin * inv
            out = local_attention(q, k, v)
            out = out.transpose(0, 2, 1, 3).reshape(b, n, INNER)
            return out @ Wo

        def ffn_layer(x, g, bln, W1, b1, W2, b2):
            mu = x.mean(-1, keepdims=True)
            var = ((x - mu) ** 2).mean(-1, keepdims=True)
            xn = (x - mu) / jnp.sqrt(var + 1e-05) * g + bln
            hg = xn @ W1 + b1
            a, gate = jnp.split(hg, 2, -1)
            return a * jax.nn.gelu(gate, approximate=False) @ W2 + b2
        key = jax.random.key(seed)
        ks = jax.random.split(key, 8)
        B, N = (2, 256)
        init = lambda k, shape: jax.random.normal(k, shape, jnp.float32) * 0.02
        return {'x': jax.random.normal(ks[0], (B, N, DIM), jnp.float32), 'Wqkv': init(ks[1], (DEPTH, DIM, 3 * INNER)), 'q_scale': jnp.ones((DEPTH, DIM_HEAD), jnp.float32), 'k_scale': jnp.ones((DEPTH, DIM_HEAD), jnp.float32), 'Wo': init(ks[2], (DEPTH, INNER, DIM)), 'ln_g': jnp.ones((DEPTH, DIM), jnp.float32), 'ln_b': jnp.zeros((DEPTH, DIM), jnp.float32), 'W1': init(ks[3], (DEPTH, DIM, 2 * DIM_INNER)), 'b1': jnp.zeros((DEPTH, 2 * DIM_INNER), jnp.float32), 'W2': init(ks[4], (DEPTH, DIM_INNER, DIM)), 'b2': jnp.zeros((DEPTH, DIM), jnp.float32)}
    _L0_ffn_in = _L0_ffn_setup()

    def _L1_attn_setup():
        import jax, jax.numpy as jnp
        import numpy as np
        B_, S_, D_, N_ = (4, 256, 128, 16)

        def _layernorm(y, w, b, eps=1e-05):
            mu = jnp.mean(y, axis=-1, keepdims=True)
            var = jnp.mean((y - mu) ** 2, axis=-1, keepdims=True)
            return (y - mu) * jax.lax.rsqrt(var + eps) * w + b
        key = jax.random.key(seed)
        ks = jax.random.split(key, 8)
        x = jax.random.normal(ks[0], (B_, S_, D_), dtype=jnp.float32)
        A = jax.random.normal(ks[1], (D_, N_, N_), dtype=jnp.float32) * 0.1
        Bm = jax.random.normal(ks[2], (D_, N_), dtype=jnp.float32) * 0.1
        Cm = jax.random.normal(ks[3], (D_, N_), dtype=jnp.float32) * 0.1
        Dm = jax.random.normal(ks[4], (D_,), dtype=jnp.float32) * 0.1
        ln_w = jnp.ones((D_,), dtype=jnp.float32)
        ln_b = jnp.zeros((D_,), dtype=jnp.float32)
        W_out = jax.random.normal(ks[5], (D_, D_), dtype=jnp.float32) * (1.0 / np.sqrt(D_))
        b_out = jnp.zeros((D_,), dtype=jnp.float32)
        return {'x': x, 'A': A, 'Bm': Bm, 'Cm': Cm, 'Dm': Dm, 'ln_w': ln_w, 'ln_b': ln_b, 'W_out': W_out, 'b_out': b_out}
    _L1_attn_in = _L1_attn_setup()

    def _L1_ffn_setup():
        import jax, jax.numpy as jnp
        import numpy as np
        from jax import lax
        B, S, D = (4, 256, 128)
        E = 8
        K = 2
        F = 408
        NORM_TOPK = True
        key = jax.random.key(seed)
        ks = jax.random.split(key, 8)
        sd = 0.02
        return {'x': jax.random.normal(ks[0], (B, S, D), jnp.float32), 'gate_w': jax.random.normal(ks[1], (E, D), jnp.float32) * sd, 'gate_b': jnp.zeros((E,), jnp.float32), 'up_w': jax.random.normal(ks[2], (E, F, D), jnp.float32) * sd, 'up_b': jnp.zeros((E, F), jnp.float32), 'gp_w': jax.random.normal(ks[3], (E, F, D), jnp.float32) * sd, 'gp_b': jnp.zeros((E, F), jnp.float32), 'down_w': jax.random.normal(ks[4], (E, D, F), jnp.float32) * sd, 'down_b': jnp.zeros((E, D), jnp.float32)}
    _L1_ffn_in = _L1_ffn_setup()

    def _L2_attn_setup():
        import jax, jax.numpy as jnp
        import numpy as np
        B, N, C, H, W = (2, 256, 128, 16, 8)
        HD = C // H
        SCALE = HD ** (-0.5)

        def band_mask(n, w):
            i = jnp.arange(n)[:, None]
            j = jnp.arange(n)[None, :]
            lo = jnp.where(i <= w, 0, i - w)
            hi = jnp.where(n - i <= w, n - 1, i + w)
            return (j >= lo) & (j <= hi)
        key = jax.random.key(seed)
        k1, k2, k3 = jax.random.split(key, 3)
        x = jax.random.normal(k1, (B, N, C), dtype=jnp.float32)
        Wqkv = jax.random.normal(k2, (C, 3 * C), dtype=jnp.float32) * C ** (-0.5)
        Wproj = jax.random.normal(k3, (C, C), dtype=jnp.float32) * C ** (-0.5)
        bproj = jnp.zeros((C,), dtype=jnp.float32)
        return {'x': x, 'Wqkv': Wqkv, 'Wproj': Wproj, 'bproj': bproj}
    _L2_attn_in = _L2_attn_setup()

    def _L2_ffn_setup():
        import jax, jax.numpy as jnp
        import numpy as np
        E, K, H, I, SI = (32, 8, 128, 64, 256)
        CAP = 256
        LIMIT = 7.0
        SCALE = 2.5
        B, S = (2, 256)
        key = jax.random.key(seed)
        ks = jax.random.split(key, 8)
        s = 0.02
        return {'hidden_states': jax.random.normal(ks[0], (B, S, H), jnp.float32), 'router_weight': jax.random.normal(ks[1], (E, H), jnp.float32) * s, 'e_score_correction_bias': jnp.zeros((E,), jnp.float32), 'gate_up_proj': jax.random.normal(ks[2], (E, 2 * I, H), jnp.float32) * s, 'down_proj': jax.random.normal(ks[3], (E, H, I), jnp.float32) * s, 'shared_gate': jax.random.normal(ks[4], (SI, H), jnp.float32) * s, 'shared_up': jax.random.normal(ks[5], (SI, H), jnp.float32) * s, 'shared_down': jax.random.normal(ks[6], (H, SI), jnp.float32) * s}
    _L2_ffn_in = _L2_ffn_setup()

    def _L3_attn_setup():
        import jax, jax.numpy as jnp
        import numpy as np
        H = 128
        D = 32
        CHUNK = 64
        LR = 0.1
        GRAD_SCALE = 0.1
        MAX_GRAD_NORM = 1.0
        EPS = 1e-06
        P = 2 * D * D

        def _xavier(k, shape, gain=0.1):
            fan_out, fan_in = shape
            a = gain * np.sqrt(6.0 / (fan_in + fan_out))
            return jax.random.uniform(k, shape, jnp.float32, -a, a)

        def _causal_dwconv(x, w, b):
            T = x.shape[1]
            xp = jnp.pad(x, ((0, 0), (3, 0), (0, 0)))
            y = b
            for j in range(4):
                y = y + xp[:, j:j + T, :] * w[:, j]
            return y

        def _mem_loss(p, k_t, v_t):
            W1 = p[:D * D].reshape(D, D)
            W2 = p[D * D:].reshape(D, D)
            pred = jax.nn.silu(k_t @ W1.T) @ W2.T
            return jnp.sum((pred - v_t) ** 2)
        _grad_fn = jax.vmap(jax.vmap(jax.grad(_mem_loss), in_axes=(None, 0, 0)), in_axes=(0, 0, 0))

        def _forward(hidden, Wk, Wv, Wq, Wo, ckw, ckb, cvw, cvb, cqw, cqb, mW1, mW2, aW, ab, eW, eb, tW, tb, norm_g, gW, gb):
            B, S, _ = hidden.shape
            k = _causal_dwconv(hidden @ Wk.T, ckw, ckb)
            v = _causal_dwconv(hidden @ Wv.T, cvw, cvb)
            q = _causal_dwconv(hidden @ Wq.T, cqw, cqb)
            alpha = (jax.nn.sigmoid(hidden @ aW.T + ab) * 0.1).mean(-1)
            eta = (jax.nn.sigmoid(hidden @ eW.T + eb) * 0.9 + 0.05).mean(-1)
            theta = (jax.nn.softplus(hidden @ tW.T + tb) * LR).mean(-1)
            W_state = jnp.tile(jnp.concatenate([mW1.ravel(), mW2.ravel()])[None], (B, 1))
            S_state = jnp.zeros_like(W_state)

            def step(carry, xs):
                Sm, Wm = carry
                gt, et, tt, at = xs
                Sm = et[:, None] * Sm - tt[:, None] * gt
                Wm = (1.0 - at[:, None]) * Wm + Sm
                return ((Sm, Wm), Wm)
            outs = []
            for c0 in range(0, S, CHUNK):
                sl = slice(c0, c0 + CHUNK)
                g = _grad_fn(W_state, k[:, sl], v[:, sl]) * GRAD_SCALE
                gn = jnp.maximum(jnp.linalg.norm(g, axis=-1, keepdims=True), EPS)
                g = g * jnp.minimum(MAX_GRAD_NORM / gn, 1.0)
                g = jax.lax.stop_gradient(g)
                xs = (jnp.swapaxes(g, 0, 1), eta[:, sl].T, theta[:, sl].T, alpha[:, sl].T)
                (S_state, W_state), Wtraj = jax.lax.scan(step, (S_state, W_state), xs)
                Wtraj = jnp.swapaxes(Wtraj, 0, 1)
                T = Wtraj.shape[1]
                W1t = Wtraj[..., :D * D].reshape(B, T, D, D)
                W2t = Wtraj[..., D * D:].reshape(B, T, D, D)
                h = jax.nn.silu(jnp.einsum('btd,btod->bto', q[:, sl], W1t))
                outs.append(jnp.einsum('bto,btpo->btp', h, W2t))
            retrieved = jnp.concatenate(outs, axis=1)
            out = retrieved @ Wo.T
            out = out * jax.lax.rsqrt(jnp.mean(out * out, -1, keepdims=True) + EPS) * norm_g
            gate = hidden @ gW.T + gb
            return out * gate
        key = jax.random.key(seed)
        ks = jax.random.split(key, 24)
        B, S = (1, 128)
        return {'hidden': jax.random.normal(ks[0], (B, S, H), jnp.float32), 'Wk': _xavier(ks[1], (D, H)), 'Wv': _xavier(ks[2], (D, H)), 'Wq': _xavier(ks[3], (D, H)), 'Wo': _xavier(ks[4], (H, D)), 'ckw': jax.random.normal(ks[5], (D, 4), jnp.float32) * 0.05, 'ckb': jnp.zeros((D,), jnp.float32), 'cvw': jax.random.normal(ks[6], (D, 4), jnp.float32) * 0.05, 'cvb': jnp.zeros((D,), jnp.float32), 'cqw': jax.random.normal(ks[7], (D, 4), jnp.float32) * 0.05, 'cqb': jnp.zeros((D,), jnp.float32), 'mW1': _xavier(ks[8], (D, D)), 'mW2': _xavier(ks[9], (D, D)), 'aW': jax.random.normal(ks[10], (D, H), jnp.float32) * 0.02, 'ab': jnp.zeros((D,), jnp.float32), 'eW': jax.random.normal(ks[11], (D, H), jnp.float32) * 0.02, 'eb': jnp.zeros((D,), jnp.float32), 'tW': jax.random.normal(ks[12], (D, H), jnp.float32) * 0.02, 'tb': jnp.zeros((D,), jnp.float32), 'norm_g': jnp.ones((H,), jnp.float32), 'gW': jnp.zeros((H, H), jnp.float32), 'gb': jnp.ones((H,), jnp.float32)}
    _L3_attn_in = _L3_attn_setup()

    def _L3_ffn_setup():
        import jax, jax.numpy as jnp
        import numpy as np
        BLOCK = 16
        _GRID = jnp.array([0.0, 0.5, 1.0, 1.5, 2.0, 3.0, 4.0, 6.0], dtype=jnp.float32)
        _MID = jnp.array([0.25, 0.75, 1.25, 1.75, 2.5, 3.5, 5.0], dtype=jnp.float32)

        def fp4_quant_dequant(x):
            shape = x.shape
            xb = x.reshape(shape[:-1] + (shape[-1] // BLOCK, BLOCK))
            scale = jnp.max(jnp.abs(xb), axis=-1, keepdims=True) / 6.0
            scale = jnp.maximum(scale, jnp.float32(1e-12))
            xn = xb / scale
            idx = jnp.searchsorted(_MID, jnp.abs(xn))
            q = _GRID[idx] * jnp.sign(xn) * scale
            return q.reshape(shape)

        def fp4_linear(x, w):
            xq = fp4_quant_dequant(x)
            wq = fp4_quant_dequant(w)
            return jnp.einsum('bsk,nk->bsn', xq, wq)
        key = jax.random.key(seed)
        k1, k2, k3, k4 = jax.random.split(key, 4)
        H, I = (128, 352)
        x = jax.random.normal(k1, (4, 512, H), dtype=jnp.float32)
        w_gate = jax.random.normal(k2, (I, H), dtype=jnp.float32) * 0.02
        w_up = jax.random.normal(k3, (I, H), dtype=jnp.float32) * 0.02
        w_down = jax.random.normal(k4, (H, I), dtype=jnp.float32) * 0.02
        return {'x': x, 'w_gate': w_gate, 'w_up': w_up, 'w_down': w_down}
    _L3_ffn_in = _L3_ffn_setup()
    _d = {'L0_attn_x': _L0_attn_in['x'], 'L0_attn_Wk': _L0_attn_in['Wk'], 'L0_attn_Wq': _L0_attn_in['Wq'], 'L0_attn_Wv': _L0_attn_in['Wv'], 'L0_attn_Wu': _L0_attn_in['Wu'], 'L0_attn_kln_w': _L0_attn_in['kln_w'], 'L0_attn_kln_b': _L0_attn_in['kln_b'], 'L0_attn_qln_w': _L0_attn_in['qln_w'], 'L0_attn_qln_b': _L0_attn_in['qln_b'], 'L0_ffn_Wqkv': _L0_ffn_in['Wqkv'], 'L0_ffn_q_scale': _L0_ffn_in['q_scale'], 'L0_ffn_k_scale': _L0_ffn_in['k_scale'], 'L0_ffn_Wo': _L0_ffn_in['Wo'], 'L0_ffn_ln_g': _L0_ffn_in['ln_g'], 'L0_ffn_ln_b': _L0_ffn_in['ln_b'], 'L0_ffn_W1': _L0_ffn_in['W1'], 'L0_ffn_b1': _L0_ffn_in['b1'], 'L0_ffn_W2': _L0_ffn_in['W2'], 'L0_ffn_b2': _L0_ffn_in['b2'], 'L1_attn_A': _L1_attn_in['A'], 'L1_attn_Bm': _L1_attn_in['Bm'], 'L1_attn_Cm': _L1_attn_in['Cm'], 'L1_attn_Dm': _L1_attn_in['Dm'], 'L1_attn_ln_w': _L1_attn_in['ln_w'], 'L1_attn_ln_b': _L1_attn_in['ln_b'], 'L1_attn_W_out': _L1_attn_in['W_out'], 'L1_attn_b_out': _L1_attn_in['b_out'], 'L1_ffn_gate_w': _L1_ffn_in['gate_w'], 'L1_ffn_gate_b': _L1_ffn_in['gate_b'], 'L1_ffn_up_w': _L1_ffn_in['up_w'], 'L1_ffn_up_b': _L1_ffn_in['up_b'], 'L1_ffn_gp_w': _L1_ffn_in['gp_w'], 'L1_ffn_gp_b': _L1_ffn_in['gp_b'], 'L1_ffn_down_w': _L1_ffn_in['down_w'], 'L1_ffn_down_b': _L1_ffn_in['down_b'], 'L2_attn_Wqkv': _L2_attn_in['Wqkv'], 'L2_attn_Wproj': _L2_attn_in['Wproj'], 'L2_attn_bproj': _L2_attn_in['bproj'], 'L2_ffn_router_weight': _L2_ffn_in['router_weight'], 'L2_ffn_e_score_correction_bias': _L2_ffn_in['e_score_correction_bias'], 'L2_ffn_gate_up_proj': _L2_ffn_in['gate_up_proj'], 'L2_ffn_down_proj': _L2_ffn_in['down_proj'], 'L2_ffn_shared_gate': _L2_ffn_in['shared_gate'], 'L2_ffn_shared_up': _L2_ffn_in['shared_up'], 'L2_ffn_shared_down': _L2_ffn_in['shared_down'], 'L3_attn_Wk': _L3_attn_in['Wk'], 'L3_attn_Wv': _L3_attn_in['Wv'], 'L3_attn_Wq': _L3_attn_in['Wq'], 'L3_attn_Wo': _L3_attn_in['Wo'], 'L3_attn_ckw': _L3_attn_in['ckw'], 'L3_attn_ckb': _L3_attn_in['ckb'], 'L3_attn_cvw': _L3_attn_in['cvw'], 'L3_attn_cvb': _L3_attn_in['cvb'], 'L3_attn_cqw': _L3_attn_in['cqw'], 'L3_attn_cqb': _L3_attn_in['cqb'], 'L3_attn_mW1': _L3_attn_in['mW1'], 'L3_attn_mW2': _L3_attn_in['mW2'], 'L3_attn_aW': _L3_attn_in['aW'], 'L3_attn_ab': _L3_attn_in['ab'], 'L3_attn_eW': _L3_attn_in['eW'], 'L3_attn_eb': _L3_attn_in['eb'], 'L3_attn_tW': _L3_attn_in['tW'], 'L3_attn_tb': _L3_attn_in['tb'], 'L3_attn_norm_g': _L3_attn_in['norm_g'], 'L3_attn_gW': _L3_attn_in['gW'], 'L3_attn_gb': _L3_attn_in['gb'], 'L3_ffn_w_gate': _L3_ffn_in['w_gate'], 'L3_ffn_w_up': _L3_ffn_in['w_up'], 'L3_ffn_w_down': _L3_ffn_in['w_down']}
    _x0 = _d['L0_attn_x']
    _d['L0_attn_x'] = jax.random.normal(jax.random.fold_in(jax.random.key(seed), 1), (8, 512, 128), dtype=_x0.dtype)
    del _x0
    return _d

def reference(L0_attn_x, L0_attn_Wk, L0_attn_Wq, L0_attn_Wv, L0_attn_Wu, L0_attn_kln_w, L0_attn_kln_b, L0_attn_qln_w, L0_attn_qln_b, L0_ffn_Wqkv, L0_ffn_q_scale, L0_ffn_k_scale, L0_ffn_Wo, L0_ffn_ln_g, L0_ffn_ln_b, L0_ffn_W1, L0_ffn_b1, L0_ffn_W2, L0_ffn_b2, L1_attn_A, L1_attn_Bm, L1_attn_Cm, L1_attn_Dm, L1_attn_ln_w, L1_attn_ln_b, L1_attn_W_out, L1_attn_b_out, L1_ffn_gate_w, L1_ffn_gate_b, L1_ffn_up_w, L1_ffn_up_b, L1_ffn_gp_w, L1_ffn_gp_b, L1_ffn_down_w, L1_ffn_down_b, L2_attn_Wqkv, L2_attn_Wproj, L2_attn_bproj, L2_ffn_router_weight, L2_ffn_e_score_correction_bias, L2_ffn_gate_up_proj, L2_ffn_down_proj, L2_ffn_shared_gate, L2_ffn_shared_up, L2_ffn_shared_down, L3_attn_Wk, L3_attn_Wv, L3_attn_Wq, L3_attn_Wo, L3_attn_ckw, L3_attn_ckb, L3_attn_cvw, L3_attn_cvb, L3_attn_cqw, L3_attn_cqb, L3_attn_mW1, L3_attn_mW2, L3_attn_aW, L3_attn_ab, L3_attn_eW, L3_attn_eb, L3_attn_tW, L3_attn_tb, L3_attn_norm_g, L3_attn_gW, L3_attn_gb, L3_ffn_w_gate, L3_ffn_w_up, L3_ffn_w_down):

    def _L0_attn_ref(x, Wk, Wq, Wv, Wu, kln_w, kln_b, qln_w, qln_b):
        import jax, jax.numpy as jnp
        import numpy as np
        HEADS = 16
        LN_EPS = 1e-05

        def _ln(v, w, b):
            mu = jnp.mean(v, axis=-1, keepdims=True)
            var = jnp.mean(jnp.square(v - mu), axis=-1, keepdims=True)
            return (v - mu) * jax.lax.rsqrt(var + LN_EPS) * w + b
        b, t, e = x.shape
        h = HEADS
        s = e // h
        k = (x @ Wk.T).reshape(b, t, h, s)
        q = (x @ Wq.T).reshape(b, t, h, s)
        v = (x @ Wv.T).reshape(b, t, h, s)
        k = _ln(k, kln_w, kln_b)
        q = _ln(q, qln_w, qln_b)
        scalefactor = 1.0 / np.sqrt(s).astype(np.float32)
        dot = jnp.einsum('bqhs,bkhs->bhqk', q, k) * scalefactor
        causal = jnp.triu(jnp.ones((t, t), dtype=bool), k=1)
        dot = jnp.where(causal, -jnp.inf, dot)
        attn = jax.nn.softmax(dot, axis=-1)
        out = jnp.einsum('bhqk,bkhs->bqhs', attn, v).reshape(b, t, e)
        return out @ Wu.T

    def _L0_ffn_ref(x, Wqkv, q_scale, k_scale, Wo, ln_g, ln_b, W1, b1, W2, b2):
        import jax, jax.numpy as jnp
        import numpy as np
        DIM = 128
        DEPTH = 6
        HEADS = 16
        DIM_HEAD = 64
        WINDOW = 32
        INNER = HEADS * DIM_HEAD
        DIM_INNER = int(DIM * 4 * 2 / 3)
        QK_SCALE = 8.0

        def shift_tokens(t):
            a, s = jnp.split(t, 2, -1)
            s = jnp.pad(s, ((0, 0), (1, 0), (0, 0)))[:, :-1]
            return jnp.concatenate([a, s], -1)

        def l2norm(t):
            return t / jnp.maximum(jnp.linalg.norm(t, axis=-1, keepdims=True), 1e-12)

        def rotate_half(x):
            x1, x2 = jnp.split(x, 2, -1)
            return jnp.concatenate([-x2, x1], -1)

        def rotary_tables(n):
            half = jnp.arange(0, DIM_HEAD, 2, dtype=jnp.float32)
            inv_freq = 1.0 / 10000.0 ** (half / DIM_HEAD)
            t = jnp.arange(n, dtype=jnp.float32)
            freqs = t[:, None] * inv_freq[None, :]
            freqs = jnp.concatenate([freqs, freqs], -1)
            base_scale = (half + 0.4 * DIM_HEAD) / (1.4 * DIM_HEAD)
            power = (t - n // 2) / (WINDOW // 2)
            scale = base_scale[None, :] ** power[:, None]
            scale = jnp.concatenate([scale, scale], -1)
            return (freqs, scale)

        def local_attention(q, k, v):
            b, h, n, d = q.shape
            w = WINDOW
            nw = n // w
            bq = q.reshape(b, h, nw, w, d)
            bk = k.reshape(b, h, nw, w, d)
            bv = v.reshape(b, h, nw, w, d)

            def look(t):
                p = jnp.pad(t, ((0, 0), (0, 0), (1, 0), (0, 0), (0, 0)))
                return jnp.concatenate([p[:, :, :nw], p[:, :, 1:]], axis=3)
            bk2, bv2 = (look(bk), look(bv))
            seq = jnp.arange(n).reshape(nw, w)
            seq_p = jnp.pad(seq, ((1, 0), (0, 0)), constant_values=-1)
            jt = jnp.concatenate([seq_p[:nw], seq_p[1:]], axis=1)
            it = seq[:, :, None]
            jb = jt[:, None, :]
            mask = (it < jb) | (it > jb + w) | (jb == -1)
            sim = jnp.einsum('bhwie,bhwje->bhwij', bq, bk2) * QK_SCALE
            sim = jnp.where(mask, -jnp.finfo(sim.dtype).max, sim)
            attn = jax.nn.softmax(sim, -1)
            out = jnp.einsum('bhwij,bhwje->bhwie', attn, bv2)
            return out.reshape(b, h, n, d)

        def attn_layer(x, Wqkv, qs, ksc, Wo):
            b, n, _ = x.shape
            qkv = x @ Wqkv
            q, k, v = jnp.split(qkv, 3, -1)
            sh = lambda t: t.reshape(b, n, HEADS, DIM_HEAD).transpose(0, 2, 1, 3)
            q, k, v = (sh(q), sh(k), sh(v))
            q = l2norm(q) * qs
            k = l2norm(k) * ksc
            freqs, scale = rotary_tables(n)
            cos, sin = (jnp.cos(freqs), jnp.sin(freqs))
            q = q * cos * scale + rotate_half(q) * sin * scale
            inv = 1.0 / scale
            k = k * cos * inv + rotate_half(k) * sin * inv
            out = local_attention(q, k, v)
            out = out.transpose(0, 2, 1, 3).reshape(b, n, INNER)
            return out @ Wo

        def ffn_layer(x, g, bln, W1, b1, W2, b2):
            mu = x.mean(-1, keepdims=True)
            var = ((x - mu) ** 2).mean(-1, keepdims=True)
            xn = (x - mu) / jnp.sqrt(var + 1e-05) * g + bln
            hg = xn @ W1 + b1
            a, gate = jnp.split(hg, 2, -1)
            return a * jax.nn.gelu(gate, approximate=False) @ W2 + b2
        for i in range(DEPTH):
            x = attn_layer(shift_tokens(x), Wqkv[i], q_scale[i], k_scale[i], Wo[i]) + x
            x = ffn_layer(shift_tokens(x), ln_g[i], ln_b[i], W1[i], b1[i], W2[i], b2[i]) + x
        return x

    def _L1_attn_ref(x, A, Bm, Cm, Dm, ln_w, ln_b, W_out, b_out):
        import jax, jax.numpy as jnp
        import numpy as np
        B_, S_, D_, N_ = (4, 256, 128, 16)

        def _layernorm(y, w, b, eps=1e-05):
            mu = jnp.mean(y, axis=-1, keepdims=True)
            var = jnp.mean((y - mu) ** 2, axis=-1, keepdims=True)
            return (y - mu) * jax.lax.rsqrt(var + eps) * w + b
        bsz = x.shape[0]
        h0 = jnp.zeros((bsz, A.shape[0], A.shape[1]), dtype=x.dtype)

        def step(h, x_t):
            h = jnp.einsum('dnm,bdm->bdn', A, h) + Bm[None] * x_t[..., None]
            y_t = jnp.einsum('dn,bdn->bd', Cm, h) + Dm * x_t
            return (h, y_t)
        _, y = jax.lax.scan(step, h0, jnp.swapaxes(x, 0, 1))
        y = jnp.swapaxes(y, 0, 1)
        y = _layernorm(y, ln_w, ln_b)
        y = jax.nn.gelu(y, approximate=False)
        y = y @ W_out.T + b_out
        return x + y

    def _L1_ffn_ref(x, gate_w, gate_b, up_w, up_b, gp_w, gp_b, down_w, down_b):
        import jax, jax.numpy as jnp
        import numpy as np
        from jax import lax
        B, S, D = (4, 256, 128)
        E = 8
        K = 2
        F = 408
        NORM_TOPK = True
        bs, slen, dim = x.shape
        xf = x.reshape(-1, dim)
        N = xf.shape[0]
        scores = jax.nn.softmax(xf @ gate_w.T + gate_b, axis=-1)
        top_w, top_idx = lax.top_k(scores, K)
        if NORM_TOPK:
            top_w = top_w / (top_w.sum(-1, keepdims=True) + 1e-20)
        comb = jnp.zeros((N, E), xf.dtype).at[jnp.arange(N)[:, None], top_idx].add(top_w)

        def step(acc, p):
            uw, ub, gw, gb, dw, db, w = p
            h = jax.nn.silu((xf @ gw.T + gb) * (xf @ uw.T + ub))
            return (acc + w[:, None] * (h @ dw.T + db), None)
        y0 = jnp.zeros_like(xf)
        y, _ = lax.scan(step, y0, (up_w, up_b, gp_w, gp_b, down_w, down_b, comb.T))
        return y.reshape(bs, slen, dim)

    def _L2_attn_ref(x, Wqkv, Wproj, bproj):
        import jax, jax.numpy as jnp
        import numpy as np
        B, N, C, H, W = (2, 256, 128, 16, 8)
        HD = C // H
        SCALE = HD ** (-0.5)

        def band_mask(n, w):
            i = jnp.arange(n)[:, None]
            j = jnp.arange(n)[None, :]
            lo = jnp.where(i <= w, 0, i - w)
            hi = jnp.where(n - i <= w, n - 1, i + w)
            return (j >= lo) & (j <= hi)
        b, n, c = x.shape
        qkv = (x @ Wqkv).reshape(b, n, 3, H, HD)
        qkv = jnp.transpose(qkv, (2, 0, 3, 1, 4))
        q, k, v = (qkv[0], qkv[1], qkv[2])
        attn = jnp.einsum('bhqd,bhkd->bhqk', q, k) * SCALE
        mask = band_mask(n, W)
        attn = jnp.where(mask[None, None], attn, jnp.float32(-1000000000.0))
        attn = jax.nn.softmax(attn, axis=-1)
        out = jnp.einsum('bhqk,bhkd->bhqd', attn, v)
        out = jnp.transpose(out, (0, 2, 1, 3)).reshape(b, n, c)
        return out @ Wproj + bproj

    def _L2_ffn_ref(hidden_states, router_weight, e_score_correction_bias, gate_up_proj, down_proj, shared_gate, shared_up, shared_down):
        import jax, jax.numpy as jnp
        import numpy as np
        E, K, H, I, SI = (32, 8, 128, 64, 256)
        CAP = 256
        LIMIT = 7.0
        SCALE = 2.5
        B, S = (2, 256)
        b, s, _ = hidden_states.shape
        T = b * s
        x = hidden_states.reshape(T, H)
        logits = x.astype(jnp.float32) @ router_weight.astype(jnp.float32).T
        scores = jax.nn.sigmoid(logits)
        _, idx = jax.lax.top_k(scores + e_score_correction_bias, K)
        w = jnp.take_along_axis(scores, idx, axis=1)
        w = w / (w.sum(-1, keepdims=True) + 1e-20) * SCALE
        e_flat = idx.reshape(-1)
        onehot = jax.nn.one_hot(e_flat, E, dtype=jnp.int32)
        pos = jnp.cumsum(onehot, axis=0) - onehot
        pos = jnp.take_along_axis(pos, e_flat[:, None], axis=1)[:, 0]
        keep = pos < CAP
        slot = jnp.where(keep, e_flat * CAP + pos, E * CAP)
        tok = jnp.arange(T * K) // K
        buf = jnp.zeros((E * CAP + 1, H), x.dtype).at[slot].set(x[tok])
        xe = buf[:E * CAP].reshape(E, CAP, H)
        gu = jnp.einsum('ech,eoh->eco', xe, gate_up_proj)
        g, u = (gu[..., :I], gu[..., I:])
        g = jnp.minimum(g, LIMIT)
        u = jnp.clip(u, -LIMIT, LIMIT)
        h = jax.nn.silu(g) * u
        ye = jnp.einsum('eci,ehi->ech', h, down_proj)
        yp = ye.reshape(E * CAP, H)[jnp.minimum(slot, E * CAP - 1)]
        yp = jnp.where(keep[:, None], yp, 0.0) * w.reshape(-1)[:, None]
        routed = jax.ops.segment_sum(yp, tok, num_segments=T).reshape(b, s, H)
        shared = jax.nn.silu(hidden_states @ shared_gate.T) * (hidden_states @ shared_up.T) @ shared_down.T
        return routed + shared

    def _L3_attn_ref(hidden, Wk, Wv, Wq, Wo, ckw, ckb, cvw, cvb, cqw, cqb, mW1, mW2, aW, ab, eW, eb, tW, tb, norm_g, gW, gb):
        import jax, jax.numpy as jnp
        import numpy as np
        H = 128
        D = 32
        CHUNK = 64
        LR = 0.1
        GRAD_SCALE = 0.1
        MAX_GRAD_NORM = 1.0
        EPS = 1e-06
        P = 2 * D * D

        def _xavier(k, shape, gain=0.1):
            fan_out, fan_in = shape
            a = gain * np.sqrt(6.0 / (fan_in + fan_out))
            return jax.random.uniform(k, shape, jnp.float32, -a, a)

        def _causal_dwconv(x, w, b):
            T = x.shape[1]
            xp = jnp.pad(x, ((0, 0), (3, 0), (0, 0)))
            y = b
            for j in range(4):
                y = y + xp[:, j:j + T, :] * w[:, j]
            return y

        def _mem_loss(p, k_t, v_t):
            W1 = p[:D * D].reshape(D, D)
            W2 = p[D * D:].reshape(D, D)
            pred = jax.nn.silu(k_t @ W1.T) @ W2.T
            return jnp.sum((pred - v_t) ** 2)
        _grad_fn = jax.vmap(jax.vmap(jax.grad(_mem_loss), in_axes=(None, 0, 0)), in_axes=(0, 0, 0))

        def _forward(hidden, Wk, Wv, Wq, Wo, ckw, ckb, cvw, cvb, cqw, cqb, mW1, mW2, aW, ab, eW, eb, tW, tb, norm_g, gW, gb):
            B, S, _ = hidden.shape
            k = _causal_dwconv(hidden @ Wk.T, ckw, ckb)
            v = _causal_dwconv(hidden @ Wv.T, cvw, cvb)
            q = _causal_dwconv(hidden @ Wq.T, cqw, cqb)
            alpha = (jax.nn.sigmoid(hidden @ aW.T + ab) * 0.1).mean(-1)
            eta = (jax.nn.sigmoid(hidden @ eW.T + eb) * 0.9 + 0.05).mean(-1)
            theta = (jax.nn.softplus(hidden @ tW.T + tb) * LR).mean(-1)
            W_state = jnp.tile(jnp.concatenate([mW1.ravel(), mW2.ravel()])[None], (B, 1))
            S_state = jnp.zeros_like(W_state)

            def step(carry, xs):
                Sm, Wm = carry
                gt, et, tt, at = xs
                Sm = et[:, None] * Sm - tt[:, None] * gt
                Wm = (1.0 - at[:, None]) * Wm + Sm
                return ((Sm, Wm), Wm)
            outs = []
            for c0 in range(0, S, CHUNK):
                sl = slice(c0, c0 + CHUNK)
                g = _grad_fn(W_state, k[:, sl], v[:, sl]) * GRAD_SCALE
                gn = jnp.maximum(jnp.linalg.norm(g, axis=-1, keepdims=True), EPS)
                g = g * jnp.minimum(MAX_GRAD_NORM / gn, 1.0)
                g = jax.lax.stop_gradient(g)
                xs = (jnp.swapaxes(g, 0, 1), eta[:, sl].T, theta[:, sl].T, alpha[:, sl].T)
                (S_state, W_state), Wtraj = jax.lax.scan(step, (S_state, W_state), xs)
                Wtraj = jnp.swapaxes(Wtraj, 0, 1)
                T = Wtraj.shape[1]
                W1t = Wtraj[..., :D * D].reshape(B, T, D, D)
                W2t = Wtraj[..., D * D:].reshape(B, T, D, D)
                h = jax.nn.silu(jnp.einsum('btd,btod->bto', q[:, sl], W1t))
                outs.append(jnp.einsum('bto,btpo->btp', h, W2t))
            retrieved = jnp.concatenate(outs, axis=1)
            out = retrieved @ Wo.T
            out = out * jax.lax.rsqrt(jnp.mean(out * out, -1, keepdims=True) + EPS) * norm_g
            gate = hidden @ gW.T + gb
            return out * gate
        return _forward(hidden, Wk, Wv, Wq, Wo, ckw, ckb, cvw, cvb, cqw, cqb, mW1, mW2, aW, ab, eW, eb, tW, tb, norm_g, gW, gb)

    def _L3_ffn_ref(x, w_gate, w_up, w_down):
        import jax, jax.numpy as jnp
        import numpy as np
        BLOCK = 16
        _GRID = jnp.array([0.0, 0.5, 1.0, 1.5, 2.0, 3.0, 4.0, 6.0], dtype=jnp.float32)
        _MID = jnp.array([0.25, 0.75, 1.25, 1.75, 2.5, 3.5, 5.0], dtype=jnp.float32)

        def fp4_quant_dequant(x):
            shape = x.shape
            xb = x.reshape(shape[:-1] + (shape[-1] // BLOCK, BLOCK))
            scale = jnp.max(jnp.abs(xb), axis=-1, keepdims=True) / 6.0
            scale = jnp.maximum(scale, jnp.float32(1e-12))
            xn = xb / scale
            idx = jnp.searchsorted(_MID, jnp.abs(xn))
            q = _GRID[idx] * jnp.sign(xn) * scale
            return q.reshape(shape)

        def fp4_linear(x, w):
            xq = fp4_quant_dequant(x)
            wq = fp4_quant_dequant(w)
            return jnp.einsum('bsk,nk->bsn', xq, wq)
        gate = fp4_linear(x, w_gate)
        y = fp4_linear(x, w_up)
        h = jax.nn.silu(gate) * y
        return fp4_linear(h, w_down)
    x = L0_attn_x
    xn = _layernorm(x, axis=-1)
    x = x + _L0_attn_ref(xn, L0_attn_Wk, L0_attn_Wq, L0_attn_Wv, L0_attn_Wu, L0_attn_kln_w, L0_attn_kln_b, L0_attn_qln_w, L0_attn_qln_b) + _L0_ffn_ref(xn, L0_ffn_Wqkv, L0_ffn_q_scale, L0_ffn_k_scale, L0_ffn_Wo, L0_ffn_ln_g, L0_ffn_ln_b, L0_ffn_W1, L0_ffn_b1, L0_ffn_W2, L0_ffn_b2)
    xn = _layernorm(x, axis=-1)
    x = x + _L1_attn_ref(xn, L1_attn_A, L1_attn_Bm, L1_attn_Cm, L1_attn_Dm, L1_attn_ln_w, L1_attn_ln_b, L1_attn_W_out, L1_attn_b_out) + _L1_ffn_ref(xn, L1_ffn_gate_w, L1_ffn_gate_b, L1_ffn_up_w, L1_ffn_up_b, L1_ffn_gp_w, L1_ffn_gp_b, L1_ffn_down_w, L1_ffn_down_b)
    xn = _layernorm(x, axis=-1)
    x = x + _L2_attn_ref(xn, L2_attn_Wqkv, L2_attn_Wproj, L2_attn_bproj) + _L2_ffn_ref(xn, L2_ffn_router_weight, L2_ffn_e_score_correction_bias, L2_ffn_gate_up_proj, L2_ffn_down_proj, L2_ffn_shared_gate, L2_ffn_shared_up, L2_ffn_shared_down)
    xn = _layernorm(x, axis=-1)
    x = x + _L3_attn_ref(xn, L3_attn_Wk, L3_attn_Wv, L3_attn_Wq, L3_attn_Wo, L3_attn_ckw, L3_attn_ckb, L3_attn_cvw, L3_attn_cvb, L3_attn_cqw, L3_attn_cqb, L3_attn_mW1, L3_attn_mW2, L3_attn_aW, L3_attn_ab, L3_attn_eW, L3_attn_eb, L3_attn_tW, L3_attn_tb, L3_attn_norm_g, L3_attn_gW, L3_attn_gb) + _L3_ffn_ref(xn, L3_ffn_w_gate, L3_ffn_w_up, L3_ffn_w_down)
    return x

_drawn_inputs = setup_inputs


def setup_inputs(seed=0):
    import zlib

    import numpy as np

    out = dict(_drawn_inputs(seed))
    spreads = {'L0_attn_kln_w': (1.0, 0.6),
     'L0_attn_kln_b': (0.0, 0.8),
     'L0_attn_qln_w': (1.0, 0.6),
     'L0_attn_qln_b': (0.0, 0.8),
     'L0_ffn_q_scale': (1.0, 0.6),
     'L0_ffn_k_scale': (1.0, 0.6),
     'L0_ffn_ln_g': (1.0, 0.6),
     'L0_ffn_ln_b': (0.0, 0.8),
     'L0_ffn_b1': (0.0, 0.8),
     'L0_ffn_b2': (0.0, 0.1),
     'L1_attn_ln_w': (1.0, 0.2),
     'L1_attn_ln_b': (0.0, 0.437),
     'L1_attn_b_out': (0.0, 0.1),
     'L1_ffn_gate_b': (0.0, 0.615),
     'L1_ffn_up_b': (0.0, 0.8),
     'L1_ffn_gp_b': (0.0, 0.8),
     'L1_ffn_down_b': (0.0, 0.335),
     'L2_attn_bproj': (0.0, 0.289),
     'L2_ffn_e_score_correction_bias': (0.0, 0.8),
     'L3_attn_ckb': (0.0, 0.8),
     'L3_attn_cvb': (0.0, 0.8),
     'L3_attn_cqb': (0.0, 0.8),
     'L3_attn_ab': (0.0, 0.8),
     'L3_attn_eb': (0.0, 0.8),
     'L3_attn_tb': (0.0, 0.8),
     'L3_attn_norm_g': (1.0, 0.6),
     'L3_attn_gW': (0.0, 0.8),
     'L3_attn_gb': (1.0, 0.6)}
    factors = {'L0_attn_Wk': 8.0,
     'L0_attn_Wq': 8.0,
     'L0_attn_Wv': 8.0,
     'L0_attn_Wu': 8.0,
     'L0_ffn_W1': 3.565,
     'L0_ffn_W2': 3.486,
     'L1_ffn_gate_w': 2.756,
     'L1_ffn_up_w': 8.0,
     'L1_ffn_gp_w': 8.0,
     'L1_ffn_down_w': 8.0,
     'L2_ffn_router_weight': 8.0,
     'L2_ffn_gate_up_proj': 8.0,
     'L2_ffn_down_proj': 8.0,
     'L2_ffn_shared_gate': 8.0,
     'L2_ffn_shared_up': 8.0,
     'L2_ffn_shared_down': 8.0,
     'L3_attn_Wk': 8.0,
     'L3_attn_Wv': 8.0,
     'L3_attn_Wq': 8.0,
     'L3_attn_Wo': 8.0,
     'L3_attn_ckw': 8.0,
     'L3_attn_cvw': 8.0,
     'L3_attn_cqw': 8.0,
     'L3_attn_mW1': 8.0,
     'L3_attn_mW2': 8.0,
     'L3_attn_aW': 8.0,
     'L3_attn_eW': 8.0,
     'L3_attn_tW': 8.0,
     'L3_ffn_w_gate': 8.0,
     'L3_ffn_w_up': 8.0,
     'L3_ffn_w_down': 8.0}
    for name, (base, spread) in spreads.items():
        noise = np.random.default_rng([zlib.crc32(name.encode()), seed]).standard_normal(out[name].shape)
        drawn = base * np.exp(spread * noise) if base else spread * noise
        out[name] = jnp.asarray(drawn.astype(out[name].dtype))
    for name, factor in factors.items():
        out[name] = (out[name] * factor).astype(out[name].dtype)
    return out
```

```python
from contextlib import ExitStack

import numpy as np
import concourse.bass as bass
from concourse import mybir

P, B, T, D = 128, 8, 4, 128
F32 = mybir.dt.float32; BF16 = mybir.dt.bfloat16
ALU = mybir.AluOpType; ACT = mybir.ActivationFunctionType; AX = mybir.AxisListType

def bcast(ap, axis, n):
    dims = [list(x) for x in ap.ap]
    return bass.AP(ap.tensor, ap.offset, dims[:axis] + [[0, n]] + dims[axis:])

def rows(ap, n=P):
    return bass.AP(ap.tensor, ap.offset, [[0, n]] + [list(x) for x in ap.ap])


def clear(nc, sems):
    numbers = sorted(s.num for s in sems)
    with nc.Block() as block:
        @block.sync
        def _(sp):
            first = numbers[0]
            for n, after in zip(numbers, numbers[1:] + [None]):
                if after != n + 1:
                    sp.sem_clear(range(first, n + 1))
                    first = after


HOST_ONLY = ("Wk", "Wq", "Wv", "Wu", "W_out", "gate_w", "up_w", "gp_w", "down_w", "up_b", "gp_b", "gate_up_proj", "down_proj",
             "shared_gate", "shared_up", "shared_down", "router_weight", "aW", "eW", "tW", "gW", "mW1")


def layer_norm(nc, X, XF, name):
    with ExitStack() as ctx:
        sb = lambda n, s, d=F32: ctx.enter_context(nc.sbuf_tensor(name + n, s, d))
        st = sb("st", [P, 4, 6]); mv = sb("mv", [P, 4, 2]); ve = sb("ve", [P, 2, 4]); rs = sb("rs", [P, 4]); mh = sb("mh", [P, 4])
        names = "stats passed aggr eps rstd done power_set"
        S = {n: ctx.enter_context(nc.semaphore(name + n)) for n in names.split()}
        with nc.Block() as block:
            @block.vector
            def _(v):
                Xv = X[:].rearrange("p (b j) c -> p b j c", b=B)
                with v.Fori(0, B) as b:
                    v.wait_ge(S["done"], b)
                    for j in range(4):
                        m = nc.vector.bn_stats(st[:, j, :], Xv[:, b, j, :])
                    m.then_inc(S["stats"], 1)
                    v.wait_ge(S["stats"], b + 1)
                    v.sem_inc(S["passed"], 1)
                    for j in range(4):
                        m = nc.vector.bn_aggr(mv[:, j, :], st[:, j, :])
                    m.then_inc(S["aggr"], 1)
                    v.wait_ge(S["aggr"], b + 1)
                    nc.vector.tensor_scalar(ve[:, 0], mv[:, :, 1], 1e-5, None, ALU.add).then_inc(S["eps"], 1)
                    v.wait_ge(S["rstd"], b + 1)
                    for j in range(4):
                        m = nc.vector.tensor_scalar(XF[:, b, j + 1, :], Xv[:, b, j, :], mv[:, j, 0:1], rs[:, j:j + 1], ALU.subtract, ALU.mult)
                    m.then_inc(S["done"], 1)

            @block.gpsimd
            def _(g):
                nc.gpsimd.memset(mh[:], -0.5).then_inc(S["power_set"], 1)
                g.wait_ge(S["power_set"], 1)
                with g.Fori(0, B) as b:
                    g.wait_ge(S["eps"], b + 1)
                    nc.gpsimd.tensor_tensor(rs[:], ve[:, 0], mh[:], ALU.pow).then_inc(S["rstd"], 1)
        clear(nc, S.values())


AH, AD, PADH = 16, 8, 32

def causal_attention(nc, X, XF, c, w):
    with ExitStack() as ctx:
        sb = lambda n, s, d=F32: ctx.enter_context(nc.sbuf_tensor("A" + n, s, d))
        ps = lambda n, s, d=F32: ctx.enter_context(nc.psum_tensor("A" + n, s, d))
        sem = lambda n: ctx.enter_context(nc.semaphore("A" + n))
        wcat = sb("wcat", [P, 384]); wu = sb("wu", [P, D]); hw = sb("hw", [P, 2, 2, AD])
        mh = sb("mh", [P, 4, 32])
        tri = sb("tri", [P, 2, P], BF16); identb = sb("identb", [P, P], BF16)
        xb = sb("xb", [P, 4, D]); xT = sb("xT", [P, 512])
        s1 = sb("s1", [P, 4, 32]); cen = sb("cen", [P, 4, 32, AD]); sq = sb("sq", [P, 4, 32, AD]); vr = sb("vr", [P, 4, 32])
        kp = sb("kp", [P, 4, AH, PADH]); qp = sb("qp", [P, 4, AH, PADH])
        kT = sb("kT", [P, 4, 512]); qT = sb("qT", [P, 4, 512])
        V9 = sb("V9", [P, 4, AH, AD + 1]); PT = sb("PT", [P, 2, 1536])
        rd = sb("rd", [P, 4, AH]); on = sb("on", [P, 4, AH, AD]); oT = sb("oT", [P, 512])
        psA = ps("psA", [P, 3072]); psB = ps("psB", [P, 1024])
        ident = c["ident"]
        S = {n: sem(n) for n in """loaded ones w_scaled xb_ready x_turned xT_ready qkv_ready v_ready h_sum h_mean h_cen h_sq h_var h_eps h_rstd
          h_norm h_gain kq_ready k_turned kT_ready q_turned qT_ready s_ready mx_done q2_turned qT2_ready st_ready exp_done
          av_done rd_ready on_ready o_turned oT_ready y_ready y_added""".split()}
        with nc.Block() as block:
            @block.sync
            def _(sp):
                L = S["loaded"]
                for k, n in enumerate(("Wk", "Wq", "Wv")):
                    sp.dma_start(wcat[:, 128 * k:128 * k + 128], w[n + "T"]).then_inc(L, 16)
                sp.dma_start(wu[:], w["WuT"]).then_inc(L, 16)
                for k, n in enumerate(("kln", "qln")):
                    sp.dma_start(hw[:, k, 0, :], rows(w[n + "_w"])).then_inc(L, 16)
                    sp.dma_start(hw[:, k, 1, :], rows(w[n + "_b"])).then_inc(L, 16)
                sp.dma_start(tri[:], w["c_tri"]).then_inc(L, 16)
                sp.dma_start(identb[:], w["c_identb"]).then_inc(L, 16)
                sp.wait_ge(L, 160)
            @block.vector
            def _(v):
                nc.vector.memset(kp[:], 0.0).then_inc(S["ones"], 1)
                nc.vector.memset(qp[:], 0.0)
                nc.vector.memset(V9[:], 1.0)
                v.wait_ge(S["ones"], 1)
                nc.vector.memset(kp[:, :, :, AD:AD + 1], 1.0)
                v.wait_ge(S["loaded"], 160)
                nc.vector.tensor_scalar(hw[:, 1], hw[:, 1], float(AD) ** -0.5, None, ALU.mult)
            @block.gpsimd
            def _(g):
                nc.gpsimd.memset(mh[:], -0.5)

        def lay(n):
            return {4: (0, 512), 3: (512, 384), 1: (896, 128), 2: (1024, 256)}[n]

        with nc.Block() as block:
            @block.tensor
            def _(pe):
                with pe.Fori(0, B) as b:
                    pe.wait_ge(S["xb_ready"], b + 1)
                    pe.wait_ge(S["exp_done"], b * 48)
                    for j in range(4):
                        m = nc.tensor.transpose(psA[:, j * P:(j + 1) * P], xb[:, j, :], ident[:])
                    m.then_inc(S["x_turned"], 1)
                    pe.wait_ge(S["xT_ready"], b + 1)
                    for j in range(4):
                        m = nc.tensor.matmul(psA[:, 512 * (j + 1):512 * (j + 1) + 384], xT[:, j * P:(j + 1) * P], wcat[:], start=True, stop=True)
                    m.then_inc(S["qkv_ready"], 1)
                    pe.wait_ge(S["kq_ready"], b + 1)
                    pe.wait_ge(S["v_ready"], b + 1)
                    for g in range(4):
                        for j in range(4):
                            m = nc.tensor.transpose(psA[:, g * 512 + j * P:g * 512 + (j + 1) * P], kp[:, j, 4 * g:4 * g + 4, :], ident[:])
                    m.then_inc(S["k_turned"], 1)
                    pe.wait_ge(S["y_added"], b)
                    for g in range(4):
                        tgt = psA[:, 2048 + g * 512:2560 + g * 512] if g < 2 else psB[:, (g - 2) * 512:(g - 1) * 512]
                        for j in range(4):
                            m = nc.tensor.transpose(tgt[:, j * P:(j + 1) * P], qp[:, j, 4 * g:4 * g + 4, :], ident[:])
                    m.then_inc(S["q_turned"], 1)
                    pe.wait_ge(S["kT_ready"], b + 1)
                    pe.wait_ge(S["qT_ready"], b + 1)
                    for h in range(AH):
                        r = slice(32 * (h % 4), 32 * (h % 4) + AD)
                        if h >= 2:
                            pe.wait_ge(S["mx_done"], b * AH + h - 1)
                        for qi in range(4):
                            o, n = lay(qi + 1)
                            o += 1536 * (h % 2)
                            nc.tensor.matmul(psA[:, o:o + n], qT[r, h // 4, qi * P:(qi + 1) * P], kT[r, h // 4, 0:n], start=True, stop=True)
                            m = nc.tensor.matmul(psA[:, o + n - P:o + n], identb[:], tri[:, 0, :], start=False, stop=True, skip_group_check=True)
                        m.then_inc(S["s_ready"], 1)
                    pe.wait_ge(S["mx_done"], (b + 1) * AH)
                    for g in range(4):
                        tgt = psA[:, g * 512:g * 512 + 512]
                        for j in range(4):
                            m = nc.tensor.transpose(tgt[:, j * P:(j + 1) * P], qp[:, j, 4 * g:4 * g + 4, :], ident[:])
                    m.then_inc(S["q2_turned"], 1)
                    pe.wait_ge(S["qT2_ready"], b + 1)

                    def st(h):
                        r = slice(32 * (h % 4), 32 * (h % 4) + AD + 1)
                        if h >= 2:
                            pe.wait_ge(S["exp_done"], b * 48 + 3 * (h - 1))
                        for kj in range(4):
                            o, n = lay(4 - kj)
                            o += 1536 * (h % 2)
                            nc.tensor.matmul(psA[:, o:o + n], kT[r, h // 4, kj * P:(kj + 1) * P], qT[r, h // 4, kj * P:512], start=True, stop=True)
                            m = nc.tensor.matmul(psA[:, o:o + P], identb[:], tri[:, 1, :], start=False, stop=True, skip_group_check=True)
                        m.then_inc(S["st_ready"], 1)

                    def av(h):
                        pe.wait_ge(S["exp_done"], b * 48 + 3 * (h + 1))
                        for qi in range(4):
                            for kj in range(qi + 1):
                                o = lay(4 - kj)[0] + (qi - kj) * P
                                oo = (qi // 2) * 512 + (qi % 2) * 144 + h * 9
                                m = nc.tensor.matmul(psB[:, oo:oo + 9], PT[:, h % 2, o:o + P], V9[:, kj, h, :],
                                                     start=(kj == 0), stop=(kj == qi))
                        m.then_inc(S["av_done"], 1)

                    st(0)
                    for h in range(1, AH):
                        st(h)
                        av(h - 1)
                    av(AH - 1)
                    pe.wait_ge(S["on_ready"], b + 1)
                    for j in range(4):
                        m = nc.tensor.transpose(psB[:, j * P:(j + 1) * P], on[:, j], ident[:])
                    m.then_inc(S["o_turned"], 1)
                    pe.wait_ge(S["oT_ready"], b + 1)
                    for j in range(4):
                        m = nc.tensor.matmul(psB[:, 512 + j * P:512 + (j + 1) * P], oT[:, j * P:(j + 1) * P], wu[:], start=True, stop=True)
                    m.then_inc(S["y_ready"], 1)

            @block.scalar
            def _(act):
                with act.Fori(0, B) as b:
                    act.wait_ge(S["x_turned"], b)
                    nc.scalar.activation(xb[:], XF[:, b, 1:5, :], ACT.Copy).then_inc(S["xb_ready"], 1)
                    act.wait_ge(S["h_cen"], b + 1)
                    act.wait_ge(S["av_done"], b * AH)
                    nc.scalar.activation(V9[:, :, :, 0:AD], psA[:, 512:2560].rearrange("p (j x) -> p j x", j=4)[:, :, 256:384].rearrange("p j (h d) -> p j h d", h=AH), ACT.Copy).then_inc(S["v_ready"], 1)
                    act.wait_ge(S["k_turned"], b + 1)
                    nc.scalar.activation(kT[:].rearrange("p a b -> p (a b)"), psA[:, 0:2048], ACT.Copy).then_inc(S["kT_ready"], 1)
                    act.wait_ge(S["q2_turned"], b + 1)
                    nc.scalar.activation(qT[:].rearrange("p a b -> p (a b)"), psA[:, 0:2048], ACT.Copy).then_inc(S["qT2_ready"], 1)
                    for h in range(AH):
                        act.wait_ge(S["st_ready"], b * AH + h + 1)
                        if h >= 2:
                            act.wait_ge(S["av_done"], b * AH + h - 1)
                        for a, n in ((0, 512), (512, 512), (1024, 256)):
                            nc.scalar.activation(PT[:, h % 2, a:a + n], psA[:, 1536 * (h % 2) + a:1536 * (h % 2) + a + n], ACT.Exp).then_inc(S["exp_done"], 1)
                    act.wait_ge(S["o_turned"], b + 1)
                    nc.scalar.activation(oT[:], psB[:, 0:512], ACT.Copy).then_inc(S["oT_ready"], 1)

            @block.vector
            def _(v):
                with v.Fori(0, B) as b:
                    v.wait_ge(S["x_turned"], b + 1)
                    v.wait_ge(S["qkv_ready"], b)
                    nc.vector.tensor_copy(xT[:], psA[:, 0:512]).then_inc(S["xT_ready"], 1)
                    v.wait_ge(S["qkv_ready"], b + 1)
                    kq = psA[:, 512:2560].rearrange("p (j x) -> p j x", j=4)[:, :, 0:256].rearrange("p j (h d) -> p j h d", d=AD)
                    nc.vector.tensor_reduce(s1[:], kq, AX.X, ALU.add).then_inc(S["h_sum"], 1)
                    v.wait_ge(S["h_sum"], b + 1)
                    nc.vector.tensor_scalar(s1[:], s1[:], -1.0 / AD, None, ALU.mult).then_inc(S["h_mean"], 1)
                    v.wait_ge(S["h_mean"], b + 1)
                    nc.vector.tensor_tensor(cen[:], kq, bcast(s1[:], 3, AD), ALU.add).then_inc(S["h_cen"], 1)
                    v.wait_ge(S["h_sq"], b + 1)
                    nc.vector.tensor_reduce(vr[:], sq[:], AX.X, ALU.add).then_inc(S["h_var"], 1)
                    v.wait_ge(S["h_var"], b + 1)
                    nc.vector.tensor_scalar(vr[:], vr[:], 1.0 / AD, 1e-5, ALU.mult, ALU.add).then_inc(S["h_eps"], 1)
                    v.wait_ge(S["h_norm"], b + 1)
                    for k in range(2):
                        x = cen[:, :, 16 * k:16 * k + 16, :]
                        nc.vector.tensor_tensor(x, x, bcast(bcast(hw[:, k, 0, :], 1, 16), 1, 4), ALU.mult).then_inc(S["h_gain"], 1)
                    for k, dst in ((0, kp), (1, qp)):
                        v.wait_ge(S["h_gain"], 2 * b + k + 1)
                        x = cen[:, :, 16 * k:16 * k + 16, :]
                        m = nc.vector.tensor_tensor(dst[:, :, :, 0:AD], x, bcast(bcast(hw[:, k, 1, :], 1, 16), 1, 4), ALU.add)
                    m.then_inc(S["kq_ready"], 1)
                    v.wait_ge(S["q_turned"], b + 1)
                    nc.vector.tensor_copy(qT[:, 0:2].rearrange("p a b -> p (a b)"), psA[:, 2048:3072])
                    nc.vector.tensor_copy(qT[:, 2:4].rearrange("p a b -> p (a b)"), psB[:]).then_inc(S["qT_ready"], 1)
                    for h in range(AH):
                        v.wait_ge(S["s_ready"], b * AH + h + 1)
                        for qi in range(4):
                            o, n = lay(qi + 1)
                            o += 1536 * (h % 2)
                            m = nc.vector.tensor_reduce(qp[:, qi, h, AD:AD + 1], psA[:, o:o + n], AX.X, ALU.max, negate=True)
                        m.then_inc(S["mx_done"], 1)
                    v.wait_ge(S["av_done"], (b + 1) * AH)
                    ov = bass.AP(psB[:].tensor, psB[:].offset, [[1024, P], [512, 2], [144, 2], [9, AH], [1, 9]])
                    for k in range(2):
                        o2 = psB[:, 512 * k:512 * k + 288].rearrange("p (a h d) -> p a h d", a=2, d=9)
                        nc.vector.reciprocal(rd[:, 2 * k:2 * k + 2], o2[:, :, :, AD]).then_inc(S["rd_ready"], 1)
                    for k in range(2):
                        o2 = psB[:, 512 * k:512 * k + 288].rearrange("p (a h d) -> p a h d", a=2, d=9)
                        v.wait_ge(S["rd_ready"], 2 * b + k + 1)
                        m = nc.vector.tensor_tensor(on[:, 2 * k:2 * k + 2], o2[:, :, :, 0:AD], bcast(rd[:, 2 * k:2 * k + 2], 3, AD), ALU.mult)
                    m.then_inc(S["on_ready"], 1)
                    v.wait_ge(S["y_ready"], b + 1)
                    xv = X[:].rearrange("p (b j) c -> p b j c", b=B)
                    nc.vector.tensor_tensor(xv[:, b], psB[:, 512:1024].rearrange("p (j c) -> p j c", j=4), xv[:, b], ALU.add).then_inc(S["y_added"], 1)

            @block.gpsimd
            def _(g):
                with g.Fori(0, B) as b:
                    g.wait_ge(S["h_cen"], b + 1)
                    nc.gpsimd.tensor_tensor(sq[:], cen[:], cen[:], ALU.mult).then_inc(S["h_sq"], 1)
                    g.wait_ge(S["h_eps"], b + 1)
                    nc.gpsimd.tensor_tensor(vr[:], vr[:], mh[:], ALU.pow).then_inc(S["h_rstd"], 1)
                    g.wait_ge(S["h_rstd"], b + 1)
                    nc.gpsimd.tensor_tensor(cen[:], cen[:], bcast(vr[:], 3, AD), ALU.mult).then_inc(S["h_norm"], 1)
        clear(nc, S.values())


def attention_consts():
    a = np.arange(128)
    tri = np.zeros((128, 2, 128), np.float32)
    tri[:, 0] = np.where(a[None, :] > a[:, None], -1e30, 0)
    tri[:, 1] = np.where(a[:, None] > a[None, :], -1e30, 0)
    return {"c_tri": tri.astype("bfloat16")}


LAYERS, LH, LD, LW = 6, 16, 64, 32
INNER = LH * LD
FF = 341
FC = (114, 114, 113)

def local_layers(nc, XF, c, w):
    with ExitStack() as ctx:
        sb = lambda n, s, d=F32: ctx.enter_context(nc.sbuf_tensor("L" + n, s, d))
        ps = lambda n, s, d=F32: ctx.enter_context(nc.psum_tensor("L" + n, s, d))
        sem = lambda n: ctx.enter_context(nc.semaphore("L" + n))
        XA = sb("XA", [P, B, 5, D])
        wqk = sb("wqk", [P, 2048]); uw = sb("uw", [P, LH, D])
        trig = sb("trig", [P, 4, 4, LD]); tab = sb("tab", [P, 4, 4, LD]); scl = sb("scl", [P, 4, LD])
        mask = sb("mask", [P, 4, 512], BF16); identb = sb("identb", [P, P], BF16)
        shift = sb("shift", [P, 2, P]); mhalf = sb("mhalf", [P, 32])
        wv = sb("wv", [P, 1024]); wvT = sb("wvT", [P, 8, P]); wo = sb("wo", [P, 8, D])
        w1 = sb("w1", [P, 2 * FF]); w2 = sb("w2", [P, 3, D]); b1 = sb("b1", [P, 6]); b2 = sb("b2", [1, D]); ones1 = sb("ones1", [1, P])
        lng = sb("lng", [P, 2])
        xs = sb("xs", [P, D]); xsT = sb("xsT", [P, P])
        sq = sb("sq", [P, 2048]); ss = sb("ss", [P, 32]); rn = sb("rn", [P, 32])
        ra = sb("ra", [P, 2, 1024]); rb = sb("rb", [P, 2, 1024])
        qT = sb("qT", [P, 8, P]); kT = sb("kT", [P, 8, LW + P])
        U = sb("U", [P, LH, D]); Up = sb("Up", [P, LH, D])
        pr = sb("pr", [P, LH, 64]); nmx = sb("nmx", [P, LH]); den = sb("den", [P, LH]); rden = sb("rden", [P, LH])
        BD = sb("BD", [P, LH, P]); BP = sb("BP", [P, LH, LW])
        psQ = ps("psQ", [P, 1024]); psK = ps("psK", [P, 1024]); psU = ps("psU", [P, 1024]); psT = ps("psT", [P, 512]); psO = ps("psO", [P, 512])
        xs4 = sq[:, 0:512].rearrange("p (j c) -> p j c", j=4); xn4 = sq[:, 512:1024].rearrange("p (j c) -> p j c", j=4)
        xnT = sq[:, 1024:1536]
        G = ra[:, :, :].rearrange("p a b -> p (a b)")[:, 0:1536].rearrange("p (a b) -> p a b", a=3)
        Hh = rb[:, :, :].rearrange("p a b -> p (a b)")[:, 0:1536].rearrange("p (a b) -> p a b", a=3)
        st = sb("st", [P, 4, 6]); mv = sb("mv", [P, 4, 2]); rs = sb("rs", [P, 4]); ve = sb("ve", [P, 4])
        ident = c["ident"]
        S = {n: sem(n) for n in """const_loaded zeroed w_loaded wv_turned wvT_ready uw_summed uw_half uw_ready scl_tab
          half_copied shifted xs_ready xs_turned xsT_ready q_ready k_ready sq_done ss_ready ss_sum rn_ready
          q_rot k_rot q_add k_add q_nrm k_nrm u_ready u_copied q_turned k_turned qT_ready kT_ready s_ready mx_ready d_ready exp_done
          den_ready rden_ready p_ready bd_ready o_ready x_added kept
          f_shift f_xs f_bn f_var f_rstd0 f_rstd f_xn f_turn f_xnT f_gate f_gelu f_a f_h f_out f_added f_half passed""".split()}
        XFv, XAv = XF, XA

        with nc.Block() as block:
            @block.sync
            def _(sp):
                sp.dma_start(trig[:], w["c_trig"].rearrange("k (j p) d -> p k j d", p=P)).then_inc(S["const_loaded"], 16)
                sp.dma_start(mask[:], w["c_lmask"]).then_inc(S["const_loaded"], 16)
                sp.dma_start(identb[:], w["c_identb"]).then_inc(S["const_loaded"], 16)
                sp.dma_start(shift[:], w["c_shift"].rearrange("k p n -> p k n")).then_inc(S["const_loaded"], 16)
                sp.wait_ge(S["const_loaded"], 64)

            @block.vector
            def _(v):
                nc.vector.memset(XA[:, :, 0, :], 0.0)
                nc.vector.memset(kT[:, :, 0:LW], 0.0)
                nc.vector.memset(Up[96:128], 0.0)
                nc.vector.memset(ones1[:], 1.0)
                nc.vector.memset(BD[:], 0.0).then_inc(S["zeroed"], 1)

            @block.gpsimd
            def _(g):
                nc.gpsimd.memset(mhalf[:], -0.5)

        with nc.Fori(0, LAYERS) as l:
            with nc.Block() as block:
                @block.sync
                def _(sp):
                    n = S["w_loaded"]
                    Wq = w["Wqkv"]
                    sp.dma_start(wqk[:], Wq[l, :, 0:2048]).then_inc(n, 16)
                    sp.dma_start(wv[:], Wq[l, :, 2048:3072]).then_inc(n, 16)
                    sp.dma_start(wo[:], w["Wo"][l].rearrange("(h p) c -> p h c", p=P)).then_inc(n, 16)
                    for k, nm in ((0, "q_scale"), (2, "k_scale")):
                        sp.dma_start(scl[:, k, :], rows(w[nm][l])).then_inc(n, 16)
                        sp.dma_start(scl[:, k + 1, 0:32], rows(w[nm][l, 32:64])).then_inc(n, 16)
                        sp.dma_start(scl[:, k + 1, 32:64], rows(w[nm][l, 0:32])).then_inc(n, 16)
                    sp.dma_start(w1[:], w["W1"][l]).then_inc(n, 16)
                    sp.dma_start(w2[0:114, 0:2, :], w["W2"][l, 0:228, :].rearrange("(k p) c -> p k c", p=114)).then_inc(n, 16)
                    sp.dma_start(w2[0:113, 2, :], w["W2"][l, 228:341, :]).then_inc(n, 16)
                    for k in range(6):
                        f0 = (k // 3) * FF + (k % 3) * 114
                        nf = FC[k % 3]
                        sp.dma_start(b1[0:nf, k:k + 1], w["b1"][l, f0:f0 + nf].unsqueeze(1)).then_inc(n, 16)
                    sp.dma_start(b2[:], w["b2"][l].unsqueeze(0)).then_inc(n, 16)
                    sp.dma_start(lng[:, 0:1], w["ln_g"][l].unsqueeze(1)).then_inc(n, 16)
                    sp.dma_start(lng[:, 1:2], w["ln_b"][l].unsqueeze(1)).then_inc(n, 16)

                @block.tensor
                def _(pe):
                    pe.wait_ge(S["w_loaded"], l * (16 * 21) + 16 * 21)
                    for j in range(8):
                        m = nc.tensor.transpose(psQ[:, j * P:(j + 1) * P], wv[:, j * P:(j + 1) * P], ident[:])
                    m.then_inc(S["wv_turned"], 1)
                    pe.wait_ge(S["wvT_ready"], l + 1)
                    for h in range(LH):
                        r = slice(64 * (h % 2), 64 * (h % 2) + 64)
                        tgt = (psK if h % 2 else psU)[:, (h // 2) * P:(h // 2 + 1) * P]
                        m = nc.tensor.matmul(tgt, wvT[r, h // 2, :], wo[r, h // 2, :], start=True, stop=True)
                    m.then_inc(S["uw_summed"], 1)

                @block.vector
                def _(v):
                    v.wait_ge(S["wv_turned"], l + 1)
                    nc.vector.tensor_copy(wvT[:].rearrange("p a b -> p (a b)"), psQ[:]).then_inc(S["wvT_ready"], 1)
                    v.wait_ge(S["uw_summed"], l + 1)
                    uv = uw[:].rearrange("p (a two) c -> p two a c", two=2)
                    nc.vector.tensor_copy(uv[:, 0], psU[:].rearrange("p (a c) -> p a c", a=8))
                    nc.vector.tensor_copy(uv[:, 1], psK[:].rearrange("p (a c) -> p a c", a=8)).then_inc(S["uw_ready"], 1)

                @block.gpsimd
                def _(g):
                    g.wait_ge(S["w_loaded"], l * (16 * 21) + 16 * 21)
                    for k in range(4):
                        nc.gpsimd.tensor_tensor(tab[:, k], trig[:, k], bcast(scl[:, k, :], 1, 4), ALU.mult).then_inc(S["scl_tab"], 1)

            with nc.Block() as block:
                @block.tensor
                def _(pe):
                    with pe.Fori(0, B) as b:
                        with pe.Fori(0, 4) as j:
                            i = l * 32 + b * 4 + j
                            pe.wait_ge(S["xsT_ready"], i)
                            nc.tensor.matmul(psT[:, 0:64], shift[:, 0, :], XF[:, b, j + 1, 64:128], start=True, stop=False)
                            nc.tensor.matmul(psT[:, 0:64], shift[:, 1, :], XF[:, b, j, 64:128], start=False, stop=True).then_inc(S["shifted"], 1)
                            pe.wait_ge(S["half_copied"], i + 1)
                            pe.wait_ge(S["xs_ready"], i + 1)
                            nc.tensor.transpose(psT[:, 0:P], xs[:], ident[:]).then_inc(S["xs_turned"], 1)
                            pe.wait_ge(S["xsT_ready"], i + 1)
                            pe.wait_ge(S["qT_ready"], i)
                            for n in range(2):
                                m = nc.tensor.matmul(psQ[:, n * 512:(n + 1) * 512], xsT[:], wqk[:, n * 512:(n + 1) * 512], start=True, stop=True)
                            m.then_inc(S["q_ready"], 1)
                            pe.wait_ge(S["kT_ready"], i)
                            for n in range(2):
                                m = nc.tensor.matmul(psK[:, n * 512:(n + 1) * 512], xsT[:], wqk[:, 1024 + n * 512:1024 + (n + 1) * 512], start=True, stop=True)
                            m.then_inc(S["k_ready"], 1)
                            pe.wait_ge(S["d_ready"], i)
                            for h2 in range(2):
                                if h2:
                                    pe.wait_ge(S["u_copied"], i * 2 + 1)
                                for n in range(2):
                                    a = h2 * 8 + n * 4
                                    m = nc.tensor.matmul(psU[:, n * 512:(n + 1) * 512], xsT[:], uw[:, a:a + 4, :], start=True, stop=True)
                                m.then_inc(S["u_ready"], 1)
                            pe.wait_ge(S["q_nrm"], i + 1)
                            pe.wait_ge(S["sq_done"], 2 * i + 2)
                            for k in range(8):
                                m = nc.tensor.transpose(psQ[:, k * P:(k + 1) * P], ra[:, 0, k * P:(k + 1) * P], ident[:])
                            m.then_inc(S["q_turned"], 1)
                            pe.wait_ge(S["k_nrm"], i + 1)
                            for k in range(8):
                                m = nc.tensor.transpose(psK[:, k * P:(k + 1) * P], ra[:, 1, k * P:(k + 1) * P], ident[:])
                            m.then_inc(S["k_turned"], 1)
                            pe.wait_ge(S["u_copied"], i * 2 + 2)
                            pe.wait_ge(S["qT_ready"], i + 1)
                            pe.wait_ge(S["kT_ready"], i + 1)
                            for par in range(2):
                                bank = psU[:, par * 512:(par + 1) * 512]
                                nc.tensor.matmul(bank, identb[:], mask[:, j, :], start=True, stop=True)
                                for hp in range(8):
                                    for wd in range(4):
                                        r = slice(64 * par, 64 * par + 64)
                                        m = nc.tensor.matmul(psU[32 * wd:32 * wd + 32, par * 512 + hp * 64:par * 512 + hp * 64 + 64],
                                                             qT[r, hp, 32 * wd:32 * wd + 32], kT[r, hp, 32 * wd:32 * wd + 64],
                                                             start=False, stop=True, skip_group_check=True)
                            m.then_inc(S["s_ready"], 1)
                            pe.wait_ge(S["bd_ready"], i + 1)
                            pe.wait_ge(S["x_added"], i)
                            for k in range(LH):
                                nc.tensor.matmul(psO[:, 0:D], BD[:, k, :], U[:, (k % 8) * 2 + k // 8, :], start=(k == 0), stop=True, skip_group_check=True)
                            for k in range(LH):
                                m = nc.tensor.matmul(psO[0:32, 0:D], BP[96:128, k, :], Up[96:128, (k % 8) * 2 + k // 8, :], start=False, stop=True, skip_group_check=True, tile_position=(96, 0))
                            m.then_inc(S["o_ready"], 1)

                @block.scalar
                def _(act):
                    with act.Fori(0, B) as b:
                        with act.Fori(0, 4) as j:
                            i = l * 32 + b * 4 + j
                            act.wait_ge(S["xs_turned"], i)
                            nc.scalar.activation(xs[:, 0:64], XF[:, b, j + 1, 0:64], ACT.Copy).then_inc(S["half_copied"], 1)
                            act.wait_ge(S["q_ready"], i + 1)
                            act.wait_ge(S["ss_ready"], i)
                            nc.scalar.activation(sq[:, 0:1024], psQ[:], ACT.Square).then_inc(S["sq_done"], 1)
                            act.wait_ge(S["k_ready"], i + 1)
                            nc.scalar.activation(sq[:, 1024:2048], psK[:], ACT.Square).then_inc(S["sq_done"], 1)
                            act.wait_ge(S["kept"], 2 * i)
                            for h2 in range(2):
                                act.wait_ge(S["u_ready"], 2 * i + h2 + 1)
                                nc.scalar.activation(U[:, 8 * h2:8 * h2 + 8, :].rearrange("p a b -> p (a b)"), psU[:], ACT.Copy).then_inc(S["u_copied"], 1)
                            act.wait_ge(S["q_turned"], i + 1)
                            act.wait_ge(S["s_ready"], i)
                            nc.scalar.activation(qT[:].rearrange("p a b -> p (a b)"), psQ[:], ACT.Copy).then_inc(S["qT_ready"], 1)
                            act.wait_ge(S["k_turned"], i + 1)
                            nc.scalar.activation(kT[:, :, LW:LW + P], psK[:].rearrange("p (a b) -> p a b", a=8), ACT.Copy).then_inc(S["kT_ready"], 1)
                            act.wait_ge(S["d_ready"], i + 1)
                            nc.scalar.activation(pr[:], pr[:], ACT.Exp).then_inc(S["exp_done"], 1)
                            act.wait_ge(S["s_ready"], i + 1)
                            nc.scalar.activation(kT[:, :, 0:LW], kT[:, :, P:P + LW], ACT.Copy).then_inc(S["kept"], 1)
                            act.wait_ge(S["o_ready"], i + 1)
                            nc.scalar.activation(Up[96:128], U[96:128], ACT.Copy).then_inc(S["kept"], 1)

                @block.vector
                def _(v):
                    with v.Fori(0, B) as b:
                        with v.Fori(0, 4) as j:
                            i = l * 32 + b * 4 + j
                            v.wait_ge(S["shifted"], i + 1)
                            v.wait_ge(S["xs_turned"], i)
                            nc.vector.tensor_copy(xs[:, 64:128], psT[:, 0:64]).then_inc(S["xs_ready"], 1)
                            v.wait_ge(S["xs_turned"], i + 1)
                            v.wait_ge(S["u_ready"], 2 * i)
                            nc.vector.tensor_copy(xsT[:], psT[:, 0:P]).then_inc(S["xsT_ready"], 1)
                            for s, psX, rdy, rot in ((0, psQ, "q_ready", "q_rot"), (1, psK, "k_ready", "k_rot")):
                                v.wait_ge(S[rdy], i + 1)
                                v.wait_ge(S["sq_done"], 2 * i + s + 1)
                                v.wait_ge(S[("q_turned", "k_turned")[s]], i)
                                p4 = psX[:].rearrange("p (h d) -> p h d", h=LH)
                                A = ra[:, s].rearrange("p (h d) -> p h d", h=LH)
                                Bb = rb[:, s].rearrange("p (h d) -> p h d", h=LH)
                                nc.vector.tensor_tensor(A, p4, bcast(tab[:, 2 * s, j, :], 1, LH), ALU.mult)
                                nc.vector.tensor_tensor(Bb[:, :, 0:32], p4[:, :, 32:64], bcast(tab[:, 2 * s + 1, j, 0:32], 1, LH), ALU.mult)
                                nc.vector.tensor_tensor(Bb[:, :, 32:64], p4[:, :, 0:32], bcast(tab[:, 2 * s + 1, j, 32:64], 1, LH), ALU.mult).then_inc(S[rot], 1)
                            v.wait_ge(S["sq_done"], 2 * i + 2)
                            v.wait_ge(S["rn_ready"], i)
                            nc.vector.tensor_reduce(ss[:], sq[:].rearrange("p (h d) -> p h d", d=LD), AX.X, ALU.add).then_inc(S["ss_sum"], 1)
                            v.wait_ge(S["ss_sum"], i + 1)
                            nc.vector.tensor_scalar(ss[:], ss[:], 1e-24, None, ALU.max).then_inc(S["ss_ready"], 1)
                            v.wait_ge(S["s_ready"], i + 1)
                            sv = psU[:].rearrange("p (h d) -> p h d", d=64)
                            nc.vector.tensor_reduce(nmx[:], sv, AX.X, ALU.max, negate=True).then_inc(S["mx_ready"], 1)
                            v.wait_ge(S["mx_ready"], i + 1)
                            nc.vector.tensor_tensor(pr[:], sv, bcast(nmx[:], 2, 64), ALU.add).then_inc(S["d_ready"], 1)
                            v.wait_ge(S["exp_done"], i + 1)
                            nc.vector.tensor_reduce(den[:], pr[:], AX.X, ALU.add).then_inc(S["den_ready"], 1)
                            v.wait_ge(S["den_ready"], i + 1)
                            nc.vector.reciprocal(rden[:], den[:]).then_inc(S["rden_ready"], 1)
                            v.wait_ge(S["p_ready"], i + 1)
                            v.wait_ge(S["o_ready"], i)
                            for wd in range(4):
                                r = slice(32 * wd, 32 * wd + 32)
                                nc.vector.transpose(BD[r, :, r.start:r.stop], pr[r, :, 32:64])
                                if wd:
                                    nc.vector.transpose(BD[r.start - 32:r.start, :, r.start:r.stop], pr[r, :, 0:32])
                            nc.vector.transpose(BP[96:128], pr[0:32, :, 0:32]).then_inc(S["bd_ready"], 1)
                            v.wait_ge(S["o_ready"], i + 1)
                            nc.vector.tensor_tensor(XA[:, b, j + 1, :], psO[:, 0:D], XF[:, b, j + 1, :], ALU.add).then_inc(S["x_added"], 1)

                @block.gpsimd
                def _(g):
                    with g.Fori(0, B) as b:
                        with g.Fori(0, 4) as j:
                            i = l * 32 + b * 4 + j
                            g.wait_ge(S["q_rot"], i + 1)
                            nc.gpsimd.tensor_tensor(ra[:, 0], ra[:, 0], rb[:, 0], ALU.add).then_inc(S["q_add"], 1)
                            g.wait_ge(S["k_rot"], i + 1)
                            nc.gpsimd.tensor_tensor(ra[:, 1], ra[:, 1], rb[:, 1], ALU.add).then_inc(S["k_add"], 1)
                            g.wait_ge(S["ss_ready"], i + 1)
                            nc.gpsimd.tensor_tensor(rn[:], ss[:], mhalf[:], ALU.pow).then_inc(S["rn_ready"], 1)
                            g.wait_ge(S["rn_ready"], i + 1)
                            g.wait_ge(S["q_add"], i + 1)
                            g.wait_ge(S["k_add"], i + 1)
                            for s, nm in ((0, "q_nrm"), (1, "k_nrm")):
                                A = ra[:, s].rearrange("p (h d) -> p h d", h=LH)
                                nc.gpsimd.tensor_tensor(A, A, bcast(rn[:, 16 * s:16 * s + 16], 2, LD), ALU.mult).then_inc(S[nm], 1)
                            g.wait_ge(S["rden_ready"], i + 1)
                            nc.gpsimd.tensor_tensor(pr[:], pr[:], bcast(rden[:], 2, 64), ALU.mult).then_inc(S["p_ready"], 1)

            with nc.Block() as block:
                @block.tensor
                def _(pe):
                    with pe.Fori(0, B) as b:
                        i = l * B + b
                        pe.wait_ge(S["f_xnT"], i)
                        for j in range(4):
                            nc.tensor.matmul(psT[:, j * 64:j * 64 + 64], shift[:, 0, :], XA[:, b, j + 1, 64:128], start=True, stop=False)
                            m = nc.tensor.matmul(psT[:, j * 64:j * 64 + 64], shift[:, 1, :], XA[:, b, j, 64:128], start=False, stop=True)
                        m.then_inc(S["f_shift"], 1)
                        pe.wait_ge(S["f_xn"], i + 1)
                        for j in range(4):
                            m = nc.tensor.transpose(psT[:, j * P:(j + 1) * P], xn4[:, j, :], ident[:])
                        m.then_inc(S["f_turn"], 1)
                        pe.wait_ge(S["f_xnT"], i + 1)
                        pe.wait_ge(S["f_h"], i)
                        banks = [psQ[:, 0:512], psQ[:, 512:1024], psK[:, 0:512], psK[:, 512:1024], psU[:, 0:512], psU[:, 512:1024]]
                        for s, nm in ((1, "f_gate"), (0, "f_a")):
                            for k in range(3):
                                f0 = s * FF + k * 114
                                m = nc.tensor.matmul(banks[s * 3 + k][0:FC[k], :], w1[:, f0:f0 + FC[k]], xnT, start=True, stop=True)
                            m.then_inc(S[nm], 1)
                        pe.wait_ge(S["f_h"], i + 1)
                        pe.wait_ge(S["f_added"], i)
                        for j in range(4):
                            o = psO[:, j * P:(j + 1) * P]
                            nc.tensor.matmul(o, ones1[:], b2[:], start=True, stop=False)
                            for k in range(3):
                                m = nc.tensor.matmul(o, Hh[0:FC[k], k, j * P:(j + 1) * P], w2[0:FC[k], k, :], start=False, stop=(k == 2))
                        m.then_inc(S["f_out"], 1)

                @block.scalar
                def _(act):
                    with act.Fori(0, B) as b:
                        i = l * B + b
                        act.wait_ge(S["f_bn"], i)
                        act.wait_ge(S["f_xn"], i)
                        nc.scalar.activation(xs4[:, :, 0:64], XA[:, b, 1:5, 0:64], ACT.Copy).then_inc(S["f_half"], 1)
                        act.wait_ge(S["f_turn"], i + 1)
                        act.wait_ge(S["f_a"], i)
                        nc.scalar.activation(xnT, psT[:], ACT.Identity, bias=lng[:, 1:2], scale=lng[:, 0:1]).then_inc(S["f_xnT"], 1)
                        act.wait_ge(S["f_gate"], i + 1)
                        act.wait_ge(S["f_h"], i)
                        banks = [psK[:, 512:1024], psU[:, 0:512], psU[:, 512:1024]]
                        for k in range(3):
                            m = nc.scalar.activation(G[0:FC[k], k, :], banks[k][0:FC[k], :], ACT.Gelu, bias=b1[0:FC[k], 3 + k:4 + k])
                        m.then_inc(S["f_gelu"], 1)

                @block.vector
                def _(v):
                    with v.Fori(0, B) as b:
                        i = l * B + b
                        v.wait_ge(S["f_shift"], i + 1)
                        nc.vector.tensor_copy(xs4[:, :, 64:128], psT[:, 0:256].rearrange("p (j c) -> p j c", j=4)).then_inc(S["f_xs"], 1)
                        v.wait_ge(S["f_xs"], i + 1)
                        v.wait_ge(S["f_half"], i + 1)
                        for j in range(4):
                            m = nc.vector.bn_stats(st[:, j, :], xs4[:, j, :])
                        m.then_inc(S["f_bn"], 1)
                        v.wait_ge(S["f_bn"], i + 1)
                        v.sem_inc(S["passed"], 1)
                        for j in range(4):
                            m = nc.vector.bn_aggr(mv[:, j, :], st[:, j, :])
                        m.then_inc(S["f_var"], 1)
                        v.wait_ge(S["f_var"], i + 1)
                        v.wait_ge(S["f_rstd"], i)
                        nc.vector.tensor_scalar(ve[:], mv[:, :, 1], 1e-5, None, ALU.add).then_inc(S["f_rstd0"], 1)
                        v.wait_ge(S["f_rstd"], i + 1)
                        v.wait_ge(S["f_turn"], i)
                        for j in range(4):
                            m = nc.vector.tensor_scalar(xn4[:, j, :], xs4[:, j, :], mv[:, j, 0:1], rs[:, j:j + 1], ALU.subtract, ALU.mult)
                        m.then_inc(S["f_xn"], 1)
                        v.wait_ge(S["f_a"], i + 1)
                        v.wait_ge(S["f_gelu"], i + 1)
                        v.wait_ge(S["f_out"], i)
                        banks = [psQ[:, 0:512], psQ[:, 512:1024], psK[:, 0:512]]
                        for k in range(3):
                            m = nc.vector.scalar_tensor_tensor(out=Hh[0:FC[k], k, :], in0=banks[k][0:FC[k], :], scalar=b1[0:FC[k], k:k + 1], in1=G[0:FC[k], k, :], op0=ALU.add, op1=ALU.mult)
                        m.then_inc(S["f_h"], 1)
                        v.wait_ge(S["f_out"], i + 1)
                        nc.vector.tensor_tensor(XF[:, b, 1:5, :], psO[:].rearrange("p (j c) -> p j c", j=4), XA[:, b, 1:5, :], ALU.add).then_inc(S["f_added"], 1)

                @block.gpsimd
                def _(g):
                    with g.Fori(0, B) as b:
                        i = l * B + b
                        g.wait_ge(S["f_xn"], i)
                        g.wait_ge(S["f_rstd0"], i + 1)
                        nc.gpsimd.tensor_tensor(rs[:], ve[:], mhalf[:, 0:4], ALU.pow).then_inc(S["f_rstd"], 1)
        clear(nc, S.values())


def local_consts():
    n = 512
    half = np.arange(0, LD, 2, dtype=np.float32)
    inv = (1.0 / (np.float32(10000.0) ** (half / LD))).astype(np.float32)
    t = np.arange(n, dtype=np.float32)
    fr = (t[:, None] * inv[None]).astype(np.float32)
    fr = np.concatenate([fr, fr], -1)
    base = ((half + np.float32(0.4 * LD)) / np.float32(1.4 * LD)).astype(np.float32)
    power = ((t - n // 2) / 16).astype(np.float32)
    sc = (base[None] ** power[:, None]).astype(np.float32)
    sc = np.concatenate([sc, sc], -1)
    cos, sin = np.cos(fr).astype(np.float32), np.sin(fr).astype(np.float32)
    sgn = np.concatenate([-np.ones(32), np.ones(32)]).astype(np.float32)
    inv_s = (1.0 / sc).astype(np.float32)
    trig = np.stack([8 * cos * sc, 8 * sin * sc * sgn, cos * inv_s, sin * inv_s * sgn]).astype(np.float32)
    m = np.zeros((128, 4, 8, 64), np.float32)
    q = np.arange(128) % 32
    for k in range(64):
        bad = (q < k - 32) | (q > k) if True else None
        m[:, :, :, k] = np.where(bad, -1e30, 0)[:, None, None]
    m[0:32, 0, :, 0:32] = -1e30
    sh = np.zeros((2, 128, 128), np.float32)
    sh[0, np.arange(127), np.arange(1, 128)] = 1
    sh[1, 127, 0] = 1
    return {"c_trig": trig, "c_lmask": m.reshape(128, 4, 512).astype("bfloat16"), "c_shift": sh,
            "c_identb": np.eye(128, dtype="bfloat16")}


SN, HALFK, SEQ = 16, 32, 512

def state_space(nc, X, XF, c, w):
    with ExitStack() as ctx:
        sb = lambda n, s, d=F32: ctx.enter_context(nc.sbuf_tensor("R" + n, s, d))
        ps = lambda n, s, d=F32: ctx.enter_context(nc.psum_tensor("R" + n, s, d))
        sem = lambda n: ctx.enter_context(nc.semaphore("R" + n))
        GD = 16
        pw = sb("pw", [P, 6, SN, SN]); Bv = sb("Bv", [P, HALFK, SN]); Cu = sb("Cu", [P, SN, SN]); Dm = sb("Dm", [P, 1])
        tmp = sb("tmp", [P, 4096]); kpad = sb("kpad", [P, 640])
        toep = sb("toep", [P, GD, SEQ])
        Y = sb("Y", [P, 32, D])
        wo = sb("wo", [P, D]); bo = sb("bo", [1, D]); ones1 = sb("ones1", [1, P]); lnp = sb("lnp", [P, 2]); flip = sb("flip", [P, P])
        st = sb("st", [P, 4, 6]); mv = sb("mv", [P, 4, 2]); ve = sb("ve", [P, 4]); rs = sb("rs", [P, 4]); mh = sb("mh", [P, 4])
        xn4 = sb("xn4", [P, 4, D]); gT = sb("gT", [P, 512])
        conv = ps("conv", [P, 512]); psT = ps("psT", [P, 512]); psO = ps("psO", [P, 512])
        scratch = nc.dram_tensor("Rkernels", (P + 1, 640), F32).ap()
        ident = c["ident"]
        S = {n: sem(n) for n in """loaded prod power bprod bvec cprod cvec kprod kern d_added zeroed stored toep_loaded conv_done conv_copied
          bn aggr eps rstd xhat turned gelu out added passed""".split()}
        with nc.Block() as block:
            @block.sync
            def _(sp):
                L = S["loaded"]
                sp.dma_start(pw[:, 0], w["A"]).then_inc(L, 16)
                sp.dma_start(Bv[:, 0, :], w["Bm"]).then_inc(L, 16)
                sp.dma_start(Cu[:, 0, :], w["Cm"]).then_inc(L, 16)
                sp.dma_start(Dm[:], w["Dm"].unsqueeze(1)).then_inc(L, 16)
                sp.dma_start(wo[:], w["W_outT"]).then_inc(L, 16)
                sp.dma_start(bo[:], w["b_out"].unsqueeze(0)).then_inc(L, 16)
                sp.dma_start(lnp[:, 0:1], w["ln_w"].unsqueeze(1)).then_inc(L, 16)
                sp.dma_start(lnp[:, 1:2], w["ln_b"].unsqueeze(1)).then_inc(L, 16)
                sp.dma_start(flip[:], w["c_flip"]).then_inc(L, 16)
                sp.wait_ge(S["d_added"], 1)
                sp.dma_start(scratch[0:P], kpad[:]).then_inc(S["stored"], 16)
                sp.wait_ge(S["stored"], 16)
            @block.gpsimd
            def _(g):
                nc.gpsimd.memset(mh[:], -0.5)
            @block.vector
            def _(v):
                nc.vector.memset(ones1[:], 1.0)
                nc.vector.memset(kpad[:], 0.0).then_inc(S["zeroed"], 1)
                v.wait_ge(S["zeroed"], 1)
                v.wait_ge(S["loaded"], 144)
                t3 = tmp[:].rearrange("p (a b c) -> p a b c", a=SN, b=SN)
                with v.Fori(0, 5) as i:
                    M = pw[:, i]
                    v.wait_ge(S["power"], i)
                    nc.vector.tensor_tensor(t3, bcast(M, 2, SN), bcast(bass.AP(M.tensor, M.offset, [list(M.ap[0]), [1, SN], [SN, SN]]), 1, SN), ALU.mult).then_inc(S["prod"], 1)
                    v.wait_ge(S["prod"], i + 1)
                    nc.vector.tensor_reduce(pw[:, i + 1], t3, AX.X, ALU.add).then_inc(S["power"], 1)
                t2 = tmp[:, 0:256].rearrange("p (a b) -> p a b", a=SN)
                v.wait_ge(S["power"], 5)
                with v.Fori(0, HALFK - 1) as i:
                    v.wait_ge(S["bvec"], i)
                    nc.vector.tensor_tensor(t2, pw[:, 0], bcast(Bv[:, i, :], 1, SN), ALU.mult).then_inc(S["bprod"], 1)
                    v.wait_ge(S["bprod"], i + 1)
                    nc.vector.tensor_reduce(Bv[:, i + 1, :], t2, AX.X, ALU.add).then_inc(S["bvec"], 1)
                M = pw[:, 5]
                MT = bass.AP(M.tensor, M.offset, [list(M.ap[0]), [1, SN], [SN, SN]])
                v.wait_ge(S["bvec"], HALFK - 1)
                with v.Fori(0, SN - 1) as i:
                    v.wait_ge(S["cvec"], i)
                    nc.vector.tensor_tensor(t2, bcast(Cu[:, i, :], 1, SN), MT, ALU.mult).then_inc(S["cprod"], 1)
                    v.wait_ge(S["cprod"], i + 1)
                    nc.vector.tensor_reduce(Cu[:, i + 1, :], t2, AX.X, ALU.add).then_inc(S["cvec"], 1)
                for k in range(2):
                    v.wait_ge(S["cvec"], SN - 1)
                    if k:
                        v.wait_ge(S["kern"], k)
                    t4 = tmp[:].rearrange("p (a b c) -> p a b c", a=8, b=HALFK)
                    nc.vector.tensor_tensor(t4, bcast(Cu[:, 8 * k:8 * k + 8, :], 2, HALFK), bcast(Bv[:], 1, 8), ALU.mult).then_inc(S["kprod"], 1)
                    v.wait_ge(S["kprod"], k + 1)
                    back = bass.AP(kpad[:].tensor, kpad[:, SEQ - 1 - 256 * k:SEQ].offset, [[640, P], [-HALFK, 8], [-1, HALFK]])
                    nc.vector.tensor_reduce(back, t4, AX.X, ALU.add).then_inc(S["kern"], 1)
                v.wait_ge(S["kern"], 2)
                nc.vector.tensor_tensor(kpad[:, SEQ - 1:SEQ], kpad[:, SEQ - 1:SEQ], Dm[:], ALU.add).then_inc(S["d_added"], 1)

        def taps(k, lag):
            return toep[:, k, SEQ - P - lag * P:SEQ - lag * P]

        with nc.Block() as block:
            @block.sync
            def _(sp):
                with sp.Fori(0, P // GD) as i:
                    sp.wait_ge(S["conv_done"], i)
                    src = bass.AP(scratch.tensor, i * (GD * 640), [[1, P], [640, GD], [1, SEQ]])
                    sp.dma_start(toep[:], src).then_inc(S["toep_loaded"], 16)
            @block.tensor
            def _(pe):
                with pe.Fori(0, P // GD) as i:
                    pe.wait_ge(S["toep_loaded"], i * 16 + 16)
                    pe.wait_ge(S["conv_copied"], i)
                    for k in range(GD):
                        o4 = conv[:, k * 32:k * 32 + 32].rearrange("p (b j) -> p b j", b=B)
                        for lag in range(4):
                            m = nc.tensor.matmul(o4[:, :, lag:4], taps(k, lag), XF[:, :, 1:5 - lag, i * GD + k], start=(lag == 0), stop=True, skip_group_check=True)
                    m.then_inc(S["conv_done"], 1)
                with pe.Fori(0, B) as b:
                    pe.wait_ge(S["xhat"], b + 1)
                    pe.wait_ge(S["gelu"], b)
                    for j in range(4):
                        m = nc.tensor.matmul(psT[:, j * P:(j + 1) * P], xn4[:, j, :], flip[:], start=True, stop=True)
                    m.then_inc(S["turned"], 1)
                    pe.wait_ge(S["gelu"], b + 1)
                    pe.wait_ge(S["added"], 2 * b)
                    for j in range(4):
                        o = psO[:, j * P:(j + 1) * P]
                        nc.tensor.matmul(o, ones1[:], bo[:], start=True, stop=False)
                        m = nc.tensor.matmul(o, gT[:, j * P:(j + 1) * P], wo[:], start=False, stop=True)
                    m.then_inc(S["out"], 1)
            @block.scalar
            def _(act):
                with act.Fori(0, P // GD) as i:
                    act.wait_ge(S["conv_done"], i + 1)
                    nc.scalar.activation(Y[:, :, bass.ds(i * GD, GD)], conv[:].rearrange("p (k t) -> p t k", k=GD), ACT.Copy).then_inc(S["conv_copied"], 1)
                with act.Fori(0, B) as b:
                    act.wait_ge(S["turned"], b + 1)
                    act.wait_ge(S["out"], b)
                    nc.scalar.activation(gT[:], psT[:], ACT.Gelu, bias=lnp[:, 1:2], scale=lnp[:, 0:1]).then_inc(S["gelu"], 1)
            @block.vector
            def _(v):
                Yv = Y[:].rearrange("p (b j) c -> p b j c", b=B)
                Xv = X[:].rearrange("p (b j) c -> p b j c", b=B)
                v.wait_ge(S["conv_copied"], P // GD)
                with v.Fori(0, B) as b:
                    for j in range(4):
                        m = nc.vector.bn_stats(st[:, j, :], Yv[:, b, j, :])
                    m.then_inc(S["bn"], 1)
                    v.wait_ge(S["bn"], b + 1)
                    v.sem_inc(S["passed"], 1)
                    for j in range(4):
                        m = nc.vector.bn_aggr(mv[:, j, :], st[:, j, :])
                    m.then_inc(S["aggr"], 1)
                    v.wait_ge(S["aggr"], b + 1)
                    v.wait_ge(S["rstd"], b)
                    nc.vector.tensor_scalar(ve[:], mv[:, :, 1], 1e-5, None, ALU.add).then_inc(S["eps"], 1)
                    v.wait_ge(S["rstd"], b + 1)
                    v.wait_ge(S["turned"], b)
                    for j in range(4):
                        m = nc.vector.tensor_scalar(xn4[:, j, :], Yv[:, b, j, :], mv[:, j, 0:1], rs[:, j:j + 1], ALU.subtract, ALU.mult)
                    m.then_inc(S["xhat"], 1)
                    v.wait_ge(S["out"], b + 1)
                    nc.vector.tensor_tensor(Xv[:, b], psO[:].rearrange("p (j c) -> p j c", j=4), Xv[:, b], ALU.add).then_inc(S["added"], 1)
                    v.wait_ge(S["added"], 2 * b + 1)
                    nc.vector.tensor_tensor(Xv[:, b], XF[:, b, 1:5, :], Xv[:, b], ALU.add).then_inc(S["added"], 1)
            @block.gpsimd
            def _(g):
                with g.Fori(0, B) as b:
                    g.wait_ge(S["xhat"], b)
                    g.wait_ge(S["eps"], b + 1)
                    nc.gpsimd.tensor_tensor(rs[:], ve[:], mh[:], ALU.pow).then_inc(S["rstd"], 1)
        clear(nc, S.values())


E1, K1, F1, FQ = 8, 2, 408, 102

def top2_experts(nc, X, XF, c, w):
    with ExitStack() as ctx:
        sb = lambda n, s, d=F32: ctx.enter_context(nc.sbuf_tensor("E" + n, s, d))
        ps = lambda n, s, d=F32: ctx.enter_context(nc.psum_tensor("E" + n, s, d))
        sem = lambda n: ctx.enter_context(nc.semaphore("E" + n))
        up = sb("up", [P, E1, F1]); gp = sb("gp", [P, E1, F1]); dn = sb("dn", [FQ, E1, 4, D])
        ub = sb("ub", [FQ, E1, 4]); gb = sb("gb", [FQ, E1, 4]); db = sb("db", [1, E1, D])
        gw = sb("gw", [P, E1]); gbias = sb("gbias", [1, E1]); ones1 = sb("ones1", [1, P])
        before = sb("before", [P, E1, E1])
        xb = sb("xb", [P, 4, D]); xT = sb("xT", [P, 512])
        lg = sb("lg", [P, 4, E1]); mx = sb("mx", [P, 4]); sm = sb("sm", [P, 4]); sc = sb("sc", [P, 4, E1])
        gt = sb("gt", [P, 4, E1, E1]); eq = sb("eq", [P, 4, E1, E1]); rk = sb("rk", [P, 4, E1]); comb = sb("comb", [P, 4, E1])
        us = sb("us", [FQ, 2, 512]); hg = sb("hg", [FQ, 2, 512]); hs = sb("hs", [FQ, 2, 4, 512])
        psUG = ps("psUG", [P, 2, 2, 512]); psT = ps("psT", [P, 512]); psR = ps("psR", [P, 512]); psO = ps("psO", [P, 2, 512])
        ident = c["ident"]
        S = {n: sem(n) for n in """loaded ones xb_ready turned xT_ready logits r_max r_sub r_exp r_sum r_rec r_score r_cmp r_eqm r_or r_rank
          r_sel r_tot r_inv comb_ready u_ready g_ready us_ready hg_ready hs_ready out_ready added""".split()}
        with nc.Block() as block:
            @block.sync
            def _(sp):
                L = S["loaded"]
                sp.dma_start(gw[:], w["gate_wT"]).then_inc(L, 16)
                sp.dma_start(gbias[:], w["gate_b"].unsqueeze(0)).then_inc(L, 16)
                sp.dma_start(before[:], w["c_before"]).then_inc(L, 16)
                for a, n in ((up, "up_wT"), (gp, "gp_wT")):
                    sp.dma_start(a[:], w[n].rearrange("e d f -> d e f")).then_inc(L, 16)
                sp.dma_start(dn[:].rearrange("p e k d -> p (e k) d"), w["down_wT"].rearrange("e (k p) d -> p (e k) d", p=FQ)).then_inc(L, 16)
                for a, n in ((ub, "up_b4"), (gb, "gp_b4")):
                    sp.dma_start(a[:], w[n]).then_inc(L, 16)
                sp.dma_start(db[:], w["down_b"].unsqueeze(0)).then_inc(L, 16)
                sp.wait_ge(L, 144)
            @block.vector
            def _(v):
                nc.vector.memset(ones1[:], 1.0)

        def us_of(k): return us[:, k % 2, :]
        with nc.Block() as block:
            @block.tensor
            def _(pe):
                with pe.Fori(0, B) as b:
                    pe.wait_ge(S["xb_ready"], b + 1)
                    for j in range(4):
                        m = nc.tensor.transpose(psT[:, j * P:(j + 1) * P], xb[:, j, :], ident[:])
                    m.then_inc(S["turned"], 1)
                    pe.wait_ge(S["xT_ready"], b + 1)
                    for j in range(4):
                        nc.tensor.matmul(psR[:, 8 * j:8 * j + 8], ones1[:], gbias[:], start=True, stop=False)
                        m = nc.tensor.matmul(psR[:, 8 * j:8 * j + 8], xT[:, j * P:(j + 1) * P], gw[:], start=False, stop=True)
                    m.then_inc(S["logits"], 1)

                    def inner(e):
                        for k in range(4):
                            n = e * 4 + k
                            if n >= 2:
                                pe.wait_ge(S["hg_ready"], b * 32 + n - 1)
                            else:
                                pe.wait_ge(S["hg_ready"], b * 32)
                            nc.tensor.matmul(psUG[0:FQ, n % 2, 0, :], up[:, e, k * FQ:(k + 1) * FQ], xT[:], start=True, stop=True).then_inc(S["u_ready"], 1)
                            nc.tensor.matmul(psUG[0:FQ, n % 2, 1, :], gp[:, e, k * FQ:(k + 1) * FQ], xT[:], start=True, stop=True).then_inc(S["g_ready"], 1)

                    def down(e):
                        pe.wait_ge(S["hs_ready"], b * 32 + 4 * (e + 1))
                        if e >= 2:
                            pe.wait_ge(S["added"], b * 8 + e - 1)
                        else:
                            pe.wait_ge(S["added"], b * 8)
                        for j in range(4):
                            o = psO[:, e % 2, j * P:(j + 1) * P]
                            nc.tensor.matmul(o, ones1[:], db[:, e, :], start=True, stop=False)
                            for k in range(4):
                                m = nc.tensor.matmul(o, hs[:, e % 2, k, j * P:(j + 1) * P], dn[:, e, k, :], start=False, stop=(k == 3))
                        m.then_inc(S["out_ready"], 1)

                    inner(0)
                    for e in range(1, E1):
                        inner(e)
                        down(e - 1)
                    down(E1 - 1)

            @block.scalar
            def _(act):
                with act.Fori(0, B) as b:
                    act.wait_ge(S["turned"], b)
                    nc.scalar.activation(xb[:], XF[:, b, 1:5, :], ACT.Copy).then_inc(S["xb_ready"], 1)
                    act.wait_ge(S["r_sub"], b + 1)
                    nc.scalar.activation(lg[:], lg[:], ACT.Exp).then_inc(S["r_exp"], 1)
                    for n in range(32):
                        act.wait_ge(S["u_ready"], b * 32 + n + 1)
                        if n < 2:
                            act.wait_ge(S["hg_ready"], b * 32)
                        else:
                            act.wait_ge(S["hg_ready"], b * 32 + n - 1)
                        nc.scalar.activation(us[:, n % 2, :], psUG[0:FQ, n % 2, 0, :], ACT.Identity, bias=ub[:, n // 4, n % 4:n % 4 + 1]).then_inc(S["us_ready"], 1)
                        act.wait_ge(S["hg_ready"], b * 32 + n + 1)
                        if n // 4 >= 2:
                            act.wait_ge(S["out_ready"], b * 8 + n // 4 - 1)
                        nc.scalar.activation(hs[:, (n // 4) % 2, n % 4, :], hg[:, n % 2, :], ACT.Silu).then_inc(S["hs_ready"], 1)

            @block.vector
            def _(v):
                Xv = X[:].rearrange("p (b j) c -> p b j c", b=B)
                with v.Fori(0, B) as b:
                    v.wait_ge(S["turned"], b + 1)
                    v.wait_ge(S["out_ready"], b * 8)
                    nc.vector.tensor_copy(xT[:], psT[:]).then_inc(S["xT_ready"], 1)
                    v.wait_ge(S["logits"], b + 1)
                    lp = psR[:, 0:32].rearrange("p (j e) -> p j e", j=4)
                    nc.vector.tensor_reduce(mx[:], lp, AX.X, ALU.max, negate=True).then_inc(S["r_max"], 1)
                    v.wait_ge(S["r_max"], b + 1)
                    nc.vector.tensor_tensor(lg[:], lp, bcast(mx[:], 2, E1), ALU.add).then_inc(S["r_sub"], 1)
                    v.wait_ge(S["r_exp"], b + 1)
                    nc.vector.tensor_reduce(sm[:], lg[:], AX.X, ALU.add).then_inc(S["r_sum"], 1)
                    v.wait_ge(S["r_sum"], b + 1)
                    nc.vector.reciprocal(sm[:], sm[:]).then_inc(S["r_rec"], 1)
                    v.wait_ge(S["r_rec"], b + 1)
                    nc.vector.tensor_tensor(sc[:], lg[:], bcast(sm[:], 2, E1), ALU.mult).then_inc(S["r_score"], 1)
                    v.wait_ge(S["r_score"], b + 1)
                    for j in range(4):
                        other, own = bcast(sc[:, j, :], 1, E1), bcast(sc[:, j, :], 2, E1)
                        nc.vector.tensor_tensor(gt[:, j], other, own, ALU.is_gt)
                        m = nc.vector.tensor_tensor(eq[:, j], other, own, ALU.is_equal)
                    m.then_inc(S["r_cmp"], 1)
                    v.wait_ge(S["r_cmp"], b + 1)
                    nc.vector.tensor_tensor(eq[:], eq[:], bcast(before[:], 1, 4), ALU.mult).then_inc(S["r_eqm"], 1)
                    v.wait_ge(S["r_eqm"], b + 1)
                    nc.vector.tensor_tensor(gt[:], gt[:], eq[:], ALU.add).then_inc(S["r_or"], 1)
                    v.wait_ge(S["r_or"], b + 1)
                    nc.vector.tensor_reduce(rk[:], gt[:], AX.X, ALU.add).then_inc(S["r_rank"], 1)
                    v.wait_ge(S["r_rank"], b + 1)
                    nc.vector.scalar_tensor_tensor(out=sc[:], in0=rk[:], scalar=K1 - 0.5, in1=sc[:], op0=ALU.is_lt, op1=ALU.mult).then_inc(S["r_sel"], 1)
                    v.wait_ge(S["r_sel"], b + 1)
                    nc.vector.tensor_reduce(sm[:], sc[:], AX.X, ALU.add).then_inc(S["r_tot"], 1)
                    v.wait_ge(S["r_tot"], b + 1)
                    nc.vector.tensor_scalar(sm[:], sm[:], 1e-20, None, ALU.add).then_inc(S["r_inv"], 1)
                    v.wait_ge(S["r_inv"], 2 * b + 1)
                    nc.vector.reciprocal(sm[:], sm[:]).then_inc(S["r_inv"], 1)
                    v.wait_ge(S["r_inv"], 2 * b + 2)
                    nc.vector.tensor_tensor(comb[:], sc[:], bcast(sm[:], 2, E1), ALU.mult).then_inc(S["comb_ready"], 1)

                    def add(e):
                        v.wait_ge(S["out_ready"], b * 8 + e + 1)
                        if e == 0:
                            v.wait_ge(S["comb_ready"], b + 1)
                        if e:
                            v.wait_ge(S["added"], b * 8 + e)
                        for j in range(4):
                            m = nc.vector.scalar_tensor_tensor(out=Xv[:, b, j], in0=psO[:, e % 2, j * P:(j + 1) * P], scalar=comb[:, j, e:e + 1], in1=Xv[:, b, j], op0=ALU.mult, op1=ALU.add)
                        m.then_inc(S["added"], 1)

                    for n in range(32):
                        v.wait_ge(S["us_ready"], b * 32 + n + 1)
                        v.wait_ge(S["g_ready"], b * 32 + n + 1)
                        if n < 2:
                            v.wait_ge(S["hs_ready"], b * 32)
                        else:
                            v.wait_ge(S["hs_ready"], b * 32 + n - 1)
                        nc.vector.scalar_tensor_tensor(out=hg[:, n % 2, :], in0=psUG[0:FQ, n % 2, 1, :], scalar=gb[:, n // 4, n % 4:n % 4 + 1], in1=us[:, n % 2, :], op0=ALU.add, op1=ALU.mult).then_inc(S["hg_ready"], 1)
                        if n >= 8 and n % 4 == 3:
                            add(n // 4 - 2)
                    add(E1 - 2)
                    add(E1 - 1)
        clear(nc, S.values())


def top2_consts():
    a = np.arange(E1)
    return {"c_before": np.broadcast_to((a[None, :] < a[:, None]).astype(np.float32), (128, 8, 8)).copy()}

def top2_layout(w):
    return {"gate_wT": np.ascontiguousarray(w["gate_w"].T),
            "up_wT": np.ascontiguousarray(w["up_w"].transpose(0, 2, 1)), "gp_wT": np.ascontiguousarray(w["gp_w"].transpose(0, 2, 1)),
            "down_wT": np.ascontiguousarray(w["down_w"].transpose(0, 2, 1)),
            "up_b4": np.ascontiguousarray(w["up_b"].reshape(8, 4, FQ).transpose(2, 0, 1)), "gp_b4": np.ascontiguousarray(w["gp_b"].reshape(8, 4, FQ).transpose(2, 0, 1))}


NH, ND, NPAD, NW = 16, 8, 32, 8
KS = P + 2 * NW
QS = P + 2 * NPAD

def banded_attention(nc, X, XF, c, w):
    with ExitStack() as ctx:
        sb = lambda n, s, d=F32: ctx.enter_context(nc.sbuf_tensor("N" + n, s, d))
        ps = lambda n, s, d=F32: ctx.enter_context(nc.psum_tensor("N" + n, s, d))
        sem = lambda n: ctx.enter_context(nc.semaphore("N" + n))
        wqkv = sb("wqkv", [P, 384]); wp = sb("wp", [P, D]); bp = sb("bp", [1, D]); ones1 = sb("ones1", [1, P])
        mq = sb("mq", [P, 3, 2 * KS], BF16); mk = sb("mk", [P, 2 * QS], BF16); identb = sb("identb", [P, P], BF16)
        xb = sb("xb", [P, 4, D]); xT = sb("xT", [P, 512])
        kp = sb("kp", [P, 4, NH, NPAD]); qp = sb("qp", [P, 4, NH, NPAD])
        kT = sb("kT", [P, 4, 512 + 2 * NPAD]); qT = sb("qT", [P, 4, 512 + 2 * NPAD])
        V9 = sb("V9", [P, 4, NH, ND + 1]); PT = sb("PT", [P, 2, 4, 2, QS])
        rd = sb("rd", [P, 4, NH]); on = sb("on", [P, 4, NH, ND]); oT = sb("oT", [P, 512])
        psA = ps("psA", [P, 6, 512]); psB = ps("psB", [P, 1024])
        ident = c["ident"]
        S = {n: sem(n) for n in """loaded zeroed xb_ready x_turned xT_ready qkv_ready q_scaled v_ready kq_ready k_turned kT_ready
          q_turned qT_ready s_ready mx_done q2_turned qT2_ready st_ready exp_done
          av_done rd_ready on_ready o_turned oT_ready y_ready y_added""".split()}
        with nc.Block() as block:
            @block.sync
            def _(sp):
                L = S["loaded"]
                sp.dma_start(wqkv[:], w["Wqkv"]).then_inc(L, 16)
                sp.dma_start(wp[:], w["Wproj"]).then_inc(L, 16)
                sp.dma_start(bp[:], w["bproj"].unsqueeze(0)).then_inc(L, 16)
                sp.dma_start(mq[:], w["c_bandq"]).then_inc(L, 16)
                sp.dma_start(mk[:], w["c_bandk"]).then_inc(L, 16)
                sp.dma_start(identb[:], w["c_identb"]).then_inc(L, 16)
                sp.wait_ge(L, 96)
            @block.vector
            def _(v):
                nc.vector.memset(kp[:], 0.0).then_inc(S["zeroed"], 1)
                nc.vector.memset(qp[:], 0.0)
                nc.vector.memset(kT[:], 0.0)
                nc.vector.memset(qT[:], 0.0)
                nc.vector.memset(V9[:], 1.0)
                nc.vector.memset(ones1[:], 1.0)
                v.wait_ge(S["zeroed"], 1)
                nc.vector.memset(kp[:, :, :, ND:ND + 1], 1.0)

        def pair(n):
            return n % 4 + 8 * (n // 4), n % 4 + 8 * (n // 4) + 4

        with nc.Block() as block:
            @block.tensor
            def _(pe):
                with pe.Fori(0, B) as b:
                    pe.wait_ge(S["xb_ready"], b + 1)
                    pe.wait_ge(S["exp_done"], b * 32)
                    for j in range(4):
                        m = nc.tensor.transpose(psA[:, 0, j * P:(j + 1) * P], xb[:, j, :], ident[:])
                    m.then_inc(S["x_turned"], 1)
                    pe.wait_ge(S["xT_ready"], b + 1)
                    for j in range(4):
                        m = nc.tensor.matmul(psA[:, j + 1, 0:384], xT[:, j * P:(j + 1) * P], wqkv[:], start=True, stop=True)
                    m.then_inc(S["qkv_ready"], 1)
                    pe.wait_ge(S["kq_ready"], b + 1)
                    pe.wait_ge(S["v_ready"], b + 1)
                    for g in range(4):
                        for j in range(4):
                            m = nc.tensor.transpose(psA[:, g, j * P:(j + 1) * P], kp[:, j, 4 * g:4 * g + 4, :], ident[:])
                    m.then_inc(S["k_turned"], 1)
                    pe.wait_ge(S["y_added"], b)
                    for g in range(4):
                        tgt = psA[:, 4 + g, :] if g < 2 else psB[:, (g - 2) * 512:(g - 1) * 512]
                        for j in range(4):
                            m = nc.tensor.transpose(tgt[:, j * P:(j + 1) * P], qp[:, j, 4 * g:4 * g + 4, :], ident[:])
                    m.then_inc(S["q_turned"], 1)
                    pe.wait_ge(S["kT_ready"], b + 1)
                    pe.wait_ge(S["qT_ready"], b + 1)
                    for n in range(32):
                        j = n // 8
                        if n >= 6:
                            pe.wait_ge(S["mx_done"], b * 32 + n - 5)
                        bank = psA[:, n % 6, :]
                        nc.tensor.matmul(bank[:, 0:2 * KS], identb[:], mq[:, (0, 1, 1, 2)[j], :], start=True, stop=True)
                        for a, h in enumerate(pair(n % 8)):
                            r = slice(32 * (h % 4), 32 * (h % 4) + ND)
                            k0 = NPAD + j * P - NW
                            m = nc.tensor.matmul(bank[:, a * KS:(a + 1) * KS], qT[r, h // 4, NPAD + j * P:NPAD + (j + 1) * P], kT[r, h // 4, k0:k0 + KS],
                                                 start=False, stop=True, skip_group_check=True)
                        m.then_inc(S["s_ready"], 1)
                    pe.wait_ge(S["mx_done"], (b + 1) * 32)
                    for g in range(4):
                        for j in range(4):
                            m = nc.tensor.transpose(psA[:, g, j * P:(j + 1) * P], qp[:, j, 4 * g:4 * g + 4, :], ident[:])
                    m.then_inc(S["q2_turned"], 1)
                    pe.wait_ge(S["qT2_ready"], b + 1)

                    def st(n):
                        hp, kj = n // 4, n % 4
                        if n >= 6:
                            pe.wait_ge(S["exp_done"], b * 32 + n - 5)
                        bank = psA[:, n % 6, 0:2 * QS]
                        nc.tensor.matmul(bank, identb[:], mk[:], start=True, stop=True)
                        for a, h in enumerate(pair(hp)):
                            r = slice(32 * (h % 4), 32 * (h % 4) + ND + 1)
                            m = nc.tensor.matmul(bank[:, a * QS:(a + 1) * QS], kT[r, h // 4, NPAD + kj * P:NPAD + (kj + 1) * P], qT[r, h // 4, kj * P:kj * P + QS],
                                                 start=False, stop=True, skip_group_check=True)
                        m.then_inc(S["st_ready"], 1)

                    def av(hp):
                        pe.wait_ge(S["exp_done"], b * 32 + 4 * (hp + 1))
                        for a, h in enumerate(pair(hp)):
                            for j in range(4):
                                oo = (j // 2) * 512 + (j % 2) * 144 + h * 9
                                m = nc.tensor.matmul(psB[:, oo:oo + 9], PT[:, hp % 2, j, a, NPAD:NPAD + P], V9[:, j, h, :], start=True, stop=True)
                                if j > 0:
                                    m = nc.tensor.matmul(psB[0:32, oo:oo + 9], PT[:, hp % 2, j - 1, a, NPAD + P:QS], V9[:, j - 1, h, :], start=False, stop=True, skip_group_check=True)
                                if j < 3:
                                    m = nc.tensor.matmul(psB[96:128, oo:oo + 9], PT[:, hp % 2, j + 1, a, 0:NPAD], V9[:, j + 1, h, :], start=False, stop=True, skip_group_check=True, tile_position=(0, 96))
                        m.then_inc(S["av_done"], 1)

                    for n in range(32):
                        st(n)
                        if n >= 7 and n % 4 == 3:
                            av(n // 4 - 1)
                    av(7)
                    pe.wait_ge(S["on_ready"], b + 1)
                    for j in range(4):
                        m = nc.tensor.transpose(psB[:, j * P:(j + 1) * P], on[:, j], ident[:])
                    m.then_inc(S["o_turned"], 1)
                    pe.wait_ge(S["oT_ready"], b + 1)
                    for j in range(4):
                        o = psB[:, 512 + j * P:512 + (j + 1) * P]
                        nc.tensor.matmul(o, ones1[:], bp[:], start=True, stop=False)
                        m = nc.tensor.matmul(o, oT[:, j * P:(j + 1) * P], wp[:], start=False, stop=True)
                    m.then_inc(S["y_ready"], 1)

            @block.scalar
            def _(act):
                with act.Fori(0, B) as b:
                    act.wait_ge(S["x_turned"], b)
                    nc.scalar.activation(xb[:], XF[:, b, 1:5, :], ACT.Copy).then_inc(S["xb_ready"], 1)
                    act.wait_ge(S["kq_ready"], b + 1)
                    nc.scalar.activation(V9[:, :, :, 0:ND], psA[:, 1:5, 256:384].rearrange("p j (h d) -> p j h d", h=NH), ACT.Copy).then_inc(S["v_ready"], 1)
                    act.wait_ge(S["k_turned"], b + 1)
                    nc.scalar.activation(kT[:, :, NPAD:NPAD + 512], psA[:, 0:4, :], ACT.Copy).then_inc(S["kT_ready"], 1)
                    act.wait_ge(S["q2_turned"], b + 1)
                    nc.scalar.activation(qT[:, :, NPAD:NPAD + 512], psA[:, 0:4, :], ACT.Copy).then_inc(S["qT2_ready"], 1)
                    for n in range(32):
                        act.wait_ge(S["st_ready"], b * 32 + n + 1)
                        if n // 4 >= 2:
                            act.wait_ge(S["av_done"], b * 8 + n // 4 - 1)
                        nc.scalar.activation(PT[:, (n // 4) % 2, n % 4], psA[:, n % 6, 0:2 * QS].rearrange("p (h q) -> p h q", h=2), ACT.Exp).then_inc(S["exp_done"], 1)
                    act.wait_ge(S["o_turned"], b + 1)
                    nc.scalar.activation(oT[:], psB[:, 0:512], ACT.Copy).then_inc(S["oT_ready"], 1)

            @block.vector
            def _(v):
                with v.Fori(0, B) as b:
                    v.wait_ge(S["x_turned"], b + 1)
                    v.wait_ge(S["qkv_ready"], b)
                    nc.vector.tensor_copy(xT[:], psA[:, 0, :]).then_inc(S["xT_ready"], 1)
                    v.wait_ge(S["qkv_ready"], b + 1)
                    nc.vector.tensor_scalar(qp[:, :, :, 0:ND], psA[:, 1:5, 0:128].rearrange("p j (h d) -> p j h d", h=NH), float(ND) ** -0.5, None, ALU.mult).then_inc(S["q_scaled"], 1)
                    nc.vector.tensor_copy(kp[:, :, :, 0:ND], psA[:, 1:5, 128:256].rearrange("p j (h d) -> p j h d", h=NH)).then_inc(S["kq_ready"], 1)
                    v.wait_ge(S["q_turned"], b + 1)
                    nc.vector.tensor_copy(qT[:, 0:2, NPAD:NPAD + 512], psA[:, 4:6, :])
                    nc.vector.tensor_copy(qT[:, 2:4, NPAD:NPAD + 512], psB[:].rearrange("p (g t) -> p g t", g=2)).then_inc(S["qT_ready"], 1)
                    for n in range(32):
                        j, h0 = n // 8, pair(n % 8)[0]
                        v.wait_ge(S["s_ready"], b * 32 + n + 1)
                        nc.vector.tensor_reduce(qp[:, j, h0:h0 + 5:4, ND], psA[:, n % 6, 0:2 * KS].rearrange("p (h k) -> p h k", h=2), AX.X, ALU.max, negate=True).then_inc(S["mx_done"], 1)
                    v.wait_ge(S["av_done"], (b + 1) * 8)
                    for k in range(2):
                        o2 = psB[:, 512 * k:512 * k + 288].rearrange("p (a h d) -> p a h d", a=2, d=9)
                        nc.vector.reciprocal(rd[:, 2 * k:2 * k + 2], o2[:, :, :, ND]).then_inc(S["rd_ready"], 1)
                    for k in range(2):
                        o2 = psB[:, 512 * k:512 * k + 288].rearrange("p (a h d) -> p a h d", a=2, d=9)
                        v.wait_ge(S["rd_ready"], 2 * b + k + 1)
                        m = nc.vector.tensor_tensor(on[:, 2 * k:2 * k + 2], o2[:, :, :, 0:ND], bcast(rd[:, 2 * k:2 * k + 2], 3, ND), ALU.mult)
                    m.then_inc(S["on_ready"], 1)
                    v.wait_ge(S["y_ready"], b + 1)
                    xv = X[:].rearrange("p (b j) c -> p b j c", b=B)
                    nc.vector.tensor_tensor(xv[:, b], psB[:, 512:1024].rearrange("p (j c) -> p j c", j=4), xv[:, b], ALU.add).then_inc(S["y_added"], 1)
        clear(nc, S.values())


def banded_consts():
    q = np.arange(P)[:, None]
    kk = np.arange(KS)[None] - NW
    near = np.where(np.abs(kk - q) <= NW, 0, -1e30)
    a = np.zeros((P, 3, 2, KS), np.float32)
    for t in range(3):
        m = near.copy()
        if t == 0:
            m[:, :NW] = -1e30
        if t == 2:
            m[:, KS - NW:] = -1e30
        a[:, t] = m[:, None]
    qq = np.arange(QS)[None] - NPAD
    k = np.where(np.abs(qq - q) <= NW, 0, -1e30)
    return {"c_bandq": a.reshape(P, 3, 2 * KS).astype("bfloat16"), "c_bandk": np.tile(k, 2).astype("bfloat16")}


E2, K2, HP2, CAP = 32, 8, 16, 256
LIMIT, ROUTED = 7.0, 2.5

def capped_experts(nc, X, XF, c, w):
    with ExitStack() as ctx:
        sb = lambda n, s, d=F32: ctx.enter_context(nc.sbuf_tensor("C" + n, s, d))
        ps = lambda n, s, d=F32: ctx.enter_context(nc.psum_tensor("C" + n, s, d))
        sem = lambda n: ctx.enter_context(nc.semaphore("C" + n))
        NP = HP2 + 2
        gw = sb("gw", [P, NP, P]); uw = sb("uw", [P, NP, P]); dw = sb("dw", [P, NP, D])
        rw = sb("rw", [P, E2]); bias = sb("bias", [P, E2]); spread = sb("spread", [E2, HP2, P])
        tri = sb("tri", [P, P], BF16); ones = sb("ones", [P, P], BF16); cum = sb("cum", [P, E2], BF16)
        xb = sb("xb", [P, 4, D]); xT = sb("xT", [P, 512])
        sc = sb("sc", [P, 4, E2]); sel = sb("sel", [P, 4, E2]); top = sb("top", [P, 4, 8]); rep = sb("rep", [P, 4, E2])
        mask = sb("mask", [P, 4, E2]); maskb = sb("maskb", [P, 4, E2], BF16); csum = sb("csum", [P, E2]); kept = sb("kept", [P, 4, E2]); sw = sb("sw", [P, 4, E2])
        tot = sb("tot", [P, 4]); comb = sb("comb", [P, 4, E2]); wT = sb("wT", [E2, 512])
        gs = sb("gs", [P, 2, 512]); us = sb("us", [P, 2, 512]); gl = sb("gl", [P, 2, 512]); hs = sb("hs", [P, 2, 512])
        psG = ps("psG", [P, 2, 512]); psU = ps("psU", [P, 2, 512]); psW = ps("psW", [P, 2, 512]); psT = ps("psT", [P, 512]); psO = ps("psO", [P, 512])
        ident = c["ident"]
        S = {n: sem(n) for n in """loaded ones xb_ready turned xT_ready logits score r_sel r_top r_rep r_mask r_maskb pos r_kept r_sw r_tot r_eps r_inv
          r_scale comb_ready comb_turned wT_ready r_csum r_cum g_ready u_ready w_ready g_min u_clip silu mixed h_ready out_ready added""".split()}
        with nc.Block() as block:
            @block.sync
            def _(sp):
                L = S["loaded"]
                for a, n in ((gw, "gate"), (uw, "up")):
                    sp.dma_start(a[:, 0:HP2, :], w[n + "_pairs"]).then_inc(L, 16)
                    sp.dma_start(a[:, HP2:NP, :], w["shared_" + n + "T"].rearrange("d (k p) -> d k p", k=2)).then_inc(L, 16)
                sp.dma_start(dw[:, 0:HP2, :], w["down_pairs"].rearrange("k p d -> p k d")).then_inc(L, 16)
                sp.dma_start(dw[:, HP2:NP, :], w["shared_downT"].rearrange("(k p) d -> p k d", k=2)).then_inc(L, 16)
                sp.dma_start(rw[:], w["router_weightT"]).then_inc(L, 16)
                sp.dma_start(bias[:], rows(w["e_score_correction_bias"])).then_inc(L, 16)
                sp.dma_start(spread[:], w["c_spread"]).then_inc(L, 16)
                sp.dma_start(tri[:], w["c_earlier"]).then_inc(L, 16)
                sp.wait_ge(L, 160)
            @block.vector
            def _(v):
                nc.vector.memset(ones[:], 1.0)
                nc.vector.memset(cum[:], 0.0)

        with nc.Block() as block:
            @block.tensor
            def _(pe):
                with pe.Fori(0, B) as b:
                    pe.wait_ge(S["xb_ready"], b + 1)
                    pe.wait_ge(S["added"], b)
                    for j in range(4):
                        m = nc.tensor.transpose(psT[:, j * P:(j + 1) * P], xb[:, j, :], ident[:])
                    m.then_inc(S["turned"], 1)
                    pe.wait_ge(S["xT_ready"], b + 1)
                    for j in range(4):
                        m = nc.tensor.matmul(psT[:, E2 * j:E2 * j + E2], xT[:, j * P:(j + 1) * P], rw[:], start=True, stop=True)
                    m.then_inc(S["logits"], 1)
                    pe.wait_ge(S["r_maskb"], b + 1)
                    pe.wait_ge(S["score"], b + 1)
                    for j in range(4):
                        o = psO[:, E2 * j:E2 * j + E2]
                        nc.tensor.matmul(o, tri[:], maskb[:, j, :], start=True, stop=False)
                        for k in range(j):
                            nc.tensor.matmul(o, ones[:], maskb[:, k, :], start=False, stop=False)
                        m = nc.tensor.matmul(o, ones[:], cum[:], start=False, stop=True)
                    m.then_inc(S["pos"], 1)
                    pe.wait_ge(S["comb_ready"], b + 1)
                    for j in range(4):
                        m = nc.tensor.transpose(psT[0:E2, j * P:(j + 1) * P], comb[:, j, :], ident[:])
                    m.then_inc(S["comb_turned"], 1)
                    pe.wait_ge(S["wT_ready"], b + 1)

                    def inner(n):
                        q = n % 2
                        if n >= 2:
                            pe.wait_ge(S["h_ready"], b * NP + n - 1)
                        else:
                            pe.wait_ge(S["h_ready"], b * NP)
                        nc.tensor.matmul(psG[:, q, :], gw[:, n, :], xT[:], start=True, stop=True).then_inc(S["g_ready"], 1)
                        nc.tensor.matmul(psU[:, q, :], uw[:, n, :], xT[:], start=True, stop=True).then_inc(S["u_ready"], 1)
                        if n < HP2:
                            nc.tensor.matmul(psW[:, q, :], spread[:, n, :], wT[:], start=True, stop=True).then_inc(S["w_ready"], 1)

                    def down(n):
                        pe.wait_ge(S["h_ready"], b * NP + n + 1)
                        for j in range(4):
                            m = nc.tensor.matmul(psO[:, j * P:(j + 1) * P], hs[:, n % 2, j * P:(j + 1) * P], dw[:, n, :],
                                                 start=(n == 0 and j == 0), stop=True, skip_group_check=True)
                        m.then_inc(S["out_ready"], 1)

                    inner(0)
                    for n in range(1, NP):
                        inner(n)
                        down(n - 1)
                    down(NP - 1)

            @block.scalar
            def _(act):
                with act.Fori(0, B) as b:
                    act.wait_ge(S["turned"], b)
                    nc.scalar.activation(xb[:], XF[:, b, 1:5, :], ACT.Copy).then_inc(S["xb_ready"], 1)
                    act.wait_ge(S["logits"], b + 1)
                    nc.scalar.activation(sc[:], psT[:, 0:4 * E2].rearrange("p (j e) -> p j e", j=4), ACT.Sigmoid).then_inc(S["score"], 1)
                    act.wait_ge(S["comb_turned"], b + 1)
                    nc.scalar.activation(wT[:], psT[0:E2, :], ACT.Copy).then_inc(S["wT_ready"], 1)
                    for n in range(NP):
                        q = n % 2
                        if n < HP2:
                            act.wait_ge(S["g_min"], b * HP2 + n + 1)
                            if n >= 2:
                                act.wait_ge(S["mixed"], b * HP2 + n - 1)
                            nc.scalar.activation(gl[:, q, :], gs[:, q, :], ACT.Silu).then_inc(S["silu"], 1)
                        else:
                            act.wait_ge(S["g_ready"], b * NP + n + 1)
                            act.wait_ge(S["mixed"], b * HP2 + n - 1 if n == HP2 else b * HP2 + HP2)
                            nc.scalar.activation(gl[:, q, :], psG[:, q, :], ACT.Silu).then_inc(S["silu"], 1)

            @block.gpsimd
            def _(g):
                with g.Fori(0, B) as b:
                    for n in range(HP2):
                        g.wait_ge(S["silu"], b * NP + n + 1)
                        g.wait_ge(S["u_clip"], b * HP2 + n + 1)
                        nc.gpsimd.tensor_tensor(us[:, n % 2, :], us[:, n % 2, :], gl[:, n % 2, :], ALU.mult).then_inc(S["mixed"], 1)

            @block.vector
            def _(v):
                Xv = X[:].rearrange("p (b j) c -> p b j c", b=B)
                with v.Fori(0, B) as b:
                    v.wait_ge(S["turned"], b + 1)
                    nc.vector.tensor_copy(xT[:], psT[:]).then_inc(S["xT_ready"], 1)
                    v.wait_ge(S["score"], b + 1)
                    nc.vector.tensor_tensor(sel[:], sc[:], bcast(bias[:], 1, 4), ALU.add).then_inc(S["r_sel"], 1)
                    v.wait_ge(S["r_sel"], b + 1)
                    v.sem_inc(S["ones"], 1)
                    for j in range(4):
                        m = nc.vector.max(top[:, j, :], sel[:, j, :])
                    m.then_inc(S["r_top"], 1)
                    v.wait_ge(S["r_top"], b + 1)
                    v.sem_inc(S["ones"], 1)
                    for j in range(4):
                        m = nc.vector.match_replace(rep[:, j, :], top[:, j, :], sel[:, j, :], -3e38)
                    m.then_inc(S["r_rep"], 1)
                    v.wait_ge(S["r_rep"], b + 1)
                    nc.vector.tensor_tensor(mask[:], sel[:], rep[:], ALU.not_equal).then_inc(S["r_mask"], 1)
                    v.wait_ge(S["r_mask"], b + 1)
                    nc.vector.tensor_copy(maskb[:], mask[:]).then_inc(S["r_maskb"], 1)
                    nc.vector.tensor_tensor(sw[:], sc[:], mask[:], ALU.mult).then_inc(S["r_sw"], 1)
                    v.wait_ge(S["r_sw"], b + 1)
                    nc.vector.tensor_reduce(tot[:], sw[:], AX.X, ALU.add).then_inc(S["r_tot"], 1)
                    v.wait_ge(S["r_tot"], b + 1)
                    nc.vector.tensor_scalar(tot[:], tot[:], 1e-20, None, ALU.add).then_inc(S["r_eps"], 1)
                    v.wait_ge(S["r_eps"], b + 1)
                    nc.vector.reciprocal(tot[:], tot[:]).then_inc(S["r_inv"], 1)
                    v.wait_ge(S["r_inv"], b + 1)
                    nc.vector.tensor_tensor(sw[:], sw[:], bcast(tot[:], 2, E2), ALU.mult).then_inc(S["r_scale"], 1)
                    v.wait_ge(S["pos"], b + 1)
                    v.wait_ge(S["r_scale"], b + 1)
                    nc.vector.scalar_tensor_tensor(out=kept[:], in0=psO[:, 0:4 * E2].rearrange("p (j e) -> p j e", j=4), scalar=CAP - 0.5, in1=sw[:], op0=ALU.is_lt, op1=ALU.mult).then_inc(S["r_kept"], 1)
                    v.wait_ge(S["r_kept"], b + 1)
                    nc.vector.tensor_scalar(comb[:], kept[:], ROUTED, None, ALU.mult).then_inc(S["comb_ready"], 1)
                    nc.vector.tensor_reduce(csum[:], mask[:].rearrange("p j e -> p e j"), AX.X, ALU.add).then_inc(S["r_csum"], 1)
                    v.wait_ge(S["r_csum"], b + 1)
                    nc.vector.tensor_tensor(cum[:], cum[:], csum[:], ALU.add).then_inc(S["r_cum"], 1)
                    def mix(n):
                        q = n % 2
                        if n < HP2:
                            v.wait_ge(S["mixed"], b * HP2 + n + 1)
                            v.wait_ge(S["w_ready"], b * HP2 + n + 1)
                            if n >= 2:
                                v.wait_ge(S["out_ready"], b * NP + n - 1)
                            nc.vector.tensor_tensor(hs[:, q, :], psW[:, q, :], us[:, q, :], ALU.mult).then_inc(S["h_ready"], 1)
                        else:
                            v.wait_ge(S["silu"], b * NP + n + 1)
                            v.wait_ge(S["u_ready"], b * NP + n + 1)
                            v.wait_ge(S["out_ready"], b * NP + n - 1)
                            nc.vector.tensor_tensor(hs[:, q, :], psU[:, q, :], gl[:, q, :], ALU.mult).then_inc(S["h_ready"], 1)

                    for n in range(NP):
                        q = n % 2
                        if n < HP2:
                            v.wait_ge(S["g_ready"], b * NP + n + 1)
                            if n >= 2:
                                v.wait_ge(S["silu"], b * NP + n - 1)
                            nc.vector.tensor_scalar(gs[:, q, :], psG[:, q, :], LIMIT, None, ALU.min).then_inc(S["g_min"], 1)
                            v.wait_ge(S["u_ready"], b * NP + n + 1)
                            v.wait_ge(S["h_ready"], b * NP + (n - 1 if n >= 2 else 0))
                            nc.vector.tensor_scalar(us[:, q, :], psU[:, q, :], LIMIT, -LIMIT, ALU.min, ALU.max).then_inc(S["u_clip"], 1)
                        if n >= 1:
                            mix(n - 1)
                    mix(NP - 1)
                    v.wait_ge(S["out_ready"], (b + 1) * NP)
                    nc.vector.tensor_tensor(Xv[:, b], psO[:].rearrange("p (j c) -> p j c", j=4), Xv[:, b], ALU.add).then_inc(S["added"], 1)
        clear(nc, S.values())


def capped_consts():
    a = np.arange(P)
    s = np.zeros((E2, HP2, P), np.float32)
    for p in range(HP2):
        s[2 * p, p, 0:64] = 1
        s[2 * p + 1, p, 64:] = 1
    return {"c_spread": s, "c_earlier": (a[:, None] < a[None, :]).astype("bfloat16")}

def capped_layout(w):
    gu, t = w["gate_up_proj"], np.ascontiguousarray
    pairs = lambda x: t(x.reshape(HP2, 2, 64, 128).transpose(3, 0, 1, 2).reshape(128, HP2, 128))
    return {"gate_pairs": pairs(gu[:, :64]), "up_pairs": pairs(gu[:, 64:]),
            "down_pairs": t(w["down_proj"].transpose(0, 2, 1).reshape(HP2, 128, 128)),
            "shared_gateT": t(w["shared_gate"].T), "shared_upT": t(w["shared_up"].T), "shared_downT": t(w["shared_down"].T),
            "router_weightT": t(w["router_weight"].T)}


QI, QB = 352, 16
ROWS4 = 88
QSTEPS = 12
DOWN = ((0, 128), (128, 128), (256, 96))

class Steps:
    def __init__(self, eng, sem, base):
        self.eng, self.sem, self.base, self.n = eng, sem, base, 0

    def __call__(self, ins):
        self.n += 1
        ins.then_inc(self.sem, 1)
        self.eng.wait_ge(self.sem, self.base + self.n)

def fp4(nc, v, step, src, out, t, signs_of, signs_ready):
    p, nb = src.shape[0], src.shape[1]
    am, xn, ab, hi, lo = (t[k][0:p, 0:nb] for k in ("am", "xn", "ab", "hi", "lo"))
    rc = t["rc"][0:p, 0:nb]
    step(nc.vector.tensor_reduce(am, src, AX.X, ALU.max, apply_absolute_value=True))
    step(nc.vector.tensor_scalar(am, am, 1.0 / 6.0, 1e-12, ALU.mult, ALU.max))
    step(nc.vector.reciprocal(rc, am))
    step(nc.vector.tensor_tensor(xn, src, bcast(rc, 2, QB), ALU.mult))
    signs_of()
    step(nc.vector.scalar_tensor_tensor(out=ab, in0=xn, scalar=-1.0, in1=xn, op0=ALU.mult, op1=ALU.max))
    nc.vector.tensor_scalar(hi, ab, 5.0, 2.0, ALU.is_gt, ALU.mult)
    step(nc.vector.tensor_scalar(lo, ab, 0.25, None, ALU.is_gt))
    nc.vector.scalar_tensor_tensor(out=hi, in0=ab, scalar=3.5, in1=hi, op0=ALU.is_gt, op1=ALU.add)
    step(nc.vector.scalar_tensor_tensor(out=lo, in0=ab, scalar=0.75, in1=lo, op0=ALU.is_gt, op1=ALU.add))
    nc.vector.scalar_tensor_tensor(out=hi, in0=ab, scalar=2.5, in1=hi, op0=ALU.is_gt, op1=ALU.add)
    step(nc.vector.scalar_tensor_tensor(out=lo, in0=ab, scalar=1.25, in1=lo, op0=ALU.is_gt, op1=ALU.add))
    step(nc.vector.scalar_tensor_tensor(out=lo, in0=ab, scalar=1.75, in1=lo, op0=ALU.is_gt, op1=ALU.add))
    step(nc.vector.scalar_tensor_tensor(out=lo, in0=lo, scalar=0.5, in1=hi, op0=ALU.mult, op1=ALU.add))
    signs_ready()
    step(nc.vector.tensor_tensor(lo, lo, t["sg"][0:p, 0:nb], ALU.mult))
    step(nc.vector.tensor_tensor(out, lo, bcast(am, 2, QB), ALU.mult))

def fp4_ffn(nc, X, XF, c, w):
    with ExitStack() as ctx:
        sb = lambda n, s, d=F32: ctx.enter_context(nc.sbuf_tensor("F" + n, s, d))
        ps = lambda n, s, d=F32: ctx.enter_context(nc.psum_tensor("F" + n, s, d))
        sem = lambda n: ctx.enter_context(nc.semaphore("F" + n))
        raw = sb("raw", [P, 3, 32, QB])
        wq = sb("wq", [P, 3, 32, QB])
        gT = sb("gT", [P, QI]); uT = sb("uT", [P, QI]); dT = sb("dT", [P, 3, D])
        t = {k: sb(k, [P, 32, QB]) for k in ("xn", "ab", "hi", "lo", "sg")}
        t.update({k: sb(k, [P, 32]) for k in ("am", "rc")})
        xq = sb("xq", [P, 32, QB]); xqT = sb("xqT", [P, 512])
        sl = sb("sl", [P, QI]); h = sb("h", [P, 22, QB]); hq = sb("hq", [P, 22, QB]); hT = sb("hT", [P, 3, P])
        psT = ps("psT", [P, 512]); psG = ps("psG", [P, 2, 512]); psU = ps("psU", [P, 2, 512]); psH = ps("psH", [P, 512]); psO = ps("psO", [P, 512]); psW = ps("psW", [P, 512])
        ident = c["ident"]
        S = {n: sem(n) for n in """loaded wsteps wxn wsign wquant wturned wcopied steps xn sign xq_ready x_turned xT_ready g_ready u_ready
          silu h_ready hq_ready h_turned hT_ready out added""".split()}
        NBW = (32, 32, 22)

        def wsrc(k): return raw[0:ROWS4, k] if k < 2 else raw[:, 2, 0:22]
        def wdst(k): return wq[0:ROWS4, k] if k < 2 else wq[:, 2, 0:22]
        with nc.Block() as block:
            @block.sync
            def _(sp):
                L = S["loaded"]
                for k, n in enumerate(("w_gate", "w_up")):
                    sp.dma_start(raw[0:ROWS4, k].rearrange("p (a b) c -> p a (b c)", a=4), w[n].rearrange("(a p) c -> p a c", p=ROWS4)).then_inc(L, 16)
                sp.dma_start(raw[:, 2, 0:22].rearrange("p b c -> p (b c)"), w["w_down"]).then_inc(L, 16)
                sp.wait_ge(L, 48)
            @block.vector
            def _(v):
                v.wait_ge(S["loaded"], 48)
                step = Steps(v, S["wsteps"], 0)
                for k in range(3):
                    fp4(nc, v, step, wsrc(k), wdst(k), t, lambda: v.sem_inc(S["wxn"], 1), lambda: v.wait_ge(S["wsign"], k + 1))
                v.sem_inc(S["wquant"], 1)
                for k in range(3):
                    v.wait_ge(S["wturned"], k + 1)
                    if k < 2:
                        nc.vector.tensor_copy((gT, uT)[k][:], psT[:, 0:QI]).then_inc(S["wcopied"], 1)
                    else:
                        nc.vector.tensor_copy(dT[:, 0:2, :], psT[:, 0:256].rearrange("p (a b) -> p a b", a=2))
                        nc.vector.tensor_copy(dT[0:96, 2, :], psT[0:96, 256:384]).then_inc(S["wcopied"], 1)
            @block.scalar
            def _(act):
                for k in range(3):
                    act.wait_ge(S["wxn"], k + 1)
                    nb = NBW[k]
                    p = ROWS4 if k < 2 else P
                    nc.scalar.activation(t["sg"][0:p, 0:nb], t["xn"][0:p, 0:nb], ACT.Sign).then_inc(S["wsign"], 1)
            @block.tensor
            def _(pe):
                pe.wait_ge(S["wquant"], 1)
                for k in range(3):
                    if k:
                        pe.wait_ge(S["wcopied"], k)
                    if k < 2:
                        for a in range(4):
                            m = nc.tensor.transpose(psT[:, a * ROWS4:(a + 1) * ROWS4], wq[0:ROWS4, k, 8 * a:8 * a + 8, :], ident[0:ROWS4, 0:ROWS4])
                    else:
                        flat = wq[:, 2].rearrange("p b c -> p (b c)")
                        for a, (f0, nf) in enumerate(DOWN):
                            m = nc.tensor.transpose(psT[0:nf, a * P:(a + 1) * P], flat[:, f0:f0 + nf], ident[:])
                    m.then_inc(S["wturned"], 1)

        with nc.Block() as block:
            @block.tensor
            def _(pe):
                with pe.Fori(0, B) as b:
                    pe.wait_ge(S["xq_ready"], b + 1)
                    for j in range(4):
                        m = nc.tensor.transpose(psT[:, j * P:(j + 1) * P], xq[:, 8 * j:8 * j + 8, :], ident[:])
                    m.then_inc(S["x_turned"], 1)
                    pe.wait_ge(S["xT_ready"], b + 1)

                    def inner(j):
                        pe.wait_ge(S["h_ready"], b * 4 + (j - 1 if j >= 2 else 0))
                        nc.tensor.matmul(psG[:, j % 2, 0:QI], xqT[:, j * P:(j + 1) * P], gT[:], start=True, stop=True).then_inc(S["g_ready"], 1)
                        nc.tensor.matmul(psU[:, j % 2, 0:QI], xqT[:, j * P:(j + 1) * P], uT[:], start=True, stop=True).then_inc(S["u_ready"], 1)

                    inner(0)
                    for j in range(4):
                        if j < 3:
                            inner(j + 1)
                        pe.wait_ge(S["hq_ready"], b * 4 + j + 1)
                        flat = hq[:].rearrange("p b c -> p (b c)")
                        for a, (f0, nf) in enumerate(DOWN):
                            m = nc.tensor.transpose(psH[0:nf, a * P:(a + 1) * P], flat[:, f0:f0 + nf], ident[:])
                        m.then_inc(S["h_turned"], 1)
                        pe.wait_ge(S["hT_ready"], b * 4 + j + 1)
                        if j == 0:
                            pe.wait_ge(S["added"], b)
                        for a, (f0, nf) in enumerate(DOWN):
                            m = nc.tensor.matmul(psO[:, j * P:(j + 1) * P], hT[0:nf, a, :], dT[0:nf, a, :], start=(a == 0), stop=(a == 2))
                        m.then_inc(S["out"], 1)
            @block.scalar
            def _(act):
                with act.Fori(0, B) as b:
                    act.wait_ge(S["xn"], b * 5 + 1)
                    nc.scalar.activation(t["sg"][:], t["xn"][:], ACT.Sign).then_inc(S["sign"], 1)
                    for j in range(4):
                        act.wait_ge(S["g_ready"], b * 4 + j + 1)
                        act.wait_ge(S["h_ready"], b * 4 + j)
                        nc.scalar.activation(sl[:], psG[:, j % 2, 0:QI], ACT.Silu).then_inc(S["silu"], 1)
                        act.wait_ge(S["xn"], b * 5 + j + 2)
                        nc.scalar.activation(t["sg"][:, 0:22], t["xn"][:, 0:22], ACT.Sign).then_inc(S["sign"], 1)
                        act.wait_ge(S["h_turned"], b * 4 + j + 1)
                        act.wait_ge(S["out"], b * 4 + j)
                        nc.scalar.activation(hT[:, 0:2, :], psH[:, 0:256].rearrange("p (a q) -> p a q", a=2), ACT.Copy)
                        nc.scalar.activation(hT[0:96, 2, :], psH[0:96, 256:384], ACT.Copy).then_inc(S["hT_ready"], 1)
            @block.vector
            def _(v):
                Xv = X[:].rearrange("p (b j) c -> p b j c", b=B)
                with v.Fori(0, B) as b:
                    step = Steps(v, S["steps"], b * (QSTEPS * 5))
                    v.wait_ge(S["x_turned"], b)
                    src = XF[:, b, 1:5, :].rearrange("p j (n q) -> p (j n) q", q=QB)
                    fp4(nc, v, step, src, xq[:], t, lambda: v.sem_inc(S["xn"], 1), lambda: v.wait_ge(S["sign"], b * 5 + 1))
                    v.sem_inc(S["xq_ready"], 1)
                    v.wait_ge(S["x_turned"], b + 1)
                    v.wait_ge(S["u_ready"], 4 * b)
                    nc.vector.tensor_copy(xqT[:], psT[:]).then_inc(S["xT_ready"], 1)
                    for j in range(4):
                        v.wait_ge(S["silu"], b * 4 + j + 1)
                        v.wait_ge(S["u_ready"], b * 4 + j + 1)
                        nc.vector.tensor_tensor(h[:].rearrange("p a b -> p (a b)"), psU[:, j % 2, 0:QI], sl[:], ALU.mult).then_inc(S["h_ready"], 1)
                        v.wait_ge(S["h_ready"], b * 4 + j + 1)
                        v.wait_ge(S["h_turned"], b * 4 + j)
                        fp4(nc, v, step, h[:], hq[:], t, lambda: v.sem_inc(S["xn"], 1), lambda: v.wait_ge(S["sign"], b * 5 + j + 2))
                        v.sem_inc(S["hq_ready"], 1)
                    v.wait_ge(S["out"], (b + 1) * 4)
                    nc.vector.tensor_tensor(Xv[:, b], psO[:].rearrange("p (j c) -> p j c", j=4), Xv[:, b], ALU.add).then_inc(S["added"], 1)
        clear(nc, S.values())


MD, CH, NC, G = 32, 64, 8, 2

def neural_memory(nc, X, XF, c, w):
    with ExitStack() as ctx:
        sb = lambda n, s, d=F32: ctx.enter_context(nc.sbuf_tensor("M" + n, s, d))
        ps = lambda n, s, d=F32: ctx.enter_context(nc.psum_tensor("M" + n, s, d))
        sem = lambda n: ctx.enter_context(nc.semaphore("M" + n))
        wp = sb("wp", [P, 6, MD]); cw = sb("cw", [P, 3, 4]); cb = sb("cb", [P, 6])
        mean = sb("mean", [P, P]); pick = sb("pick", [P, 4, CH]); pick1 = sb("pick1", [P, 4]); bd = sb("bd", [P, P])
        start = sb("start", [P, 2, 512]); inj = sb("inj", [CH, 512])
        half = sb("half", [CH, 4]); mhalf = sb("mhalf", [P, 4])
        woT = sb("woT", [P, D]); gwT = sb("gwT", [P, D]); gb = sb("gb", [1, D]); ones1 = sb("ones1", [1, P]); ng = sb("ng", [P, D])
        xb = sb("xb", [P, 4, D]); xT = sb("xT", [P, B, 512])
        T = {k: sb(k, [P, G, 512]) for k in ("K", "V", "Q", "QW", "QS", "AW", "AS", "AS0", "RET")}
        mw = sb("mw", [CH, G, 4, 512]); mse = sb("mse", [CH, G, NC, 4]); th = sb("th", [CH, G, NC, 4]); k2 = sb("k2", [CH, G, NC, 4])
        kqm = sb("kqm", [CH, G, NC, 4 * CH])
        kw = sb("kw", [CH, G, NC, P]); ks = sb("ks", [CH, G, NC, P])
        W3 = sb("W3", [P, G, 3, P]); S3 = sb("S3", [P, G, 3, P])
        ident = c["ident"]
        S = {n: sem(n) for n in """loaded zeroed xb_ready turned xT_ready projected conv gates signs absd sexp slog splus a_mean om_ready e_mean et_ready
          scans sel_a sel_e m64_ready theta th_copied qbd_ready kq_ready kqm_ready ktok_ready kw_ready chain x_kept""".split()}
        kinds = ("k", "v", "q", "a", "e", "t")
        with nc.Block() as block:
            @block.sync
            def _(sp):
                L = S["loaded"]
                for k, n in enumerate(("WkT", "WvT", "WqT", "aWT", "eWT", "tWT")):
                    sp.dma_start(wp[:, k, :], w[n]).then_inc(L, 16)
                for r in range(4):
                    q = slice(32 * r, 32 * r + 32)
                    for k, n in enumerate(("ck", "cv", "cq")):
                        sp.dma_start(cw[q, k, :], w[n + "w"]).then_inc(L, 16)
                        sp.dma_start(cb[q, k:k + 1], w[n + "b"].unsqueeze(1)).then_inc(L, 16)
                    for k, n in enumerate(("ab", "eb", "tb")):
                        sp.dma_start(cb[q, 3 + k:4 + k], w[n].unsqueeze(1)).then_inc(L, 16)
                    sp.dma_start(woT[q], w["WoT"]).then_inc(L, 16)
                for a, n in ((mean, "c_mean"), (pick, "c_pick"), (pick1, "c_pick1"), (bd, "c_bd"), (start, "c_start"), (inj, "c_inj"), (gwT, "gWT"), (gb, None), (ng, None)):
                    src = w[n] if n else (w["gb"].unsqueeze(0) if a is gb else rows(w["norm_g"]))
                    sp.dma_start(a[:], src).then_inc(L, 16)
                sp.wait_ge(S["zeroed"], 1)
                for g in range(G):
                    for r in range(4):
                        q = slice(32 * r, 32 * r + 32)
                        for k, n in enumerate(("mW1T", "mW2T", "mW2")):
                            sp.dma_start(W3[q, g, k, q], w[n]).then_inc(L, 16)
                sp.wait_ge(L, 16 * (6 + 40 + 9 + 24))
            @block.vector
            def _(v):
                nc.vector.memset(W3[:], 0.0).then_inc(S["zeroed"], 1)
                nc.vector.memset(S3[:], 0.0)
                nc.vector.memset(half[:], 0.5)
                nc.vector.memset(mhalf[:], -0.5)
                nc.vector.memset(ones1[:], 1.0)

        with ExitStack() as inner:
            isb = lambda n, s: inner.enter_context(nc.sbuf_tensor("M" + n, s, F32))
            xs4 = isb("xs4", [P, 4, 512])
            sg = isb("sg", [P, 3, 512]); rl = isb("rl", [P, 512]); om = isb("om", [P, 512]); et = isb("et", [P, 512]); dn = isb("dn", [P, 2, 512])
            m64 = isb("m64", [CH, 2, 512]); s64 = isb("s64", [CH, 512])
            qbd = isb("qbd", [P, NC, 4, CH]); ksq = isb("ksq", [CH, NC, P])
            psP = inner.enter_context(nc.psum_tensor("MpsP", [P, 6, 512], F32)); psT = inner.enter_context(nc.psum_tensor("MpsT", [P, 512], F32)); psM = inner.enter_context(nc.psum_tensor("MpsM", [P, 512], F32))
            kstage = rl
            with nc.Block() as block:
                @block.tensor
                def _(pe):
                    with pe.Fori(0, G) as g:
                        for r in range(4):
                            n = g * 4 + r
                            pe.wait_ge(S["xb_ready"], n + 1)
                            pe.wait_ge(S["xT_ready"], n)
                            for j in range(4):
                                m = nc.tensor.transpose(psT[:, j * P:(j + 1) * P], xb[:, j, :], ident[:])
                            m.then_inc(S["turned"], 1)
                        pe.wait_ge(S["xT_ready"], g * 4 + 4)
                        pe.wait_ge(S["kqm_ready"], g)
                        pe.wait_ge(S["kw_ready"], g)
                        for k in range(6):
                            for r in range(4):
                                m = nc.tensor.matmul(psP[32 * r:32 * r + 32, k, :], wp[:, k, :], xs4[:, r, :], start=True, stop=True, tile_position=(0, 32 * r))
                        m.then_inc(S["projected"], 1)
                        pe.wait_ge(S["signs"], g + 1)
                        pe.wait_ge(S["th_copied"], g)
                        nc.tensor.matmul(psM[:], mean[:], sg[:, 0, :], start=True, stop=True).then_inc(S["a_mean"], 1)
                        pe.wait_ge(S["om_ready"], g + 1)
                        nc.tensor.matmul(psM[:], mean[:], sg[:, 1, :], start=True, stop=True).then_inc(S["e_mean"], 1)
                        pe.wait_ge(S["et_ready"], g + 1)
                        for r in range(4):
                            pe.wait_ge(S["m64_ready"], 2 * (g * 4 + r))
                            nc.tensor.matmul(psM[0:CH, :], pick[:, r, :], sg[:, 0, :], start=True, stop=True).then_inc(S["sel_a"], 1)
                            pe.wait_ge(S["m64_ready"], 2 * (g * 4 + r) + 1)
                            nc.tensor.matmul(psM[0:CH, :], pick[:, r, :], sg[:, 1, :], start=True, stop=True).then_inc(S["sel_e"], 1)
                        pe.wait_ge(S["m64_ready"], 2 * (g * 4 + 4))
                        pe.wait_ge(S["splus"], g + 1)
                        for k in range(NC):
                            m = nc.tensor.matmul(psM[0:CH, 4 * k:4 * k + 4], sg[:, 2, k * CH:(k + 1) * CH], pick1[:], start=True, stop=True)
                        m.then_inc(S["theta"], 1)
                        pe.wait_ge(S["qbd_ready"], g + 1)
                        for k in range(NC):
                            o = psP[0:CH, k // 2, (k % 2) * 256:(k % 2) * 256 + 256]
                            m = nc.tensor.matmul(o, kstage[:, k * CH:(k + 1) * CH], qbd[:, k], start=True, stop=True)
                        m.then_inc(S["kq_ready"], 1)
                        for k in range(NC):
                            m = nc.tensor.transpose(psP[0:CH, 4 + k // 4, (k % 4) * P:(k % 4 + 1) * P], kstage[:, k * CH:(k + 1) * CH], ident[:])
                        m.then_inc(S["ktok_ready"], 1)

                @block.scalar
                def _(act):
                    with act.Fori(0, G) as g:
                        for r in range(4):
                            n = g * 4 + r
                            act.wait_ge(S["turned"], n)
                            nc.scalar.activation(xb[:], XF[:, n, 1:5, :], ACT.Copy).then_inc(S["xb_ready"], 1)
                        act.wait_ge(S["xT_ready"], g * 4 + 4)
                        nc.scalar.activation(xT[:, bass.ds(g * 4, 4), :], xs4[:], ACT.Copy).then_inc(S["x_kept"], 1)
                        act.wait_ge(S["projected"], g + 1)
                        act.wait_ge(S["theta"], g)
                        for k in range(2):
                            nc.scalar.activation(sg[:, k, :], psP[:, 3 + k, :], ACT.Sigmoid, bias=cb[:, 3 + k:4 + k])
                        nc.scalar.activation(sg[:, 2, :], psP[:, 5, :], ACT.Abs, bias=cb[:, 5:6]).then_inc(S["signs"], 1)
                        act.wait_ge(S["signs"], g + 1)
                        nc.scalar.activation(sg[:, 2, :], sg[:, 2, :], ACT.Exp, scale=-1.0).then_inc(S["sexp"], 1)
                        act.wait_ge(S["sexp"], g + 1)
                        nc.scalar.activation(sg[:, 2, :], sg[:, 2, :], ACT.Ln, bias=1.0).then_inc(S["slog"], 1)

                @block.vector
                def _(v):
                    nc.vector.memset(qbd[:], 0.0).then_inc(S["zeroed"], 1)
                    with v.Fori(0, G) as g:
                        step = Steps(v, S["chain"], g * 27)
                        for r in range(4):
                            n = g * 4 + r
                            v.wait_ge(S["turned"], n + 1)
                            v.wait_ge(S["projected"], g)
                            v.wait_ge(S["x_kept"], g)
                            nc.vector.tensor_copy(xs4[:, r, :], psT[:]).then_inc(S["xT_ready"], 1)
                        v.wait_ge(S["projected"], g + 1)
                        outs = [T[k][:, g, :] for k in "KVQ"]
                        for k in range(3):
                            m = nc.vector.tensor_scalar(outs[k], psP[:, k, :], cw[:, k, 3:4], cb[:, k:k + 1], ALU.mult, ALU.add)
                        step(m)
                        for back in (1, 2, 3):
                            for k in range(3):
                                m = nc.vector.scalar_tensor_tensor(out=outs[k][:, back:512], in0=psP[:, k, 0:512 - back], scalar=cw[:, k, 3 - back:4 - back], in1=outs[k][:, back:512], op0=ALU.mult, op1=ALU.add)
                            step(m)
                        v.wait_ge(S["signs"], g + 1)
                        step(nc.vector.tensor_scalar(rl[:], psP[:, 5, :], cb[:, 5:6], 0.0, ALU.add, ALU.max))
                        v.wait_ge(S["slog"], g + 1)
                        nc.vector.tensor_tensor(sg[:, 2, :], sg[:, 2, :], rl[:], ALU.add).then_inc(S["splus"], 1)
                        v.wait_ge(S["a_mean"], g + 1)
                        nc.vector.tensor_scalar(om[:], psM[:], -0.1, 1.0, ALU.mult, ALU.add).then_inc(S["om_ready"], 1)
                        v.wait_ge(S["e_mean"], g + 1)
                        nc.vector.tensor_scalar(et[:], psM[:], 0.9, 0.05, ALU.mult, ALU.add).then_inc(S["et_ready"], 1)
                        v.wait_ge(S["et_ready"], g + 1)
                        notfirst, first = start[:, 0, :], start[:, 1, :]
                        aw, as_, as0 = T["AW"][:, g, :], T["AS"][:, g, :], T["AS0"][:, g, :]
                        nc.vector.tensor_tensor(dn[:, 0], om[:], notfirst, ALU.mult)
                        step(nc.vector.tensor_tensor(dn[:, 1], om[:], first, ALU.mult))
                        step(nc.vector.tensor_tensor_scan(aw, dn[:, 0], dn[:, 1], 0.0, ALU.mult, ALU.add))
                        nc.vector.tensor_tensor(dn[:, 1], et[:], first, ALU.mult)
                        step(nc.vector.tensor_tensor(om[:], et[:], notfirst, ALU.mult))
                        step(nc.vector.tensor_tensor_scan(as0, om[:], dn[:, 1], 0.0, ALU.mult, ALU.add))
                        step(nc.vector.tensor_tensor_scan(as_, dn[:, 0], as0, 0.0, ALU.mult, ALU.add))
                        nc.vector.tensor_tensor(T["QW"][:, g, :], T["Q"][:, g, :], aw, ALU.mult)
                        step(nc.vector.tensor_tensor(T["QS"][:, g, :], T["Q"][:, g, :], as_, ALU.mult))
                        for r in range(4):
                            n = g * 4 + r
                            v.wait_ge(S["sel_a"], n + 1)
                            nc.vector.tensor_scalar(m64[:, 0], psM[0:CH, :], -0.1, 1.0, ALU.mult, ALU.add).then_inc(S["m64_ready"], 1)
                            v.wait_ge(S["sel_e"], n + 1)
                            nc.vector.tensor_scalar(m64[:, 1], psM[0:CH, :], 0.9, 0.05, ALU.mult, ALU.add).then_inc(S["m64_ready"], 1)
                            v.wait_ge(S["m64_ready"], 2 * n + 2)
                            step(nc.vector.tensor_tensor(m64[:], m64[:], bcast(start[0:CH, 0, :], 1, 2), ALU.mult))
                            step(nc.vector.tensor_tensor_scan(s64[:], m64[:, 1], inj[:], 0.0, ALU.mult, ALU.add))
                            nc.vector.tensor_copy(mse[:, g, :, r], s64[:].rearrange("p (c t) -> p c t", c=NC)[:, :, CH - 1])
                            step(nc.vector.tensor_tensor_scan(mw[:, g, r, :], m64[:, 0], s64[:], 0.0, ALU.mult, ALU.add))
                        v.wait_ge(S["theta"], g + 1)
                        nc.vector.tensor_copy(th[:, g], psM[0:CH, 0:32].rearrange("p (c r) -> p c r", c=NC)).then_inc(S["th_copied"], 1)
                        v.wait_ge(S["splus"], g + 1)
                        nc.vector.tensor_scalar(rl[:], T["K"][:, g, :], 1.0, None, ALU.mult)
                        for r in range(4):
                            q = slice(32 * r, 32 * r + 32)
                            m = nc.vector.tensor_copy(qbd[q, :, r, :], T["Q"][q, g, :].rearrange("p (c t) -> p c t", c=NC))
                        m.then_inc(S["qbd_ready"], 1)
                        v.wait_ge(S["kq_ready"], g + 1)
                        kqv = psP[0:CH, 0:4, :].rearrange("p a (b x) -> p (a b) x", b=2).rearrange("p c (r t) -> p c r t", r=4)
                        mwv = mw[:, g].rearrange("p r (c t) -> p c r t", c=NC)
                        nc.vector.tensor_tensor(kqm[:, g].rearrange("p c (r t) -> p c r t", r=4), kqv, mwv, ALU.mult).then_inc(S["kqm_ready"], 1)
                        v.wait_ge(S["ktok_ready"], g + 1)
                        ktk = psP[0:CH, 4:6, :].rearrange("p a (b x) -> p (a b) x", b=4).rearrange("p c (r d) -> p c r d", r=4)
                        last = mwv[:, :, :, CH - 1]
                        step(nc.vector.tensor_tensor(kw[:, g].rearrange("p c (r d) -> p c r d", r=4), ktk, bcast(last, 3, MD), ALU.mult))
                        step(nc.vector.tensor_tensor(ks[:, g].rearrange("p c (r d) -> p c r d", r=4), ktk, bcast(mse[:, g], 3, MD), ALU.mult))
                        step(nc.vector.tensor_copy(ksq[:].rearrange("p c (r d) -> p c r d", r=4), ktk))
                        step(nc.vector.tensor_tensor(ksq[:], ksq[:], ksq[:], ALU.mult))
                        nc.vector.tensor_reduce(k2[:, g], ksq[:].rearrange("p c (r d) -> p c r d", r=4), AX.X, ALU.add).then_inc(S["kw_ready"], 1)

        with ExitStack() as inner:
            isb = lambda n, s: inner.enter_context(nc.sbuf_tensor("M" + n, s, F32))
            psZ = inner.enter_context(nc.psum_tensor("MpsZ", [P, 2, 512], F32)); psR = inner.enter_context(nc.psum_tensor("MpsR", [P, 2, 512], F32))
            psK = inner.enter_context(nc.psum_tensor("MpsK", [P, 2, 512], F32)); psW = inner.enter_context(nc.psum_tensor("MpsW", [P, 2, 512], F32))
            sig = isb("sig", [P, G, CH]); hT = isb("hT", [P, G, CH]); om1 = isb("om1", [P, G, CH]); eT = isb("eT", [P, G, CH]); dz = isb("dz", [P, G, CH])
            tok = isb("tok", [CH, G, 3, P]); sqr = isb("sqr", [CH, G, 3, P]); n2 = isb("n2", [CH, G, 3, 4]); nn = isb("nn", [CH, G, 2, 4]); ce = isb("ce", [CH, G, 4])
            src = isb("src", [CH, G, 2, P]); hw = isb("hw", [CH, G, 2, P])
            sq = isb("sq", [P, G, CH]); h2 = isb("h2", [P, G, CH]); h2w = isb("h2w", [P, G, 2, CH]); h2bd = isb("h2bd", [P, G, 4, CH]); hhm = isb("hhm", [CH, G, 4 * CH])
            upd = isb("upd", [P, G, 6, P]); t3 = isb("t3", [P, G, 3, P])
            stg = isb("stg", [P, G, 3, CH]); stt = isb("stt", [CH, G, 2, P])
            R = {n: sem("r_" + n) for n in """staged z sig h om1 ds pred e dh dz turned tok sqr n2 pow ce src zq sq h2 h2w hh hhm out ret hw upd masked t3 w3 chain zero clear""".split()}
            kqs = isb("kqs", [CH, G, 4 * CH])
            with nc.Block() as block:
                @block.tensor
                def _(pe):
                    with pe.Fori(0, NC) as k:
                        t0 = k * CH
                        n = [k * G + g for g in range(G)]
                        for g in range(G):
                            pe.wait_ge(R["w3"], k * G)
                            pe.wait_ge(R["ret"], k * G)
                            nc.tensor.matmul(psZ[:, g, 0:CH], W3[:, g, 0, :], T["K"][:, g, bass.ds(t0, CH)], start=True, stop=True).then_inc(R["z"], 1)
                            pe.wait_ge(R["h"], n[g] + 1)
                            nc.tensor.matmul(psZ[:, g, CH:2 * CH], W3[:, g, 1, :], hT[:, g, :], start=True, stop=True).then_inc(R["pred"], 1)
                            pe.wait_ge(R["e"], n[g] + 1)
                            nc.tensor.matmul(psZ[:, g, 2 * CH:3 * CH], W3[:, g, 2, :], eT[:, g, :], start=True, stop=True).then_inc(R["dh"], 1)
                            pe.wait_ge(R["dz"], n[g] + 1)
                            pe.sem_inc(R["clear"], 1)
                            for a, x in enumerate((hT, eT, dz)):
                                m = nc.tensor.transpose(psK[0:CH, g, a * P:(a + 1) * P], x[:, g, :], ident[:])
                            m.then_inc(R["turned"], 1)
                        for g in range(G):
                            pe.wait_ge(R["src"], n[g] + 1)
                            o = psR[:, g, 0:CH]
                            nc.tensor.matmul(o, W3[:, g, 0, :], T["QW"][:, g, bass.ds(t0, CH)], start=True, stop=True)
                            nc.tensor.matmul(o, S3[:, g, 0, :], T["QS"][:, g, bass.ds(t0, CH)], start=False, stop=True, skip_group_check=True)
                            for r in range(4):
                                q = slice(32 * r, 32 * r + 32)
                                m = nc.tensor.matmul(psR[q, g, 0:CH], src[:, g, 1, q], kqs[:, g, r * CH:(r + 1) * CH], start=False, stop=True, skip_group_check=True, tile_position=(0, 32 * r))
                            m.then_inc(R["zq"], 1)
                            pe.wait_ge(R["h2w"], n[g] + 1)
                            nc.tensor.matmul(psR[0:CH, g, 128:128 + 4 * CH], hT[:, g, :], h2bd[:, g], start=True, stop=True).then_inc(R["hh"], 1)
                            pe.wait_ge(R["hhm"], n[g] + 1)
                            o = psR[:, g, 0:CH]
                            nc.tensor.matmul(o, W3[:, g, 1, :], h2w[:, g, 0, :], start=True, stop=True)
                            nc.tensor.matmul(o, S3[:, g, 1, :], h2w[:, g, 1, :], start=False, stop=True, skip_group_check=True)
                            for r in range(4):
                                q = slice(32 * r, 32 * r + 32)
                                m = nc.tensor.matmul(psR[q, g, 0:CH], src[:, g, 0, q], hhm[:, g, r * CH:(r + 1) * CH], start=False, stop=True, skip_group_check=True, tile_position=(0, 32 * r))
                            m.then_inc(R["out"], 1)
                        for g in range(G):
                            pe.wait_ge(R["hw"], n[g] + 1)
                            pe.wait_ge(R["masked"], k * G + g)
                            for a in range(2):
                                o = lambda s: psW[:, a, s * P:(s + 1) * P]
                                nc.tensor.matmul(o(0), stt[:, g, a, :], src[:, g, 1, :], start=True, stop=True)
                                nc.tensor.matmul(o(1), hw[:, g, a, :], src[:, g, 0, :], start=True, stop=True)
                                m = nc.tensor.matmul(o(2), src[:, g, 0, :], hw[:, g, a, :], start=True, stop=True)
                            m.then_inc(R["upd"], 1)

                @block.scalar
                def _(act):
                    with act.Fori(0, NC) as k:
                        t0 = k * CH
                        n = [k * G + g for g in range(G)]
                        for g in range(G):
                            act.wait_ge(R["upd"], k * G)
                            nc.scalar.activation(kqs[:, g, :], kqm[:, g, k, :], ACT.Copy)
                            nc.scalar.activation(stt[:, g, 0, :], kw[:, g, k, :], ACT.Copy)
                            nc.scalar.activation(stt[:, g, 1, :], ks[:, g, k, :], ACT.Copy).then_inc(R["staged"], 1)
                        for g in range(G):
                            act.wait_ge(R["z"], n[g] + 1)
                            nc.scalar.activation(sig[:, g, :], psZ[:, g, 0:CH], ACT.Sigmoid).then_inc(R["sig"], 1)
                            act.wait_ge(R["turned"], n[g] + 1)
                            nc.scalar.activation(tok[:, g].rearrange("p a b -> p (a b)"), psK[0:CH, g, 0:3 * P], ACT.Copy).then_inc(R["tok"], 1)
                        for g in range(G):
                            act.wait_ge(R["zq"], n[g] + 1)
                            nc.scalar.activation(sq[:, g, :], psR[:, g, 0:CH], ACT.Sigmoid).then_inc(R["sq"], 1)
                            act.wait_ge(R["out"], n[g] + 1)
                            nc.scalar.activation(T["RET"][:, g, bass.ds(t0, CH)], psR[:, g, 0:CH], ACT.Copy).then_inc(R["ret"], 1)

                @block.gpsimd
                def _(g_):
                    with g_.Fori(0, NC) as k:
                        for g in range(G):
                            n = k * G + g
                            g_.wait_ge(R["n2"], n + 1)
                            nc.gpsimd.tensor_tensor(nn[:, g, 0, :], nn[:, g, 0, :], half[:], ALU.pow).then_inc(R["pow"], 1)

                @block.vector
                def _(v):
                    nc.vector.memset(h2bd[:], 0.0).then_inc(R["zero"], 1)
                    v.wait_ge(R["zero"], 1)
                    with v.Fori(0, NC) as k:
                        t0 = k * CH
                        step = Steps(v, R["chain"], k * 24)
                        n = [k * G + g for g in range(G)]
                        for g in range(G):
                            v.wait_ge(R["sig"], n[g] + 1)
                            z = psZ[:, g, 0:CH]
                            nc.vector.tensor_tensor(hT[:, g, :], z, sig[:, g, :], ALU.mult).then_inc(R["h"], 1)
                            step(nc.vector.tensor_scalar(om1[:, g, :], sig[:, g, :], -1.0, 1.0, ALU.mult, ALU.add))
                            v.wait_ge(R["h"], n[g] + 1)
                            step(nc.vector.tensor_tensor(om1[:, g, :], om1[:, g, :], hT[:, g, :], ALU.mult))
                            step(nc.vector.tensor_tensor(om1[:, g, :], om1[:, g, :], sig[:, g, :], ALU.add))
                            v.wait_ge(R["pred"], n[g] + 1)
                            nc.vector.tensor_tensor(eT[:, g, :], psZ[:, g, CH:2 * CH], T["V"][:, g, bass.ds(t0, CH)], ALU.subtract).then_inc(R["e"], 1)
                            v.wait_ge(R["dh"], n[g] + 1)
                            nc.vector.tensor_tensor(dz[:, g, :], psZ[:, g, 2 * CH:3 * CH], om1[:, g, :], ALU.mult).then_inc(R["dz"], 1)
                        for g in range(G):
                            v.wait_ge(R["tok"], n[g] + 1)
                            step(nc.vector.tensor_tensor(sqr[:, g], tok[:, g], tok[:, g], ALU.mult))
                            step(nc.vector.tensor_reduce(n2[:, g], sqr[:, g].rearrange("p a (r d) -> p a r d", r=4), AX.X, ALU.add))
                            nc.vector.tensor_tensor(nn[:, g, 0, :], n2[:, g, 0, :], n2[:, g, 1, :], ALU.mult)
                            step(nc.vector.tensor_tensor(nn[:, g, 1, :], n2[:, g, 2, :], k2[:, g, k, :], ALU.mult))
                            nc.vector.tensor_tensor(nn[:, g, 0, :], nn[:, g, 0, :], nn[:, g, 1, :], ALU.add).then_inc(R["n2"], 1)
                        for g in range(G):
                            v.wait_ge(R["pow"], n[g] + 1)
                            step(nc.vector.tensor_scalar(ce[:, g, :], nn[:, g, 0, :], 0.2, 1e-6, ALU.mult, ALU.max))
                            step(nc.vector.reciprocal(ce[:, g, :], ce[:, g, :]))
                            step(nc.vector.tensor_scalar(ce[:, g, :], ce[:, g, :], 1.0, 0.2, ALU.min, ALU.mult))
                            step(nc.vector.tensor_tensor(ce[:, g, :], ce[:, g, :], th[:, g, k, :], ALU.mult))
                            v.wait_ge(R["staged"], n[g] + 1)
                            nc.vector.tensor_tensor(src[:, g].rearrange("p a (r d) -> p a r d", r=4), tok[:, g, 1:3].rearrange("p a (r d) -> p a r d", r=4),
                                                    bcast(bcast(ce[:, g, :], 2, MD), 1, 2), ALU.mult).then_inc(R["src"], 1)
                            ht = tok[:, g, 0].rearrange("p (r d) -> p r d", r=4)
                            mwv = mw[:, g].rearrange("p r (c t) -> p c r t", c=NC)
                            nc.vector.tensor_tensor(hw[:, g, 0].rearrange("p (r d) -> p r d", r=4), ht, bcast(mwv[:, k, :, CH - 1], 2, MD), ALU.mult)
                            nc.vector.tensor_tensor(hw[:, g, 1].rearrange("p (r d) -> p r d", r=4), ht, bcast(mse[:, g, k, :], 2, MD), ALU.mult).then_inc(R["hw"], 1)
                        for g in range(G):
                            v.wait_ge(R["sq"], n[g] + 1)
                            step(nc.vector.tensor_tensor(h2[:, g, :], psR[:, g, 0:CH], sq[:, g, :], ALU.mult))
                            nc.vector.tensor_tensor(h2w[:, g, 0, :], h2[:, g, :], T["AW"][:, g, bass.ds(t0, CH)], ALU.mult)
                            nc.vector.tensor_tensor(h2w[:, g, 1, :], h2[:, g, :], T["AS"][:, g, bass.ds(t0, CH)], ALU.mult)
                            for r in range(4):
                                q = slice(32 * r, 32 * r + 32)
                                m = nc.vector.tensor_copy(h2bd[q, g, r, :], h2[q, g, :])
                            m.then_inc(R["h2w"], 1)
                            v.wait_ge(R["hh"], n[g] + 1)
                            mwc = mw[:, g].rearrange("p r (c t) -> p c r t", c=NC)[:, k]
                            nc.vector.tensor_tensor(hhm[:, g].rearrange("p (r t) -> p r t", r=4), psR[0:CH, g, 128:128 + 4 * CH].rearrange("p (r t) -> p r t", r=4), mwc, ALU.mult).then_inc(R["hhm"], 1)
                        for g in range(G):
                            v.wait_ge(R["upd"], n[g] + 1)
                            m = nc.vector.tensor_tensor(upd[:, g].rearrange("p (a s) x -> p a s x", a=2), psW[:, :, 0:3 * P].rearrange("p a (s x) -> p a s x", s=3), bcast(bcast(bd[:], 1, 3), 1, 2), ALU.mult)
                            m.then_inc(R["masked"], 1)
                            v.wait_ge(R["masked"], n[g] + 1)
                            v.wait_ge(R["out"], n[g] + 1)
                            at = bass.ds(t0 + CH - 1, 1)
                            step(nc.vector.scalar_tensor_tensor(out=t3[:, g], in0=S3[:, g], scalar=T["AS"][:, g, at], in1=upd[:, g, 0:3], op0=ALU.mult, op1=ALU.add))
                            nc.vector.scalar_tensor_tensor(out=S3[:, g], in0=S3[:, g], scalar=T["AS0"][:, g, at], in1=upd[:, g, 3:6], op0=ALU.mult, op1=ALU.add)
                            nc.vector.scalar_tensor_tensor(out=W3[:, g], in0=W3[:, g], scalar=T["AW"][:, g, at], in1=t3[:, g], op0=ALU.mult, op1=ALU.add).then_inc(R["w3"], 1)

        clear(nc, S.values())
        clear(nc, R.values())

        with ExitStack() as inner:
            isb = lambda n, s: inner.enter_context(nc.sbuf_tensor("M" + n, s, F32))
            psY = inner.enter_context(nc.psum_tensor("MpsY", [P, 2, 512], F32)); psG = inner.enter_context(nc.psum_tensor("MpsG", [P, 2, 512], F32))
            rg = isb("rg", [P, 512]); xg = isb("xg", [P, 2, 512]); ysq = isb("ysq", [P, 4, D]); ss = isb("ss", [P, 4]); y = isb("y", [P, 4, D])
            R = {n: sem("o_" + n) for n in "rg xg y gate sq ss eps rstd yn chain added".split()}
            with nc.Block() as block:
                @block.scalar
                def _(act):
                    with act.Fori(0, G) as g:
                        act.wait_ge(R["y"], g * 4)
                        nc.scalar.activation(rg[:], T["RET"][:, g, :], ACT.Copy).then_inc(R["rg"], 1)
                        for r in range(4):
                            act.wait_ge(R["gate"], g * 4 + (r - 1 if r >= 2 else 0))
                            nc.scalar.activation(xg[:, r % 2, :], xT[:, g * 4 + r, :], ACT.Copy).then_inc(R["xg"], 1)
                            act.wait_ge(R["y"], g * 4 + r + 1)
                            act.wait_ge(R["ss"], g * 4 + r)
                            nc.scalar.activation(ysq[:].rearrange("p a b -> p (a b)"), psY[:, r % 2, :], ACT.Square).then_inc(R["sq"], 1)
                @block.tensor
                def _(pe):
                    with pe.Fori(0, G) as g:
                        for r in range(4):
                            n = g * 4 + r
                            q = slice(32 * r, 32 * r + 32)
                            pe.wait_ge(R["rg"], g + 1)
                            pe.wait_ge(R["added"], g * 4 + (r - 1 if r >= 2 else 0))
                            for j in range(4):
                                m = nc.tensor.matmul(psY[:, r % 2, j * P:(j + 1) * P], rg[q, j * P:(j + 1) * P], woT[q, :], start=True, stop=True)
                            m.then_inc(R["y"], 1)
                            pe.wait_ge(R["xg"], n + 1)
                            for j in range(4):
                                o = psG[:, r % 2, j * P:(j + 1) * P]
                                nc.tensor.matmul(o, ones1[:], gb[:], start=True, stop=False)
                                m = nc.tensor.matmul(o, xg[:, r % 2, j * P:(j + 1) * P], gwT[:], start=False, stop=True)
                            m.then_inc(R["gate"], 1)
                @block.gpsimd
                def _(g_):
                    with g_.Fori(0, B) as n:
                        g_.wait_ge(R["eps"], n + 1)
                        nc.gpsimd.tensor_tensor(ss[:], ss[:], mhalf[:], ALU.pow).then_inc(R["rstd"], 1)
                @block.vector
                def _(v):
                    Xv = X[:].rearrange("p (b j) c -> p b j c", b=B)
                    with v.Fori(0, G) as g:
                        step = Steps(v, R["chain"], g * 16)
                        for r in range(4):
                            n = g * 4 + r
                            v.wait_ge(R["sq"], n + 1)
                            nc.vector.tensor_reduce(ss[:], ysq[:], AX.X, ALU.add).then_inc(R["ss"], 1)
                            v.wait_ge(R["ss"], n + 1)
                            nc.vector.tensor_scalar(ss[:], ss[:], 1.0 / D, 1e-6, ALU.mult, ALU.add).then_inc(R["eps"], 1)
                            v.wait_ge(R["rstd"], n + 1)
                            step(nc.vector.tensor_tensor(y[:], psY[:, r % 2, :].rearrange("p (j c) -> p j c", j=4), bcast(ss[:], 2, D), ALU.mult))
                            step(nc.vector.tensor_tensor(y[:], y[:], bcast(ng[:], 1, 4), ALU.mult))
                            v.wait_ge(R["gate"], n + 1)
                            step(nc.vector.tensor_tensor(y[:], psG[:, r % 2, :].rearrange("p (j c) -> p j c", j=4), y[:], ALU.mult))
                            step(nc.vector.tensor_tensor(Xv[:, n], y[:], Xv[:, n], ALU.add))
                            v.sem_inc(R["added"], 1)
        clear(nc, R.values())


def memory_consts():
    bd = np.kron(np.eye(4), np.ones((32, 32))).astype(np.float32)
    pick = np.zeros((P, 4, CH), np.float32)
    pick1 = np.zeros((P, 4), np.float32)
    for r in range(4):
        pick[32 * r:32 * r + 32, r] = 1 / 32
        pick1[32 * r:32 * r + 32, r] = -0.1 / 32
    t = np.arange(512)
    first = np.broadcast_to((t % CH == 0).astype(np.float32), (P, 512))
    start = np.stack([1 - first, first], 1).copy()
    inj = (t[None] % CH == np.arange(CH)[:, None]).astype(np.float32)
    return {"c_mean": bd / 32, "c_bd": bd, "c_pick": pick, "c_pick1": pick1, "c_start": start, "c_inj": inj}

def memory_layout(w):
    t = np.ascontiguousarray
    return {**{n + "T": t(w[n].T) for n in ("Wk", "Wv", "Wq", "aW", "eW", "tW", "Wo", "gW", "mW1", "mW2")}}


def network(nc, x, ident_in, w, out):
    with ExitStack() as ctx:
        X = ctx.enter_context(nc.sbuf_tensor("X", [P, 32, D], F32))
        XF = ctx.enter_context(nc.sbuf_tensor("XF", [P, B, 5, D], F32))
        ident = ctx.enter_context(nc.sbuf_tensor("ident", [P, P], F32))
        io = ctx.enter_context(nc.semaphore("io")); summed = ctx.enter_context(nc.semaphore("summed"))
        c = {"ident": ident}
        xt, ot = (a.rearrange("b (j p) c -> p (b j) c", p=P) for a in (x, out))
        with nc.Block() as block:
            @block.sync
            def _(sp):
                sp.dma_start(X[:], xt).then_inc(io, 16)
                sp.dma_start(ident[:], ident_in).then_inc(io, 16)
                sp.wait_ge(io, 32)
            @block.vector
            def _(v):
                nc.vector.memset(XF[:, :, 0, :], 0.0)

        layer_norm(nc, X, XF, "n0")
        causal_attention(nc, X, XF, c, w["L0_attn"])
        local_layers(nc, XF, c, w["L0_ffn"])
        with nc.Block() as block:
            @block.vector
            def _(v):
                xv = X[:].rearrange("p (b j) c -> p b (j c)", b=B)
                nc.vector.tensor_tensor(xv, XF[:, :, 1:5, :].rearrange("p b j c -> p b (j c)"), xv, ALU.add).then_inc(summed, 1)
        layer_norm(nc, X, XF, "n1")
        state_space(nc, X, XF, c, w["L1_attn"])
        top2_experts(nc, X, XF, c, w["L1_ffn"])
        layer_norm(nc, X, XF, "n2")
        banded_attention(nc, X, XF, c, w["L2_attn"])
        capped_experts(nc, X, XF, c, w["L2_ffn"])
        layer_norm(nc, X, XF, "n3")
        neural_memory(nc, X, XF, c, w["L3_attn"])
        fp4_ffn(nc, X, XF, c, w["L3_ffn"])
        with nc.Block() as block:
            @block.sync
            def _(sp):
                sp.dma_start(ot, X[:]).then_inc(io, 16)
                sp.wait_ge(io, 48)


def kernel(**inputs):
    import numpy as _np
    import concourse.bacc as _bacc
    from concourse import mybir as _mybir
    from concourse.bass_utils import run_bass_kernel_spmd as _run

    inputs = {k: _np.asarray(v) for k, v in inputs.items()}
    sub = lambda p: {k[len(p) + 1:]: v for k, v in inputs.items() if k.startswith(p + "_")}
    t = _np.ascontiguousarray
    identb = {"c_identb": _np.eye(P).astype("bfloat16")}
    stages = {p: sub(p) for p in ("L0_attn", "L0_ffn", "L1_attn", "L1_ffn", "L2_attn", "L2_ffn", "L3_attn", "L3_ffn")}
    s = stages["L0_attn"]
    s.update({n + "T": t(s[n].T) for n in ("Wk", "Wq", "Wv", "Wu")}, **attention_consts(), **identb)
    x = s.pop("x")
    stages["L0_ffn"].update(local_consts(), **identb)
    s = stages["L1_attn"]
    s.update({"W_outT": t(s["W_out"].T), "c_flip": t(_np.eye(P, dtype=_np.float32)[::-1])})
    s = stages["L1_ffn"]
    s.update(top2_consts(), **top2_layout(s))
    stages["L2_attn"].update(banded_consts(), **identb)
    s = stages["L2_ffn"]
    s.update(capped_consts(), **capped_layout(s))
    s = stages["L3_attn"]
    s.update(memory_consts(), **memory_layout(s))

    nc = _bacc.Bacc("TRN2", target_bir_lowering=False, num_devices=1)
    arrays = {}

    def given(name, a):
        arrays[name] = t(a)
        return nc.dram_tensor(name, a.shape, _mybir.dt.from_np(a.dtype), kind="ExternalInput").ap()

    xin, ident_in = given("x", x), given("identity", _np.eye(P, dtype=_np.float32))
    w = {p: {n: given(p + "_" + n, a) for n, a in d.items() if n not in HOST_ONLY} for p, d in stages.items()}
    out = nc.dram_tensor("out_0", x.shape, F32, kind="ExternalOutput").ap()
    network(nc, xin, ident_in, w, out)
    r = _run(nc, [arrays], core_ids=[0])
    return r.results[0]["out_0"]
```

```python
from contextlib import ExitStack

import numpy as np
import concourse.bass as bass
from concourse import mybir

P, B, T, D = 128, 8, 4, 128
F32 = mybir.dt.float32; BF16 = mybir.dt.bfloat16
ALU = mybir.AluOpType; ACT = mybir.ActivationFunctionType; AX = mybir.AxisListType

def bcast(ap, axis, n):
    dims = [list(x) for x in ap.ap]
    return bass.AP(ap.tensor, ap.offset, dims[:axis] + [[0, n]] + dims[axis:])

def rows(ap, n=P):
    return bass.AP(ap.tensor, ap.offset, [[0, n]] + [list(x) for x in ap.ap])


def clear(nc, sems):
    numbers = sorted(s.num for s in sems)
    with nc.Block() as block:
        @block.sync
        def _(sp):
            first = numbers[0]
            for n, after in zip(numbers, numbers[1:] + [None]):
                if after != n + 1:
                    sp.sem_clear(range(first, n + 1))
                    first = after

def start_at_one(nc, S, names):
    with nc.Block() as block:
        @block.sync
        def _(sp):
            for n in names.split():
                sp.sem_inc(S[n], 1)


HOST_ONLY = ("Wk", "Wq", "Wv", "Wu", "W_out", "gate_w", "up_w", "gp_w", "down_w", "up_b", "gp_b", "gate_up_proj", "down_proj",
             "shared_gate", "shared_up", "shared_down", "router_weight", "aW", "eW", "tW", "gW", "mW1")


def layer_norm(nc, X, XF, name):
    with ExitStack() as ctx:
        sb = lambda n, s, d=F32: ctx.enter_context(nc.sbuf_tensor(name + n, s, d))
        st = sb("st", [P, 4, 6]); mv = sb("mv", [P, 4, 2]); ve = sb("ve", [P, 2, 4]); rs = sb("rs", [P, 4]); mh = sb("mh", [P, 4])
        names = "stats passed aggr eps rstd done power_set"
        S = {n: ctx.enter_context(nc.semaphore(name + n)) for n in names.split()}
        start_at_one(nc, S, "done")
        with nc.Block() as block:
            @block.vector
            def _(v):
                Xv = X[:].rearrange("p (b j) c -> p b j c", b=B)
                with v.Fori(0, B) as b:
                    v.wait_ge(S["done"], b + 1)
                    for j in range(4):
                        m = nc.vector.bn_stats(st[:, j, :], Xv[:, b, j, :])
                    m.then_inc(S["stats"], 1)
                    v.wait_ge(S["stats"], b + 1)
                    v.sem_inc(S["passed"], 1)
                    for j in range(4):
                        m = nc.vector.bn_aggr(mv[:, j, :], st[:, j, :])
                    m.then_inc(S["aggr"], 1)
                    v.wait_ge(S["aggr"], b + 1)
                    nc.vector.tensor_scalar(ve[:, 0], mv[:, :, 1], 1e-5, None, ALU.add).then_inc(S["eps"], 1)
                    v.wait_ge(S["rstd"], b + 1)
                    for j in range(4):
                        m = nc.vector.tensor_scalar(XF[:, b, j + 1, :], Xv[:, b, j, :], mv[:, j, 0:1], rs[:, j:j + 1], ALU.subtract, ALU.mult)
                    m.then_inc(S["done"], 1)

            @block.gpsimd
            def _(g):
                nc.gpsimd.memset(mh[:], -0.5).then_inc(S["power_set"], 1)
                g.wait_ge(S["power_set"], 1)
                with g.Fori(0, B) as b:
                    g.wait_ge(S["eps"], b + 1)
                    nc.gpsimd.tensor_tensor(rs[:], ve[:, 0], mh[:], ALU.pow).then_inc(S["rstd"], 1)
        clear(nc, S.values())


AH, AD, PADH = 16, 8, 64
VPAD = 32
PARTS = 6 * AD
K_PARTS = {"h": (0, 3, 5), "m": (1, 4), "l": (2,)}
Q_PARTS = {"h": (0, 1, 2), "m": (3, 4), "l": (5,)}

def causal_attention(nc, X, XF, c, w):
    with ExitStack() as ctx:
        sb = lambda n, s, d=F32: ctx.enter_context(nc.sbuf_tensor("A" + n, s, d))
        ps = lambda n, s, d=F32: ctx.enter_context(nc.psum_tensor("A" + n, s, d))
        sem = lambda n: ctx.enter_context(nc.semaphore("A" + n))
        wcat = sb("wcat", [P, 384]); wu = sb("wu", [P, D]); hw = sb("hw", [P, 2, 2, AD])
        mh = sb("mh", [P, 4, 32])
        tri = sb("tri", [P, 2, P], BF16); identb = sb("identb", [P, P], BF16)
        xb = sb("xb", [P, 4, D]); xT = sb("xT", [P, 512])
        s1 = sb("s1", [P, 4, 32]); cen = sb("cen", [P, 4, 32, AD]); sq = sb("sq", [P, 4, 32, AD]); vr = sb("vr", [P, 4, 32])
        kp = sb("kp", [P, 4, AH, PADH], BF16); qp = sb("qp", [P, 4, AH, PADH], BF16); nm = sb("nm", [P, 4, AH])
        kT = sb("kT", [P, 8, 512], BF16); qT = sb("qT", [P, 8, 512], BF16)
        Vp = sb("Vp", [P, 4, AH, VPAD]); OT = sb("OT", [P, 4, 512]); PT = sb("PT", [P, 2, 1536])
        rd = sb("rd", [P, 4, AH]); on = sb("on", [P, 4, AH, AD]); oT = sb("oT", [P, 512])
        psA = ps("psA", [P, 3072]); psB = ps("psB", [P, 1024])
        ident = c["ident"]
        S = {n: sem(n) for n in """loaded ones w_scaled xb_ready x_turned xT_ready qkv_ready v_ready h_sum h_mean h_cen h_sq h_var h_eps h_rstd
          h_norm h_gain h_bias part_h rest_m part_m part_l repeated k_turned kT_ready q_turned qT_ready s_ready mx_done
          nm_h nm_m nm_parts q2_turned qT2_ready st_ready exp_done
          av_done o_kept ot_turned rd_ready on_ready o_turned oT_ready y_ready y_added""".split()}
        start_at_one(nc, S, "exp_done y_added mx_done x_turned av_done qkv_ready")
        with nc.Block() as block:
            @block.sync
            def _(sp):
                L = S["loaded"]
                for k, n in enumerate(("Wk", "Wq", "Wv")):
                    sp.dma_start(wcat[:, 128 * k:128 * k + 128], w[n + "T"]).then_inc(L, 16)
                sp.dma_start(wu[:], w["WuT"]).then_inc(L, 16)
                for k, n in enumerate(("kln", "qln")):
                    sp.dma_start(hw[:, k, 0, :], rows(w[n + "_w"])).then_inc(L, 16)
                    sp.dma_start(hw[:, k, 1, :], rows(w[n + "_b"])).then_inc(L, 16)
                sp.dma_start(tri[:], w["c_tri"]).then_inc(L, 16)
                sp.dma_start(identb[:], w["c_identb"]).then_inc(L, 16)
                sp.wait_ge(L, 160)
            @block.vector
            def _(v):
                nc.vector.memset(kp[:], 0.0)
                nc.vector.memset(qp[:], 0.0).then_inc(S["ones"], 1)
                nc.vector.memset(Vp[:], 0.0).then_inc(S["ones"], 1)
                v.wait_ge(S["ones"], 2)
                nc.vector.memset(Vp[:, :, :, AD:AD + 1], 1.0)
                nc.vector.memset(kp[:, :, :, PARTS:PARTS + 3], 1.0)
                v.wait_ge(S["loaded"], 160)
                nc.vector.tensor_scalar(hw[:, 1], hw[:, 1], float(AD) ** -0.5, None, ALU.mult)
            @block.gpsimd
            def _(g):
                nc.gpsimd.memset(mh[:], -0.5)

        def lay(n):
            return {4: (0, 512), 3: (512, 384), 1: (896, 128), 2: (1024, 256)}[n]

        with nc.Block() as block:
            @block.tensor
            def _(pe):
                with pe.Fori(0, B) as b:
                    pe.wait_ge(S["xb_ready"], b + 1)
                    pe.wait_ge(S["exp_done"], b * 48 + 1)
                    for j in range(4):
                        m = nc.tensor.transpose(psA[:, j * P:(j + 1) * P], xb[:, j, :], ident[:])
                    m.then_inc(S["x_turned"], 1)
                    pe.wait_ge(S["xT_ready"], b + 1)
                    for j in range(4):
                        m = nc.tensor.matmul(psA[:, 512 * (j + 1):512 * (j + 1) + 384], xT[:, j * P:(j + 1) * P], wcat[:], start=True, stop=True)
                    m.then_inc(S["qkv_ready"], 1)
                    pe.wait_ge(S["v_ready"], b + 1)
                    pe.wait_ge(S["y_added"], b + 1)
                    pe.wait_ge(S["part_l"], 2 * b + 2)
                    pe.wait_ge(S["repeated"], b + 1)

                    def turn(src, half, turned):
                        for g in range(4 * half, 4 * half + 4):
                            tgt = psA[:, g * 512:g * 512 + 512] if g < 6 else psB[:, (g - 6) * 512:(g - 5) * 512]
                            for j in range(4):
                                m = nc.tensor.matmul(tgt[:, j * P:(j + 1) * P], src[:, j, 2 * g:2 * g + 2, :], identb[:], start=True, stop=True)
                        m.then_inc(S[turned], 1)

                    turn(kp, 0, "k_turned")
                    turn(kp, 1, "k_turned")
                    pe.wait_ge(S["kT_ready"], 2 * b + 2)
                    turn(qp, 0, "q_turned")
                    turn(qp, 1, "q_turned")
                    pe.wait_ge(S["qT_ready"], 2 * b + 2)
                    for h in range(AH):
                        r = slice(64 * (h % 2), 64 * (h % 2) + PARTS)
                        if h >= 2:
                            pe.wait_ge(S["mx_done"], b * AH + h)
                        for qi in range(4):
                            o, n = lay(qi + 1)
                            o += 1536 * (h % 2)
                            nc.tensor.matmul(psA[:, o:o + n], qT[r, h // 2, qi * P:(qi + 1) * P], kT[r, h // 2, 0:n], start=True, stop=True)
                            m = nc.tensor.matmul(psA[:, o + n - P:o + n], identb[:], tri[:, 0, :], start=False, stop=True, skip_group_check=True)
                        m.then_inc(S["s_ready"], 1)
                    pe.wait_ge(S["mx_done"], (b + 1) * AH + 1)
                    pe.wait_ge(S["nm_parts"], b + 1)
                    turn(qp, 0, "q2_turned")
                    turn(qp, 1, "q2_turned")
                    pe.wait_ge(S["qT2_ready"], 2 * b + 2)

                    def st(h):
                        r = slice(64 * (h % 2), 64 * (h % 2) + PARTS + 3)
                        if h >= 2:
                            pe.wait_ge(S["exp_done"], b * 48 + 3 * (h - 1) + 1)
                        for kj in range(4):
                            o, n = lay(4 - kj)
                            o += 1536 * (h % 2)
                            nc.tensor.matmul(psA[:, o:o + n], kT[r, h // 2, kj * P:(kj + 1) * P], qT[r, h // 2, kj * P:512], start=True, stop=True)
                            m = nc.tensor.matmul(psA[:, o:o + P], identb[:], tri[:, 1, :], start=False, stop=True, skip_group_check=True)
                        m.then_inc(S["st_ready"], 1)

                    def av(h):
                        g, r = h // 4, 32 * (h % 4)
                        pe.wait_ge(S["exp_done"], b * 48 + 3 * (h + 1) + 1)
                        if h % 4 == 0 and g >= 2:
                            pe.wait_ge(S["o_kept"], b * 4 + g - 1)
                        for kj in range(4):
                            o, n = lay(4 - kj)
                            m = nc.tensor.matmul(psB[r:r + 32, (g % 2) * 512 + kj * P:(g % 2) * 512 + 512], Vp[:, kj, h, :], PT[:, h % 2, o:o + n],
                                                 start=(kj == 0), stop=True, skip_group_check=True, tile_position=(0, r))
                        m.then_inc(S["av_done"], 1)

                    st(0)
                    for h in range(1, AH):
                        st(h)
                        av(h - 1)
                    av(AH - 1)
                    pe.wait_ge(S["o_kept"], b * 4 + 4)
                    for j in range(4):
                        for g in range(4):
                            m = nc.tensor.transpose(psA[:, j * 512 + g * P:j * 512 + (g + 1) * P], OT[:, g, j * P:(j + 1) * P], ident[:])
                    m.then_inc(S["ot_turned"], 1)
                    pe.wait_ge(S["on_ready"], b + 1)
                    for j in range(4):
                        m = nc.tensor.transpose(psB[:, j * P:(j + 1) * P], on[:, j], ident[:])
                    m.then_inc(S["o_turned"], 1)
                    pe.wait_ge(S["oT_ready"], b + 1)
                    for j in range(4):
                        m = nc.tensor.matmul(psB[:, 512 + j * P:512 + (j + 1) * P], oT[:, j * P:(j + 1) * P], wu[:], start=True, stop=True)
                    m.then_inc(S["y_ready"], 1)

            @block.scalar
            def _(act):
                with act.Fori(0, B) as b:
                    act.wait_ge(S["x_turned"], b + 1)
                    nc.scalar.activation(xb[:], XF[:, b, 1:5, :], ACT.Copy).then_inc(S["xb_ready"], 1)
                    act.wait_ge(S["h_cen"], b + 1)
                    act.wait_ge(S["av_done"], b * AH + 1)
                    nc.scalar.activation(Vp[:, :, :, 0:AD], psA[:, 512:2560].rearrange("p (j x) -> p j x", j=4)[:, :, 256:384].rearrange("p j (h d) -> p j h d", h=AH), ACT.Copy).then_inc(S["v_ready"], 1)
                    for part, first in (("h", 0), ("m", 1)):
                        act.wait_ge(S["part_" + part], 2 * b + 2)
                        for t, where in ((kp, K_PARTS), (qp, Q_PARTS)):
                            k0 = where[part][0] * AD
                            for k in where[part][1:]:
                                m = nc.scalar.activation(t[:, :, :, k * AD:k * AD + AD], t[:, :, :, k0:k0 + AD], ACT.Copy)
                    m.then_inc(S["repeated"], 1)
                    for dst, turned, ready in ((kT, "k_turned", "kT_ready"), (qT, "q_turned", "qT_ready"), (qT, "q2_turned", "qT2_ready")):
                        act.wait_ge(S[turned], 2 * b + 1)
                        nc.scalar.activation(dst[:, 0:4].rearrange("p a b -> p (a b)"), psA[:, 0:2048], ACT.Copy).then_inc(S[ready], 1)
                    for h in range(AH):
                        act.wait_ge(S["st_ready"], b * AH + h + 1)
                        if h >= 2:
                            act.wait_ge(S["av_done"], b * AH + h)
                        for a, n in ((0, 512), (512, 512), (1024, 256)):
                            nc.scalar.activation(PT[:, h % 2, a:a + n], psA[:, 1536 * (h % 2) + a:1536 * (h % 2) + a + n], ACT.Exp).then_inc(S["exp_done"], 1)
                    act.wait_ge(S["o_turned"], b + 1)
                    nc.scalar.activation(oT[:], psB[:, 0:512], ACT.Copy).then_inc(S["oT_ready"], 1)

            @block.vector
            def _(v):
                with v.Fori(0, B) as b:
                    v.wait_ge(S["x_turned"], b + 2)
                    v.wait_ge(S["qkv_ready"], b + 1)
                    nc.vector.tensor_copy(xT[:], psA[:, 0:512]).then_inc(S["xT_ready"], 1)
                    v.wait_ge(S["qkv_ready"], b + 2)
                    kq = psA[:, 512:2560].rearrange("p (j x) -> p j x", j=4)[:, :, 0:256].rearrange("p j (h d) -> p j h d", d=AD)
                    nc.vector.tensor_reduce(s1[:], kq, AX.X, ALU.add).then_inc(S["h_sum"], 1)
                    v.wait_ge(S["h_sum"], b + 1)
                    nc.vector.tensor_scalar(s1[:], s1[:], -1.0 / AD, None, ALU.mult).then_inc(S["h_mean"], 1)
                    v.wait_ge(S["h_mean"], b + 1)
                    nc.vector.tensor_tensor(cen[:], kq, bcast(s1[:], 3, AD), ALU.add).then_inc(S["h_cen"], 1)
                    v.wait_ge(S["h_sq"], b + 1)
                    nc.vector.tensor_reduce(vr[:], sq[:], AX.X, ALU.add).then_inc(S["h_var"], 1)
                    v.wait_ge(S["h_var"], b + 1)
                    nc.vector.tensor_scalar(vr[:], vr[:], 1.0 / AD, 1e-5, ALU.mult, ALU.add).then_inc(S["h_eps"], 1)
                    v.wait_ge(S["h_norm"], b + 1)
                    for k in range(2):
                        x = cen[:, :, 16 * k:16 * k + 16, :]
                        nc.vector.tensor_tensor(x, x, bcast(bcast(hw[:, k, 0, :], 1, 16), 1, 4), ALU.mult).then_inc(S["h_gain"], 1)
                    for k in range(2):
                        v.wait_ge(S["h_gain"], 2 * b + k + 1)
                        x = cen[:, :, 16 * k:16 * k + 16, :]
                        nc.vector.tensor_tensor(x, x, bcast(bcast(hw[:, k, 1, :], 1, 16), 1, 4), ALU.add).then_inc(S["h_bias"], 1)
                    sides = [(cen[:, :, 0:16, :], kp, K_PARTS), (cen[:, :, 16:32, :], qp, Q_PARTS)]
                    block_of = lambda t, where, part: t[:, :, :, where[part][0] * AD:where[part][0] * AD + AD]
                    for k, (x, t, where) in enumerate(sides):
                        v.wait_ge(S["h_bias"], 2 * b + k + 1)
                        nc.vector.tensor_copy(block_of(t, where, "h"), x).then_inc(S["part_h"], 1)
                    for k, (x, t, where) in enumerate(sides):
                        v.wait_ge(S["part_h"], 2 * b + k + 1)
                        nc.vector.tensor_tensor(x, x, block_of(t, where, "h"), ALU.subtract).then_inc(S["rest_m"], 1)
                    for k, (x, t, where) in enumerate(sides):
                        v.wait_ge(S["rest_m"], 2 * b + k + 1)
                        nc.vector.tensor_copy(block_of(t, where, "m"), x).then_inc(S["part_m"], 1)
                    for k, (x, t, where) in enumerate(sides):
                        v.wait_ge(S["part_m"], 2 * b + k + 1)
                        nc.vector.tensor_tensor(block_of(t, where, "l"), x, block_of(t, where, "m"), ALU.subtract).then_inc(S["part_l"], 1)

                    def last_groups(dst, turned, ready):
                        v.wait_ge(S[turned], 2 * b + 2)
                        nc.vector.tensor_copy(dst[:, 4:6].rearrange("p a b -> p (a b)"), psA[:, 2048:3072])
                        nc.vector.tensor_copy(dst[:, 6:8].rearrange("p a b -> p (a b)"), psB[:]).then_inc(S[ready], 1)

                    last_groups(kT, "k_turned", "kT_ready")
                    last_groups(qT, "q_turned", "qT_ready")
                    for h in range(AH):
                        v.wait_ge(S["s_ready"], b * AH + h + 1)
                        for qi in range(4):
                            o, n = lay(qi + 1)
                            o += 1536 * (h % 2)
                            m = nc.vector.tensor_reduce(nm[:, qi, h:h + 1], psA[:, o:o + n], AX.X, ALU.max, negate=True)
                        m.then_inc(S["mx_done"], 1)
                    v.wait_ge(S["mx_done"], (b + 1) * AH + 1)
                    nc.vector.tensor_copy(qp[:, :, :, PARTS], nm[:]).then_inc(S["nm_h"], 1)
                    v.wait_ge(S["nm_h"], 2 * b + 1)
                    nc.vector.tensor_tensor(nm[:], nm[:], qp[:, :, :, PARTS], ALU.subtract).then_inc(S["nm_h"], 1)
                    v.wait_ge(S["nm_h"], 2 * b + 2)
                    nc.vector.tensor_copy(qp[:, :, :, PARTS + 1], nm[:]).then_inc(S["nm_m"], 1)
                    v.wait_ge(S["nm_m"], b + 1)
                    nc.vector.tensor_tensor(qp[:, :, :, PARTS + 2], nm[:], qp[:, :, :, PARTS + 1], ALU.subtract).then_inc(S["nm_parts"], 1)
                    last_groups(qT, "q2_turned", "qT2_ready")
                    for g in range(4):
                        v.wait_ge(S["av_done"], b * AH + 4 * (g + 1) + 1)
                        nc.vector.tensor_copy(OT[:, g], psB[:, (g % 2) * 512:(g % 2) * 512 + 512]).then_inc(S["o_kept"], 1)
                    v.wait_ge(S["ot_turned"], b + 1)
                    ov = psA[:, 0:2048].rearrange("p (j h d) -> p j h d", j=4, h=AH)
                    nc.vector.reciprocal(rd[:], ov[:, :, :, AD]).then_inc(S["rd_ready"], 1)
                    v.wait_ge(S["rd_ready"], b + 1)
                    nc.vector.tensor_tensor(on[:], ov[:, :, :, 0:AD], bcast(rd[:], 3, AD), ALU.mult).then_inc(S["on_ready"], 1)
                    v.wait_ge(S["y_ready"], b + 1)
                    xv = X[:].rearrange("p (b j) c -> p b j c", b=B)
                    nc.vector.tensor_tensor(xv[:, b], psB[:, 512:1024].rearrange("p (j c) -> p j c", j=4), xv[:, b], ALU.add).then_inc(S["y_added"], 1)

            @block.gpsimd
            def _(g):
                with g.Fori(0, B) as b:
                    g.wait_ge(S["h_cen"], b + 1)
                    nc.gpsimd.tensor_tensor(sq[:], cen[:], cen[:], ALU.mult).then_inc(S["h_sq"], 1)
                    g.wait_ge(S["h_eps"], b + 1)
                    nc.gpsimd.tensor_tensor(vr[:], vr[:], mh[:], ALU.pow).then_inc(S["h_rstd"], 1)
                    g.wait_ge(S["h_rstd"], b + 1)
                    nc.gpsimd.tensor_tensor(cen[:], cen[:], bcast(vr[:], 3, AD), ALU.mult).then_inc(S["h_norm"], 1)
        clear(nc, S.values())


def attention_consts():
    a = np.arange(128)
    tri = np.zeros((128, 2, 128), np.float32)
    tri[:, 0] = np.where(a[None, :] > a[:, None], -1e30, 0)
    tri[:, 1] = np.where(a[:, None] > a[None, :], -1e30, 0)
    return {"c_tri": tri.astype("bfloat16")}


LAYERS, LH, LD, LW = 6, 16, 64, 32
INNER = LH * LD
FF = 341
FC = (114, 114, 113)

TILE_COUNTS = {n: 1 for n in """half_copied shifted xs_ready xs_turned xsT_ready q_ready k_ready q_rot k_rot q_add k_add
    q_nrm k_nrm q_turned k_turned qT_ready kT_ready up_ready s_ready mx_ready d_ready exp_done den_ready rden_ready
    p_ready bd_ready o_ready x_added kept""".split()}
TILE_COUNTS.update(sq_done=2, ss_sum=2, ss_ready=2, rn_ready=2, u_ready=4, u_copied=4)

FF_COUNTS = "f_shift f_xs f_bn f_var f_rstd0 f_rstd f_xn f_turn f_xnT f_gate f_gelu f_a f_h f_out f_added f_half".split()

def local_layers(nc, XF, c, w):
    with ExitStack() as ctx:
        sb = lambda n, s, d=F32: ctx.enter_context(nc.sbuf_tensor("L" + n, s, d))
        ps = lambda n, s, d=F32: ctx.enter_context(nc.psum_tensor("L" + n, s, d))
        sem = lambda n: ctx.enter_context(nc.semaphore("L" + n))
        XA = sb("XA", [P, B, 5, D])
        wqk = sb("wqk", [P, 2048]); uw = sb("uw", [P, LH, D])
        trig = sb("trig", [P, 4, 4, LD]); tab = sb("tab", [P, 4, 4, LD]); scl = sb("scl", [P, 4, LD])
        mask = sb("mask", [P, 2, 512], BF16); identb = sb("identb", [P, P], BF16)
        shift = sb("shift", [P, 2, P]); mhalf = sb("mhalf", [P, 32])
        wv = sb("wv", [P, 1024]); wvT = sb("wvT", [P, 8, P]); wo = sb("wo", [P, 8, D])
        w1 = sb("w1", [P, 2 * FF]); w2 = sb("w2", [P, 3, D]); b1 = sb("b1", [P, 6]); b2 = sb("b2", [1, D]); ones1 = sb("ones1", [1, P])
        lng = sb("lng", [P, 2])
        xs = sb("xs", [P, D]); xsT = sb("xsT", [P, 2, P])
        sq = sb("sq", [P, 2048]); ss = sb("ss", [P, 32]); rn = sb("rn", [P, 32])
        ra = sb("ra", [P, 2, 1024]); rb = sb("rb", [P, 2, 1024])
        qz = sb("qz", [P, 8, 4, 64]); kT = sb("kT", [P, 8, LW + P])
        U = sb("U", [P, 4, LH, D]); Up = sb("Up", [P, 4, 4, D])
        pr = sb("pr", [P, 2, LH, 64]); nmx = sb("nmx", [P, LH]); den = sb("den", [P, LH]); rden = sb("rden", [P, LH])
        BD = sb("BD", [P, LH, P]); BP = sb("BP", [P, 4, LW])
        psQ = ps("psQ", [P, 1024]); psK = ps("psK", [P, 1024]); psU = ps("psU", [P, 1024]); psT = ps("psT", [P, 512]); psO = ps("psO", [P, 512])
        xs4 = sq[:, 0:512].rearrange("p (j c) -> p j c", j=4); xn4 = sq[:, 512:1024].rearrange("p (j c) -> p j c", j=4)
        xnT = sq[:, 1024:1536]
        G = ra[:, :, :].rearrange("p a b -> p (a b)")[:, 0:1536].rearrange("p (a b) -> p a b", a=3)
        Hh = rb[:, :, :].rearrange("p a b -> p (a b)")[:, 0:1536].rearrange("p (a b) -> p a b", a=3)
        st = sb("st", [P, 4, 6]); mv = sb("mv", [P, 4, 2]); rs = sb("rs", [P, 4]); ve = sb("ve", [P, 4])
        ident = c["ident"]
        S = {n: sem(n) for n in """const_loaded zeroed w_loaded wv_turned wvT_ready uw_summed uw_half uw_ready scl_tab
          half_copied shifted xs_ready xs_turned xsT_ready q_ready k_ready sq_done ss_ready ss_sum rn_ready
          q_rot k_rot q_add k_add q_nrm k_nrm u_ready u_copied q_turned k_turned qT_ready kT_ready up_ready s_ready mx_ready d_ready exp_done
          den_ready rden_ready p_ready bd_ready o_ready x_added kept
          f_shift f_xs f_bn f_var f_rstd0 f_rstd f_xn f_turn f_xnT f_gate f_gelu f_a f_h f_out f_added f_half passed""".split()}
        XFv, XAv = XF, XA

        with nc.Block() as block:
            @block.sync
            def _(sp):
                sp.dma_start(trig[:], w["c_trig"].rearrange("k (j p) d -> p k j d", p=P)).then_inc(S["const_loaded"], 16)
                sp.dma_start(mask[:], w["c_lmask"]).then_inc(S["const_loaded"], 16)
                sp.dma_start(identb[:], w["c_identb"]).then_inc(S["const_loaded"], 16)
                sp.dma_start(shift[:], w["c_shift"].rearrange("k p n -> p k n")).then_inc(S["const_loaded"], 16)
                sp.wait_ge(S["const_loaded"], 64)

            @block.vector
            def _(v):
                nc.vector.memset(XA[:, :, 0, :], 0.0)
                nc.vector.memset(kT[:, :, 0:LW], 0.0)
                nc.vector.memset(Up[:], 0.0)
                nc.vector.memset(qz[:], 0.0)
                nc.vector.memset(ones1[:], 1.0)
                nc.vector.memset(BD[:], 0.0).then_inc(S["zeroed"], 1)

            @block.gpsimd
            def _(g):
                nc.gpsimd.memset(mhalf[:], -0.5)

            @block.scalar
            def _(act):
                for n, per_tile in TILE_COUNTS.items():
                    act.sem_inc(S[n], 2 * per_tile)
                for n in FF_COUNTS:
                    act.sem_inc(S[n], 1)

        with nc.Fori(0, LAYERS) as l:
            with nc.Block() as block:
                @block.sync
                def _(sp):
                    n = S["w_loaded"]
                    Wq = w["Wqkv"]
                    sp.dma_start(wqk[:], Wq[l, :, 0:2048]).then_inc(n, 16)
                    sp.dma_start(wv[:], Wq[l, :, 2048:3072]).then_inc(n, 16)
                    sp.dma_start(wo[:], w["Wo"][l].rearrange("(h p) c -> p h c", p=P)).then_inc(n, 16)
                    for k, nm in ((0, "q_scale"), (2, "k_scale")):
                        sp.dma_start(scl[:, k, :], rows(w[nm][l])).then_inc(n, 16)
                        sp.dma_start(scl[:, k + 1, 0:32], rows(w[nm][l, 32:64])).then_inc(n, 16)
                        sp.dma_start(scl[:, k + 1, 32:64], rows(w[nm][l, 0:32])).then_inc(n, 16)
                    sp.dma_start(w1[:], w["W1"][l]).then_inc(n, 16)
                    sp.dma_start(w2[0:114, 0:2, :], w["W2"][l, 0:228, :].rearrange("(k p) c -> p k c", p=114)).then_inc(n, 16)
                    sp.dma_start(w2[0:113, 2, :], w["W2"][l, 228:341, :]).then_inc(n, 16)
                    for k in range(6):
                        f0 = (k // 3) * FF + (k % 3) * 114
                        nf = FC[k % 3]
                        sp.dma_start(b1[0:nf, k:k + 1], w["b1"][l, f0:f0 + nf].unsqueeze(1)).then_inc(n, 16)
                    sp.dma_start(b2[:], w["b2"][l].unsqueeze(0)).then_inc(n, 16)
                    sp.dma_start(lng[:, 0:1], w["ln_g"][l].unsqueeze(1)).then_inc(n, 16)
                    sp.dma_start(lng[:, 1:2], w["ln_b"][l].unsqueeze(1)).then_inc(n, 16)

                @block.tensor
                def _(pe):
                    pe.wait_ge(S["w_loaded"], l * (16 * 21) + 16 * 21)
                    for j in range(8):
                        m = nc.tensor.transpose(psQ[:, j * P:(j + 1) * P], wv[:, j * P:(j + 1) * P], ident[:])
                    m.then_inc(S["wv_turned"], 1)
                    pe.wait_ge(S["wvT_ready"], l + 1)
                    for h in range(LH):
                        r = slice(64 * (h % 2), 64 * (h % 2) + 64)
                        tgt = (psK if h % 2 else psU)[:, (h // 2) * P:(h // 2 + 1) * P]
                        m = nc.tensor.matmul(tgt, wvT[r, h // 2, :], wo[r, h // 2, :], start=True, stop=True)
                    m.then_inc(S["uw_summed"], 1)

                @block.vector
                def _(v):
                    v.wait_ge(S["wv_turned"], l + 1)
                    nc.vector.tensor_copy(wvT[:].rearrange("p a b -> p (a b)"), psQ[:]).then_inc(S["wvT_ready"], 1)
                    v.wait_ge(S["uw_summed"], l + 1)
                    uv = uw[:].rearrange("p (a two) c -> p two a c", two=2)
                    nc.vector.tensor_copy(uv[:, 0], psU[:].rearrange("p (a c) -> p a c", a=8))
                    nc.vector.tensor_copy(uv[:, 1], psK[:].rearrange("p (a c) -> p a c", a=8)).then_inc(S["uw_ready"], 1)

                @block.gpsimd
                def _(g):
                    g.wait_ge(S["w_loaded"], l * (16 * 21) + 16 * 21)
                    for k in range(4):
                        nc.gpsimd.tensor_tensor(tab[:, k], trig[:, k], bcast(scl[:, k, :], 1, 4), ALU.mult).then_inc(S["scl_tab"], 1)

            count = lambda b, j: l * 32 + b * 4 + (j + 2)
            moved = lambda b, j, n: (b + (j + n) // 4, (j + n) % 4)
            with nc.Block() as block:
                @block.tensor
                def _(pe):
                    def shift_in(b, j):
                        nc.tensor.matmul(psT[:, 0:64], shift[:, 0, :], XF[:, b, j + 1, 64:128], start=True, stop=False)
                        nc.tensor.matmul(psT[:, 0:64], shift[:, 1, :], XF[:, b, j, 64:128], start=False, stop=True).then_inc(S["shifted"], 1)

                    def turn_x(i):
                        pe.wait_ge(S["half_copied"], i + 1)
                        pe.wait_ge(S["xs_ready"], i + 1)
                        nc.tensor.transpose(psT[:, P:2 * P], xs[:], ident[:]).then_inc(S["xs_turned"], 1)

                    def project_qk(i, j):
                        pe.wait_ge(S["xsT_ready"], i + 1)
                        for s, psX, free, ready in ((0, psQ, "qT_ready", "q_ready"), (1, psK, "kT_ready", "k_ready")):
                            pe.wait_ge(S[free], i)
                            for n in range(2):
                                c0 = s * 1024 + n * 512
                                m = nc.tensor.matmul(psX[:, n * 512:(n + 1) * 512], xsT[:, j % 2, :], wqk[:, c0:c0 + 512], start=True, stop=True)
                            m.then_inc(S[ready], 1)

                    def turn(i, s, psX, normed, turned):
                        pe.wait_ge(S[normed], i + 1)
                        for k in range(8):
                            m = nc.tensor.transpose(psX[:, k * P:(k + 1) * P], ra[:, s, k * P:(k + 1) * P], ident[:])
                        m.then_inc(S[turned], 1)

                    def project_u(i, j):
                        pe.wait_ge(S["d_ready"], i)
                        for n in range(4):
                            if n > 1:
                                pe.wait_ge(S["u_copied"], 4 * i + (n - 1))
                            nc.tensor.matmul(psU[:, (n % 2) * 512:(n % 2) * 512 + 512], xsT[:, j % 2, :], uw[:, 4 * n:4 * n + 4, :], start=True, stop=True).then_inc(S["u_ready"], 1)

                    def scores(i, j):
                        pe.wait_ge(S["qT_ready"], i + 1)
                        pe.wait_ge(S["kT_ready"], i + 1)
                        pe.wait_ge(S["u_copied"], 4 * i + 4)
                        for a in range(2):
                            nc.tensor.matmul(psU[:, a * 512:(a + 1) * 512], identb[:], mask[:, 0 if j + a == 0 else 1, :], start=True, stop=True)
                            for hp in range(8):
                                for wp in range(2):
                                    wd = 2 * a + wp
                                    m = nc.tensor.matmul(psU[64 * wp:64 * wp + 64, a * 512 + hp * 64:a * 512 + hp * 64 + 64],
                                                         qz[:, hp, wd, :], kT[:, hp, 32 * wd:32 * wd + 64],
                                                         start=False, stop=True, skip_group_check=True)
                        m.then_inc(S["s_ready"], 1)

                    def mix(i, j):
                        pe.wait_ge(S["bd_ready"], i + 1)
                        pe.wait_ge(S["up_ready"], i)
                        pe.wait_ge(S["x_added"], i)
                        for k in range(LH):
                            nc.tensor.matmul(psO[:, 0:D], BD[:, k, :], U[:, j, (k % 8) * 2 + k // 8, :], start=(k == 0), stop=True, skip_group_check=True)
                        for k in range(4):
                            m = nc.tensor.matmul(psO[0:32, 0:D], BP[:, k, :], Up[:, (j + 3) % 4, k, :], start=False, stop=True, skip_group_check=True)
                        m.then_inc(S["o_ready"], 1)

                    def step(b, j, mixes=True, left=9):
                        i = count(b, j)
                        if left > 0:
                            project_qk(i + 1, (j + 1) % 4)
                        scores(i, j)
                        if mixes:
                            mix(i - 2, (j + 2) % 4)
                        if left > 1:
                            shift_in(*moved(b, j, 2))
                        if left > 0:
                            project_u(i + 1, (j + 1) % 4)
                            turn(i + 1, 0, psQ, "q_nrm", "q_turned")
                        if left > 1:
                            turn_x(i + 2)
                        if left > 0:
                            turn(i + 1, 1, psK, "k_nrm", "k_turned")

                    i = count(0, 0)
                    shift_in(0, 0)
                    turn_x(i)
                    project_qk(i, 0)
                    shift_in(0, 1)
                    project_u(i, 0)
                    turn(i, 0, psQ, "q_nrm", "q_turned")
                    turn_x(i + 1)
                    turn(i, 1, psK, "k_nrm", "k_turned")
                    for j in range(4):
                        step(0, j, mixes=(j > 1))
                    with pe.Fori(1, B - 1) as b:
                        for j in range(4):
                            step(b, j)
                    for j in range(4):
                        step(B - 1, j, left=3 - j)
                    mix(count(B - 1, 2), 2)
                    mix(count(B - 1, 3), 3)

                @block.scalar
                def _(act):
                    def half(b, j, i):
                        act.wait_ge(S["xs_turned"], i)
                        nc.scalar.activation(xs[:, 0:64], XF[:, b, j + 1, 0:64], ACT.Copy).then_inc(S["half_copied"], 1)

                    def square(i, s, psX, ready):
                        act.wait_ge(S[ready], i + 1)
                        act.wait_ge(S["ss_ready"], 2 * i - (1 - s))
                        nc.scalar.activation(sq[:, s * 1024:(s + 1) * 1024], psX[:], ACT.Square).then_inc(S["sq_done"], 1)

                    def evacuate(i, j):
                        for n in range(4):
                            act.wait_ge(S["u_ready"], 4 * i + (n + 1))
                            nc.scalar.activation(U[:, j, 4 * n:4 * n + 4, :].rearrange("p a b -> p (a b)"), psU[:, (n % 2) * 512:(n % 2) * 512 + 512], ACT.Copy).then_inc(S["u_copied"], 1)
                        act.wait_ge(S["q_turned"], i + 1)
                        qv = psQ[:].rearrange("p (h w q) -> p h w q", h=8, w=4)
                        nc.scalar.activation(qz[0:64, :, :, 0:32], qv[0:64], ACT.Copy)
                        nc.scalar.activation(qz[64:128, :, :, 32:64], qv[64:128], ACT.Copy).then_inc(S["qT_ready"], 1)
                        act.wait_ge(S["k_turned"], i + 1)
                        act.wait_ge(S["kept"], i)
                        nc.scalar.activation(kT[:, :, LW:LW + P], psK[:].rearrange("p (a b) -> p a b", a=8), ACT.Copy).then_inc(S["kT_ready"], 1)

                    def step(b, j, left=9):
                        i = count(b, j)
                        if left > 0:
                            square(i + 1, 0, psQ, "q_ready")
                            square(i + 1, 1, psK, "k_ready")
                        act.wait_ge(S["s_ready"], i + 1)
                        nc.scalar.activation(kT[:, :, 0:LW], kT[:, :, P:P + LW], ACT.Copy).then_inc(S["kept"], 1)
                        act.wait_ge(S["u_copied"], 4 * i + 4)
                        for g in range(4):
                            h0 = 8 * (g % 2) + g // 2
                            m = nc.scalar.activation(Up[32 * g:32 * g + 32, j], U[96:128, j, h0:h0 + 7:2, :], ACT.Copy)
                        m.then_inc(S["up_ready"], 1)
                        act.wait_ge(S["d_ready"], i + 1)
                        nc.scalar.activation(pr[:, j % 2], pr[:, j % 2], ACT.Exp).then_inc(S["exp_done"], 1)
                        if left > 1:
                            half(*moved(b, j, 2), i + 2)
                        if left > 0:
                            evacuate(i + 1, (j + 1) % 4)

                    i = count(0, 0)
                    half(0, 0, i)
                    square(i, 0, psQ, "q_ready")
                    square(i, 1, psK, "k_ready")
                    half(0, 1, i + 1)
                    evacuate(i, 0)
                    with act.Fori(0, B - 1) as b:
                        for j in range(4):
                            step(b, j)
                    for j in range(4):
                        step(B - 1, j, left=3 - j)

                @block.vector
                def _(v):
                    def shifted_half(i):
                        v.wait_ge(S["shifted"], i + 1)
                        v.wait_ge(S["xs_turned"], i)
                        nc.vector.tensor_copy(xs[:, 64:128], psT[:, 0:64]).then_inc(S["xs_ready"], 1)

                    def turned_x(i, j):
                        v.wait_ge(S["xs_turned"], i + 1)
                        v.wait_ge(S["u_ready"], 4 * i - 4)
                        nc.vector.tensor_copy(xsT[:, j % 2, :], psT[:, P:2 * P]).then_inc(S["xsT_ready"], 1)

                    def rotate(i, j, s, psX, ready, turned, rot, add):
                        v.wait_ge(S[ready], i + 1)
                        v.wait_ge(S["sq_done"], 2 * i + (s + 1))
                        v.wait_ge(S[turned], i)
                        p4 = psX[:].rearrange("p (h d) -> p h d", h=LH)
                        A = ra[:, s].rearrange("p (h d) -> p h d", h=LH)
                        Bb = rb[:, s].rearrange("p (h d) -> p h d", h=LH)
                        nc.vector.tensor_tensor(A, p4, bcast(tab[:, 2 * s, j, :], 1, LH), ALU.mult)
                        nc.vector.tensor_tensor(Bb[:, :, 0:32], p4[:, :, 32:64], bcast(tab[:, 2 * s + 1, j, 0:32], 1, LH), ALU.mult)
                        nc.vector.tensor_tensor(Bb[:, :, 32:64], p4[:, :, 0:32], bcast(tab[:, 2 * s + 1, j, 32:64], 1, LH), ALU.mult).then_inc(S[rot], 1)
                        v.wait_ge(S["rn_ready"], 2 * i + (s - 1))
                        nc.vector.tensor_reduce(ss[:, 16 * s:16 * s + 16], sq[:, s * 1024:(s + 1) * 1024].rearrange("p (h d) -> p h d", d=LD), AX.X, ALU.add).then_inc(S["ss_sum"], 1)
                        v.wait_ge(S[rot], i + 1)
                        nc.vector.tensor_tensor(ra[:, s], ra[:, s], rb[:, s], ALU.add).then_inc(S[add], 1)
                        v.wait_ge(S["ss_sum"], 2 * i + (s + 1))
                        nc.vector.tensor_scalar(ss[:, 16 * s:16 * s + 16], ss[:, 16 * s:16 * s + 16], 1e-24, None, ALU.max).then_inc(S["ss_ready"], 1)

                    def add_x(b, j, i):
                        v.wait_ge(S["o_ready"], i + 1)
                        nc.vector.tensor_tensor(XA[:, b, j + 1, :], psO[:, 0:D], XF[:, b, j + 1, :], ALU.add).then_inc(S["x_added"], 1)

                    def turn_probs(i, j):
                        v.wait_ge(S["p_ready"], i + 1)
                        v.wait_ge(S["o_ready"], i)
                        for a in range(2):
                            for wp in range(2):
                                wd = 2 * a + wp
                                q = slice(32 * wd, 32 * wd + 32)
                                for par in range(2):
                                    r = slice(64 * wp + 32 * par, 64 * wp + 32 * par + 32)
                                    h = slice(8 * par, 8 * par + 8)
                                    src = pr[r, j % 2, 8 * a:8 * a + 8]
                                    nc.vector.transpose(BD[q, h, q], src[:, :, 32:64])
                                    if wd:
                                        nc.vector.transpose(BD[q.start - 32:q.start, h, q], src[:, :, 0:32])
                        for g in range(4):
                            m = nc.vector.transpose(BP[32 * g:32 * g + 32], pr[32 * (g // 2):32 * (g // 2) + 32, j % 2, 4 * (g % 2):4 * (g % 2) + 4, 0:32])
                        m.then_inc(S["bd_ready"], 1)

                    Q = (0, psQ, "q_ready", "q_turned", "q_rot", "q_add")
                    K = (1, psK, "k_ready", "k_turned", "k_rot", "k_add")

                    def step(b, j, turns=True, adds=True, left=9):
                        i = count(b, j)
                        if left > 0:
                            rotate(i + 1, (j + 1) % 4, *Q)
                        v.wait_ge(S["s_ready"], i + 1)
                        sv = psU[:].rearrange("p (h d) -> p h d", d=64)
                        nc.vector.tensor_reduce(nmx[:], sv, AX.X, ALU.max, negate=True).then_inc(S["mx_ready"], 1)
                        v.wait_ge(S["mx_ready"], i + 1)
                        v.wait_ge(S["bd_ready"], i - 1)
                        nc.vector.tensor_tensor(pr[:, j % 2], sv, bcast(nmx[:], 2, 64), ALU.add).then_inc(S["d_ready"], 1)
                        if left > 0:
                            rotate(i + 1, (j + 1) % 4, *K)
                        if left > 1:
                            shifted_half(i + 2)
                        v.wait_ge(S["exp_done"], i + 1)
                        nc.vector.tensor_reduce(den[:], pr[:, j % 2], AX.X, ALU.add).then_inc(S["den_ready"], 1)
                        if left > 1:
                            turned_x(i + 2, j)
                        v.wait_ge(S["den_ready"], i + 1)
                        v.wait_ge(S["p_ready"], i)
                        nc.vector.reciprocal(rden[:], den[:]).then_inc(S["rden_ready"], 1)
                        if adds:
                            add_x(*moved(b, j, -2), i - 2)
                        if turns:
                            turn_probs(i - 1, j + 1)

                    i = count(0, 0)
                    shifted_half(i)
                    turned_x(i, 0)
                    rotate(i, 0, *Q)
                    rotate(i, 0, *K)
                    shifted_half(i + 1)
                    turned_x(i + 1, 1)
                    for j in range(4):
                        step(0, j, turns=(j > 0), adds=(j > 1))
                    with v.Fori(1, B - 1) as b:
                        for j in range(4):
                            step(b, j)
                    for j in range(4):
                        step(B - 1, j, left=3 - j)
                    i = count(B - 1, 3)
                    add_x(B - 1, 2, i - 1)
                    turn_probs(i, 3)
                    add_x(B - 1, 3, i)

                @block.gpsimd
                def _(g):
                    def unit(i, s, add, nrm):
                        g.wait_ge(S["ss_ready"], 2 * i + (s + 1))
                        nc.gpsimd.tensor_tensor(rn[:, 16 * s:16 * s + 16], ss[:, 16 * s:16 * s + 16], mhalf[:, 16 * s:16 * s + 16], ALU.pow).then_inc(S["rn_ready"], 1)
                        g.wait_ge(S["rn_ready"], 2 * i + (s + 1))
                        g.wait_ge(S[add], i + 1)
                        A = ra[:, s].rearrange("p (h d) -> p h d", h=LH)
                        nc.gpsimd.tensor_tensor(A, A, bcast(rn[:, 16 * s:16 * s + 16], 2, LD), ALU.mult).then_inc(S[nrm], 1)

                    def step(i, j, left=9):
                        if left > 0:
                            unit(i + 1, 0, "q_add", "q_nrm")
                            unit(i + 1, 1, "k_add", "k_nrm")
                        g.wait_ge(S["rden_ready"], i + 1)
                        nc.gpsimd.tensor_tensor(pr[:, j % 2], pr[:, j % 2], bcast(rden[:], 2, 64), ALU.mult).then_inc(S["p_ready"], 1)

                    i = count(0, 0)
                    unit(i, 0, "q_add", "q_nrm")
                    unit(i, 1, "k_add", "k_nrm")
                    with g.Fori(0, B - 1) as b:
                        for j in range(4):
                            step(count(b, j), j)
                    for j in range(4):
                        step(count(B - 1, j), j, left=3 - j)

            with nc.Block() as block:
                @block.tensor
                def _(pe):
                    with pe.Fori(0, B) as b:
                        i = l * B + b + 1
                        pe.wait_ge(S["f_xnT"], i)
                        for j in range(4):
                            nc.tensor.matmul(psT[:, j * 64:j * 64 + 64], shift[:, 0, :], XA[:, b, j + 1, 64:128], start=True, stop=False)
                            m = nc.tensor.matmul(psT[:, j * 64:j * 64 + 64], shift[:, 1, :], XA[:, b, j, 64:128], start=False, stop=True)
                        m.then_inc(S["f_shift"], 1)
                        pe.wait_ge(S["f_xn"], i + 1)
                        for j in range(4):
                            m = nc.tensor.transpose(psT[:, j * P:(j + 1) * P], xn4[:, j, :], ident[:])
                        m.then_inc(S["f_turn"], 1)
                        pe.wait_ge(S["f_xnT"], i + 1)
                        pe.wait_ge(S["f_h"], i)
                        banks = [psQ[:, 0:512], psQ[:, 512:1024], psK[:, 0:512], psK[:, 512:1024], psU[:, 0:512], psU[:, 512:1024]]
                        for s, nm in ((1, "f_gate"), (0, "f_a")):
                            for k in range(3):
                                f0 = s * FF + k * 114
                                m = nc.tensor.matmul(banks[s * 3 + k][0:FC[k], :], w1[:, f0:f0 + FC[k]], xnT, start=True, stop=True)
                            m.then_inc(S[nm], 1)
                        pe.wait_ge(S["f_h"], i + 1)
                        pe.wait_ge(S["f_added"], i)
                        for j in range(4):
                            o = psO[:, j * P:(j + 1) * P]
                            nc.tensor.matmul(o, ones1[:], b2[:], start=True, stop=False)
                            for k in range(3):
                                m = nc.tensor.matmul(o, Hh[0:FC[k], k, j * P:(j + 1) * P], w2[0:FC[k], k, :], start=False, stop=(k == 2))
                        m.then_inc(S["f_out"], 1)

                @block.scalar
                def _(act):
                    with act.Fori(0, B) as b:
                        i = l * B + b + 1
                        act.wait_ge(S["f_bn"], i)
                        act.wait_ge(S["f_xn"], i)
                        nc.scalar.activation(xs4[:, :, 0:64], XA[:, b, 1:5, 0:64], ACT.Copy).then_inc(S["f_half"], 1)
                        act.wait_ge(S["f_turn"], i + 1)
                        act.wait_ge(S["f_a"], i)
                        nc.scalar.activation(xnT, psT[:], ACT.Identity, bias=lng[:, 1:2], scale=lng[:, 0:1]).then_inc(S["f_xnT"], 1)
                        act.wait_ge(S["f_gate"], i + 1)
                        act.wait_ge(S["f_h"], i)
                        banks = [psK[:, 512:1024], psU[:, 0:512], psU[:, 512:1024]]
                        for k in range(3):
                            m = nc.scalar.activation(G[0:FC[k], k, :], banks[k][0:FC[k], :], ACT.Gelu, bias=b1[0:FC[k], 3 + k:4 + k])
                        m.then_inc(S["f_gelu"], 1)

                @block.vector
                def _(v):
                    with v.Fori(0, B) as b:
                        i = l * B + b + 1
                        v.wait_ge(S["f_shift"], i + 1)
                        nc.vector.tensor_copy(xs4[:, :, 64:128], psT[:, 0:256].rearrange("p (j c) -> p j c", j=4)).then_inc(S["f_xs"], 1)
                        v.wait_ge(S["f_xs"], i + 1)
                        v.wait_ge(S["f_half"], i + 1)
                        for j in range(4):
                            m = nc.vector.bn_stats(st[:, j, :], xs4[:, j, :])
                        m.then_inc(S["f_bn"], 1)
                        v.wait_ge(S["f_bn"], i + 1)
                        v.sem_inc(S["passed"], 1)
                        for j in range(4):
                            m = nc.vector.bn_aggr(mv[:, j, :], st[:, j, :])
                        m.then_inc(S["f_var"], 1)
                        v.wait_ge(S["f_var"], i + 1)
                        v.wait_ge(S["f_rstd"], i)
                        nc.vector.tensor_scalar(ve[:], mv[:, :, 1], 1e-5, None, ALU.add).then_inc(S["f_rstd0"], 1)
                        v.wait_ge(S["f_rstd"], i + 1)
                        v.wait_ge(S["f_turn"], i)
                        for j in range(4):
                            m = nc.vector.tensor_scalar(xn4[:, j, :], xs4[:, j, :], mv[:, j, 0:1], rs[:, j:j + 1], ALU.subtract, ALU.mult)
                        m.then_inc(S["f_xn"], 1)
                        v.wait_ge(S["f_a"], i + 1)
                        v.wait_ge(S["f_gelu"], i + 1)
                        v.wait_ge(S["f_out"], i)
                        banks = [psQ[:, 0:512], psQ[:, 512:1024], psK[:, 0:512]]
                        for k in range(3):
                            m = nc.vector.scalar_tensor_tensor(out=Hh[0:FC[k], k, :], in0=banks[k][0:FC[k], :], scalar=b1[0:FC[k], k:k + 1], in1=G[0:FC[k], k, :], op0=ALU.add, op1=ALU.mult)
                        m.then_inc(S["f_h"], 1)
                        v.wait_ge(S["f_out"], i + 1)
                        nc.vector.tensor_tensor(XF[:, b, 1:5, :], psO[:].rearrange("p (j c) -> p j c", j=4), XA[:, b, 1:5, :], ALU.add).then_inc(S["f_added"], 1)

                @block.gpsimd
                def _(g):
                    with g.Fori(0, B) as b:
                        i = l * B + b + 1
                        g.wait_ge(S["f_xn"], i)
                        g.wait_ge(S["f_rstd0"], i + 1)
                        nc.gpsimd.tensor_tensor(rs[:], ve[:], mhalf[:, 0:4], ALU.pow).then_inc(S["f_rstd"], 1)
        clear(nc, S.values())


def local_consts():
    n = 512
    half = np.arange(0, LD, 2, dtype=np.float32)
    inv = (1.0 / (np.float32(10000.0) ** (half / LD))).astype(np.float32)
    t = np.arange(n, dtype=np.float32)
    fr = (t[:, None] * inv[None]).astype(np.float32)
    fr = np.concatenate([fr, fr], -1)
    base = ((half + np.float32(0.4 * LD)) / np.float32(1.4 * LD)).astype(np.float32)
    power = ((t - n // 2) / 16).astype(np.float32)
    sc = (base[None] ** power[:, None]).astype(np.float32)
    sc = np.concatenate([sc, sc], -1)
    cos, sin = np.cos(fr).astype(np.float32), np.sin(fr).astype(np.float32)
    sgn = np.concatenate([-np.ones(32), np.ones(32)]).astype(np.float32)
    inv_s = (1.0 / sc).astype(np.float32)
    trig = np.stack([8 * cos * sc, 8 * sin * sc * sgn, cos * inv_s, sin * inv_s * sgn]).astype(np.float32)
    m = np.zeros((128, 2, 8, 64), np.float32)
    q = np.arange(128) % 32
    for k in range(64):
        bad = (q < k - 32) | (q > k)
        m[:, :, :, k] = np.where(bad, -1e30, 0)[:, None, None]
    m[0:64, 0, :, 0:32] = -1e30
    sh = np.zeros((2, 128, 128), np.float32)
    sh[0, np.arange(127), np.arange(1, 128)] = 1
    sh[1, 127, 0] = 1
    return {"c_trig": trig, "c_lmask": m.reshape(128, 2, 512).astype("bfloat16"), "c_shift": sh,
            "c_identb": np.eye(128, dtype="bfloat16")}


SN, HALFK, SEQ = 16, 32, 512

def state_space(nc, X, XF, c, w):
    with ExitStack() as ctx:
        sb = lambda n, s, d=F32: ctx.enter_context(nc.sbuf_tensor("R" + n, s, d))
        ps = lambda n, s, d=F32: ctx.enter_context(nc.psum_tensor("R" + n, s, d))
        sem = lambda n: ctx.enter_context(nc.semaphore("R" + n))
        GD = 16
        pw = sb("pw", [P, 6, SN, SN]); Bv = sb("Bv", [P, HALFK, SN]); Cu = sb("Cu", [P, SN, SN]); Dm = sb("Dm", [P, 1])
        tmp = sb("tmp", [P, 4096]); kpad = sb("kpad", [P, 640])
        toep = sb("toep", [P, GD, SEQ])
        Y = sb("Y", [P, 32, D])
        wo = sb("wo", [P, D]); bo = sb("bo", [1, D]); ones1 = sb("ones1", [1, P]); lnp = sb("lnp", [P, 2]); flip = sb("flip", [P, P])
        st = sb("st", [P, 4, 6]); mv = sb("mv", [P, 4, 2]); ve = sb("ve", [P, 4]); rs = sb("rs", [P, 4]); mh = sb("mh", [P, 4])
        xn4 = sb("xn4", [P, 4, D]); gT = sb("gT", [P, 512])
        conv = ps("conv", [P, 512]); psT = ps("psT", [P, 512]); psO = ps("psO", [P, 512])
        scratch = nc.dram_tensor("Rkernels", (P + 1, 640), F32).ap()
        ident = c["ident"]
        S = {n: sem(n) for n in """loaded prod power bprod bvec cprod cvec kprod kern d_added zeroed stored toep_loaded conv_done conv_copied
          bn aggr eps rstd xhat turned gelu out added passed""".split()}
        start_at_one(nc, S, "power bvec cvec kern conv_done conv_copied gelu added out rstd turned xhat")
        with nc.Block() as block:
            @block.sync
            def _(sp):
                L = S["loaded"]
                sp.dma_start(pw[:, 0], w["A"]).then_inc(L, 16)
                sp.dma_start(Bv[:, 0, :], w["Bm"]).then_inc(L, 16)
                sp.dma_start(Cu[:, 0, :], w["Cm"]).then_inc(L, 16)
                sp.dma_start(Dm[:], w["Dm"].unsqueeze(1)).then_inc(L, 16)
                sp.dma_start(wo[:], w["W_outT"]).then_inc(L, 16)
                sp.dma_start(bo[:], w["b_out"].unsqueeze(0)).then_inc(L, 16)
                sp.dma_start(lnp[:, 0:1], w["ln_w"].unsqueeze(1)).then_inc(L, 16)
                sp.dma_start(lnp[:, 1:2], w["ln_b"].unsqueeze(1)).then_inc(L, 16)
                sp.dma_start(flip[:], w["c_flip"]).then_inc(L, 16)
                sp.wait_ge(S["d_added"], 1)
                sp.dma_start(scratch[0:P], kpad[:]).then_inc(S["stored"], 16)
                sp.wait_ge(S["stored"], 16)
            @block.gpsimd
            def _(g):
                nc.gpsimd.memset(mh[:], -0.5)
            @block.vector
            def _(v):
                nc.vector.memset(ones1[:], 1.0)
                nc.vector.memset(kpad[:], 0.0).then_inc(S["zeroed"], 1)
                v.wait_ge(S["zeroed"], 1)
                v.wait_ge(S["loaded"], 144)
                t3 = tmp[:].rearrange("p (a b c) -> p a b c", a=SN, b=SN)
                with v.Fori(0, 5) as i:
                    M = pw[:, i]
                    v.wait_ge(S["power"], i + 1)
                    nc.vector.tensor_tensor(t3, bcast(M, 2, SN), bcast(bass.AP(M.tensor, M.offset, [list(M.ap[0]), [1, SN], [SN, SN]]), 1, SN), ALU.mult).then_inc(S["prod"], 1)
                    v.wait_ge(S["prod"], i + 1)
                    nc.vector.tensor_reduce(pw[:, i + 1], t3, AX.X, ALU.add).then_inc(S["power"], 1)
                t2 = tmp[:, 0:256].rearrange("p (a b) -> p a b", a=SN)
                v.wait_ge(S["power"], 6)
                with v.Fori(0, HALFK - 1) as i:
                    v.wait_ge(S["bvec"], i + 1)
                    nc.vector.tensor_tensor(t2, pw[:, 0], bcast(Bv[:, i, :], 1, SN), ALU.mult).then_inc(S["bprod"], 1)
                    v.wait_ge(S["bprod"], i + 1)
                    nc.vector.tensor_reduce(Bv[:, i + 1, :], t2, AX.X, ALU.add).then_inc(S["bvec"], 1)
                M = pw[:, 5]
                MT = bass.AP(M.tensor, M.offset, [list(M.ap[0]), [1, SN], [SN, SN]])
                v.wait_ge(S["bvec"], HALFK)
                with v.Fori(0, SN - 1) as i:
                    v.wait_ge(S["cvec"], i + 1)
                    nc.vector.tensor_tensor(t2, bcast(Cu[:, i, :], 1, SN), MT, ALU.mult).then_inc(S["cprod"], 1)
                    v.wait_ge(S["cprod"], i + 1)
                    nc.vector.tensor_reduce(Cu[:, i + 1, :], t2, AX.X, ALU.add).then_inc(S["cvec"], 1)
                for k in range(2):
                    v.wait_ge(S["cvec"], SN)
                    if k:
                        v.wait_ge(S["kern"], k + 1)
                    t4 = tmp[:].rearrange("p (a b c) -> p a b c", a=8, b=HALFK)
                    nc.vector.tensor_tensor(t4, bcast(Cu[:, 8 * k:8 * k + 8, :], 2, HALFK), bcast(Bv[:], 1, 8), ALU.mult).then_inc(S["kprod"], 1)
                    v.wait_ge(S["kprod"], k + 1)
                    back = bass.AP(kpad[:].tensor, kpad[:, SEQ - 1 - 256 * k:SEQ].offset, [[640, P], [-HALFK, 8], [-1, HALFK]])
                    nc.vector.tensor_reduce(back, t4, AX.X, ALU.add).then_inc(S["kern"], 1)
                v.wait_ge(S["kern"], 3)
                nc.vector.tensor_tensor(kpad[:, SEQ - 1:SEQ], kpad[:, SEQ - 1:SEQ], Dm[:], ALU.add).then_inc(S["d_added"], 1)

        def taps(k, lag):
            return toep[:, k, SEQ - P - lag * P:SEQ - lag * P]

        with nc.Block() as block:
            @block.sync
            def _(sp):
                with sp.Fori(0, P // GD) as i:
                    sp.wait_ge(S["conv_done"], i + 1)
                    src = bass.AP(scratch.tensor, i * (GD * 640), [[1, P], [640, GD], [1, SEQ]])
                    sp.dma_start(toep[:], src).then_inc(S["toep_loaded"], 16)
            @block.tensor
            def _(pe):
                with pe.Fori(0, P // GD) as i:
                    pe.wait_ge(S["toep_loaded"], i * 16 + 16)
                    pe.wait_ge(S["conv_copied"], i + 1)
                    for k in range(GD):
                        o4 = conv[:, k * 32:k * 32 + 32].rearrange("p (b j) -> p b j", b=B)
                        for lag in range(4):
                            m = nc.tensor.matmul(o4[:, :, lag:4], taps(k, lag), XF[:, :, 1:5 - lag, i * GD + k], start=(lag == 0), stop=True, skip_group_check=True)
                    m.then_inc(S["conv_done"], 1)
                with pe.Fori(0, B) as b:
                    pe.wait_ge(S["xhat"], b + 2)
                    pe.wait_ge(S["gelu"], b + 1)
                    for j in range(4):
                        m = nc.tensor.matmul(psT[:, j * P:(j + 1) * P], xn4[:, j, :], flip[:], start=True, stop=True)
                    m.then_inc(S["turned"], 1)
                    pe.wait_ge(S["gelu"], b + 2)
                    pe.wait_ge(S["added"], 2 * b + 1)
                    for j in range(4):
                        o = psO[:, j * P:(j + 1) * P]
                        nc.tensor.matmul(o, ones1[:], bo[:], start=True, stop=False)
                        m = nc.tensor.matmul(o, gT[:, j * P:(j + 1) * P], wo[:], start=False, stop=True)
                    m.then_inc(S["out"], 1)
            @block.scalar
            def _(act):
                with act.Fori(0, P // GD) as i:
                    act.wait_ge(S["conv_done"], i + 2)
                    nc.scalar.activation(Y[:, :, bass.ds(i * GD, GD)], conv[:].rearrange("p (k t) -> p t k", k=GD), ACT.Copy).then_inc(S["conv_copied"], 1)
                with act.Fori(0, B) as b:
                    act.wait_ge(S["turned"], b + 2)
                    act.wait_ge(S["out"], b + 1)
                    nc.scalar.activation(gT[:], psT[:], ACT.Gelu, bias=lnp[:, 1:2], scale=lnp[:, 0:1]).then_inc(S["gelu"], 1)
            @block.vector
            def _(v):
                Yv = Y[:].rearrange("p (b j) c -> p b j c", b=B)
                Xv = X[:].rearrange("p (b j) c -> p b j c", b=B)
                v.wait_ge(S["conv_copied"], P // GD + 1)
                with v.Fori(0, B) as b:
                    for j in range(4):
                        m = nc.vector.bn_stats(st[:, j, :], Yv[:, b, j, :])
                    m.then_inc(S["bn"], 1)
                    v.wait_ge(S["bn"], b + 1)
                    v.sem_inc(S["passed"], 1)
                    for j in range(4):
                        m = nc.vector.bn_aggr(mv[:, j, :], st[:, j, :])
                    m.then_inc(S["aggr"], 1)
                    v.wait_ge(S["aggr"], b + 1)
                    v.wait_ge(S["rstd"], b + 1)
                    nc.vector.tensor_scalar(ve[:], mv[:, :, 1], 1e-5, None, ALU.add).then_inc(S["eps"], 1)
                    v.wait_ge(S["rstd"], b + 2)
                    v.wait_ge(S["turned"], b + 1)
                    for j in range(4):
                        m = nc.vector.tensor_scalar(xn4[:, j, :], Yv[:, b, j, :], mv[:, j, 0:1], rs[:, j:j + 1], ALU.subtract, ALU.mult)
                    m.then_inc(S["xhat"], 1)
                    v.wait_ge(S["out"], b + 2)
                    nc.vector.tensor_tensor(Xv[:, b], psO[:].rearrange("p (j c) -> p j c", j=4), Xv[:, b], ALU.add).then_inc(S["added"], 1)
                    v.wait_ge(S["added"], 2 * b + 2)
                    nc.vector.tensor_tensor(Xv[:, b], XF[:, b, 1:5, :], Xv[:, b], ALU.add).then_inc(S["added"], 1)
            @block.gpsimd
            def _(g):
                with g.Fori(0, B) as b:
                    g.wait_ge(S["xhat"], b + 1)
                    g.wait_ge(S["eps"], b + 1)
                    nc.gpsimd.tensor_tensor(rs[:], ve[:], mh[:], ALU.pow).then_inc(S["rstd"], 1)
        clear(nc, S.values())


E1, K1, F1, FQ = 8, 2, 408, 102

def top2_experts(nc, X, XF, c, w):
    with ExitStack() as ctx:
        sb = lambda n, s, d=F32: ctx.enter_context(nc.sbuf_tensor("E" + n, s, d))
        ps = lambda n, s, d=F32: ctx.enter_context(nc.psum_tensor("E" + n, s, d))
        sem = lambda n: ctx.enter_context(nc.semaphore("E" + n))
        up = sb("up", [P, E1, F1]); gp = sb("gp", [P, E1, F1]); dn = sb("dn", [FQ, E1, 4, D])
        ub = sb("ub", [FQ, E1, 4]); gb = sb("gb", [FQ, E1, 4]); db = sb("db", [1, E1, D])
        gw = sb("gw", [P, E1]); gbias = sb("gbias", [1, E1]); ones1 = sb("ones1", [1, P])
        before = sb("before", [P, E1, E1])
        xb = sb("xb", [P, 4, D]); xT = sb("xT", [P, 512])
        lg = sb("lg", [P, 4, E1]); mx = sb("mx", [P, 4]); sm = sb("sm", [P, 4]); sc = sb("sc", [P, 4, E1])
        gt = sb("gt", [P, 4, E1, E1]); eq = sb("eq", [P, 4, E1, E1]); rk = sb("rk", [P, 4, E1]); comb = sb("comb", [P, 4, E1])
        us = sb("us", [FQ, 2, 512]); hg = sb("hg", [FQ, 2, 512]); hs = sb("hs", [FQ, 2, 4, 512])
        psUG = ps("psUG", [P, 2, 2, 512]); psT = ps("psT", [P, 512]); psR = ps("psR", [P, 512]); psO = ps("psO", [P, 2, 512])
        ident = c["ident"]
        S = {n: sem(n) for n in """loaded ones xb_ready turned xT_ready logits r_max r_sub r_exp r_sum r_rec r_score r_cmp r_eqm r_or r_rank
          r_sel r_tot r_inv comb_ready u_ready g_ready us_ready hg_ready hs_ready out_ready added""".split()}
        start_at_one(nc, S, "hg_ready added turned out_ready hs_ready")
        with nc.Block() as block:
            @block.sync
            def _(sp):
                L = S["loaded"]
                sp.dma_start(gw[:], w["gate_wT"]).then_inc(L, 16)
                sp.dma_start(gbias[:], w["gate_b"].unsqueeze(0)).then_inc(L, 16)
                sp.dma_start(before[:], w["c_before"]).then_inc(L, 16)
                for a, n in ((up, "up_wT"), (gp, "gp_wT")):
                    sp.dma_start(a[:], w[n].rearrange("e d f -> d e f")).then_inc(L, 16)
                sp.dma_start(dn[:].rearrange("p e k d -> p (e k) d"), w["down_wT"].rearrange("e (k p) d -> p (e k) d", p=FQ)).then_inc(L, 16)
                for a, n in ((ub, "up_b4"), (gb, "gp_b4")):
                    sp.dma_start(a[:], w[n]).then_inc(L, 16)
                sp.dma_start(db[:], w["down_b"].unsqueeze(0)).then_inc(L, 16)
                sp.wait_ge(L, 144)
            @block.vector
            def _(v):
                nc.vector.memset(ones1[:], 1.0)

        def us_of(k): return us[:, k % 2, :]
        with nc.Block() as block:
            @block.tensor
            def _(pe):
                with pe.Fori(0, B) as b:
                    pe.wait_ge(S["xb_ready"], b + 1)
                    for j in range(4):
                        m = nc.tensor.transpose(psT[:, j * P:(j + 1) * P], xb[:, j, :], ident[:])
                    m.then_inc(S["turned"], 1)
                    pe.wait_ge(S["xT_ready"], b + 1)
                    for j in range(4):
                        nc.tensor.matmul(psR[:, 8 * j:8 * j + 8], ones1[:], gbias[:], start=True, stop=False)
                        m = nc.tensor.matmul(psR[:, 8 * j:8 * j + 8], xT[:, j * P:(j + 1) * P], gw[:], start=False, stop=True)
                    m.then_inc(S["logits"], 1)

                    def inner(e):
                        for k in range(4):
                            n = e * 4 + k
                            if n >= 2:
                                pe.wait_ge(S["hg_ready"], b * 32 + n)
                            else:
                                pe.wait_ge(S["hg_ready"], b * 32 + 1)
                            nc.tensor.matmul(psUG[0:FQ, n % 2, 0, :], up[:, e, k * FQ:(k + 1) * FQ], xT[:], start=True, stop=True).then_inc(S["u_ready"], 1)
                            nc.tensor.matmul(psUG[0:FQ, n % 2, 1, :], gp[:, e, k * FQ:(k + 1) * FQ], xT[:], start=True, stop=True).then_inc(S["g_ready"], 1)

                    def down(e):
                        pe.wait_ge(S["hs_ready"], b * 32 + 4 * (e + 1) + 1)
                        if e >= 2:
                            pe.wait_ge(S["added"], b * 8 + e)
                        else:
                            pe.wait_ge(S["added"], b * 8 + 1)
                        for j in range(4):
                            o = psO[:, e % 2, j * P:(j + 1) * P]
                            nc.tensor.matmul(o, ones1[:], db[:, e, :], start=True, stop=False)
                            for k in range(4):
                                m = nc.tensor.matmul(o, hs[:, e % 2, k, j * P:(j + 1) * P], dn[:, e, k, :], start=False, stop=(k == 3))
                        m.then_inc(S["out_ready"], 1)

                    inner(0)
                    for e in range(1, E1):
                        inner(e)
                        down(e - 1)
                    down(E1 - 1)

            @block.scalar
            def _(act):
                with act.Fori(0, B) as b:
                    act.wait_ge(S["turned"], b + 1)
                    nc.scalar.activation(xb[:], XF[:, b, 1:5, :], ACT.Copy).then_inc(S["xb_ready"], 1)
                    act.wait_ge(S["r_sub"], b + 1)
                    nc.scalar.activation(lg[:], lg[:], ACT.Exp).then_inc(S["r_exp"], 1)
                    for n in range(32):
                        act.wait_ge(S["u_ready"], b * 32 + n + 1)
                        if n < 2:
                            act.wait_ge(S["hg_ready"], b * 32 + 1)
                        else:
                            act.wait_ge(S["hg_ready"], b * 32 + n)
                        nc.scalar.activation(us[:, n % 2, :], psUG[0:FQ, n % 2, 0, :], ACT.Identity, bias=ub[:, n // 4, n % 4:n % 4 + 1]).then_inc(S["us_ready"], 1)
                        act.wait_ge(S["hg_ready"], b * 32 + n + 2)
                        if n // 4 >= 2:
                            act.wait_ge(S["out_ready"], b * 8 + n // 4)
                        nc.scalar.activation(hs[:, (n // 4) % 2, n % 4, :], hg[:, n % 2, :], ACT.Silu).then_inc(S["hs_ready"], 1)

            @block.vector
            def _(v):
                Xv = X[:].rearrange("p (b j) c -> p b j c", b=B)
                with v.Fori(0, B) as b:
                    v.wait_ge(S["turned"], b + 2)
                    v.wait_ge(S["out_ready"], b * 8 + 1)
                    nc.vector.tensor_copy(xT[:], psT[:]).then_inc(S["xT_ready"], 1)
                    v.wait_ge(S["logits"], b + 1)
                    lp = psR[:, 0:32].rearrange("p (j e) -> p j e", j=4)
                    nc.vector.tensor_reduce(mx[:], lp, AX.X, ALU.max, negate=True).then_inc(S["r_max"], 1)
                    v.wait_ge(S["r_max"], b + 1)
                    nc.vector.tensor_tensor(lg[:], lp, bcast(mx[:], 2, E1), ALU.add).then_inc(S["r_sub"], 1)
                    v.wait_ge(S["r_exp"], b + 1)
                    nc.vector.tensor_reduce(sm[:], lg[:], AX.X, ALU.add).then_inc(S["r_sum"], 1)
                    v.wait_ge(S["r_sum"], b + 1)
                    nc.vector.reciprocal(sm[:], sm[:]).then_inc(S["r_rec"], 1)
                    v.wait_ge(S["r_rec"], b + 1)
                    nc.vector.tensor_tensor(sc[:], lg[:], bcast(sm[:], 2, E1), ALU.mult).then_inc(S["r_score"], 1)
                    v.wait_ge(S["r_score"], b + 1)
                    for j in range(4):
                        other, own = bcast(sc[:, j, :], 1, E1), bcast(sc[:, j, :], 2, E1)
                        nc.vector.tensor_tensor(gt[:, j], other, own, ALU.is_gt)
                        m = nc.vector.tensor_tensor(eq[:, j], other, own, ALU.is_equal)
                    m.then_inc(S["r_cmp"], 1)
                    v.wait_ge(S["r_cmp"], b + 1)
                    nc.vector.tensor_tensor(eq[:], eq[:], bcast(before[:], 1, 4), ALU.mult).then_inc(S["r_eqm"], 1)
                    v.wait_ge(S["r_eqm"], b + 1)
                    nc.vector.tensor_tensor(gt[:], gt[:], eq[:], ALU.add).then_inc(S["r_or"], 1)
                    v.wait_ge(S["r_or"], b + 1)
                    nc.vector.tensor_reduce(rk[:], gt[:], AX.X, ALU.add).then_inc(S["r_rank"], 1)
                    v.wait_ge(S["r_rank"], b + 1)
                    nc.vector.scalar_tensor_tensor(out=sc[:], in0=rk[:], scalar=K1 - 0.5, in1=sc[:], op0=ALU.is_lt, op1=ALU.mult).then_inc(S["r_sel"], 1)
                    v.wait_ge(S["r_sel"], b + 1)
                    nc.vector.tensor_reduce(sm[:], sc[:], AX.X, ALU.add).then_inc(S["r_tot"], 1)
                    v.wait_ge(S["r_tot"], b + 1)
                    nc.vector.tensor_scalar(sm[:], sm[:], 1e-20, None, ALU.add).then_inc(S["r_inv"], 1)
                    v.wait_ge(S["r_inv"], 2 * b + 1)
                    nc.vector.reciprocal(sm[:], sm[:]).then_inc(S["r_inv"], 1)
                    v.wait_ge(S["r_inv"], 2 * b + 2)
                    nc.vector.tensor_tensor(comb[:], sc[:], bcast(sm[:], 2, E1), ALU.mult).then_inc(S["comb_ready"], 1)

                    def add(e):
                        v.wait_ge(S["out_ready"], b * 8 + e + 2)
                        if e == 0:
                            v.wait_ge(S["comb_ready"], b + 1)
                        if e:
                            v.wait_ge(S["added"], b * 8 + e + 1)
                        for j in range(4):
                            m = nc.vector.scalar_tensor_tensor(out=Xv[:, b, j], in0=psO[:, e % 2, j * P:(j + 1) * P], scalar=comb[:, j, e:e + 1], in1=Xv[:, b, j], op0=ALU.mult, op1=ALU.add)
                        m.then_inc(S["added"], 1)

                    for n in range(32):
                        v.wait_ge(S["us_ready"], b * 32 + n + 1)
                        v.wait_ge(S["g_ready"], b * 32 + n + 1)
                        if n < 2:
                            v.wait_ge(S["hs_ready"], b * 32 + 1)
                        else:
                            v.wait_ge(S["hs_ready"], b * 32 + n)
                        nc.vector.scalar_tensor_tensor(out=hg[:, n % 2, :], in0=psUG[0:FQ, n % 2, 1, :], scalar=gb[:, n // 4, n % 4:n % 4 + 1], in1=us[:, n % 2, :], op0=ALU.add, op1=ALU.mult).then_inc(S["hg_ready"], 1)
                        if n >= 8 and n % 4 == 3:
                            add(n // 4 - 2)
                    add(E1 - 2)
                    add(E1 - 1)
        clear(nc, S.values())


def top2_consts():
    a = np.arange(E1)
    return {"c_before": np.broadcast_to((a[None, :] < a[:, None]).astype(np.float32), (128, 8, 8)).copy()}

def top2_layout(w):
    return {"gate_wT": np.ascontiguousarray(w["gate_w"].T),
            "up_wT": np.ascontiguousarray(w["up_w"].transpose(0, 2, 1)), "gp_wT": np.ascontiguousarray(w["gp_w"].transpose(0, 2, 1)),
            "down_wT": np.ascontiguousarray(w["down_w"].transpose(0, 2, 1)),
            "up_b4": np.ascontiguousarray(w["up_b"].reshape(8, 4, FQ).transpose(2, 0, 1)), "gp_b4": np.ascontiguousarray(w["gp_b"].reshape(8, 4, FQ).transpose(2, 0, 1))}


NH, ND, NPAD, NW = 16, 8, 32, 8
KS = P + 2 * NW
QS = P + 2 * NPAD

def banded_attention(nc, X, XF, c, w):
    with ExitStack() as ctx:
        sb = lambda n, s, d=F32: ctx.enter_context(nc.sbuf_tensor("N" + n, s, d))
        ps = lambda n, s, d=F32: ctx.enter_context(nc.psum_tensor("N" + n, s, d))
        sem = lambda n: ctx.enter_context(nc.semaphore("N" + n))
        wqkv = sb("wqkv", [P, 384]); wp = sb("wp", [P, D]); bp = sb("bp", [1, D]); ones1 = sb("ones1", [1, P])
        mq = sb("mq", [P, 3, 2 * KS], BF16); mk = sb("mk", [P, 2 * QS], BF16); identb = sb("identb", [P, P], BF16)
        xb = sb("xb", [P, 4, D]); xT = sb("xT", [P, 512])
        kp = sb("kp", [P, 4, NH, PADH], BF16); qp = sb("qp", [P, 4, NH, PADH], BF16); nm = sb("nm", [P, 4, NH])
        kq = sb("kq", [P, 4, 2 * NH, ND])
        kT = sb("kT", [P, 8, 512 + 2 * NPAD], BF16); qT = sb("qT", [P, 8, 512 + 2 * NPAD], BF16)
        Vp = sb("Vp", [P, 4, NH, VPAD]); OT = sb("OT", [P, 4, 512]); PT = sb("PT", [P, 2, 4, 2, QS])
        rd = sb("rd", [P, 4, NH]); on = sb("on", [P, 4, NH, ND]); oT = sb("oT", [P, 512])
        psA = ps("psA", [P, 6, 512]); psB = ps("psB", [P, 1024])
        ident = c["ident"]
        S = {n: sem(n) for n in """loaded zeroed xb_ready x_turned xT_ready qkv_ready kq_copied v_ready part_h rest_m part_m part_l repeated k_turned kT_ready
          q_turned qT_ready s_ready mx_done nm_h nm_m nm_parts q2_turned qT2_ready st_ready exp_done
          av_done o_kept ot_turned rd_ready on_ready o_turned oT_ready y_ready y_added""".split()}
        start_at_one(nc, S, "exp_done y_added mx_done x_turned av_done qkv_ready")
        with nc.Block() as block:
            @block.sync
            def _(sp):
                L = S["loaded"]
                sp.dma_start(wqkv[:], w["Wqkv"]).then_inc(L, 16)
                sp.dma_start(wp[:], w["Wproj"]).then_inc(L, 16)
                sp.dma_start(bp[:], w["bproj"].unsqueeze(0)).then_inc(L, 16)
                sp.dma_start(mq[:], w["c_bandq"]).then_inc(L, 16)
                sp.dma_start(mk[:], w["c_bandk"]).then_inc(L, 16)
                sp.dma_start(identb[:], w["c_identb"]).then_inc(L, 16)
                sp.wait_ge(L, 96)
            @block.vector
            def _(v):
                nc.vector.memset(kp[:], 0.0)
                nc.vector.memset(qp[:], 0.0)
                nc.vector.memset(kT[:], 0.0)
                nc.vector.memset(qT[:], 0.0)
                nc.vector.memset(ones1[:], 1.0)
                nc.vector.memset(Vp[:], 0.0).then_inc(S["zeroed"], 1)
                v.wait_ge(S["zeroed"], 1)
                nc.vector.memset(kp[:, :, :, PARTS:PARTS + 3], 1.0)
                nc.vector.memset(Vp[:, :, :, ND:ND + 1], 1.0)

        def pair(n):
            return n % 2 + 4 * (n // 2), n % 2 + 4 * (n // 2) + 2

        with nc.Block() as block:
            @block.tensor
            def _(pe):
                with pe.Fori(0, B) as b:
                    pe.wait_ge(S["xb_ready"], b + 1)
                    pe.wait_ge(S["exp_done"], b * 32 + 1)
                    for j in range(4):
                        m = nc.tensor.transpose(psA[:, 0, j * P:(j + 1) * P], xb[:, j, :], ident[:])
                    m.then_inc(S["x_turned"], 1)
                    pe.wait_ge(S["xT_ready"], b + 1)
                    for j in range(4):
                        m = nc.tensor.matmul(psA[:, j + 1, 0:384], xT[:, j * P:(j + 1) * P], wqkv[:], start=True, stop=True)
                    m.then_inc(S["qkv_ready"], 1)
                    pe.wait_ge(S["v_ready"], b + 1)
                    pe.wait_ge(S["y_added"], b + 1)
                    pe.wait_ge(S["part_l"], 2 * b + 2)
                    pe.wait_ge(S["repeated"], b + 1)

                    def turn(src, half, turned):
                        for g in range(4 * half, 4 * half + 4):
                            tgt = psA[:, g, :] if g < 6 else psB[:, (g - 6) * 512:(g - 5) * 512]
                            for j in range(4):
                                m = nc.tensor.matmul(tgt[:, j * P:(j + 1) * P], src[:, j, 2 * g:2 * g + 2, :], identb[:], start=True, stop=True)
                        m.then_inc(S[turned], 1)

                    turn(kp, 0, "k_turned")
                    turn(kp, 1, "k_turned")
                    pe.wait_ge(S["kT_ready"], 2 * b + 2)
                    turn(qp, 0, "q_turned")
                    turn(qp, 1, "q_turned")
                    pe.wait_ge(S["qT_ready"], 2 * b + 2)
                    for n in range(32):
                        j = n // 8
                        if n >= 6:
                            pe.wait_ge(S["mx_done"], b * 32 + n - 4)
                        bank = psA[:, n % 6, :]
                        nc.tensor.matmul(bank[:, 0:2 * KS], identb[:], mq[:, (0, 1, 1, 2)[j], :], start=True, stop=True)
                        for a, h in enumerate(pair(n % 8)):
                            r = slice(64 * (h % 2), 64 * (h % 2) + PARTS)
                            k0 = NPAD + j * P - NW
                            m = nc.tensor.matmul(bank[:, a * KS:(a + 1) * KS], qT[r, h // 2, NPAD + j * P:NPAD + (j + 1) * P], kT[r, h // 2, k0:k0 + KS],
                                                 start=False, stop=True, skip_group_check=True)
                        m.then_inc(S["s_ready"], 1)
                    pe.wait_ge(S["mx_done"], (b + 1) * 32 + 1)
                    pe.wait_ge(S["nm_parts"], b + 1)
                    turn(qp, 0, "q2_turned")
                    turn(qp, 1, "q2_turned")
                    pe.wait_ge(S["qT2_ready"], 2 * b + 2)

                    def st(n):
                        hp, kj = n // 4, n % 4
                        if n >= 6:
                            pe.wait_ge(S["exp_done"], b * 32 + n - 4)
                        bank = psA[:, n % 6, 0:2 * QS]
                        nc.tensor.matmul(bank, identb[:], mk[:], start=True, stop=True)
                        for a, h in enumerate(pair(hp)):
                            r = slice(64 * (h % 2), 64 * (h % 2) + PARTS + 3)
                            m = nc.tensor.matmul(bank[:, a * QS:(a + 1) * QS], kT[r, h // 2, NPAD + kj * P:NPAD + (kj + 1) * P], qT[r, h // 2, kj * P:kj * P + QS],
                                                 start=False, stop=True, skip_group_check=True)
                        m.then_inc(S["st_ready"], 1)

                    def av(hp):
                        g = hp // 2
                        pe.wait_ge(S["exp_done"], b * 32 + 4 * (hp + 1) + 1)
                        if hp % 2 == 0 and g >= 2:
                            pe.wait_ge(S["o_kept"], b * 4 + g - 1)
                        for a, h in enumerate(pair(hp)):
                            r = 32 * (h % 4)
                            for kj in range(4):
                                q0, q1 = max(kj * P - NPAD, 0), min(kj * P + P + NPAD, 512)
                                s0 = q0 - (kj * P - NPAD)
                                m = nc.tensor.matmul(psB[r:r + 32, (g % 2) * 512 + q0:(g % 2) * 512 + q1], Vp[:, kj, h, :], PT[:, hp % 2, kj, a, s0:s0 + q1 - q0],
                                                     start=(kj == 0), stop=True, skip_group_check=True, tile_position=(0, r))
                        m.then_inc(S["av_done"], 1)

                    for n in range(32):
                        st(n)
                        if n >= 7 and n % 4 == 3:
                            av(n // 4 - 1)
                    av(7)
                    pe.wait_ge(S["o_kept"], b * 4 + 4)
                    for j in range(4):
                        for g in range(4):
                            m = nc.tensor.transpose(psA[:, j, g * P:(g + 1) * P], OT[:, g, j * P:(j + 1) * P], ident[:])
                    m.then_inc(S["ot_turned"], 1)
                    pe.wait_ge(S["on_ready"], b + 1)
                    for j in range(4):
                        m = nc.tensor.transpose(psB[:, j * P:(j + 1) * P], on[:, j], ident[:])
                    m.then_inc(S["o_turned"], 1)
                    pe.wait_ge(S["oT_ready"], b + 1)
                    for j in range(4):
                        o = psB[:, 512 + j * P:512 + (j + 1) * P]
                        nc.tensor.matmul(o, ones1[:], bp[:], start=True, stop=False)
                        m = nc.tensor.matmul(o, oT[:, j * P:(j + 1) * P], wp[:], start=False, stop=True)
                    m.then_inc(S["y_ready"], 1)

            @block.scalar
            def _(act):
                with act.Fori(0, B) as b:
                    act.wait_ge(S["x_turned"], b + 1)
                    nc.scalar.activation(xb[:], XF[:, b, 1:5, :], ACT.Copy).then_inc(S["xb_ready"], 1)
                    act.wait_ge(S["kq_copied"], b + 1)
                    nc.scalar.activation(Vp[:, :, :, 0:ND], psA[:, 1:5, 256:384].rearrange("p j (h d) -> p j h d", h=NH), ACT.Copy).then_inc(S["v_ready"], 1)
                    for part in ("h", "m"):
                        act.wait_ge(S["part_" + part], 2 * b + 2)
                        for t, where in ((kp, K_PARTS), (qp, Q_PARTS)):
                            k0 = where[part][0] * ND
                            for k in where[part][1:]:
                                m = nc.scalar.activation(t[:, :, :, k * ND:k * ND + ND], t[:, :, :, k0:k0 + ND], ACT.Copy)
                    m.then_inc(S["repeated"], 1)
                    for dst, turned, ready in ((kT, "k_turned", "kT_ready"), (qT, "q_turned", "qT_ready"), (qT, "q2_turned", "qT2_ready")):
                        act.wait_ge(S[turned], 2 * b + 1)
                        nc.scalar.activation(dst[:, 0:4, NPAD:NPAD + 512], psA[:, 0:4, :], ACT.Copy).then_inc(S[ready], 1)
                    for n in range(32):
                        act.wait_ge(S["st_ready"], b * 32 + n + 1)
                        if n // 4 >= 2:
                            act.wait_ge(S["av_done"], b * 8 + n // 4)
                        nc.scalar.activation(PT[:, (n // 4) % 2, n % 4], psA[:, n % 6, 0:2 * QS].rearrange("p (h q) -> p h q", h=2), ACT.Exp).then_inc(S["exp_done"], 1)
                    act.wait_ge(S["o_turned"], b + 1)
                    nc.scalar.activation(oT[:], psB[:, 0:512], ACT.Copy).then_inc(S["oT_ready"], 1)

            @block.vector
            def _(v):
                with v.Fori(0, B) as b:
                    v.wait_ge(S["x_turned"], b + 2)
                    v.wait_ge(S["qkv_ready"], b + 1)
                    nc.vector.tensor_copy(xT[:], psA[:, 0, :]).then_inc(S["xT_ready"], 1)
                    v.wait_ge(S["qkv_ready"], b + 2)
                    nc.vector.tensor_scalar(kq[:, :, NH:2 * NH, :], psA[:, 1:5, 0:128].rearrange("p j (h d) -> p j h d", h=NH), float(ND) ** -0.5, None, ALU.mult)
                    nc.vector.tensor_copy(kq[:, :, 0:NH, :], psA[:, 1:5, 128:256].rearrange("p j (h d) -> p j h d", h=NH)).then_inc(S["kq_copied"], 1)
                    v.wait_ge(S["kq_copied"], b + 1)
                    sides = [(kq[:, :, 0:NH, :], kp, K_PARTS), (kq[:, :, NH:2 * NH, :], qp, Q_PARTS)]
                    block_of = lambda t, where, part: t[:, :, :, where[part][0] * ND:where[part][0] * ND + ND]
                    for k, (x, t, where) in enumerate(sides):
                        nc.vector.tensor_copy(block_of(t, where, "h"), x).then_inc(S["part_h"], 1)
                    for k, (x, t, where) in enumerate(sides):
                        v.wait_ge(S["part_h"], 2 * b + k + 1)
                        nc.vector.tensor_tensor(x, x, block_of(t, where, "h"), ALU.subtract).then_inc(S["rest_m"], 1)
                    for k, (x, t, where) in enumerate(sides):
                        v.wait_ge(S["rest_m"], 2 * b + k + 1)
                        nc.vector.tensor_copy(block_of(t, where, "m"), x).then_inc(S["part_m"], 1)
                    for k, (x, t, where) in enumerate(sides):
                        v.wait_ge(S["part_m"], 2 * b + k + 1)
                        nc.vector.tensor_tensor(block_of(t, where, "l"), x, block_of(t, where, "m"), ALU.subtract).then_inc(S["part_l"], 1)

                    def last_groups(dst, turned, ready):
                        v.wait_ge(S[turned], 2 * b + 2)
                        nc.vector.tensor_copy(dst[:, 4:6, NPAD:NPAD + 512], psA[:, 4:6, :])
                        nc.vector.tensor_copy(dst[:, 6:8, NPAD:NPAD + 512], psB[:].rearrange("p (g t) -> p g t", g=2)).then_inc(S[ready], 1)

                    last_groups(kT, "k_turned", "kT_ready")
                    last_groups(qT, "q_turned", "qT_ready")
                    for n in range(32):
                        j, h0 = n // 8, pair(n % 8)[0]
                        v.wait_ge(S["s_ready"], b * 32 + n + 1)
                        nc.vector.tensor_reduce(nm[:, j, h0:h0 + 3:2], psA[:, n % 6, 0:2 * KS].rearrange("p (h k) -> p h k", h=2), AX.X, ALU.max, negate=True).then_inc(S["mx_done"], 1)
                    v.wait_ge(S["mx_done"], (b + 1) * 32 + 1)
                    nc.vector.tensor_copy(qp[:, :, :, PARTS], nm[:]).then_inc(S["nm_h"], 1)
                    v.wait_ge(S["nm_h"], 2 * b + 1)
                    nc.vector.tensor_tensor(nm[:], nm[:], qp[:, :, :, PARTS], ALU.subtract).then_inc(S["nm_h"], 1)
                    v.wait_ge(S["nm_h"], 2 * b + 2)
                    nc.vector.tensor_copy(qp[:, :, :, PARTS + 1], nm[:]).then_inc(S["nm_m"], 1)
                    v.wait_ge(S["nm_m"], b + 1)
                    nc.vector.tensor_tensor(qp[:, :, :, PARTS + 2], nm[:], qp[:, :, :, PARTS + 1], ALU.subtract).then_inc(S["nm_parts"], 1)
                    last_groups(qT, "q2_turned", "qT2_ready")
                    for g in range(4):
                        v.wait_ge(S["av_done"], b * 8 + 2 * (g + 1) + 1)
                        nc.vector.tensor_copy(OT[:, g], psB[:, (g % 2) * 512:(g % 2) * 512 + 512]).then_inc(S["o_kept"], 1)
                    v.wait_ge(S["ot_turned"], b + 1)
                    ov = psA[:, 0:4, :].rearrange("p j (h d) -> p j h d", d=VPAD)
                    nc.vector.reciprocal(rd[:], ov[:, :, :, ND]).then_inc(S["rd_ready"], 1)
                    v.wait_ge(S["rd_ready"], b + 1)
                    nc.vector.tensor_tensor(on[:], ov[:, :, :, 0:ND], bcast(rd[:], 3, ND), ALU.mult).then_inc(S["on_ready"], 1)
                    v.wait_ge(S["y_ready"], b + 1)
                    xv = X[:].rearrange("p (b j) c -> p b j c", b=B)
                    nc.vector.tensor_tensor(xv[:, b], psB[:, 512:1024].rearrange("p (j c) -> p j c", j=4), xv[:, b], ALU.add).then_inc(S["y_added"], 1)
        clear(nc, S.values())


def banded_consts():
    q = np.arange(P)[:, None]
    kk = np.arange(KS)[None] - NW
    near = np.where(np.abs(kk - q) <= NW, 0, -1e30)
    a = np.zeros((P, 3, 2, KS), np.float32)
    for t in range(3):
        m = near.copy()
        if t == 0:
            m[:, :NW] = -1e30
        if t == 2:
            m[:, KS - NW:] = -1e30
        a[:, t] = m[:, None]
    qq = np.arange(QS)[None] - NPAD
    k = np.where(np.abs(qq - q) <= NW, 0, -1e30)
    return {"c_bandq": a.reshape(P, 3, 2 * KS).astype("bfloat16"), "c_bandk": np.tile(k, 2).astype("bfloat16")}


E2, K2, HP2, CAP = 32, 8, 16, 256
LIMIT, ROUTED = 7.0, 2.5

def capped_experts(nc, X, XF, c, w):
    with ExitStack() as ctx:
        sb = lambda n, s, d=F32: ctx.enter_context(nc.sbuf_tensor("C" + n, s, d))
        ps = lambda n, s, d=F32: ctx.enter_context(nc.psum_tensor("C" + n, s, d))
        sem = lambda n: ctx.enter_context(nc.semaphore("C" + n))
        NP = HP2 + 2
        gw = sb("gw", [P, NP, P]); uw = sb("uw", [P, NP, P]); dw = sb("dw", [P, NP, D])
        rw = sb("rw", [P, E2]); bias = sb("bias", [P, E2]); spread = sb("spread", [E2, HP2, P])
        tri = sb("tri", [P, P], BF16); ones = sb("ones", [P, P], BF16); cum = sb("cum", [P, E2], BF16)
        xb = sb("xb", [P, 4, D]); xT = sb("xT", [P, 512])
        sc = sb("sc", [P, 4, E2]); sel = sb("sel", [P, 4, E2]); top = sb("top", [P, 4, 8]); rep = sb("rep", [P, 4, E2])
        mask = sb("mask", [P, 4, E2]); maskb = sb("maskb", [P, 4, E2], BF16); csum = sb("csum", [P, E2]); kept = sb("kept", [P, 4, E2]); sw = sb("sw", [P, 4, E2])
        tot = sb("tot", [P, 4]); comb = sb("comb", [P, 4, E2]); wT = sb("wT", [E2, 512])
        gs = sb("gs", [P, 2, 512]); us = sb("us", [P, 2, 512]); gl = sb("gl", [P, 2, 512]); hs = sb("hs", [P, 2, 512])
        psG = ps("psG", [P, 2, 512]); psU = ps("psU", [P, 2, 512]); psW = ps("psW", [P, 2, 512]); psT = ps("psT", [P, 512]); psO = ps("psO", [P, 512])
        ident = c["ident"]
        S = {n: sem(n) for n in """loaded ones xb_ready turned xT_ready logits score r_sel r_top r_rep r_mask r_maskb pos r_kept r_sw r_tot r_eps r_inv
          r_scale comb_ready comb_turned wT_ready r_csum r_cum g_ready u_ready w_ready g_min u_clip silu mixed h_ready out_ready added""".split()}
        start_at_one(nc, S, "added h_ready turned mixed out_ready silu")
        with nc.Block() as block:
            @block.sync
            def _(sp):
                L = S["loaded"]
                for a, n in ((gw, "gate"), (uw, "up")):
                    sp.dma_start(a[:, 0:HP2, :], w[n + "_pairs"]).then_inc(L, 16)
                    sp.dma_start(a[:, HP2:NP, :], w["shared_" + n + "T"].rearrange("d (k p) -> d k p", k=2)).then_inc(L, 16)
                sp.dma_start(dw[:, 0:HP2, :], w["down_pairs"].rearrange("k p d -> p k d")).then_inc(L, 16)
                sp.dma_start(dw[:, HP2:NP, :], w["shared_downT"].rearrange("(k p) d -> p k d", k=2)).then_inc(L, 16)
                sp.dma_start(rw[:], w["router_weightT"]).then_inc(L, 16)
                sp.dma_start(bias[:], rows(w["e_score_correction_bias"])).then_inc(L, 16)
                sp.dma_start(spread[:], w["c_spread"]).then_inc(L, 16)
                sp.dma_start(tri[:], w["c_earlier"]).then_inc(L, 16)
                sp.wait_ge(L, 160)
            @block.vector
            def _(v):
                nc.vector.memset(ones[:], 1.0)
                nc.vector.memset(cum[:], 0.0)

        with nc.Block() as block:
            @block.tensor
            def _(pe):
                with pe.Fori(0, B) as b:
                    pe.wait_ge(S["xb_ready"], b + 1)
                    pe.wait_ge(S["added"], b + 1)
                    for j in range(4):
                        m = nc.tensor.transpose(psT[:, j * P:(j + 1) * P], xb[:, j, :], ident[:])
                    m.then_inc(S["turned"], 1)
                    pe.wait_ge(S["xT_ready"], b + 1)
                    for j in range(4):
                        m = nc.tensor.matmul(psT[:, E2 * j:E2 * j + E2], xT[:, j * P:(j + 1) * P], rw[:], start=True, stop=True)
                    m.then_inc(S["logits"], 1)
                    pe.wait_ge(S["r_maskb"], b + 1)
                    pe.wait_ge(S["score"], b + 1)
                    for j in range(4):
                        o = psO[:, E2 * j:E2 * j + E2]
                        nc.tensor.matmul(o, tri[:], maskb[:, j, :], start=True, stop=False)
                        for k in range(j):
                            nc.tensor.matmul(o, ones[:], maskb[:, k, :], start=False, stop=False)
                        m = nc.tensor.matmul(o, ones[:], cum[:], start=False, stop=True)
                    m.then_inc(S["pos"], 1)
                    pe.wait_ge(S["comb_ready"], b + 1)
                    for j in range(4):
                        m = nc.tensor.transpose(psT[0:E2, j * P:(j + 1) * P], comb[:, j, :], ident[:])
                    m.then_inc(S["comb_turned"], 1)
                    pe.wait_ge(S["wT_ready"], b + 1)

                    def inner(n):
                        q = n % 2
                        if n >= 2:
                            pe.wait_ge(S["h_ready"], b * NP + n)
                        else:
                            pe.wait_ge(S["h_ready"], b * NP + 1)
                        nc.tensor.matmul(psG[:, q, :], gw[:, n, :], xT[:], start=True, stop=True).then_inc(S["g_ready"], 1)
                        nc.tensor.matmul(psU[:, q, :], uw[:, n, :], xT[:], start=True, stop=True).then_inc(S["u_ready"], 1)
                        if n < HP2:
                            nc.tensor.matmul(psW[:, q, :], spread[:, n, :], wT[:], start=True, stop=True).then_inc(S["w_ready"], 1)

                    def down(n):
                        pe.wait_ge(S["h_ready"], b * NP + n + 2)
                        for j in range(4):
                            m = nc.tensor.matmul(psO[:, j * P:(j + 1) * P], hs[:, n % 2, j * P:(j + 1) * P], dw[:, n, :],
                                                 start=(n == 0 and j == 0), stop=True, skip_group_check=True)
                        m.then_inc(S["out_ready"], 1)

                    inner(0)
                    for n in range(1, NP):
                        inner(n)
                        down(n - 1)
                    down(NP - 1)

            @block.scalar
            def _(act):
                with act.Fori(0, B) as b:
                    act.wait_ge(S["turned"], b + 1)
                    nc.scalar.activation(xb[:], XF[:, b, 1:5, :], ACT.Copy).then_inc(S["xb_ready"], 1)
                    act.wait_ge(S["logits"], b + 1)
                    nc.scalar.activation(sc[:], psT[:, 0:4 * E2].rearrange("p (j e) -> p j e", j=4), ACT.Sigmoid).then_inc(S["score"], 1)
                    act.wait_ge(S["comb_turned"], b + 1)
                    nc.scalar.activation(wT[:], psT[0:E2, :], ACT.Copy).then_inc(S["wT_ready"], 1)
                    for n in range(NP):
                        q = n % 2
                        if n < HP2:
                            act.wait_ge(S["g_min"], b * HP2 + n + 1)
                            if n >= 2:
                                act.wait_ge(S["mixed"], b * HP2 + n)
                            nc.scalar.activation(gl[:, q, :], gs[:, q, :], ACT.Silu).then_inc(S["silu"], 1)
                        else:
                            act.wait_ge(S["g_ready"], b * NP + n + 1)
                            act.wait_ge(S["mixed"], 1 + (b * HP2 + n - 1 if n == HP2 else b * HP2 + HP2))
                            nc.scalar.activation(gl[:, q, :], psG[:, q, :], ACT.Silu).then_inc(S["silu"], 1)

            @block.gpsimd
            def _(g):
                with g.Fori(0, B) as b:
                    for n in range(HP2):
                        g.wait_ge(S["silu"], b * NP + n + 2)
                        g.wait_ge(S["u_clip"], b * HP2 + n + 1)
                        nc.gpsimd.tensor_tensor(us[:, n % 2, :], us[:, n % 2, :], gl[:, n % 2, :], ALU.mult).then_inc(S["mixed"], 1)

            @block.vector
            def _(v):
                Xv = X[:].rearrange("p (b j) c -> p b j c", b=B)
                with v.Fori(0, B) as b:
                    v.wait_ge(S["turned"], b + 2)
                    nc.vector.tensor_copy(xT[:], psT[:]).then_inc(S["xT_ready"], 1)
                    v.wait_ge(S["score"], b + 1)
                    nc.vector.tensor_tensor(sel[:], sc[:], bcast(bias[:], 1, 4), ALU.add).then_inc(S["r_sel"], 1)
                    v.wait_ge(S["r_sel"], b + 1)
                    v.sem_inc(S["ones"], 1)
                    for j in range(4):
                        m = nc.vector.max(top[:, j, :], sel[:, j, :])
                    m.then_inc(S["r_top"], 1)
                    v.wait_ge(S["r_top"], b + 1)
                    v.sem_inc(S["ones"], 1)
                    for j in range(4):
                        m = nc.vector.match_replace(rep[:, j, :], top[:, j, :], sel[:, j, :], -3e38)
                    m.then_inc(S["r_rep"], 1)
                    v.wait_ge(S["r_rep"], b + 1)
                    nc.vector.tensor_tensor(mask[:], sel[:], rep[:], ALU.not_equal).then_inc(S["r_mask"], 1)
                    v.wait_ge(S["r_mask"], b + 1)
                    nc.vector.tensor_copy(maskb[:], mask[:]).then_inc(S["r_maskb"], 1)
                    nc.vector.tensor_tensor(sw[:], sc[:], mask[:], ALU.mult).then_inc(S["r_sw"], 1)
                    v.wait_ge(S["r_sw"], b + 1)
                    nc.vector.tensor_reduce(tot[:], sw[:], AX.X, ALU.add).then_inc(S["r_tot"], 1)
                    v.wait_ge(S["r_tot"], b + 1)
                    nc.vector.tensor_scalar(tot[:], tot[:], 1e-20, None, ALU.add).then_inc(S["r_eps"], 1)
                    v.wait_ge(S["r_eps"], b + 1)
                    nc.vector.reciprocal(tot[:], tot[:]).then_inc(S["r_inv"], 1)
                    v.wait_ge(S["r_inv"], b + 1)
                    nc.vector.tensor_tensor(sw[:], sw[:], bcast(tot[:], 2, E2), ALU.mult).then_inc(S["r_scale"], 1)
                    v.wait_ge(S["pos"], b + 1)
                    v.wait_ge(S["r_scale"], b + 1)
                    nc.vector.scalar_tensor_tensor(out=kept[:], in0=psO[:, 0:4 * E2].rearrange("p (j e) -> p j e", j=4), scalar=CAP - 0.5, in1=sw[:], op0=ALU.is_lt, op1=ALU.mult).then_inc(S["r_kept"], 1)
                    v.wait_ge(S["r_kept"], b + 1)
                    nc.vector.tensor_scalar(comb[:], kept[:], ROUTED, None, ALU.mult).then_inc(S["comb_ready"], 1)
                    nc.vector.tensor_reduce(csum[:], mask[:].rearrange("p j e -> p e j"), AX.X, ALU.add).then_inc(S["r_csum"], 1)
                    v.wait_ge(S["r_csum"], b + 1)
                    nc.vector.tensor_tensor(cum[:], cum[:], csum[:], ALU.add).then_inc(S["r_cum"], 1)
                    def mix(n):
                        q = n % 2
                        if n < HP2:
                            v.wait_ge(S["mixed"], b * HP2 + n + 2)
                            v.wait_ge(S["w_ready"], b * HP2 + n + 1)
                            if n >= 2:
                                v.wait_ge(S["out_ready"], b * NP + n)
                            nc.vector.tensor_tensor(hs[:, q, :], psW[:, q, :], us[:, q, :], ALU.mult).then_inc(S["h_ready"], 1)
                        else:
                            v.wait_ge(S["silu"], b * NP + n + 2)
                            v.wait_ge(S["u_ready"], b * NP + n + 1)
                            v.wait_ge(S["out_ready"], b * NP + n)
                            nc.vector.tensor_tensor(hs[:, q, :], psU[:, q, :], gl[:, q, :], ALU.mult).then_inc(S["h_ready"], 1)

                    for n in range(NP):
                        q = n % 2
                        if n < HP2:
                            v.wait_ge(S["g_ready"], b * NP + n + 1)
                            if n >= 2:
                                v.wait_ge(S["silu"], b * NP + n)
                            nc.vector.tensor_scalar(gs[:, q, :], psG[:, q, :], LIMIT, None, ALU.min).then_inc(S["g_min"], 1)
                            v.wait_ge(S["u_ready"], b * NP + n + 1)
                            v.wait_ge(S["h_ready"], 1 + (b * NP + (n - 1 if n >= 2 else 0)))
                            nc.vector.tensor_scalar(us[:, q, :], psU[:, q, :], LIMIT, -LIMIT, ALU.min, ALU.max).then_inc(S["u_clip"], 1)
                        if n >= 1:
                            mix(n - 1)
                    mix(NP - 1)
                    v.wait_ge(S["out_ready"], (b + 1) * NP + 1)
                    nc.vector.tensor_tensor(Xv[:, b], psO[:].rearrange("p (j c) -> p j c", j=4), Xv[:, b], ALU.add).then_inc(S["added"], 1)
        clear(nc, S.values())


def capped_consts():
    a = np.arange(P)
    s = np.zeros((E2, HP2, P), np.float32)
    for p in range(HP2):
        s[2 * p, p, 0:64] = 1
        s[2 * p + 1, p, 64:] = 1
    return {"c_spread": s, "c_earlier": (a[:, None] < a[None, :]).astype("bfloat16")}

def capped_layout(w):
    gu, t = w["gate_up_proj"], np.ascontiguousarray
    pairs = lambda x: t(x.reshape(HP2, 2, 64, 128).transpose(3, 0, 1, 2).reshape(128, HP2, 128))
    return {"gate_pairs": pairs(gu[:, :64]), "up_pairs": pairs(gu[:, 64:]),
            "down_pairs": t(w["down_proj"].transpose(0, 2, 1).reshape(HP2, 128, 128)),
            "shared_gateT": t(w["shared_gate"].T), "shared_upT": t(w["shared_up"].T), "shared_downT": t(w["shared_down"].T),
            "router_weightT": t(w["router_weight"].T)}


QI, QB = 352, 16
ROWS4 = 88
QSTEPS = 12
DOWN = ((0, 128), (128, 128), (256, 96))

class Steps:
    def __init__(self, eng, sem, base):
        self.eng, self.sem, self.base, self.n = eng, sem, base, 0

    def __call__(self, ins):
        self.n += 1
        ins.then_inc(self.sem, 1)
        self.eng.wait_ge(self.sem, self.base + self.n)

def fp4(nc, v, step, src, out, t, signs_of, signs_ready):
    p, nb = src.shape[0], src.shape[1]
    am, xn, ab, hi, lo = (t[k][0:p, 0:nb] for k in ("am", "xn", "ab", "hi", "lo"))
    rc = t["rc"][0:p, 0:nb]
    step(nc.vector.tensor_reduce(am, src, AX.X, ALU.max, apply_absolute_value=True))
    step(nc.vector.tensor_scalar(am, am, 1.0 / 6.0, 1e-12, ALU.mult, ALU.max))
    step(nc.vector.reciprocal(rc, am))
    step(nc.vector.tensor_tensor(xn, src, bcast(rc, 2, QB), ALU.mult))
    signs_of()
    step(nc.vector.scalar_tensor_tensor(out=ab, in0=xn, scalar=-1.0, in1=xn, op0=ALU.mult, op1=ALU.max))
    nc.vector.tensor_scalar(hi, ab, 5.0, 2.0, ALU.is_gt, ALU.mult)
    step(nc.vector.tensor_scalar(lo, ab, 0.25, None, ALU.is_gt))
    nc.vector.scalar_tensor_tensor(out=hi, in0=ab, scalar=3.5, in1=hi, op0=ALU.is_gt, op1=ALU.add)
    step(nc.vector.scalar_tensor_tensor(out=lo, in0=ab, scalar=0.75, in1=lo, op0=ALU.is_gt, op1=ALU.add))
    nc.vector.scalar_tensor_tensor(out=hi, in0=ab, scalar=2.5, in1=hi, op0=ALU.is_gt, op1=ALU.add)
    step(nc.vector.scalar_tensor_tensor(out=lo, in0=ab, scalar=1.25, in1=lo, op0=ALU.is_gt, op1=ALU.add))
    step(nc.vector.scalar_tensor_tensor(out=lo, in0=ab, scalar=1.75, in1=lo, op0=ALU.is_gt, op1=ALU.add))
    step(nc.vector.scalar_tensor_tensor(out=lo, in0=lo, scalar=0.5, in1=hi, op0=ALU.mult, op1=ALU.add))
    signs_ready()
    step(nc.vector.tensor_tensor(lo, lo, t["sg"][0:p, 0:nb], ALU.mult))
    step(nc.vector.tensor_tensor(out, lo, bcast(am, 2, QB), ALU.mult))

def fp4_ffn(nc, X, XF, c, w):
    with ExitStack() as ctx:
        sb = lambda n, s, d=F32: ctx.enter_context(nc.sbuf_tensor("F" + n, s, d))
        ps = lambda n, s, d=F32: ctx.enter_context(nc.psum_tensor("F" + n, s, d))
        sem = lambda n: ctx.enter_context(nc.semaphore("F" + n))
        raw = sb("raw", [P, 3, 32, QB])
        wq = sb("wq", [P, 3, 32, QB])
        gT = sb("gT", [P, QI]); uT = sb("uT", [P, QI]); dT = sb("dT", [P, 3, D])
        t = {k: sb(k, [P, 32, QB]) for k in ("xn", "ab", "hi", "lo", "sg")}
        t.update({k: sb(k, [P, 32]) for k in ("am", "rc")})
        xq = sb("xq", [P, 32, QB]); xqT = sb("xqT", [P, 512])
        sl = sb("sl", [P, QI]); h = sb("h", [P, 22, QB]); hq = sb("hq", [P, 22, QB]); hT = sb("hT", [P, 3, P])
        psT = ps("psT", [P, 512]); psG = ps("psG", [P, 2, 512]); psU = ps("psU", [P, 2, 512]); psH = ps("psH", [P, 512]); psO = ps("psO", [P, 512]); psW = ps("psW", [P, 512])
        ident = c["ident"]
        S = {n: sem(n) for n in """loaded wsteps wxn wsign wquant wturned wcopied steps xn sign xq_ready x_turned xT_ready g_ready u_ready
          silu h_ready hq_ready h_turned hT_ready out added""".split()}
        start_at_one(nc, S, "wcopied h_ready added out x_turned u_ready h_turned")
        NBW = (32, 32, 22)

        def wsrc(k): return raw[0:ROWS4, k] if k < 2 else raw[:, 2, 0:22]
        def wdst(k): return wq[0:ROWS4, k] if k < 2 else wq[:, 2, 0:22]
        with nc.Block() as block:
            @block.sync
            def _(sp):
                L = S["loaded"]
                for k, n in enumerate(("w_gate", "w_up")):
                    sp.dma_start(raw[0:ROWS4, k].rearrange("p (a b) c -> p a (b c)", a=4), w[n].rearrange("(a p) c -> p a c", p=ROWS4)).then_inc(L, 16)
                sp.dma_start(raw[:, 2, 0:22].rearrange("p b c -> p (b c)"), w["w_down"]).then_inc(L, 16)
                sp.wait_ge(L, 48)
            @block.vector
            def _(v):
                v.wait_ge(S["loaded"], 48)
                step = Steps(v, S["wsteps"], 0)
                for k in range(3):
                    fp4(nc, v, step, wsrc(k), wdst(k), t, lambda: v.sem_inc(S["wxn"], 1), lambda: v.wait_ge(S["wsign"], k + 1))
                v.sem_inc(S["wquant"], 1)
                for k in range(3):
                    v.wait_ge(S["wturned"], k + 1)
                    if k < 2:
                        nc.vector.tensor_copy((gT, uT)[k][:], psT[:, 0:QI]).then_inc(S["wcopied"], 1)
                    else:
                        nc.vector.tensor_copy(dT[:, 0:2, :], psT[:, 0:256].rearrange("p (a b) -> p a b", a=2))
                        nc.vector.tensor_copy(dT[0:96, 2, :], psT[0:96, 256:384]).then_inc(S["wcopied"], 1)
            @block.scalar
            def _(act):
                for k in range(3):
                    act.wait_ge(S["wxn"], k + 1)
                    nb = NBW[k]
                    p = ROWS4 if k < 2 else P
                    nc.scalar.activation(t["sg"][0:p, 0:nb], t["xn"][0:p, 0:nb], ACT.Sign).then_inc(S["wsign"], 1)
            @block.tensor
            def _(pe):
                pe.wait_ge(S["wquant"], 1)
                for k in range(3):
                    if k:
                        pe.wait_ge(S["wcopied"], k + 1)
                    if k < 2:
                        for a in range(4):
                            m = nc.tensor.transpose(psT[:, a * ROWS4:(a + 1) * ROWS4], wq[0:ROWS4, k, 8 * a:8 * a + 8, :], ident[0:ROWS4, 0:ROWS4])
                    else:
                        flat = wq[:, 2].rearrange("p b c -> p (b c)")
                        for a, (f0, nf) in enumerate(DOWN):
                            m = nc.tensor.transpose(psT[0:nf, a * P:(a + 1) * P], flat[:, f0:f0 + nf], ident[:])
                    m.then_inc(S["wturned"], 1)

        with nc.Block() as block:
            @block.tensor
            def _(pe):
                with pe.Fori(0, B) as b:
                    pe.wait_ge(S["xq_ready"], b + 1)
                    for j in range(4):
                        m = nc.tensor.transpose(psT[:, j * P:(j + 1) * P], xq[:, 8 * j:8 * j + 8, :], ident[:])
                    m.then_inc(S["x_turned"], 1)
                    pe.wait_ge(S["xT_ready"], b + 1)

                    def inner(j):
                        pe.wait_ge(S["h_ready"], 1 + (b * 4 + (j - 1 if j >= 2 else 0)))
                        nc.tensor.matmul(psG[:, j % 2, 0:QI], xqT[:, j * P:(j + 1) * P], gT[:], start=True, stop=True).then_inc(S["g_ready"], 1)
                        nc.tensor.matmul(psU[:, j % 2, 0:QI], xqT[:, j * P:(j + 1) * P], uT[:], start=True, stop=True).then_inc(S["u_ready"], 1)

                    inner(0)
                    for j in range(4):
                        if j < 3:
                            inner(j + 1)
                        pe.wait_ge(S["hq_ready"], b * 4 + j + 1)
                        flat = hq[:].rearrange("p b c -> p (b c)")
                        for a, (f0, nf) in enumerate(DOWN):
                            m = nc.tensor.transpose(psH[0:nf, a * P:(a + 1) * P], flat[:, f0:f0 + nf], ident[:])
                        m.then_inc(S["h_turned"], 1)
                        pe.wait_ge(S["hT_ready"], b * 4 + j + 1)
                        if j == 0:
                            pe.wait_ge(S["added"], b + 1)
                        for a, (f0, nf) in enumerate(DOWN):
                            m = nc.tensor.matmul(psO[:, j * P:(j + 1) * P], hT[0:nf, a, :], dT[0:nf, a, :], start=(a == 0), stop=(a == 2))
                        m.then_inc(S["out"], 1)
            @block.scalar
            def _(act):
                with act.Fori(0, B) as b:
                    act.wait_ge(S["xn"], b * 5 + 1)
                    nc.scalar.activation(t["sg"][:], t["xn"][:], ACT.Sign).then_inc(S["sign"], 1)
                    for j in range(4):
                        act.wait_ge(S["g_ready"], b * 4 + j + 1)
                        act.wait_ge(S["h_ready"], b * 4 + j + 1)
                        nc.scalar.activation(sl[:], psG[:, j % 2, 0:QI], ACT.Silu).then_inc(S["silu"], 1)
                        act.wait_ge(S["xn"], b * 5 + j + 2)
                        nc.scalar.activation(t["sg"][:, 0:22], t["xn"][:, 0:22], ACT.Sign).then_inc(S["sign"], 1)
                        act.wait_ge(S["h_turned"], b * 4 + j + 2)
                        act.wait_ge(S["out"], b * 4 + j + 1)
                        nc.scalar.activation(hT[:, 0:2, :], psH[:, 0:256].rearrange("p (a q) -> p a q", a=2), ACT.Copy)
                        nc.scalar.activation(hT[0:96, 2, :], psH[0:96, 256:384], ACT.Copy).then_inc(S["hT_ready"], 1)
            @block.vector
            def _(v):
                Xv = X[:].rearrange("p (b j) c -> p b j c", b=B)
                with v.Fori(0, B) as b:
                    step = Steps(v, S["steps"], b * (QSTEPS * 5))
                    v.wait_ge(S["x_turned"], b + 1)
                    src = XF[:, b, 1:5, :].rearrange("p j (n q) -> p (j n) q", q=QB)
                    fp4(nc, v, step, src, xq[:], t, lambda: v.sem_inc(S["xn"], 1), lambda: v.wait_ge(S["sign"], b * 5 + 1))
                    v.sem_inc(S["xq_ready"], 1)
                    v.wait_ge(S["x_turned"], b + 2)
                    v.wait_ge(S["u_ready"], 4 * b + 1)
                    nc.vector.tensor_copy(xqT[:], psT[:]).then_inc(S["xT_ready"], 1)
                    for j in range(4):
                        v.wait_ge(S["silu"], b * 4 + j + 1)
                        v.wait_ge(S["u_ready"], b * 4 + j + 2)
                        nc.vector.tensor_tensor(h[:].rearrange("p a b -> p (a b)"), psU[:, j % 2, 0:QI], sl[:], ALU.mult).then_inc(S["h_ready"], 1)
                        v.wait_ge(S["h_ready"], b * 4 + j + 2)
                        v.wait_ge(S["h_turned"], b * 4 + j + 1)
                        fp4(nc, v, step, h[:], hq[:], t, lambda: v.sem_inc(S["xn"], 1), lambda: v.wait_ge(S["sign"], b * 5 + j + 2))
                        v.sem_inc(S["hq_ready"], 1)
                    v.wait_ge(S["out"], (b + 1) * 4 + 1)
                    nc.vector.tensor_tensor(Xv[:, b], psO[:].rearrange("p (j c) -> p j c", j=4), Xv[:, b], ALU.add).then_inc(S["added"], 1)
        clear(nc, S.values())


MD, CH, NC, G = 32, 64, 8, 2

def neural_memory(nc, X, XF, c, w):
    with ExitStack() as ctx:
        sb = lambda n, s, d=F32: ctx.enter_context(nc.sbuf_tensor("M" + n, s, d))
        ps = lambda n, s, d=F32: ctx.enter_context(nc.psum_tensor("M" + n, s, d))
        sem = lambda n: ctx.enter_context(nc.semaphore("M" + n))
        wp = sb("wp", [P, 6, MD]); cw = sb("cw", [P, 3, 4]); cb = sb("cb", [P, 6])
        mean = sb("mean", [P, P]); pick = sb("pick", [P, 4, CH]); pick1 = sb("pick1", [P, 4]); bd = sb("bd", [P, P])
        start = sb("start", [P, 2, 512]); inj = sb("inj", [CH, 512])
        half = sb("half", [CH, 4]); mhalf = sb("mhalf", [P, 4])
        woT = sb("woT", [P, D]); gwT = sb("gwT", [P, D]); gb = sb("gb", [1, D]); ones1 = sb("ones1", [1, P]); ng = sb("ng", [P, D])
        xb = sb("xb", [P, 4, D]); xT = sb("xT", [P, B, 512])
        T = {k: sb(k, [P, G, 512]) for k in ("K", "V", "Q", "QW", "QS", "AW", "AS", "AS0", "RET")}
        mw = sb("mw", [CH, G, 4, 512]); mse = sb("mse", [CH, G, NC, 4]); th = sb("th", [CH, G, NC, 4]); k2 = sb("k2", [CH, G, NC, 4])
        kqm = sb("kqm", [CH, G, NC, 4 * CH])
        kw = sb("kw", [CH, G, NC, P]); ks = sb("ks", [CH, G, NC, P])
        W3 = sb("W3", [P, G, 3, P]); S3 = sb("S3", [P, G, 3, P])
        ident = c["ident"]
        S = {n: sem(n) for n in """loaded zeroed xb_ready turned xT_ready projected conv gates signs absd sexp slog splus a_mean om_ready e_mean et_ready
          scans sel_a sel_e m64_ready theta th_copied qbd_ready kq_ready kqm_ready ktok_ready kw_ready chain x_kept""".split()}
        start_at_one(nc, S, "kqm_ready kw_ready th_copied m64_ready theta projected x_kept")
        kinds = ("k", "v", "q", "a", "e", "t")
        with nc.Block() as block:
            @block.sync
            def _(sp):
                L = S["loaded"]
                for k, n in enumerate(("WkT", "WvT", "WqT", "aWT", "eWT", "tWT")):
                    sp.dma_start(wp[:, k, :], w[n]).then_inc(L, 16)
                for r in range(4):
                    q = slice(32 * r, 32 * r + 32)
                    for k, n in enumerate(("ck", "cv", "cq")):
                        sp.dma_start(cw[q, k, :], w[n + "w"]).then_inc(L, 16)
                        sp.dma_start(cb[q, k:k + 1], w[n + "b"].unsqueeze(1)).then_inc(L, 16)
                    for k, n in enumerate(("ab", "eb", "tb")):
                        sp.dma_start(cb[q, 3 + k:4 + k], w[n].unsqueeze(1)).then_inc(L, 16)
                    sp.dma_start(woT[q], w["WoT"]).then_inc(L, 16)
                for a, n in ((mean, "c_mean"), (pick, "c_pick"), (pick1, "c_pick1"), (bd, "c_bd"), (start, "c_start"), (inj, "c_inj"), (gwT, "gWT"), (gb, None), (ng, None)):
                    src = w[n] if n else (w["gb"].unsqueeze(0) if a is gb else rows(w["norm_g"]))
                    sp.dma_start(a[:], src).then_inc(L, 16)
                sp.wait_ge(S["zeroed"], 1)
                for g in range(G):
                    for r in range(4):
                        q = slice(32 * r, 32 * r + 32)
                        for k, n in enumerate(("mW1T", "mW2T", "mW2")):
                            sp.dma_start(W3[q, g, k, q], w[n]).then_inc(L, 16)
                sp.wait_ge(L, 16 * (6 + 40 + 9 + 24))
            @block.vector
            def _(v):
                nc.vector.memset(W3[:], 0.0).then_inc(S["zeroed"], 1)
                nc.vector.memset(S3[:], 0.0)
                nc.vector.memset(half[:], 0.5)
                nc.vector.memset(mhalf[:], -0.5)
                nc.vector.memset(ones1[:], 1.0)

        with ExitStack() as inner:
            isb = lambda n, s: inner.enter_context(nc.sbuf_tensor("M" + n, s, F32))
            xs4 = isb("xs4", [P, 4, 512])
            sg = isb("sg", [P, 3, 512]); rl = isb("rl", [P, 512]); om = isb("om", [P, 512]); et = isb("et", [P, 512]); dn = isb("dn", [P, 2, 512])
            m64 = isb("m64", [CH, 2, 512]); s64 = isb("s64", [CH, 512])
            qbd = isb("qbd", [P, NC, 4, CH]); ksq = isb("ksq", [CH, NC, P])
            psP = inner.enter_context(nc.psum_tensor("MpsP", [P, 6, 512], F32)); psT = inner.enter_context(nc.psum_tensor("MpsT", [P, 512], F32)); psM = inner.enter_context(nc.psum_tensor("MpsM", [P, 512], F32))
            kstage = rl
            with nc.Block() as block:
                @block.tensor
                def _(pe):
                    with pe.Fori(0, G) as g:
                        for r in range(4):
                            n = g * 4 + r
                            pe.wait_ge(S["xb_ready"], n + 1)
                            pe.wait_ge(S["xT_ready"], n)
                            for j in range(4):
                                m = nc.tensor.transpose(psT[:, j * P:(j + 1) * P], xb[:, j, :], ident[:])
                            m.then_inc(S["turned"], 1)
                        pe.wait_ge(S["xT_ready"], g * 4 + 4)
                        pe.wait_ge(S["kqm_ready"], g + 1)
                        pe.wait_ge(S["kw_ready"], g + 1)
                        for k in range(6):
                            for r in range(4):
                                m = nc.tensor.matmul(psP[32 * r:32 * r + 32, k, :], wp[:, k, :], xs4[:, r, :], start=True, stop=True, tile_position=(0, 32 * r))
                        m.then_inc(S["projected"], 1)
                        pe.wait_ge(S["signs"], g + 1)
                        pe.wait_ge(S["th_copied"], g + 1)
                        nc.tensor.matmul(psM[:], mean[:], sg[:, 0, :], start=True, stop=True).then_inc(S["a_mean"], 1)
                        pe.wait_ge(S["om_ready"], g + 1)
                        nc.tensor.matmul(psM[:], mean[:], sg[:, 1, :], start=True, stop=True).then_inc(S["e_mean"], 1)
                        pe.wait_ge(S["et_ready"], g + 1)
                        for r in range(4):
                            pe.wait_ge(S["m64_ready"], 2 * (g * 4 + r) + 1)
                            nc.tensor.matmul(psM[0:CH, :], pick[:, r, :], sg[:, 0, :], start=True, stop=True).then_inc(S["sel_a"], 1)
                            pe.wait_ge(S["m64_ready"], 2 * (g * 4 + r) + 2)
                            nc.tensor.matmul(psM[0:CH, :], pick[:, r, :], sg[:, 1, :], start=True, stop=True).then_inc(S["sel_e"], 1)
                        pe.wait_ge(S["m64_ready"], 2 * (g * 4 + 4) + 1)
                        pe.wait_ge(S["splus"], g + 1)
                        for k in range(NC):
                            m = nc.tensor.matmul(psM[0:CH, 4 * k:4 * k + 4], sg[:, 2, k * CH:(k + 1) * CH], pick1[:], start=True, stop=True)
                        m.then_inc(S["theta"], 1)
                        pe.wait_ge(S["qbd_ready"], g + 1)
                        for k in range(NC):
                            o = psP[0:CH, k // 2, (k % 2) * 256:(k % 2) * 256 + 256]
                            m = nc.tensor.matmul(o, kstage[:, k * CH:(k + 1) * CH], qbd[:, k], start=True, stop=True)
                        m.then_inc(S["kq_ready"], 1)
                        for k in range(NC):
                            m = nc.tensor.transpose(psP[0:CH, 4 + k // 4, (k % 4) * P:(k % 4 + 1) * P], kstage[:, k * CH:(k + 1) * CH], ident[:])
                        m.then_inc(S["ktok_ready"], 1)

                @block.scalar
                def _(act):
                    with act.Fori(0, G) as g:
                        for r in range(4):
                            n = g * 4 + r
                            act.wait_ge(S["turned"], n)
                            nc.scalar.activation(xb[:], XF[:, n, 1:5, :], ACT.Copy).then_inc(S["xb_ready"], 1)
                        act.wait_ge(S["xT_ready"], g * 4 + 4)
                        nc.scalar.activation(xT[:, bass.ds(g * 4, 4), :], xs4[:], ACT.Copy).then_inc(S["x_kept"], 1)
                        act.wait_ge(S["projected"], g + 2)
                        act.wait_ge(S["theta"], g + 1)
                        for k in range(2):
                            nc.scalar.activation(sg[:, k, :], psP[:, 3 + k, :], ACT.Sigmoid, bias=cb[:, 3 + k:4 + k])
                        nc.scalar.activation(sg[:, 2, :], psP[:, 5, :], ACT.Abs, bias=cb[:, 5:6]).then_inc(S["signs"], 1)
                        act.wait_ge(S["signs"], g + 1)
                        nc.scalar.activation(sg[:, 2, :], sg[:, 2, :], ACT.Exp, scale=-1.0).then_inc(S["sexp"], 1)
                        act.wait_ge(S["sexp"], g + 1)
                        nc.scalar.activation(sg[:, 2, :], sg[:, 2, :], ACT.Ln, bias=1.0).then_inc(S["slog"], 1)

                @block.vector
                def _(v):
                    nc.vector.memset(qbd[:], 0.0).then_inc(S["zeroed"], 1)
                    with v.Fori(0, G) as g:
                        step = Steps(v, S["chain"], g * 27)
                        for r in range(4):
                            n = g * 4 + r
                            v.wait_ge(S["turned"], n + 1)
                            v.wait_ge(S["projected"], g + 1)
                            v.wait_ge(S["x_kept"], g + 1)
                            nc.vector.tensor_copy(xs4[:, r, :], psT[:]).then_inc(S["xT_ready"], 1)
                        v.wait_ge(S["projected"], g + 2)
                        outs = [T[k][:, g, :] for k in "KVQ"]
                        for k in range(3):
                            m = nc.vector.tensor_scalar(outs[k], psP[:, k, :], cw[:, k, 3:4], cb[:, k:k + 1], ALU.mult, ALU.add)
                        step(m)
                        for back in (1, 2, 3):
                            for k in range(3):
                                m = nc.vector.scalar_tensor_tensor(out=outs[k][:, back:512], in0=psP[:, k, 0:512 - back], scalar=cw[:, k, 3 - back:4 - back], in1=outs[k][:, back:512], op0=ALU.mult, op1=ALU.add)
                            step(m)
                        v.wait_ge(S["signs"], g + 1)
                        step(nc.vector.tensor_scalar(rl[:], psP[:, 5, :], cb[:, 5:6], 0.0, ALU.add, ALU.max))
                        v.wait_ge(S["slog"], g + 1)
                        nc.vector.tensor_tensor(sg[:, 2, :], sg[:, 2, :], rl[:], ALU.add).then_inc(S["splus"], 1)
                        v.wait_ge(S["a_mean"], g + 1)
                        nc.vector.tensor_scalar(om[:], psM[:], -0.1, 1.0, ALU.mult, ALU.add).then_inc(S["om_ready"], 1)
                        v.wait_ge(S["e_mean"], g + 1)
                        nc.vector.tensor_scalar(et[:], psM[:], 0.9, 0.05, ALU.mult, ALU.add).then_inc(S["et_ready"], 1)
                        v.wait_ge(S["et_ready"], g + 1)
                        notfirst, first = start[:, 0, :], start[:, 1, :]
                        aw, as_, as0 = T["AW"][:, g, :], T["AS"][:, g, :], T["AS0"][:, g, :]
                        nc.vector.tensor_tensor(dn[:, 0], om[:], notfirst, ALU.mult)
                        step(nc.vector.tensor_tensor(dn[:, 1], om[:], first, ALU.mult))
                        step(nc.vector.tensor_tensor_scan(aw, dn[:, 0], dn[:, 1], 0.0, ALU.mult, ALU.add))
                        nc.vector.tensor_tensor(dn[:, 1], et[:], first, ALU.mult)
                        step(nc.vector.tensor_tensor(om[:], et[:], notfirst, ALU.mult))
                        step(nc.vector.tensor_tensor_scan(as0, om[:], dn[:, 1], 0.0, ALU.mult, ALU.add))
                        step(nc.vector.tensor_tensor_scan(as_, dn[:, 0], as0, 0.0, ALU.mult, ALU.add))
                        nc.vector.tensor_tensor(T["QW"][:, g, :], T["Q"][:, g, :], aw, ALU.mult)
                        step(nc.vector.tensor_tensor(T["QS"][:, g, :], T["Q"][:, g, :], as_, ALU.mult))
                        for r in range(4):
                            n = g * 4 + r
                            v.wait_ge(S["sel_a"], n + 1)
                            nc.vector.tensor_scalar(m64[:, 0], psM[0:CH, :], -0.1, 1.0, ALU.mult, ALU.add).then_inc(S["m64_ready"], 1)
                            v.wait_ge(S["sel_e"], n + 1)
                            nc.vector.tensor_scalar(m64[:, 1], psM[0:CH, :], 0.9, 0.05, ALU.mult, ALU.add).then_inc(S["m64_ready"], 1)
                            v.wait_ge(S["m64_ready"], 2 * n + 3)
                            step(nc.vector.tensor_tensor(m64[:], m64[:], bcast(start[0:CH, 0, :], 1, 2), ALU.mult))
                            step(nc.vector.tensor_tensor_scan(s64[:], m64[:, 1], inj[:], 0.0, ALU.mult, ALU.add))
                            nc.vector.tensor_copy(mse[:, g, :, r], s64[:].rearrange("p (c t) -> p c t", c=NC)[:, :, CH - 1])
                            step(nc.vector.tensor_tensor_scan(mw[:, g, r, :], m64[:, 0], s64[:], 0.0, ALU.mult, ALU.add))
                        v.wait_ge(S["theta"], g + 2)
                        nc.vector.tensor_copy(th[:, g], psM[0:CH, 0:32].rearrange("p (c r) -> p c r", c=NC)).then_inc(S["th_copied"], 1)
                        v.wait_ge(S["splus"], g + 1)
                        nc.vector.tensor_scalar(rl[:], T["K"][:, g, :], 1.0, None, ALU.mult)
                        for r in range(4):
                            q = slice(32 * r, 32 * r + 32)
                            m = nc.vector.tensor_copy(qbd[q, :, r, :], T["Q"][q, g, :].rearrange("p (c t) -> p c t", c=NC))
                        m.then_inc(S["qbd_ready"], 1)
                        v.wait_ge(S["kq_ready"], g + 1)
                        kqv = psP[0:CH, 0:4, :].rearrange("p a (b x) -> p (a b) x", b=2).rearrange("p c (r t) -> p c r t", r=4)
                        mwv = mw[:, g].rearrange("p r (c t) -> p c r t", c=NC)
                        nc.vector.tensor_tensor(kqm[:, g].rearrange("p c (r t) -> p c r t", r=4), kqv, mwv, ALU.mult).then_inc(S["kqm_ready"], 1)
                        v.wait_ge(S["ktok_ready"], g + 1)
                        ktk = psP[0:CH, 4:6, :].rearrange("p a (b x) -> p (a b) x", b=4).rearrange("p c (r d) -> p c r d", r=4)
                        last = mwv[:, :, :, CH - 1]
                        step(nc.vector.tensor_tensor(kw[:, g].rearrange("p c (r d) -> p c r d", r=4), ktk, bcast(last, 3, MD), ALU.mult))
                        step(nc.vector.tensor_tensor(ks[:, g].rearrange("p c (r d) -> p c r d", r=4), ktk, bcast(mse[:, g], 3, MD), ALU.mult))
                        step(nc.vector.tensor_copy(ksq[:].rearrange("p c (r d) -> p c r d", r=4), ktk))
                        step(nc.vector.tensor_tensor(ksq[:], ksq[:], ksq[:], ALU.mult))
                        nc.vector.tensor_reduce(k2[:, g], ksq[:].rearrange("p c (r d) -> p c r d", r=4), AX.X, ALU.add).then_inc(S["kw_ready"], 1)

        with ExitStack() as inner:
            isb = lambda n, s: inner.enter_context(nc.sbuf_tensor("M" + n, s, F32))
            psZ = inner.enter_context(nc.psum_tensor("MpsZ", [P, 2, 512], F32)); psR = inner.enter_context(nc.psum_tensor("MpsR", [P, 2, 512], F32))
            psK = inner.enter_context(nc.psum_tensor("MpsK", [P, 2, 512], F32)); psW = inner.enter_context(nc.psum_tensor("MpsW", [P, 2, 512], F32))
            sig = isb("sig", [P, G, CH]); hT = isb("hT", [P, G, CH]); om1 = isb("om1", [P, G, CH]); eT = isb("eT", [P, G, CH]); dz = isb("dz", [P, G, CH])
            tok = isb("tok", [CH, G, 3, P]); sqr = isb("sqr", [CH, G, 3, P]); n2 = isb("n2", [CH, G, 3, 4]); nn = isb("nn", [CH, G, 2, 4]); ce = isb("ce", [CH, G, 4])
            src = isb("src", [CH, G, 2, P]); hw = isb("hw", [CH, G, 2, P])
            sq = isb("sq", [P, G, CH]); h2 = isb("h2", [P, G, CH]); h2w = isb("h2w", [P, G, 2, CH]); h2bd = isb("h2bd", [P, G, 4, CH]); hhm = isb("hhm", [CH, G, 4 * CH])
            upd = isb("upd", [P, G, 6, P]); t3 = isb("t3", [P, G, 3, P])
            stg = isb("stg", [P, G, 3, CH]); stt = isb("stt", [CH, G, 2, P])
            R = {n: sem("r_" + n) for n in """staged z sig h om1 ds pred e dh dz turned tok sqr n2 pow ce src zq sq h2 h2w hh hhm out ret hw upd masked t3 w3 chain zero clear""".split()}
            start_at_one(nc, R, "w3 ret masked upd")
            kqs = isb("kqs", [CH, G, 4 * CH])
            with nc.Block() as block:
                @block.tensor
                def _(pe):
                    with pe.Fori(0, NC) as k:
                        t0 = k * CH
                        n = [k * G + g for g in range(G)]
                        for g in range(G):
                            pe.wait_ge(R["w3"], k * G + 1)
                            pe.wait_ge(R["ret"], k * G + 1)
                            nc.tensor.matmul(psZ[:, g, 0:CH], W3[:, g, 0, :], T["K"][:, g, bass.ds(t0, CH)], start=True, stop=True).then_inc(R["z"], 1)
                            pe.wait_ge(R["h"], n[g] + 1)
                            nc.tensor.matmul(psZ[:, g, CH:2 * CH], W3[:, g, 1, :], hT[:, g, :], start=True, stop=True).then_inc(R["pred"], 1)
                            pe.wait_ge(R["e"], n[g] + 1)
                            nc.tensor.matmul(psZ[:, g, 2 * CH:3 * CH], W3[:, g, 2, :], eT[:, g, :], start=True, stop=True).then_inc(R["dh"], 1)
                            pe.wait_ge(R["dz"], n[g] + 1)
                            pe.sem_inc(R["clear"], 1)
                            for a, x in enumerate((hT, eT, dz)):
                                m = nc.tensor.transpose(psK[0:CH, g, a * P:(a + 1) * P], x[:, g, :], ident[:])
                            m.then_inc(R["turned"], 1)
                        for g in range(G):
                            pe.wait_ge(R["src"], n[g] + 1)
                            o = psR[:, g, 0:CH]
                            nc.tensor.matmul(o, W3[:, g, 0, :], T["QW"][:, g, bass.ds(t0, CH)], start=True, stop=True)
                            nc.tensor.matmul(o, S3[:, g, 0, :], T["QS"][:, g, bass.ds(t0, CH)], start=False, stop=True, skip_group_check=True)
                            for r in range(4):
                                q = slice(32 * r, 32 * r + 32)
                                m = nc.tensor.matmul(psR[q, g, 0:CH], src[:, g, 1, q], kqs[:, g, r * CH:(r + 1) * CH], start=False, stop=True, skip_group_check=True, tile_position=(0, 32 * r))
                            m.then_inc(R["zq"], 1)
                            pe.wait_ge(R["h2w"], n[g] + 1)
                            nc.tensor.matmul(psR[0:CH, g, 128:128 + 4 * CH], hT[:, g, :], h2bd[:, g], start=True, stop=True).then_inc(R["hh"], 1)
                            pe.wait_ge(R["hhm"], n[g] + 1)
                            o = psR[:, g, 0:CH]
                            nc.tensor.matmul(o, W3[:, g, 1, :], h2w[:, g, 0, :], start=True, stop=True)
                            nc.tensor.matmul(o, S3[:, g, 1, :], h2w[:, g, 1, :], start=False, stop=True, skip_group_check=True)
                            for r in range(4):
                                q = slice(32 * r, 32 * r + 32)
                                m = nc.tensor.matmul(psR[q, g, 0:CH], src[:, g, 0, q], hhm[:, g, r * CH:(r + 1) * CH], start=False, stop=True, skip_group_check=True, tile_position=(0, 32 * r))
                            m.then_inc(R["out"], 1)
                        for g in range(G):
                            pe.wait_ge(R["hw"], n[g] + 1)
                            pe.wait_ge(R["masked"], k * G + g + 1)
                            for a in range(2):
                                o = lambda s: psW[:, a, s * P:(s + 1) * P]
                                nc.tensor.matmul(o(0), stt[:, g, a, :], src[:, g, 1, :], start=True, stop=True)
                                nc.tensor.matmul(o(1), hw[:, g, a, :], src[:, g, 0, :], start=True, stop=True)
                                m = nc.tensor.matmul(o(2), src[:, g, 0, :], hw[:, g, a, :], start=True, stop=True)
                            m.then_inc(R["upd"], 1)

                @block.scalar
                def _(act):
                    with act.Fori(0, NC) as k:
                        t0 = k * CH
                        n = [k * G + g for g in range(G)]
                        for g in range(G):
                            act.wait_ge(R["upd"], k * G + 1)
                            nc.scalar.activation(kqs[:, g, :], kqm[:, g, k, :], ACT.Copy)
                            nc.scalar.activation(stt[:, g, 0, :], kw[:, g, k, :], ACT.Copy)
                            nc.scalar.activation(stt[:, g, 1, :], ks[:, g, k, :], ACT.Copy).then_inc(R["staged"], 1)
                        for g in range(G):
                            act.wait_ge(R["z"], n[g] + 1)
                            nc.scalar.activation(sig[:, g, :], psZ[:, g, 0:CH], ACT.Sigmoid).then_inc(R["sig"], 1)
                            act.wait_ge(R["turned"], n[g] + 1)
                            nc.scalar.activation(tok[:, g].rearrange("p a b -> p (a b)"), psK[0:CH, g, 0:3 * P], ACT.Copy).then_inc(R["tok"], 1)
                        for g in range(G):
                            act.wait_ge(R["zq"], n[g] + 1)
                            nc.scalar.activation(sq[:, g, :], psR[:, g, 0:CH], ACT.Sigmoid).then_inc(R["sq"], 1)
                            act.wait_ge(R["out"], n[g] + 1)
                            nc.scalar.activation(T["RET"][:, g, bass.ds(t0, CH)], psR[:, g, 0:CH], ACT.Copy).then_inc(R["ret"], 1)

                @block.gpsimd
                def _(g_):
                    with g_.Fori(0, NC) as k:
                        for g in range(G):
                            n = k * G + g
                            g_.wait_ge(R["n2"], n + 1)
                            nc.gpsimd.tensor_tensor(nn[:, g, 0, :], nn[:, g, 0, :], half[:], ALU.pow).then_inc(R["pow"], 1)

                @block.vector
                def _(v):
                    nc.vector.memset(h2bd[:], 0.0).then_inc(R["zero"], 1)
                    v.wait_ge(R["zero"], 1)
                    with v.Fori(0, NC) as k:
                        t0 = k * CH
                        step = Steps(v, R["chain"], k * 24)
                        n = [k * G + g for g in range(G)]
                        for g in range(G):
                            v.wait_ge(R["sig"], n[g] + 1)
                            z = psZ[:, g, 0:CH]
                            nc.vector.tensor_tensor(hT[:, g, :], z, sig[:, g, :], ALU.mult).then_inc(R["h"], 1)
                            step(nc.vector.tensor_scalar(om1[:, g, :], sig[:, g, :], -1.0, 1.0, ALU.mult, ALU.add))
                            v.wait_ge(R["h"], n[g] + 1)
                            step(nc.vector.tensor_tensor(om1[:, g, :], om1[:, g, :], hT[:, g, :], ALU.mult))
                            step(nc.vector.tensor_tensor(om1[:, g, :], om1[:, g, :], sig[:, g, :], ALU.add))
                            v.wait_ge(R["pred"], n[g] + 1)
                            nc.vector.tensor_tensor(eT[:, g, :], psZ[:, g, CH:2 * CH], T["V"][:, g, bass.ds(t0, CH)], ALU.subtract).then_inc(R["e"], 1)
                            v.wait_ge(R["dh"], n[g] + 1)
                            nc.vector.tensor_tensor(dz[:, g, :], psZ[:, g, 2 * CH:3 * CH], om1[:, g, :], ALU.mult).then_inc(R["dz"], 1)
                        for g in range(G):
                            v.wait_ge(R["tok"], n[g] + 1)
                            step(nc.vector.tensor_tensor(sqr[:, g], tok[:, g], tok[:, g], ALU.mult))
                            step(nc.vector.tensor_reduce(n2[:, g], sqr[:, g].rearrange("p a (r d) -> p a r d", r=4), AX.X, ALU.add))
                            nc.vector.tensor_tensor(nn[:, g, 0, :], n2[:, g, 0, :], n2[:, g, 1, :], ALU.mult)
                            step(nc.vector.tensor_tensor(nn[:, g, 1, :], n2[:, g, 2, :], k2[:, g, k, :], ALU.mult))
                            nc.vector.tensor_tensor(nn[:, g, 0, :], nn[:, g, 0, :], nn[:, g, 1, :], ALU.add).then_inc(R["n2"], 1)
                        for g in range(G):
                            v.wait_ge(R["pow"], n[g] + 1)
                            step(nc.vector.tensor_scalar(ce[:, g, :], nn[:, g, 0, :], 0.2, 1e-6, ALU.mult, ALU.max))
                            step(nc.vector.reciprocal(ce[:, g, :], ce[:, g, :]))
                            step(nc.vector.tensor_scalar(ce[:, g, :], ce[:, g, :], 1.0, 0.2, ALU.min, ALU.mult))
                            step(nc.vector.tensor_tensor(ce[:, g, :], ce[:, g, :], th[:, g, k, :], ALU.mult))
                            v.wait_ge(R["staged"], n[g] + 1)
                            nc.vector.tensor_tensor(src[:, g].rearrange("p a (r d) -> p a r d", r=4), tok[:, g, 1:3].rearrange("p a (r d) -> p a r d", r=4),
                                                    bcast(bcast(ce[:, g, :], 2, MD), 1, 2), ALU.mult).then_inc(R["src"], 1)
                            ht = tok[:, g, 0].rearrange("p (r d) -> p r d", r=4)
                            mwv = mw[:, g].rearrange("p r (c t) -> p c r t", c=NC)
                            nc.vector.tensor_tensor(hw[:, g, 0].rearrange("p (r d) -> p r d", r=4), ht, bcast(mwv[:, k, :, CH - 1], 2, MD), ALU.mult)
                            nc.vector.tensor_tensor(hw[:, g, 1].rearrange("p (r d) -> p r d", r=4), ht, bcast(mse[:, g, k, :], 2, MD), ALU.mult).then_inc(R["hw"], 1)
                        for g in range(G):
                            v.wait_ge(R["sq"], n[g] + 1)
                            step(nc.vector.tensor_tensor(h2[:, g, :], psR[:, g, 0:CH], sq[:, g, :], ALU.mult))
                            nc.vector.tensor_tensor(h2w[:, g, 0, :], h2[:, g, :], T["AW"][:, g, bass.ds(t0, CH)], ALU.mult)
                            nc.vector.tensor_tensor(h2w[:, g, 1, :], h2[:, g, :], T["AS"][:, g, bass.ds(t0, CH)], ALU.mult)
                            for r in range(4):
                                q = slice(32 * r, 32 * r + 32)
                                m = nc.vector.tensor_copy(h2bd[q, g, r, :], h2[q, g, :])
                            m.then_inc(R["h2w"], 1)
                            v.wait_ge(R["hh"], n[g] + 1)
                            mwc = mw[:, g].rearrange("p r (c t) -> p c r t", c=NC)[:, k]
                            nc.vector.tensor_tensor(hhm[:, g].rearrange("p (r t) -> p r t", r=4), psR[0:CH, g, 128:128 + 4 * CH].rearrange("p (r t) -> p r t", r=4), mwc, ALU.mult).then_inc(R["hhm"], 1)
                        for g in range(G):
                            v.wait_ge(R["upd"], n[g] + 2)
                            m = nc.vector.tensor_tensor(upd[:, g].rearrange("p (a s) x -> p a s x", a=2), psW[:, :, 0:3 * P].rearrange("p a (s x) -> p a s x", s=3), bcast(bcast(bd[:], 1, 3), 1, 2), ALU.mult)
                            m.then_inc(R["masked"], 1)
                            v.wait_ge(R["masked"], n[g] + 2)
                            v.wait_ge(R["out"], n[g] + 1)
                            at = bass.ds(t0 + CH - 1, 1)
                            step(nc.vector.scalar_tensor_tensor(out=t3[:, g], in0=S3[:, g], scalar=T["AS"][:, g, at], in1=upd[:, g, 0:3], op0=ALU.mult, op1=ALU.add))
                            nc.vector.scalar_tensor_tensor(out=S3[:, g], in0=S3[:, g], scalar=T["AS0"][:, g, at], in1=upd[:, g, 3:6], op0=ALU.mult, op1=ALU.add)
                            nc.vector.scalar_tensor_tensor(out=W3[:, g], in0=W3[:, g], scalar=T["AW"][:, g, at], in1=t3[:, g], op0=ALU.mult, op1=ALU.add).then_inc(R["w3"], 1)

        clear(nc, S.values())
        clear(nc, R.values())

        with ExitStack() as inner:
            isb = lambda n, s: inner.enter_context(nc.sbuf_tensor("M" + n, s, F32))
            psY = inner.enter_context(nc.psum_tensor("MpsY", [P, 2, 512], F32)); psG = inner.enter_context(nc.psum_tensor("MpsG", [P, 2, 512], F32))
            rg = isb("rg", [P, 512]); xg = isb("xg", [P, 2, 512]); ysq = isb("ysq", [P, 4, D]); ss = isb("ss", [P, 4]); y = isb("y", [P, 4, D])
            R = {n: sem("o_" + n) for n in "rg xg y gate sq ss eps rstd yn chain added".split()}
            start_at_one(nc, R, "y gate ss added")
            with nc.Block() as block:
                @block.scalar
                def _(act):
                    with act.Fori(0, G) as g:
                        act.wait_ge(R["y"], g * 4 + 1)
                        nc.scalar.activation(rg[:], T["RET"][:, g, :], ACT.Copy).then_inc(R["rg"], 1)
                        for r in range(4):
                            act.wait_ge(R["gate"], 1 + (g * 4 + (r - 1 if r >= 2 else 0)))
                            nc.scalar.activation(xg[:, r % 2, :], xT[:, g * 4 + r, :], ACT.Copy).then_inc(R["xg"], 1)
                            act.wait_ge(R["y"], g * 4 + r + 2)
                            act.wait_ge(R["ss"], g * 4 + r + 1)
                            nc.scalar.activation(ysq[:].rearrange("p a b -> p (a b)"), psY[:, r % 2, :], ACT.Square).then_inc(R["sq"], 1)
                @block.tensor
                def _(pe):
                    with pe.Fori(0, G) as g:
                        for r in range(4):
                            n = g * 4 + r
                            q = slice(32 * r, 32 * r + 32)
                            pe.wait_ge(R["rg"], g + 1)
                            pe.wait_ge(R["added"], 1 + (g * 4 + (r - 1 if r >= 2 else 0)))
                            for j in range(4):
                                m = nc.tensor.matmul(psY[:, r % 2, j * P:(j + 1) * P], rg[q, j * P:(j + 1) * P], woT[q, :], start=True, stop=True)
                            m.then_inc(R["y"], 1)
                            pe.wait_ge(R["xg"], n + 1)
                            for j in range(4):
                                o = psG[:, r % 2, j * P:(j + 1) * P]
                                nc.tensor.matmul(o, ones1[:], gb[:], start=True, stop=False)
                                m = nc.tensor.matmul(o, xg[:, r % 2, j * P:(j + 1) * P], gwT[:], start=False, stop=True)
                            m.then_inc(R["gate"], 1)
                @block.gpsimd
                def _(g_):
                    with g_.Fori(0, B) as n:
                        g_.wait_ge(R["eps"], n + 1)
                        nc.gpsimd.tensor_tensor(ss[:], ss[:], mhalf[:], ALU.pow).then_inc(R["rstd"], 1)
                @block.vector
                def _(v):
                    Xv = X[:].rearrange("p (b j) c -> p b j c", b=B)
                    with v.Fori(0, G) as g:
                        step = Steps(v, R["chain"], g * 16)
                        for r in range(4):
                            n = g * 4 + r
                            v.wait_ge(R["sq"], n + 1)
                            nc.vector.tensor_reduce(ss[:], ysq[:], AX.X, ALU.add).then_inc(R["ss"], 1)
                            v.wait_ge(R["ss"], n + 2)
                            nc.vector.tensor_scalar(ss[:], ss[:], 1.0 / D, 1e-6, ALU.mult, ALU.add).then_inc(R["eps"], 1)
                            v.wait_ge(R["rstd"], n + 1)
                            step(nc.vector.tensor_tensor(y[:], psY[:, r % 2, :].rearrange("p (j c) -> p j c", j=4), bcast(ss[:], 2, D), ALU.mult))
                            step(nc.vector.tensor_tensor(y[:], y[:], bcast(ng[:], 1, 4), ALU.mult))
                            v.wait_ge(R["gate"], n + 2)
                            step(nc.vector.tensor_tensor(y[:], psG[:, r % 2, :].rearrange("p (j c) -> p j c", j=4), y[:], ALU.mult))
                            step(nc.vector.tensor_tensor(Xv[:, n], y[:], Xv[:, n], ALU.add))
                            v.sem_inc(R["added"], 1)
        clear(nc, R.values())


def memory_consts():
    bd = np.kron(np.eye(4), np.ones((32, 32))).astype(np.float32)
    pick = np.zeros((P, 4, CH), np.float32)
    pick1 = np.zeros((P, 4), np.float32)
    for r in range(4):
        pick[32 * r:32 * r + 32, r] = 1 / 32
        pick1[32 * r:32 * r + 32, r] = -0.1 / 32
    t = np.arange(512)
    first = np.broadcast_to((t % CH == 0).astype(np.float32), (P, 512))
    start = np.stack([1 - first, first], 1).copy()
    inj = (t[None] % CH == np.arange(CH)[:, None]).astype(np.float32)
    return {"c_mean": bd / 32, "c_bd": bd, "c_pick": pick, "c_pick1": pick1, "c_start": start, "c_inj": inj}

def memory_layout(w):
    t = np.ascontiguousarray
    return {**{n + "T": t(w[n].T) for n in ("Wk", "Wv", "Wq", "aW", "eW", "tW", "Wo", "gW", "mW1", "mW2")}}


def network(nc, x, ident_in, w, out):
    with ExitStack() as ctx:
        X = ctx.enter_context(nc.sbuf_tensor("X", [P, 32, D], F32))
        XF = ctx.enter_context(nc.sbuf_tensor("XF", [P, B, 5, D], F32))
        ident = ctx.enter_context(nc.sbuf_tensor("ident", [P, P], F32))
        io = ctx.enter_context(nc.semaphore("io")); summed = ctx.enter_context(nc.semaphore("summed"))
        c = {"ident": ident}
        xt, ot = (a.rearrange("b (j p) c -> p (b j) c", p=P) for a in (x, out))
        with nc.Block() as block:
            @block.sync
            def _(sp):
                sp.dma_start(X[:], xt).then_inc(io, 16)
                sp.dma_start(ident[:], ident_in).then_inc(io, 16)
                sp.wait_ge(io, 32)
            @block.vector
            def _(v):
                nc.vector.memset(XF[:, :, 0, :], 0.0)

        layer_norm(nc, X, XF, "n0")
        causal_attention(nc, X, XF, c, w["L0_attn"])
        local_layers(nc, XF, c, w["L0_ffn"])
        with nc.Block() as block:
            @block.vector
            def _(v):
                xv = X[:].rearrange("p (b j) c -> p b (j c)", b=B)
                nc.vector.tensor_tensor(xv, XF[:, :, 1:5, :].rearrange("p b j c -> p b (j c)"), xv, ALU.add).then_inc(summed, 1)
        layer_norm(nc, X, XF, "n1")
        state_space(nc, X, XF, c, w["L1_attn"])
        top2_experts(nc, X, XF, c, w["L1_ffn"])
        layer_norm(nc, X, XF, "n2")
        banded_attention(nc, X, XF, c, w["L2_attn"])
        capped_experts(nc, X, XF, c, w["L2_ffn"])
        layer_norm(nc, X, XF, "n3")
        neural_memory(nc, X, XF, c, w["L3_attn"])
        fp4_ffn(nc, X, XF, c, w["L3_ffn"])
        with nc.Block() as block:
            @block.sync
            def _(sp):
                sp.dma_start(ot, X[:]).then_inc(io, 16)
                sp.wait_ge(io, 48)


def kernel(**inputs):
    import numpy as _np
    import concourse.bacc as _bacc
    from concourse import mybir as _mybir
    from concourse.bass_utils import run_bass_kernel_spmd as _run

    inputs = {k: _np.asarray(v) for k, v in inputs.items()}
    sub = lambda p: {k[len(p) + 1:]: v for k, v in inputs.items() if k.startswith(p + "_")}
    t = _np.ascontiguousarray
    identb = {"c_identb": _np.eye(P).astype("bfloat16")}
    stages = {p: sub(p) for p in ("L0_attn", "L0_ffn", "L1_attn", "L1_ffn", "L2_attn", "L2_ffn", "L3_attn", "L3_ffn")}
    s = stages["L0_attn"]
    s.update({n + "T": t(s[n].T) for n in ("Wk", "Wq", "Wv", "Wu")}, **attention_consts(), **identb)
    x = s.pop("x")
    stages["L0_ffn"].update(local_consts(), **identb)
    s = stages["L1_attn"]
    s.update({"W_outT": t(s["W_out"].T), "c_flip": t(_np.eye(P, dtype=_np.float32)[::-1])})
    s = stages["L1_ffn"]
    s.update(top2_consts(), **top2_layout(s))
    stages["L2_attn"].update(banded_consts(), **identb)
    s = stages["L2_ffn"]
    s.update(capped_consts(), **capped_layout(s))
    s = stages["L3_attn"]
    s.update(memory_consts(), **memory_layout(s))

    nc = _bacc.Bacc("TRN2", target_bir_lowering=False, num_devices=1)
    arrays = {}

    def given(name, a):
        arrays[name] = t(a)
        return nc.dram_tensor(name, a.shape, _mybir.dt.from_np(a.dtype), kind="ExternalInput").ap()

    xin, ident_in = given("x", x), given("identity", _np.eye(P, dtype=_np.float32))
    w = {p: {n: given(p + "_" + n, a) for n, a in d.items() if n not in HOST_ONLY} for p, d in stages.items()}
    out = nc.dram_tensor("out_0", x.shape, F32, kind="ExternalOutput").ap()
    network(nc, xin, ident_in, w, out)
    r = _run(nc, [arrays], core_ids=[0])
    return r.results[0]["out_0"]
```

```python
from contextlib import ExitStack

import numpy as np
import concourse.bass as bass
from concourse import mybir

P, B, T, D = 128, 8, 4, 128
F32 = mybir.dt.float32; BF16 = mybir.dt.bfloat16
ALU = mybir.AluOpType; ACT = mybir.ActivationFunctionType; AX = mybir.AxisListType

def bcast(ap, axis, n):
    dims = [list(x) for x in ap.ap]
    return bass.AP(ap.tensor, ap.offset, dims[:axis] + [[0, n]] + dims[axis:])

def rows(ap, n=P):
    return bass.AP(ap.tensor, ap.offset, [[0, n]] + [list(x) for x in ap.ap])


def clear(nc, sems):
    numbers = sorted(s.num for s in sems)
    with nc.Block() as block:
        @block.sync
        def _(sp):
            first = numbers[0]
            for n, after in zip(numbers, numbers[1:] + [None]):
                if after != n + 1:
                    sp.sem_clear(range(first, n + 1))
                    first = after

def start_at_one(nc, S, names):
    with nc.Block() as block:
        @block.sync
        def _(sp):
            for n in names.split():
                sp.sem_inc(S[n], 1)

class Steps:
    def __init__(self, eng, sem, base):
        self.eng, self.sem, self.base, self.n = eng, sem, base, 0

    def __call__(self, ins):
        self.n += 1
        ins.then_inc(self.sem, 1)
        self.eng.wait_ge(self.sem, self.base + self.n)


HOST_ONLY = ("Wk", "Wq", "Wv", "Wu", "W_out", "gate_w", "up_w", "gp_w", "down_w", "up_b", "gp_b", "gate_up_proj", "down_proj",
             "shared_gate", "shared_up", "shared_down", "router_weight", "aW", "eW", "tW", "gW", "mW1")


def layer_norm(nc, X, XF, name):
    with ExitStack() as ctx:
        sb = lambda n, s, d=F32: ctx.enter_context(nc.sbuf_tensor(name + n, s, d))
        st = sb("st", [P, 4, 6]); mv = sb("mv", [P, 4, 2]); mean = sb("mean", [P, B, 4]); ve = sb("ve", [P, B, 4]); rs = sb("rs", [P, B, 4]); mh = sb("mh", [P, 4])
        names = "stats passed aggr eps rstd done power_set"
        S = {n: ctx.enter_context(nc.semaphore(name + n)) for n in names.split()}
        start_at_one(nc, S, "eps")
        with nc.Block() as block:
            @block.vector
            def _(v):
                Xv = X[:].rearrange("p (b j) c -> p b j c", b=B)
                with v.Fori(0, B) as b:
                    v.wait_ge(S["eps"], b + 1)
                    for j in range(4):
                        m = nc.vector.bn_stats(st[:, j, :], Xv[:, b, j, :])
                    m.then_inc(S["stats"], 1)
                    v.wait_ge(S["stats"], b + 1)
                    v.sem_inc(S["passed"], 1)
                    for j in range(4):
                        m = nc.vector.bn_aggr(mv[:, j, :], st[:, j, :])
                    m.then_inc(S["aggr"], 1)
                    v.wait_ge(S["aggr"], b + 1)
                    nc.vector.tensor_copy(mean[:, b], mv[:, :, 0])
                    nc.vector.tensor_scalar(ve[:, b], mv[:, :, 1], 1e-5, None, ALU.add).then_inc(S["eps"], 1)
                with v.Fori(0, B) as b:
                    v.wait_ge(S["rstd"], b + 1)
                    for j in range(4):
                        m = nc.vector.tensor_scalar(XF[:, b, j + 1, :], Xv[:, b, j, :], mean[:, b, j:j + 1], rs[:, b, j:j + 1], ALU.subtract, ALU.mult)
                    m.then_inc(S["done"], 1)

            @block.gpsimd
            def _(g):
                nc.gpsimd.memset(mh[:], -0.5).then_inc(S["power_set"], 1)
                g.wait_ge(S["power_set"], 1)
                with g.Fori(0, B) as b:
                    g.wait_ge(S["eps"], b + 2)
                    nc.gpsimd.tensor_tensor(rs[:, b], ve[:, b], mh[:], ALU.pow).then_inc(S["rstd"], 1)
        clear(nc, S.values())


SN, HALFK, SEQ = 16, 32, 512

def kernel_buffers(nc, ctx, w):
    sb = lambda n, s: ctx.enter_context(nc.sbuf_tensor("K" + n, s, F32))
    K = {"pw": sb("pw", [P, 6, SN, SN]), "Bv": sb("Bv", [P, HALFK, SN]), "Cu": sb("Cu", [P, SN, SN]), "Dm": sb("Dm", [P, 1]),
         "tmp": sb("tmp", [P, 4096]), "kpad": sb("kpad", [P, 640]), "w": w}
    K.update({n: ctx.enter_context(nc.semaphore("K" + n)) for n in ("loaded", "steps", "built", "stored")})
    K["scratch"] = nc.dram_tensor("Kernels", (P + 1, 640), F32).ap()
    return K


def load_and_store_kernels(sp, K):
    for t, n in ((K["pw"][:, 0], "A"), (K["Bv"][:, 0, :], "Bm"), (K["Cu"][:, 0, :], "Cm")):
        sp.dma_start(t, K["w"][n]).then_inc(K["loaded"], 16)
    sp.dma_start(K["Dm"][:], K["w"]["Dm"].unsqueeze(1)).then_inc(K["loaded"], 16)
    sp.wait_ge(K["built"], 1)
    sp.dma_start(K["scratch"][0:P], K["kpad"][:]).then_inc(K["stored"], 16)
    sp.wait_ge(K["stored"], 16)


def build_kernels(nc, g, K):
    pw, Bv, Cu, tmp, kpad = (K[n] for n in ("pw", "Bv", "Cu", "tmp", "kpad"))

    def sum_products(step, out, t, x, y):
        step(nc.gpsimd.tensor_tensor(t, x, y, ALU.mult))
        n = SN // 2
        while n > 1:
            lo, hi = (bass.AP(t.tensor, t.offset + k * n, [list(d) for d in t.ap[:-1]] + [[1, n]]) for k in range(2))
            step(nc.gpsimd.tensor_tensor(lo, lo, hi, ALU.add))
            n //= 2
        lo, hi = (bass.AP(t.tensor, t.offset + k, [list(d) for d in t.ap[:-1]]) for k in range(2))
        step(nc.gpsimd.tensor_tensor(out, lo, hi, ALU.add))

    def transposed(M):
        return bass.AP(M.tensor, M.offset, [list(M.ap[0]), [1, SN], [SN, SN]])

    steps_of = 5
    step = Steps(g, K["steps"], 0)
    step(nc.gpsimd.memset(kpad[:], 0.0))
    g.wait_ge(K["loaded"], 64)
    done = step.n
    t3 = tmp[:].rearrange("p (a b c) -> p a b c", a=SN, b=SN)
    with g.Fori(0, 5) as i:
        M = pw[:, i]
        sum_products(Steps(g, K["steps"], i * steps_of + done), pw[:, i + 1], t3, bcast(M, 2, SN), bcast(transposed(M), 1, SN))
    done += 5 * steps_of
    t2 = tmp[:, 0:256].rearrange("p (a b) -> p a b", a=SN)
    with g.Fori(0, HALFK - 1) as i:
        sum_products(Steps(g, K["steps"], i * steps_of + done), Bv[:, i + 1, :], t2, pw[:, 0], bcast(Bv[:, i, :], 1, SN))
    done += (HALFK - 1) * steps_of
    with g.Fori(0, SN - 1) as i:
        sum_products(Steps(g, K["steps"], i * steps_of + done), Cu[:, i + 1, :], t2, bcast(Cu[:, i, :], 1, SN), transposed(pw[:, 5]))
    done += (SN - 1) * steps_of
    step = Steps(g, K["steps"], done)
    t4 = tmp[:].rearrange("p (a b c) -> p a b c", a=8, b=HALFK)
    for k in range(2):
        back = bass.AP(kpad[:].tensor, kpad[:, SEQ - 1 - 256 * k:SEQ].offset, [[640, P], [-HALFK, 8], [-1, HALFK]])
        sum_products(step, back, t4, bcast(Cu[:, 8 * k:8 * k + 8, :], 2, HALFK), bcast(Bv[:], 1, 8))
    nc.gpsimd.tensor_tensor(kpad[:, SEQ - 1:SEQ], kpad[:, SEQ - 1:SEQ], K["Dm"][:], ALU.add).then_inc(K["built"], 1)


def state_space(nc, X, XF, c, w, scratch):
    with ExitStack() as ctx:
        sb = lambda n, s, d=F32: ctx.enter_context(nc.sbuf_tensor("R" + n, s, d))
        ps = lambda n, s, d=F32: ctx.enter_context(nc.psum_tensor("R" + n, s, d))
        sem = lambda n: ctx.enter_context(nc.semaphore("R" + n))
        GD = 16
        toep = sb("toep", [P, 2, GD, SEQ])
        Y = sb("Y", [P, 32, D])
        wo = sb("wo", [P, D]); bo = sb("bo", [1, D]); ones1 = sb("ones1", [1, P]); lnp = sb("lnp", [P, 2]); flip = sb("flip", [P, P])
        st = sb("st", [P, 4, 6]); mv = sb("mv", [P, 4, 2]); ve = sb("ve", [P, 4]); rs = sb("rs", [P, 4]); mh = sb("mh", [P, 4])
        xn4 = sb("xn4", [P, 4, D]); gT = sb("gT", [P, 512])
        conv = ps("conv", [P, 2, 512]); psT = ps("psT", [P, 512]); psO = ps("psO", [P, 512])
        ident = c["ident"]
        S = {n: sem(n) for n in """loaded toep_loaded0 toep_loaded1 conv_done conv_copied
          bn aggr eps rstd xhat turned gelu out added passed""".split()}
        start_at_one(nc, S, "conv_done conv_copied")
        start_at_one(nc, S, "conv_done conv_copied gelu added out rstd turned xhat")
        with nc.Block() as block:
            @block.sync
            def _(sp):
                L = S["loaded"]
                sp.dma_start(wo[:], w["W_outT"]).then_inc(L, 16)
                sp.dma_start(bo[:], w["b_out"].unsqueeze(0)).then_inc(L, 16)
                sp.dma_start(lnp[:, 0:1], w["ln_w"].unsqueeze(1)).then_inc(L, 16)
                sp.dma_start(lnp[:, 1:2], w["ln_b"].unsqueeze(1)).then_inc(L, 16)
                sp.dma_start(flip[:], w["c_flip"]).then_inc(L, 16)
                sp.wait_ge(L, 80)
            @block.gpsimd
            def _(g):
                nc.gpsimd.memset(mh[:], -0.5)
            @block.vector
            def _(v):
                nc.vector.memset(ones1[:], 1.0)

        def taps(slot, k, lag):
            return toep[:, slot, k, SEQ - P - lag * P:SEQ - lag * P]

        with nc.Block() as block:
            @block.sync
            def _(sp):
                with sp.Fori(0, P // GD // 2) as i:
                    for slot in range(2):
                        sp.wait_ge(S["conv_done"], 2 * i + (slot + 1))
                        src = bass.AP(scratch.tensor, (2 * i + slot) * (GD * 640), [[1, P], [640, GD], [1, SEQ]])
                        sp.dma_start(toep[:, slot], src).then_inc(S["toep_loaded%d" % slot], 16)
            @block.tensor
            def _(pe):
                with pe.Fori(0, P // GD // 2) as i:
                    for slot in range(2):
                        pe.wait_ge(S["toep_loaded%d" % slot], i * 16 + 16)
                        pe.wait_ge(S["conv_copied"], 2 * i + (slot + 1))
                        for k in range(GD):
                            o4 = conv[:, slot, k * 32:k * 32 + 32].rearrange("p (b j) -> p b j", b=B)
                            for lag in range(4):
                                m = nc.tensor.matmul(o4[:, :, lag:4], taps(slot, k, lag), XF[:, :, 1:5 - lag, (2 * i + slot) * GD + k], start=(lag == 0), stop=True, skip_group_check=True)
                        m.then_inc(S["conv_done"], 1)
                with pe.Fori(0, B) as b:
                    pe.wait_ge(S["xhat"], b + 2)
                    pe.wait_ge(S["gelu"], b + 1)
                    for j in range(4):
                        m = nc.tensor.matmul(psT[:, j * P:(j + 1) * P], xn4[:, j, :], flip[:], start=True, stop=True)
                    m.then_inc(S["turned"], 1)
                    pe.wait_ge(S["gelu"], b + 2)
                    pe.wait_ge(S["added"], 2 * b + 1)
                    for j in range(4):
                        o = psO[:, j * P:(j + 1) * P]
                        nc.tensor.matmul(o, ones1[:], bo[:], start=True, stop=False)
                        m = nc.tensor.matmul(o, gT[:, j * P:(j + 1) * P], wo[:], start=False, stop=True)
                    m.then_inc(S["out"], 1)
            @block.scalar
            def _(act):
                with act.Fori(0, P // GD // 2) as i:
                    for slot in range(2):
                        act.wait_ge(S["conv_done"], 2 * i + (slot + 3))
                        nc.scalar.activation(Y[:, :, bass.ds((2 * i + slot) * GD, GD)], conv[:, slot].rearrange("p (k t) -> p t k", k=GD), ACT.Copy).then_inc(S["conv_copied"], 1)
                with act.Fori(0, B) as b:
                    act.wait_ge(S["turned"], b + 2)
                    act.wait_ge(S["out"], b + 1)
                    nc.scalar.activation(gT[:], psT[:], ACT.Gelu, bias=lnp[:, 1:2], scale=lnp[:, 0:1]).then_inc(S["gelu"], 1)
            @block.vector
            def _(v):
                Yv = Y[:].rearrange("p (b j) c -> p b j c", b=B)
                Xv = X[:].rearrange("p (b j) c -> p b j c", b=B)
                v.wait_ge(S["conv_copied"], P // GD + 2)
                with v.Fori(0, B) as b:
                    for j in range(4):
                        m = nc.vector.bn_stats(st[:, j, :], Yv[:, b, j, :])
                    m.then_inc(S["bn"], 1)
                    v.wait_ge(S["bn"], b + 1)
                    v.sem_inc(S["passed"], 1)
                    for j in range(4):
                        m = nc.vector.bn_aggr(mv[:, j, :], st[:, j, :])
                    m.then_inc(S["aggr"], 1)
                    v.wait_ge(S["aggr"], b + 1)
                    v.wait_ge(S["rstd"], b + 1)
                    nc.vector.tensor_scalar(ve[:], mv[:, :, 1], 1e-5, None, ALU.add).then_inc(S["eps"], 1)
                    v.wait_ge(S["rstd"], b + 2)
                    v.wait_ge(S["turned"], b + 1)
                    for j in range(4):
                        m = nc.vector.tensor_scalar(xn4[:, j, :], Yv[:, b, j, :], mv[:, j, 0:1], rs[:, j:j + 1], ALU.subtract, ALU.mult)
                    m.then_inc(S["xhat"], 1)
                    v.wait_ge(S["out"], b + 2)
                    nc.vector.tensor_tensor(Xv[:, b], psO[:].rearrange("p (j c) -> p j c", j=4), Xv[:, b], ALU.add).then_inc(S["added"], 1)
                    v.wait_ge(S["added"], 2 * b + 2)
                    nc.vector.tensor_tensor(Xv[:, b], XF[:, b, 1:5, :], Xv[:, b], ALU.add).then_inc(S["added"], 1)
            @block.gpsimd
            def _(g):
                with g.Fori(0, B) as b:
                    g.wait_ge(S["xhat"], b + 1)
                    g.wait_ge(S["eps"], b + 1)
                    nc.gpsimd.tensor_tensor(rs[:], ve[:], mh[:], ALU.pow).then_inc(S["rstd"], 1)
        clear(nc, S.values())


AH, AD, PADH = 16, 8, 64
VPAD = 32
PARTS = 6 * AD
K_PARTS = {"h": (0, 3, 5), "m": (1, 4), "l": (2,)}
Q_PARTS = {"h": (0, 1, 2), "m": (3, 4), "l": (5,)}

def causal_attention(nc, X, XF, c, w, K):
    with ExitStack() as ctx:
        sb = lambda n, s, d=F32: ctx.enter_context(nc.sbuf_tensor("A" + n, s, d))
        ps = lambda n, s, d=F32: ctx.enter_context(nc.psum_tensor("A" + n, s, d))
        sem = lambda n: ctx.enter_context(nc.semaphore("A" + n))
        wcat = sb("wcat", [P, 384]); wu = sb("wu", [P, D]); hw = sb("hw", [P, 2, 2, AD])
        sd = sb("sd", [P, 4, 32]); nt = sb("nt", [P, 4, 32])
        tri = sb("tri", [P, 2, P], BF16); identb = sb("identb", [P, P], BF16)
        xb = sb("xb", [P, 4, D]); xT = sb("xT", [P, 512])
        s1 = sb("s1", [P, 4, 32]); cen = sb("cen", [P, 4, 32, AD]); sq = sb("sq", [P, 4, 32, AD]); vr = sb("vr", [P, 4, 32])
        kp = sb("kp", [P, 4, AH, PADH], BF16); qp = sb("qp", [P, 4, AH, PADH], BF16); nm = sb("nm", [P, 4, AH])
        kT = sb("kT", [P, 8, 512], BF16); qT = sb("qT", [P, 8, 512], BF16)
        Vp = sb("Vp", [P, 4, AH, VPAD]); OT = sb("OT", [P, 4, 512]); PT = sb("PT", [P, 2, 1536])
        rd = sb("rd", [P, 4, AH]); on = sb("on", [P, 4, AH, AD]); oT = sb("oT", [P, 512])
        psA = ps("psA", [P, 3072]); psB = ps("psB", [P, 1024])
        ident = c["ident"]
        S = {n: sem(n) for n in """loaded ones xb_ready x_turned xT_ready qkv_ready v_ready h_sum h_mean h_cen h_sq h_var h_eps h_dev h_newton h_rstd
          h_norm h_gain h_bias part_h rest_m part_m part_l repeated k_turned kT_ready q_turned qT_ready s_ready mx_done
          nm_h nm_m nm_parts q2_turned qT2_ready st_ready exp_done
          av_done o_kept ot_turned rd_ready on_ready o_turned oT_ready y_ready y_added""".split()}
        start_at_one(nc, S, "exp_done y_added mx_done x_turned av_done qkv_ready")
        with nc.Block() as block:
            @block.sync
            def _(sp):
                L = S["loaded"]
                for k, n in enumerate(("Wk", "Wq", "Wv")):
                    sp.dma_start(wcat[:, 128 * k:128 * k + 128], w[n + "T"]).then_inc(L, 16)
                sp.dma_start(wu[:], w["WuT"]).then_inc(L, 16)
                for k, n in enumerate(("kln", "qln")):
                    sp.dma_start(hw[:, k, 0, :], rows(w[n + "_w"])).then_inc(L, 16)
                    sp.dma_start(hw[:, k, 1, :], rows(w[n + "_b"])).then_inc(L, 16)
                sp.dma_start(tri[:], w["c_tri"]).then_inc(L, 16)
                sp.dma_start(identb[:], w["c_identb"]).then_inc(L, 16)
                sp.wait_ge(L, 160)
            @block.vector
            def _(v):
                nc.vector.memset(kp[:], 0.0)
                nc.vector.memset(qp[:], 0.0).then_inc(S["ones"], 1)
                nc.vector.memset(Vp[:], 0.0).then_inc(S["ones"], 1)
                v.wait_ge(S["ones"], 2)
                nc.vector.memset(Vp[:, :, :, AD:AD + 1], 1.0)
                nc.vector.memset(kp[:, :, :, PARTS:PARTS + 3], 1.0)
                v.wait_ge(S["loaded"], 160)
                nc.vector.tensor_scalar(hw[:, 1], hw[:, 1], float(AD) ** -0.5, None, ALU.mult)

        def lay(n):
            return {4: (0, 512), 3: (512, 384), 1: (896, 128), 2: (1024, 256)}[n]

        with nc.Block() as block:
            @block.sync
            def _(sp):
                load_and_store_kernels(sp, K)

            @block.gpsimd
            def _(g):
                build_kernels(nc, g, K)

            @block.tensor
            def _(pe):
                with pe.Fori(0, B) as b:
                    pe.wait_ge(S["xb_ready"], b + 1)
                    pe.wait_ge(S["exp_done"], b * 48 + 1)
                    for j in range(4):
                        m = nc.tensor.transpose(psA[:, j * P:(j + 1) * P], xb[:, j, :], ident[:])
                    m.then_inc(S["x_turned"], 1)
                    pe.wait_ge(S["xT_ready"], b + 1)
                    for j in range(4):
                        m = nc.tensor.matmul(psA[:, 512 * (j + 1):512 * (j + 1) + 384], xT[:, j * P:(j + 1) * P], wcat[:], start=True, stop=True)
                    m.then_inc(S["qkv_ready"], 1)
                    pe.wait_ge(S["v_ready"], b + 1)
                    pe.wait_ge(S["y_added"], b + 1)
                    pe.wait_ge(S["part_l"], 2 * b + 2)
                    pe.wait_ge(S["repeated"], b + 1)

                    def turn(src, half, turned):
                        for g in range(4 * half, 4 * half + 4):
                            tgt = psA[:, g * 512:g * 512 + 512] if g < 6 else psB[:, (g - 6) * 512:(g - 5) * 512]
                            for j in range(4):
                                m = nc.tensor.matmul(tgt[:, j * P:(j + 1) * P], src[:, j, 2 * g:2 * g + 2, :], identb[:], start=True, stop=True)
                        m.then_inc(S[turned], 1)

                    turn(kp, 0, "k_turned")
                    turn(kp, 1, "k_turned")
                    pe.wait_ge(S["kT_ready"], 2 * b + 2)
                    turn(qp, 0, "q_turned")
                    turn(qp, 1, "q_turned")
                    pe.wait_ge(S["qT_ready"], 2 * b + 2)
                    for h in range(AH):
                        r = slice(64 * (h % 2), 64 * (h % 2) + PARTS)
                        if h >= 2:
                            pe.wait_ge(S["mx_done"], b * AH + h)
                        for qi in range(4):
                            o, n = lay(qi + 1)
                            o += 1536 * (h % 2)
                            nc.tensor.matmul(psA[:, o:o + n], qT[r, h // 2, qi * P:(qi + 1) * P], kT[r, h // 2, 0:n], start=True, stop=True)
                            m = nc.tensor.matmul(psA[:, o + n - P:o + n], identb[:], tri[:, 0, :], start=False, stop=True, skip_group_check=True)
                        m.then_inc(S["s_ready"], 1)
                    pe.wait_ge(S["mx_done"], (b + 1) * AH + 1)
                    pe.wait_ge(S["nm_parts"], b + 1)
                    turn(qp, 0, "q2_turned")
                    turn(qp, 1, "q2_turned")
                    pe.wait_ge(S["qT2_ready"], 2 * b + 2)

                    def st(h):
                        r = slice(64 * (h % 2), 64 * (h % 2) + PARTS + 3)
                        if h >= 2:
                            pe.wait_ge(S["exp_done"], b * 48 + 3 * (h - 1) + 1)
                        for kj in range(4):
                            o, n = lay(4 - kj)
                            o += 1536 * (h % 2)
                            nc.tensor.matmul(psA[:, o:o + n], kT[r, h // 2, kj * P:(kj + 1) * P], qT[r, h // 2, kj * P:512], start=True, stop=True)
                            m = nc.tensor.matmul(psA[:, o:o + P], identb[:], tri[:, 1, :], start=False, stop=True, skip_group_check=True)
                        m.then_inc(S["st_ready"], 1)

                    def av(h):
                        g, r = h // 4, 32 * (h % 4)
                        pe.wait_ge(S["exp_done"], b * 48 + 3 * (h + 1) + 1)
                        if h % 4 == 0 and g >= 2:
                            pe.wait_ge(S["o_kept"], b * 4 + g - 1)
                        for kj in range(4):
                            o, n = lay(4 - kj)
                            m = nc.tensor.matmul(psB[r:r + 32, (g % 2) * 512 + kj * P:(g % 2) * 512 + 512], Vp[:, kj, h, :], PT[:, h % 2, o:o + n],
                                                 start=(kj == 0), stop=True, skip_group_check=True, tile_position=(0, r))
                        m.then_inc(S["av_done"], 1)

                    st(0)
                    for h in range(1, AH):
                        st(h)
                        av(h - 1)
                    av(AH - 1)
                    pe.wait_ge(S["o_kept"], b * 4 + 4)
                    for j in range(4):
                        for g in range(4):
                            m = nc.tensor.transpose(psA[:, j * 512 + g * P:j * 512 + (g + 1) * P], OT[:, g, j * P:(j + 1) * P], ident[:])
                    m.then_inc(S["ot_turned"], 1)
                    pe.wait_ge(S["on_ready"], b + 1)
                    for j in range(4):
                        m = nc.tensor.transpose(psB[:, j * P:(j + 1) * P], on[:, j], ident[:])
                    m.then_inc(S["o_turned"], 1)
                    pe.wait_ge(S["oT_ready"], b + 1)
                    for j in range(4):
                        m = nc.tensor.matmul(psB[:, 512 + j * P:512 + (j + 1) * P], oT[:, j * P:(j + 1) * P], wu[:], start=True, stop=True)
                    m.then_inc(S["y_ready"], 1)

            @block.scalar
            def _(act):
                with act.Fori(0, B) as b:
                    act.wait_ge(S["x_turned"], b + 1)
                    nc.scalar.activation(xb[:], XF[:, b, 1:5, :], ACT.Copy).then_inc(S["xb_ready"], 1)
                    act.wait_ge(S["h_cen"], b + 1)
                    nc.scalar.activation(sq[:], cen[:], ACT.Square).then_inc(S["h_sq"], 1)
                    act.wait_ge(S["av_done"], b * AH + 1)
                    nc.scalar.activation(Vp[:, :, :, 0:AD], psA[:, 512:2560].rearrange("p (j x) -> p j x", j=4)[:, :, 256:384].rearrange("p j (h d) -> p j h d", h=AH), ACT.Copy).then_inc(S["v_ready"], 1)
                    act.wait_ge(S["h_eps"], b + 1)
                    nc.scalar.activation(sd[:], vr[:], ACT.Sqrt).then_inc(S["h_dev"], 1)
                    for part, first in (("h", 0), ("m", 1)):
                        act.wait_ge(S["part_" + part], 2 * b + 2)
                        for t, where in ((kp, K_PARTS), (qp, Q_PARTS)):
                            k0 = where[part][0] * AD
                            for k in where[part][1:]:
                                m = nc.scalar.activation(t[:, :, :, k * AD:k * AD + AD], t[:, :, :, k0:k0 + AD], ACT.Copy)
                    m.then_inc(S["repeated"], 1)
                    for dst, turned, ready in ((kT, "k_turned", "kT_ready"), (qT, "q_turned", "qT_ready"), (qT, "q2_turned", "qT2_ready")):
                        act.wait_ge(S[turned], 2 * b + 1)
                        nc.scalar.activation(dst[:, 0:4].rearrange("p a b -> p (a b)"), psA[:, 0:2048], ACT.Copy).then_inc(S[ready], 1)
                    for h in range(AH):
                        act.wait_ge(S["st_ready"], b * AH + h + 1)
                        if h >= 2:
                            act.wait_ge(S["av_done"], b * AH + h)
                        for a, n in ((0, 512), (512, 512), (1024, 256)):
                            nc.scalar.activation(PT[:, h % 2, a:a + n], psA[:, 1536 * (h % 2) + a:1536 * (h % 2) + a + n], ACT.Exp).then_inc(S["exp_done"], 1)
                    act.wait_ge(S["o_turned"], b + 1)
                    nc.scalar.activation(oT[:], psB[:, 0:512], ACT.Copy).then_inc(S["oT_ready"], 1)

            @block.vector
            def _(v):
                with v.Fori(0, B) as b:
                    v.wait_ge(S["x_turned"], b + 2)
                    v.wait_ge(S["qkv_ready"], b + 1)
                    nc.vector.tensor_copy(xT[:], psA[:, 0:512]).then_inc(S["xT_ready"], 1)
                    v.wait_ge(S["qkv_ready"], b + 2)
                    kq = psA[:, 512:2560].rearrange("p (j x) -> p j x", j=4)[:, :, 0:256].rearrange("p j (h d) -> p j h d", d=AD)
                    nc.vector.tensor_reduce(s1[:], kq, AX.X, ALU.add).then_inc(S["h_sum"], 1)
                    v.wait_ge(S["h_sum"], b + 1)
                    nc.vector.tensor_scalar(s1[:], s1[:], -1.0 / AD, None, ALU.mult).then_inc(S["h_mean"], 1)
                    v.wait_ge(S["h_mean"], b + 1)
                    nc.vector.tensor_tensor(cen[:], kq, bcast(s1[:], 3, AD), ALU.add).then_inc(S["h_cen"], 1)
                    v.wait_ge(S["h_sq"], b + 1)
                    nc.vector.tensor_reduce(vr[:], sq[:], AX.X, ALU.add).then_inc(S["h_var"], 1)
                    v.wait_ge(S["h_var"], b + 1)
                    nc.vector.tensor_scalar(vr[:], vr[:], 1.0 / AD, 1e-5, ALU.mult, ALU.add).then_inc(S["h_eps"], 1)
                    v.wait_ge(S["h_dev"], b + 1)
                    nc.vector.reciprocal(sd[:], sd[:]).then_inc(S["h_newton"], 1)
                    v.wait_ge(S["h_newton"], 4 * b + 1)
                    nc.vector.tensor_tensor(nt[:], sd[:], sd[:], ALU.mult).then_inc(S["h_newton"], 1)
                    v.wait_ge(S["h_newton"], 4 * b + 2)
                    nc.vector.tensor_tensor(nt[:], nt[:], vr[:], ALU.mult).then_inc(S["h_newton"], 1)
                    v.wait_ge(S["h_newton"], 4 * b + 3)
                    nc.vector.tensor_scalar(nt[:], nt[:], -0.5, 1.5, ALU.mult, ALU.add).then_inc(S["h_newton"], 1)
                    v.wait_ge(S["h_newton"], 4 * b + 4)
                    nc.vector.tensor_tensor(sd[:], sd[:], nt[:], ALU.mult).then_inc(S["h_rstd"], 1)
                    v.wait_ge(S["h_rstd"], b + 1)
                    nc.vector.tensor_tensor(cen[:], cen[:], bcast(sd[:], 3, AD), ALU.mult).then_inc(S["h_norm"], 1)
                    v.wait_ge(S["h_norm"], b + 1)
                    for k in range(2):
                        x = cen[:, :, 16 * k:16 * k + 16, :]
                        nc.vector.tensor_tensor(x, x, bcast(bcast(hw[:, k, 0, :], 1, 16), 1, 4), ALU.mult).then_inc(S["h_gain"], 1)
                    for k in range(2):
                        v.wait_ge(S["h_gain"], 2 * b + k + 1)
                        x = cen[:, :, 16 * k:16 * k + 16, :]
                        nc.vector.tensor_tensor(x, x, bcast(bcast(hw[:, k, 1, :], 1, 16), 1, 4), ALU.add).then_inc(S["h_bias"], 1)
                    sides = [(cen[:, :, 0:16, :], kp, K_PARTS), (cen[:, :, 16:32, :], qp, Q_PARTS)]
                    block_of = lambda t, where, part: t[:, :, :, where[part][0] * AD:where[part][0] * AD + AD]
                    for k, (x, t, where) in enumerate(sides):
                        v.wait_ge(S["h_bias"], 2 * b + k + 1)
                        nc.vector.tensor_copy(block_of(t, where, "h"), x).then_inc(S["part_h"], 1)
                    for k, (x, t, where) in enumerate(sides):
                        v.wait_ge(S["part_h"], 2 * b + k + 1)
                        nc.vector.tensor_tensor(x, x, block_of(t, where, "h"), ALU.subtract).then_inc(S["rest_m"], 1)
                    for k, (x, t, where) in enumerate(sides):
                        v.wait_ge(S["rest_m"], 2 * b + k + 1)
                        nc.vector.tensor_copy(block_of(t, where, "m"), x).then_inc(S["part_m"], 1)
                    for k, (x, t, where) in enumerate(sides):
                        v.wait_ge(S["part_m"], 2 * b + k + 1)
                        nc.vector.tensor_tensor(block_of(t, where, "l"), x, block_of(t, where, "m"), ALU.subtract).then_inc(S["part_l"], 1)

                    def last_groups(dst, turned, ready):
                        v.wait_ge(S[turned], 2 * b + 2)
                        nc.vector.tensor_copy(dst[:, 4:6].rearrange("p a b -> p (a b)"), psA[:, 2048:3072])
                        nc.vector.tensor_copy(dst[:, 6:8].rearrange("p a b -> p (a b)"), psB[:]).then_inc(S[ready], 1)

                    last_groups(kT, "k_turned", "kT_ready")
                    last_groups(qT, "q_turned", "qT_ready")
                    for h in range(AH):
                        v.wait_ge(S["s_ready"], b * AH + h + 1)
                        for qi in range(4):
                            o, n = lay(qi + 1)
                            o += 1536 * (h % 2)
                            m = nc.vector.tensor_reduce(nm[:, qi, h:h + 1], psA[:, o:o + n], AX.X, ALU.max, negate=True)
                        m.then_inc(S["mx_done"], 1)
                    v.wait_ge(S["mx_done"], (b + 1) * AH + 1)
                    nc.vector.tensor_copy(qp[:, :, :, PARTS], nm[:]).then_inc(S["nm_h"], 1)
                    v.wait_ge(S["nm_h"], 2 * b + 1)
                    nc.vector.tensor_tensor(nm[:], nm[:], qp[:, :, :, PARTS], ALU.subtract).then_inc(S["nm_h"], 1)
                    v.wait_ge(S["nm_h"], 2 * b + 2)
                    nc.vector.tensor_copy(qp[:, :, :, PARTS + 1], nm[:]).then_inc(S["nm_m"], 1)
                    v.wait_ge(S["nm_m"], b + 1)
                    nc.vector.tensor_tensor(qp[:, :, :, PARTS + 2], nm[:], qp[:, :, :, PARTS + 1], ALU.subtract).then_inc(S["nm_parts"], 1)
                    last_groups(qT, "q2_turned", "qT2_ready")
                    for g in range(4):
                        v.wait_ge(S["av_done"], b * AH + 4 * (g + 1) + 1)
                        nc.vector.tensor_copy(OT[:, g], psB[:, (g % 2) * 512:(g % 2) * 512 + 512]).then_inc(S["o_kept"], 1)
                    v.wait_ge(S["ot_turned"], b + 1)
                    ov = psA[:, 0:2048].rearrange("p (j h d) -> p j h d", j=4, h=AH)
                    nc.vector.reciprocal(rd[:], ov[:, :, :, AD]).then_inc(S["rd_ready"], 1)
                    v.wait_ge(S["rd_ready"], b + 1)
                    nc.vector.tensor_tensor(on[:], ov[:, :, :, 0:AD], bcast(rd[:], 3, AD), ALU.mult).then_inc(S["on_ready"], 1)
                    v.wait_ge(S["y_ready"], b + 1)
                    xv = X[:].rearrange("p (b j) c -> p b j c", b=B)
                    nc.vector.tensor_tensor(xv[:, b], psB[:, 512:1024].rearrange("p (j c) -> p j c", j=4), xv[:, b], ALU.add).then_inc(S["y_added"], 1)

        clear(nc, S.values())


def attention_consts():
    a = np.arange(128)
    tri = np.zeros((128, 2, 128), np.float32)
    tri[:, 0] = np.where(a[None, :] > a[:, None], -1e30, 0)
    tri[:, 1] = np.where(a[:, None] > a[None, :], -1e30, 0)
    return {"c_tri": tri.astype("bfloat16")}


LAYERS, LH, LD, LW = 6, 16, 64, 32
INNER = LH * LD
FF = 341
FC = (114, 114, 113)

TILE_COUNTS = {n: 1 for n in """q_ready k_ready q_rot k_rot q_add k_add
    q_nrm k_nrm q_turned k_turned qT_ready kT_ready up_ready s_ready mx_ready d_ready exp_done den_ready rden_ready
    p_ready bd_ready o_ready x_added kept""".split()}
TILE_COUNTS.update(sq_done=2, ss_sum=2, ss_ready=2, rn_ready=2, u_ready=4, u_copied=4)

SEQUENCE_COUNTS = "half_copied shifted xs_ready xs_turned xsT_ready f_shift f_xs f_bn f_var f_rstd0 f_rstd f_xn f_turn f_xnT f_gate f_gelu f_a f_h f_out f_added f_half".split()

def local_layers(nc, XF, c, w):
    with ExitStack() as ctx:
        sb = lambda n, s, d=F32: ctx.enter_context(nc.sbuf_tensor("L" + n, s, d))
        ps = lambda n, s, d=F32: ctx.enter_context(nc.psum_tensor("L" + n, s, d))
        sem = lambda n: ctx.enter_context(nc.semaphore("L" + n))
        XA = sb("XA", [P, B, 5, D])
        wqk = sb("wqk", [P, 2048]); uw = sb("uw", [P, LH, D])
        trig = sb("trig", [P, 4, 4, LD]); tab = sb("tab", [P, 4, 4, LD]); scl = sb("scl", [P, 4, LD])
        mask = sb("mask", [P, 2, 512], BF16); identb = sb("identb", [P, P], BF16)
        shift = sb("shift", [P, 2, P]); mhalf = sb("mhalf", [P, 32])
        wv = sb("wv", [P, 1024]); wvT = sb("wvT", [P, 8, P]); wo = sb("wo", [P, 8, D])
        w1 = sb("w1", [P, 2 * FF]); w2 = sb("w2", [P, 3, D]); b1 = sb("b1", [P, 6])
        lng = sb("lng", [P, 2])
        xs = sb("xs", [P, 4, D]); xsT = sb("xsT", [P, 4, P])
        sq = sb("sq", [P, 2048]); ss = sb("ss", [P, 32]); rn = sb("rn", [P, 32])
        ra = sb("ra", [P, 2, 1024]); rb = sb("rb", [P, 2, 1024])
        qz = sb("qz", [P, 8, 4, 64]); kT = sb("kT", [P, 8, LW + P])
        U = sb("U", [P, 4, LH, D]); Up = sb("Up", [P, 4, 4, D])
        pr = sb("pr", [P, 2, LH, 64]); nmx = sb("nmx", [P, LH]); den = sb("den", [P, LH]); rden = sb("rden", [P, LH])
        BD = sb("BD", [P, LH, P]); BP = sb("BP", [P, 4, LW])
        psQ = ps("psQ", [P, 1024]); psK = ps("psK", [P, 1024]); psU = ps("psU", [P, 1024]); psT = ps("psT", [P, 512]); psO = ps("psO", [P, 512])
        xs4 = sq[:, 0:512].rearrange("p (j c) -> p j c", j=4); xn4 = sq[:, 512:1024].rearrange("p (j c) -> p j c", j=4)
        xnT = sq[:, 1024:1536]
        G = ra[:, :, :].rearrange("p a b -> p (a b)")[:, 0:1536].rearrange("p (a b) -> p a b", a=3)
        Hh = sb("Hh", [P, 3, 512])
        banks = [psQ[:, 0:512], psQ[:, 512:1024], psK[:, 0:512], psK[:, 512:1024], psU[:, 0:512], psU[:, 512:1024]]
        st = sb("st", [P, 4, 6]); mv = sb("mv", [P, 4, 2]); rs = sb("rs", [P, 4]); ve = sb("ve", [P, 4])
        ident = c["ident"]
        S = {n: sem(n) for n in """const_loaded zeroed w_loaded f_loaded wv_turned wvT_ready uw_summed uw_ready scl_tab
          half_copied shifted xs_ready xs_turned xsT_ready q_ready k_ready sq_done ss_ready ss_sum rn_ready
          q_rot k_rot q_add k_add q_nrm k_nrm u_ready u_copied q_turned k_turned qT_ready kT_ready up_ready s_ready mx_ready d_ready exp_done
          den_ready rden_ready p_ready bd_ready o_ready x_added kept
          f_shift f_xs f_bn f_var f_rstd0 f_rstd f_xn f_turn f_xnT f_gate f_gelu f_a f_h f_out f_added f_half passed""".split()}
        XFv, XAv = XF, XA

        with nc.Block() as block:
            @block.sync
            def _(sp):
                sp.dma_start(trig[:], w["c_trig"].rearrange("k (j p) d -> p k j d", p=P)).then_inc(S["const_loaded"], 16)
                sp.dma_start(mask[:], w["c_lmask"]).then_inc(S["const_loaded"], 16)
                sp.dma_start(identb[:], w["c_identb"]).then_inc(S["const_loaded"], 16)
                sp.dma_start(shift[:], w["c_shift"].rearrange("k p n -> p k n")).then_inc(S["const_loaded"], 16)
                sp.wait_ge(S["const_loaded"], 64)

            @block.vector
            def _(v):
                nc.vector.memset(XA[:, :, 0, :], 0.0)
                nc.vector.memset(kT[:, :, 0:LW], 0.0)
                nc.vector.memset(Up[:], 0.0)
                nc.vector.memset(qz[:], 0.0)
                nc.vector.memset(Hh[:], 1.0)
                nc.vector.memset(BD[:], 0.0).then_inc(S["zeroed"], 1)

            @block.gpsimd
            def _(g):
                nc.gpsimd.memset(mhalf[:], -0.5)

            @block.scalar
            def _(act):
                for n, per_tile in TILE_COUNTS.items():
                    act.sem_inc(S[n], 2 * per_tile)
                for n in SEQUENCE_COUNTS:
                    act.sem_inc(S[n], 1)

        def load_attention(sp, l):
            n = S["w_loaded"]
            Wq = w["Wqkv"]
            sp.dma_start(wqk[:], Wq[l, :, 0:2048]).then_inc(n, 16)
            sp.dma_start(wv[:], Wq[l, :, 2048:3072]).then_inc(n, 16)
            sp.dma_start(wo[:], w["Wo"][l].rearrange("(h p) c -> p h c", p=P)).then_inc(n, 16)
            for k, nm in ((0, "q_scale"), (2, "k_scale")):
                sp.dma_start(scl[:, k, :], rows(w[nm][l])).then_inc(n, 16)
                sp.dma_start(scl[:, k + 1, 0:32], rows(w[nm][l, 32:64])).then_inc(n, 16)
                sp.dma_start(scl[:, k + 1, 32:64], rows(w[nm][l, 0:32])).then_inc(n, 16)
            sp.wait_ge(n, l * (16 * 9) + 16 * 9)
            sp.sem_inc(S["passed"], 1)

        def load_feed_forward(sp, l):
            n = S["f_loaded"]
            sp.dma_start(w1[:], w["W1"][l]).then_inc(n, 16)
            sp.dma_start(w2[0:114, 0:2, :], w["W2"][l, 0:228, :].rearrange("(k p) c -> p k c", p=114)).then_inc(n, 16)
            sp.dma_start(w2[0:113, 2, :], w["W2"][l, 228:341, :]).then_inc(n, 16)
            for k in range(6):
                f0 = (k // 3) * FF + (k % 3) * 114
                nf = FC[k % 3]
                sp.dma_start(b1[0:nf, k:k + 1], w["b1"][l, f0:f0 + nf].unsqueeze(1)).then_inc(n, 16)
            sp.dma_start(w2[113:114, 2, :], w["b2"][l].unsqueeze(0)).then_inc(n, 16)
            sp.dma_start(lng[:, 0:1], w["ln_g"][l].unsqueeze(1)).then_inc(n, 16)
            sp.dma_start(lng[:, 1:2], w["ln_b"][l].unsqueeze(1)).then_inc(n, 16)
            sp.wait_ge(n, l * (16 * 12) + 16 * 12)
            sp.sem_inc(S["passed"], 1)

        with nc.Block() as block:
            @block.sync
            def _(sp):
                load_attention(sp, 0)

        with nc.Fori(0, LAYERS) as l:
            with nc.Block() as block:
                @block.tensor
                def _(pe):
                    for j in range(8):
                        m = nc.tensor.transpose(psQ[:, j * P:(j + 1) * P], wv[:, j * P:(j + 1) * P], ident[:])
                    m.then_inc(S["wv_turned"], 1)
                    pe.wait_ge(S["wvT_ready"], l + 1)
                    for h in range(LH):
                        r = slice(64 * (h % 2), 64 * (h % 2) + 64)
                        tgt = (psK if h % 2 else psU)[:, (h // 2) * P:(h // 2 + 1) * P]
                        m = nc.tensor.matmul(tgt, wvT[r, h // 2, :], wo[r, h // 2, :], start=True, stop=True)
                    m.then_inc(S["uw_summed"], 1)

                @block.vector
                def _(v):
                    v.wait_ge(S["wv_turned"], l + 1)
                    nc.vector.tensor_copy(wvT[:].rearrange("p a b -> p (a b)"), psQ[:]).then_inc(S["wvT_ready"], 1)
                    v.wait_ge(S["uw_summed"], l + 1)
                    uv = uw[:].rearrange("p (a two) c -> p two a c", two=2)
                    nc.vector.tensor_copy(uv[:, 0], psU[:].rearrange("p (a c) -> p a c", a=8))
                    nc.vector.tensor_copy(uv[:, 1], psK[:].rearrange("p (a c) -> p a c", a=8)).then_inc(S["uw_ready"], 1)

                @block.gpsimd
                def _(g):
                    for k in range(4):
                        nc.gpsimd.tensor_tensor(tab[:, k], trig[:, k], bcast(scl[:, k, :], 1, 4), ALU.mult).then_inc(S["scl_tab"], 1)

            count = lambda b, j: l * 32 + b * 4 + (j + 2)
            seq = lambda b: l * B + b + 1
            moved = lambda b, j, n: (b + (j + n) // 4, (j + n) % 4)
            with nc.Block() as block:
                @block.sync
                def _(sp):
                    load_feed_forward(sp, l)

                @block.tensor
                def _(pe):
                    def shift_in(b):
                        nc.tensor.matmul(psT[:, 0:256], shift[:, 0, :], XF[:, b, 1:5, 64:128], start=True, stop=False)
                        nc.tensor.matmul(psT[:, 0:256], shift[:, 1, :], XF[:, b, 0:4, 64:128], start=False, stop=True).then_inc(S["shifted"], 1)

                    def turn_x(q):
                        pe.wait_ge(S["half_copied"], q + 1)
                        pe.wait_ge(S["xs_ready"], q + 1)
                        for j in range(4):
                            m = nc.tensor.transpose(psT[:, j * P:(j + 1) * P], xs[:, j, :], ident[:])
                        m.then_inc(S["xs_turned"], 1)

                    def project_qk(i, j, q=None):
                        if j == 0:
                            pe.wait_ge(S["xsT_ready"], q + 1)
                        for s, psX, free, ready in ((0, psQ, "qT_ready", "q_ready"), (1, psK, "kT_ready", "k_ready")):
                            pe.wait_ge(S[free], i)
                            for n in range(2):
                                c0 = s * 1024 + n * 512
                                m = nc.tensor.matmul(psX[:, n * 512:(n + 1) * 512], xsT[:, j, :], wqk[:, c0:c0 + 512], start=True, stop=True)
                            m.then_inc(S[ready], 1)

                    def turn(i, s, psX, normed, turned):
                        pe.wait_ge(S[normed], i + 1)
                        for k in range(8):
                            m = nc.tensor.transpose(psX[:, k * P:(k + 1) * P], ra[:, s, k * P:(k + 1) * P], ident[:])
                        m.then_inc(S[turned], 1)

                    def project_u(i, j):
                        pe.wait_ge(S["d_ready"], i)
                        for n in range(4):
                            if n > 1:
                                pe.wait_ge(S["u_copied"], 4 * i + (n - 1))
                            nc.tensor.matmul(psU[:, (n % 2) * 512:(n % 2) * 512 + 512], xsT[:, j, :], uw[:, 4 * n:4 * n + 4, :], start=True, stop=True).then_inc(S["u_ready"], 1)

                    def scores(i, j):
                        pe.wait_ge(S["qT_ready"], i + 1)
                        pe.wait_ge(S["kT_ready"], i + 1)
                        pe.wait_ge(S["u_copied"], 4 * i + 4)
                        for a in range(2):
                            nc.tensor.matmul(psU[:, a * 512:(a + 1) * 512], identb[:], mask[:, 0 if j + a == 0 else 1, :], start=True, stop=True)
                            for hp in range(8):
                                for wp in range(2):
                                    wd = 2 * a + wp
                                    m = nc.tensor.matmul(psU[64 * wp:64 * wp + 64, a * 512 + hp * 64:a * 512 + hp * 64 + 64],
                                                         qz[:, hp, wd, :], kT[:, hp, 32 * wd:32 * wd + 64],
                                                         start=False, stop=True, skip_group_check=True)
                        m.then_inc(S["s_ready"], 1)

                    def mix(i, j):
                        pe.wait_ge(S["bd_ready"], i + 1)
                        pe.wait_ge(S["up_ready"], i)
                        pe.wait_ge(S["x_added"], i)
                        for k in range(LH):
                            nc.tensor.matmul(psO[:, 0:D], BD[:, k, :], U[:, j, (k % 8) * 2 + k // 8, :], start=(k == 0), stop=True, skip_group_check=True)
                        for k in range(4):
                            m = nc.tensor.matmul(psO[0:32, 0:D], BP[:, k, :], Up[:, (j + 3) % 4, k, :], start=False, stop=True, skip_group_check=True)
                        m.then_inc(S["o_ready"], 1)

                    def step(b, j, mixes=True, left=9):
                        i = count(b, j)
                        if left > 0:
                            project_qk(i + 1, (j + 1) % 4, seq(b + 1))
                        scores(i, j)
                        if mixes:
                            mix(i - 2, (j + 2) % 4)
                        if j == 1 and left > 3:
                            shift_in(b + 1)
                        if left > 0:
                            project_u(i + 1, (j + 1) % 4)
                            turn(i + 1, 0, psQ, "q_nrm", "q_turned")
                        if j == 2 and left > 3:
                            turn_x(seq(b + 1))
                        if left > 0:
                            turn(i + 1, 1, psK, "k_nrm", "k_turned")

                    i = count(0, 0)
                    shift_in(0)
                    turn_x(seq(0))
                    project_qk(i, 0, seq(0))
                    project_u(i, 0)
                    turn(i, 0, psQ, "q_nrm", "q_turned")
                    turn(i, 1, psK, "k_nrm", "k_turned")
                    for j in range(4):
                        step(0, j, mixes=(j > 1))
                    with pe.Fori(1, B - 1) as b:
                        for j in range(4):
                            step(b, j)
                    for j in range(4):
                        step(B - 1, j, left=3 - j)
                    mix(count(B - 1, 2), 2)
                    mix(count(B - 1, 3), 3)

                @block.scalar
                def _(act):
                    def half(b):
                        act.wait_ge(S["xs_turned"], seq(b))
                        nc.scalar.activation(xs[:, :, 0:64], XF[:, b, 1:5, 0:64], ACT.Copy).then_inc(S["half_copied"], 1)

                    def square(i, s, psX, ready):
                        act.wait_ge(S[ready], i + 1)
                        act.wait_ge(S["ss_ready"], 2 * i - (1 - s))
                        nc.scalar.activation(sq[:, s * 1024:(s + 1) * 1024], psX[:], ACT.Square).then_inc(S["sq_done"], 1)

                    def evacuate(i, j):
                        for n in range(4):
                            act.wait_ge(S["u_ready"], 4 * i + (n + 1))
                            nc.scalar.activation(U[:, j, 4 * n:4 * n + 4, :].rearrange("p a b -> p (a b)"), psU[:, (n % 2) * 512:(n % 2) * 512 + 512], ACT.Copy).then_inc(S["u_copied"], 1)
                        act.wait_ge(S["q_turned"], i + 1)
                        qv = psQ[:].rearrange("p (h w q) -> p h w q", h=8, w=4)
                        nc.scalar.activation(qz[0:64, :, :, 0:32], qv[0:64], ACT.Copy)
                        nc.scalar.activation(qz[64:128, :, :, 32:64], qv[64:128], ACT.Copy).then_inc(S["qT_ready"], 1)
                        act.wait_ge(S["k_turned"], i + 1)
                        act.wait_ge(S["kept"], i)
                        nc.scalar.activation(kT[:, :, LW:LW + P], psK[:].rearrange("p (a b) -> p a b", a=8), ACT.Copy).then_inc(S["kT_ready"], 1)

                    def step(b, j, left=9):
                        i = count(b, j)
                        if left > 0:
                            square(i + 1, 0, psQ, "q_ready")
                            square(i + 1, 1, psK, "k_ready")
                        act.wait_ge(S["s_ready"], i + 1)
                        nc.scalar.activation(kT[:, :, 0:LW], kT[:, :, P:P + LW], ACT.Copy).then_inc(S["kept"], 1)
                        act.wait_ge(S["u_copied"], 4 * i + 4)
                        for g in range(4):
                            h0 = 8 * (g % 2) + g // 2
                            m = nc.scalar.activation(Up[32 * g:32 * g + 32, j], U[96:128, j, h0:h0 + 7:2, :], ACT.Copy)
                        m.then_inc(S["up_ready"], 1)
                        act.wait_ge(S["d_ready"], i + 1)
                        nc.scalar.activation(pr[:, j % 2], pr[:, j % 2], ACT.Exp).then_inc(S["exp_done"], 1)
                        if j == 0 and left > 3:
                            half(b + 1)
                        if left > 0:
                            evacuate(i + 1, (j + 1) % 4)

                    i = count(0, 0)
                    half(0)
                    square(i, 0, psQ, "q_ready")
                    square(i, 1, psK, "k_ready")
                    evacuate(i, 0)
                    with act.Fori(0, B - 1) as b:
                        for j in range(4):
                            step(b, j)
                    for j in range(4):
                        step(B - 1, j, left=3 - j)

                @block.vector
                def _(v):
                    def shifted_half(b):
                        v.wait_ge(S["shifted"], seq(b) + 1)
                        v.wait_ge(S["xs_turned"], seq(b))
                        nc.vector.tensor_copy(xs[:, :, 64:128], psT[:, 0:256].rearrange("p (j c) -> p j c", j=4)).then_inc(S["xs_ready"], 1)

                    def turned_x(b):
                        v.wait_ge(S["xs_turned"], seq(b) + 1)
                        v.wait_ge(S["u_ready"], 4 * count(b, 0))
                        nc.vector.tensor_copy(xsT[:].rearrange("p j t -> p (j t)"), psT[:]).then_inc(S["xsT_ready"], 1)

                    def sum_squares(i, s):
                        v.wait_ge(S["sq_done"], 2 * i + (s + 1))
                        v.wait_ge(S["rn_ready"], 2 * i + (s - 1))
                        nc.vector.tensor_reduce(ss[:, 16 * s:16 * s + 16], sq[:, s * 1024:(s + 1) * 1024].rearrange("p (h d) -> p h d", d=LD), AX.X, ALU.add).then_inc(S["ss_sum"], 1)

                    def guard_squares(i, s):
                        v.wait_ge(S["ss_sum"], 2 * i + (s + 1))
                        nc.vector.tensor_scalar(ss[:, 16 * s:16 * s + 16], ss[:, 16 * s:16 * s + 16], 1e-24, None, ALU.max).then_inc(S["ss_ready"], 1)

                    def halves(t):
                        return t.rearrange("p (h d) -> p h d", h=LH)

                    def times_cos(i, j, s, psX, ready, turned):
                        v.wait_ge(S[ready], i + 1)
                        v.wait_ge(S["sq_done"], 2 * i + (s + 1))
                        v.wait_ge(S[turned], i)
                        nc.vector.tensor_tensor(halves(ra[:, s]), halves(psX[:]), bcast(tab[:, 2 * s, j, :], 1, LH), ALU.mult)

                    def times_sin(j, s, psX, rot):
                        x, Bb = halves(psX[:]), halves(rb[:, s])
                        nc.vector.tensor_tensor(Bb[:, :, 0:32], x[:, :, 32:64], bcast(tab[:, 2 * s + 1, j, 0:32], 1, LH), ALU.mult)
                        nc.vector.tensor_tensor(Bb[:, :, 32:64], x[:, :, 0:32], bcast(tab[:, 2 * s + 1, j, 32:64], 1, LH), ALU.mult).then_inc(S[rot], 1)

                    def rotated(i, s, rot, add):
                        v.wait_ge(S[rot], i + 1)
                        nc.vector.tensor_tensor(ra[:, s], ra[:, s], rb[:, s], ALU.add).then_inc(S[add], 1)

                    def rotate_q(i, j):
                        sum_squares(i, 0)
                        times_cos(i, j, 0, psQ, "q_ready", "q_turned")
                        guard_squares(i, 0)
                        times_sin(j, 0, psQ, "q_rot")
                        sum_squares(i, 1)
                        rotated(i, 0, "q_rot", "q_add")
                        guard_squares(i, 1)

                    def rotate_k(i, j):
                        times_cos(i, j, 1, psK, "k_ready", "k_turned")
                        times_sin(j, 1, psK, "k_rot")
                        rotated(i, 1, "k_rot", "k_add")

                    def add_x(b, j, i):
                        v.wait_ge(S["o_ready"], i + 1)
                        nc.vector.tensor_tensor(XA[:, b, j + 1, :], psO[:, 0:D], XF[:, b, j + 1, :], ALU.add).then_inc(S["x_added"], 1)

                    def turn_probs(i, j):
                        v.wait_ge(S["p_ready"], i + 1)
                        v.wait_ge(S["o_ready"], i)
                        for a in range(2):
                            for wp in range(2):
                                wd = 2 * a + wp
                                q = slice(32 * wd, 32 * wd + 32)
                                for par in range(2):
                                    r = slice(64 * wp + 32 * par, 64 * wp + 32 * par + 32)
                                    h = slice(8 * par, 8 * par + 8)
                                    src = pr[r, j % 2, 8 * a:8 * a + 8]
                                    nc.vector.transpose(BD[q, h, q], src[:, :, 32:64])
                                    if wd:
                                        nc.vector.transpose(BD[q.start - 32:q.start, h, q], src[:, :, 0:32])
                        for g in range(4):
                            m = nc.vector.transpose(BP[32 * g:32 * g + 32], pr[32 * (g // 2):32 * (g // 2) + 32, j % 2, 4 * (g % 2):4 * (g % 2) + 4, 0:32])
                        m.then_inc(S["bd_ready"], 1)

                    def step(b, j, turns=True, adds=True, left=9):
                        i = count(b, j)
                        if left > 0:
                            rotate_q(i + 1, (j + 1) % 4)
                        v.wait_ge(S["s_ready"], i + 1)
                        sv = psU[:].rearrange("p (h d) -> p h d", d=64)
                        nc.vector.tensor_reduce(nmx[:], sv, AX.X, ALU.max, negate=True).then_inc(S["mx_ready"], 1)
                        v.wait_ge(S["mx_ready"], i + 1)
                        v.wait_ge(S["bd_ready"], i - 1)
                        nc.vector.tensor_tensor(pr[:, j % 2], sv, bcast(nmx[:], 2, 64), ALU.add).then_inc(S["d_ready"], 1)
                        if left > 0:
                            rotate_k(i + 1, (j + 1) % 4)
                        if j == 1 and left > 3:
                            shifted_half(b + 1)
                        v.wait_ge(S["exp_done"], i + 1)
                        nc.vector.tensor_reduce(den[:], pr[:, j % 2], AX.X, ALU.add).then_inc(S["den_ready"], 1)
                        if j == 2 and left > 3:
                            turned_x(b + 1)
                        v.wait_ge(S["den_ready"], i + 1)
                        v.wait_ge(S["p_ready"], i)
                        nc.vector.reciprocal(rden[:], den[:]).then_inc(S["rden_ready"], 1)
                        if adds:
                            add_x(*moved(b, j, -2), i - 2)
                        if turns:
                            turn_probs(i - 1, j + 1)

                    i = count(0, 0)
                    shifted_half(0)
                    turned_x(0)
                    rotate_q(i, 0)
                    rotate_k(i, 0)
                    for j in range(4):
                        step(0, j, turns=(j > 0), adds=(j > 1))
                    with v.Fori(1, B - 1) as b:
                        for j in range(4):
                            step(b, j)
                    for j in range(4):
                        step(B - 1, j, left=3 - j)
                    i = count(B - 1, 3)
                    add_x(B - 1, 2, i - 1)
                    turn_probs(i, 3)
                    add_x(B - 1, 3, i)

                @block.gpsimd
                def _(g):
                    def unit(i, s, add, nrm):
                        g.wait_ge(S["ss_ready"], 2 * i + (s + 1))
                        nc.gpsimd.tensor_tensor(rn[:, 16 * s:16 * s + 16], ss[:, 16 * s:16 * s + 16], mhalf[:, 16 * s:16 * s + 16], ALU.pow).then_inc(S["rn_ready"], 1)
                        g.wait_ge(S["rn_ready"], 2 * i + (s + 1))
                        g.wait_ge(S[add], i + 1)
                        A = ra[:, s].rearrange("p (h d) -> p h d", h=LH)
                        nc.gpsimd.tensor_tensor(A, A, bcast(rn[:, 16 * s:16 * s + 16], 2, LD), ALU.mult).then_inc(S[nrm], 1)

                    def step(i, j, left=9):
                        if left > 0:
                            unit(i + 1, 0, "q_add", "q_nrm")
                            unit(i + 1, 1, "k_add", "k_nrm")
                        g.wait_ge(S["rden_ready"], i + 1)
                        nc.gpsimd.tensor_tensor(pr[:, j % 2], pr[:, j % 2], bcast(rden[:], 2, 64), ALU.mult).then_inc(S["p_ready"], 1)

                    i = count(0, 0)
                    unit(i, 0, "q_add", "q_nrm")
                    unit(i, 1, "k_add", "k_nrm")
                    with g.Fori(0, B - 1) as b:
                        for j in range(4):
                            step(count(b, j), j)
                    for j in range(4):
                        step(count(B - 1, j), j, left=3 - j)

            with nc.Block() as block:
                @block.sync
                def _(sp):
                    load_attention(sp, l + 1)

                @block.tensor
                def _(pe):
                    def shift_in(b):
                        nc.tensor.matmul(psT[:, 0:256], shift[:, 0, :], XA[:, b, 1:5, 64:128], start=True, stop=False)
                        nc.tensor.matmul(psT[:, 0:256], shift[:, 1, :], XA[:, b, 0:4, 64:128], start=False, stop=True).then_inc(S["f_shift"], 1)

                    def turn_x(q):
                        pe.wait_ge(S["f_xn"], q + 1)
                        for j in range(4):
                            m = nc.tensor.transpose(psT[:, j * P:(j + 1) * P], xn4[:, j, :], ident[:])
                        m.then_inc(S["f_turn"], 1)

                    def step(b, last=False):
                        q = seq(b)
                        pe.wait_ge(S["f_xnT"], q + 1)
                        if not last:
                            shift_in(b + 1)
                        pe.wait_ge(S["f_h"], q)
                        for s, nm in ((1, "f_gate"), (0, "f_a")):
                            for k in range(3):
                                f0 = s * FF + k * 114
                                m = nc.tensor.matmul(banks[s * 3 + k][0:FC[k], :], w1[:, f0:f0 + FC[k]], xnT, start=True, stop=True)
                            m.then_inc(S[nm], 1)
                        if not last:
                            turn_x(q + 1)
                        pe.wait_ge(S["f_h"], q + 1)
                        pe.wait_ge(S["f_added"], q)
                        for j in range(4):
                            o = psO[:, j * P:(j + 1) * P]
                            for k in range(3):
                                m = nc.tensor.matmul(o, Hh[0:114, k, j * P:(j + 1) * P], w2[0:114, k, :], start=(k == 0), stop=(k == 2))
                        m.then_inc(S["f_out"], 1)

                    shift_in(0)
                    turn_x(seq(0))
                    with pe.Fori(0, B - 1) as b:
                        step(b)
                    step(B - 1, last=True)

                @block.scalar
                def _(act):
                    def half(b):
                        act.wait_ge(S["f_bn"], seq(b))
                        act.wait_ge(S["f_xn"], seq(b))
                        nc.scalar.activation(xs4[:, :, 0:64], XA[:, b, 1:5, 0:64], ACT.Copy).then_inc(S["f_half"], 1)

                    def gain(q):
                        act.wait_ge(S["f_turn"], q + 1)
                        act.wait_ge(S["f_a"], q)
                        nc.scalar.activation(xnT, psT[:], ACT.Identity, bias=lng[:, 1:2], scale=lng[:, 0:1]).then_inc(S["f_xnT"], 1)

                    def step(b, last=False):
                        q = seq(b)
                        if not last:
                            half(b + 1)
                        act.wait_ge(S["f_gate"], q + 1)
                        act.wait_ge(S["f_h"], q)
                        for k in range(3):
                            m = nc.scalar.activation(G[0:FC[k], k, :], banks[3 + k][0:FC[k], :], ACT.Gelu, bias=b1[0:FC[k], 3 + k:4 + k])
                        m.then_inc(S["f_gelu"], 1)
                        if not last:
                            gain(q + 1)

                    half(0)
                    gain(seq(0))
                    with act.Fori(0, B - 1) as b:
                        step(b)
                    step(B - 1, last=True)

                @block.vector
                def _(v):
                    def normalise(b):
                        q = seq(b)
                        v.wait_ge(S["f_shift"], q + 1)
                        nc.vector.tensor_copy(xs4[:, :, 64:128], psT[:, 0:256].rearrange("p (j c) -> p j c", j=4)).then_inc(S["f_xs"], 1)
                        v.wait_ge(S["f_xs"], q + 1)
                        v.wait_ge(S["f_half"], q + 1)
                        for j in range(4):
                            m = nc.vector.bn_stats(st[:, j, :], xs4[:, j, :])
                        m.then_inc(S["f_bn"], 1)
                        v.wait_ge(S["f_bn"], q + 1)
                        v.sem_inc(S["passed"], 1)
                        for j in range(4):
                            m = nc.vector.bn_aggr(mv[:, j, :], st[:, j, :])
                        m.then_inc(S["f_var"], 1)
                        v.wait_ge(S["f_var"], q + 1)
                        v.wait_ge(S["f_rstd"], q)
                        nc.vector.tensor_scalar(ve[:], mv[:, :, 1], 1e-5, None, ALU.add).then_inc(S["f_rstd0"], 1)
                        v.wait_ge(S["f_rstd"], q + 1)
                        v.wait_ge(S["f_turn"], q)
                        for j in range(4):
                            m = nc.vector.tensor_scalar(xn4[:, j, :], xs4[:, j, :], mv[:, j, 0:1], rs[:, j:j + 1], ALU.subtract, ALU.mult)
                        m.then_inc(S["f_xn"], 1)

                    def add(b):
                        v.wait_ge(S["f_out"], seq(b) + 1)
                        nc.vector.tensor_tensor(XF[:, b, 1:5, :], psO[:].rearrange("p (j c) -> p j c", j=4), XA[:, b, 1:5, :], ALU.add).then_inc(S["f_added"], 1)

                    def step(b, first=False, last=False):
                        q = seq(b)
                        if not first:
                            add(b - 1)
                        if not last:
                            normalise(b + 1)
                        v.wait_ge(S["f_a"], q + 1)
                        v.wait_ge(S["f_gelu"], q + 1)
                        v.wait_ge(S["f_out"], q)
                        for k in range(3):
                            m = nc.vector.scalar_tensor_tensor(out=Hh[0:FC[k], k, :], in0=banks[k][0:FC[k], :], scalar=b1[0:FC[k], k:k + 1], in1=G[0:FC[k], k, :], op0=ALU.add, op1=ALU.mult)
                        m.then_inc(S["f_h"], 1)

                    normalise(0)
                    step(0, first=True)
                    with v.Fori(1, B - 1) as b:
                        step(b)
                    step(B - 1, last=True)
                    add(B - 1)

                @block.gpsimd
                def _(g):
                    with g.Fori(0, B) as b:
                        g.wait_ge(S["f_xn"], seq(b))
                        g.wait_ge(S["f_rstd0"], seq(b) + 1)
                        nc.gpsimd.tensor_tensor(rs[:], ve[:], mhalf[:, 0:4], ALU.pow).then_inc(S["f_rstd"], 1)
        clear(nc, S.values())


def local_layout(s):
    return {n: np.concatenate([s[n], s[n][:1]]) for n in ("Wqkv", "Wo", "q_scale", "k_scale")}


def local_consts():
    n = 512
    half = np.arange(0, LD, 2, dtype=np.float32)
    inv = (1.0 / (np.float32(10000.0) ** (half / LD))).astype(np.float32)
    t = np.arange(n, dtype=np.float32)
    fr = (t[:, None] * inv[None]).astype(np.float32)
    fr = np.concatenate([fr, fr], -1)
    base = ((half + np.float32(0.4 * LD)) / np.float32(1.4 * LD)).astype(np.float32)
    power = ((t - n // 2) / 16).astype(np.float32)
    sc = (base[None] ** power[:, None]).astype(np.float32)
    sc = np.concatenate([sc, sc], -1)
    cos, sin = np.cos(fr).astype(np.float32), np.sin(fr).astype(np.float32)
    sgn = np.concatenate([-np.ones(32), np.ones(32)]).astype(np.float32)
    inv_s = (1.0 / sc).astype(np.float32)
    trig = np.stack([8 * cos * sc, 8 * sin * sc * sgn, cos * inv_s, sin * inv_s * sgn]).astype(np.float32)
    m = np.zeros((128, 2, 8, 64), np.float32)
    q = np.arange(128) % 32
    for k in range(64):
        bad = (q < k - 32) | (q > k)
        m[:, :, :, k] = np.where(bad, -1e30, 0)[:, None, None]
    m[0:64, 0, :, 0:32] = -1e30
    sh = np.zeros((2, 128, 128), np.float32)
    sh[0, np.arange(127), np.arange(1, 128)] = 1
    sh[1, 127, 0] = 1
    return {"c_trig": trig, "c_lmask": m.reshape(128, 2, 512).astype("bfloat16"), "c_shift": sh,
            "c_identb": np.eye(128, dtype="bfloat16")}


E1, K1, F1, FQ = 8, 2, 408, 102

def top2_experts(nc, X, XF, c, w):
    with ExitStack() as ctx:
        sb = lambda n, s, d=F32: ctx.enter_context(nc.sbuf_tensor("E" + n, s, d))
        ps = lambda n, s, d=F32: ctx.enter_context(nc.psum_tensor("E" + n, s, d))
        sem = lambda n: ctx.enter_context(nc.semaphore("E" + n))
        up = sb("up", [P, E1, F1]); gp = sb("gp", [P, E1, F1]); dn = sb("dn", [FQ + 1, E1, 4, D])
        ub = sb("ub", [FQ, E1, 4]); gb = sb("gb", [FQ, E1, 4]);
        gw = sb("gw", [P, E1]); gbias = sb("gbias", [1, E1]); ones1 = sb("ones1", [1, P])
        before = sb("before", [P, E1, E1])
        xb = sb("xb", [P, 4, D]); xT = sb("xT", [P, 512])
        lg = sb("lg", [P, 4, E1]); mx = sb("mx", [P, 4]); sm = sb("sm", [P, 4]); sc = sb("sc", [P, 4, E1])
        gt = sb("gt", [P, 4, E1, E1]); eq = sb("eq", [P, 4, E1, E1]); rk = sb("rk", [P, 4, E1]); comb = sb("comb", [P, 4, E1])
        us = sb("us", [FQ, 2, 512]); hg = sb("hg", [FQ, 2, 512]); hs = sb("hs", [FQ + 1, 2, 4, 512])
        psUG = ps("psUG", [P, 2, 2, 512]); psT = ps("psT", [P, 512]); psR = ps("psR", [P, 512]); psO = ps("psO", [P, 2, 512])
        ident = c["ident"]
        S = {n: sem(n) for n in """loaded ones xb_ready turned xT_ready logits r_max r_sub r_exp r_sum r_rec r_score r_cmp r_eqm r_or r_rank
          r_sel r_tot r_inv comb_ready u_ready g_ready us_ready hg_ready hs_ready out_ready added""".split()}
        start_at_one(nc, S, "hg_ready added turned out_ready hs_ready")
        with nc.Block() as block:
            @block.sync
            def _(sp):
                L = S["loaded"]
                sp.dma_start(gw[:], w["gate_wT"]).then_inc(L, 16)
                sp.dma_start(gbias[:], w["gate_b"].unsqueeze(0)).then_inc(L, 16)
                sp.dma_start(before[:], w["c_before"]).then_inc(L, 16)
                for a, n in ((up, "up_wT"), (gp, "gp_wT")):
                    sp.dma_start(a[:], w[n].rearrange("e d f -> d e f")).then_inc(L, 16)
                sp.dma_start(dn[0:FQ].rearrange("p e k d -> p (e k) d"), w["down_wT"].rearrange("e (k p) d -> p (e k) d", p=FQ)).then_inc(L, 16)
                for a, n in ((ub, "up_b4"), (gb, "gp_b4")):
                    sp.dma_start(a[:], w[n]).then_inc(L, 16)
                sp.dma_start(dn[FQ:FQ + 1, :, 3, :], w["down_b"].unsqueeze(0)).then_inc(L, 16)
                sp.wait_ge(L, 144)
            @block.vector
            def _(v):
                nc.vector.memset(ones1[:], 1.0)
                nc.vector.memset(hs[:, :, 3, :], 1.0)

        def us_of(k): return us[:, k % 2, :]
        with nc.Block() as block:
            @block.tensor
            def _(pe):
                with pe.Fori(0, B) as b:
                    pe.wait_ge(S["xb_ready"], b + 1)
                    for j in range(4):
                        m = nc.tensor.transpose(psT[:, j * P:(j + 1) * P], xb[:, j, :], ident[:])
                    m.then_inc(S["turned"], 1)
                    pe.wait_ge(S["xT_ready"], b + 1)
                    for j in range(4):
                        nc.tensor.matmul(psR[:, 8 * j:8 * j + 8], ones1[:], gbias[:], start=True, stop=False)
                        m = nc.tensor.matmul(psR[:, 8 * j:8 * j + 8], xT[:, j * P:(j + 1) * P], gw[:], start=False, stop=True)
                    m.then_inc(S["logits"], 1)

                    def inner(e):
                        for k in range(4):
                            n = e * 4 + k
                            if n >= 2:
                                pe.wait_ge(S["hg_ready"], b * 32 + n)
                            else:
                                pe.wait_ge(S["hg_ready"], b * 32 + 1)
                            nc.tensor.matmul(psUG[0:FQ, n % 2, 0, :], up[:, e, k * FQ:(k + 1) * FQ], xT[:], start=True, stop=True).then_inc(S["u_ready"], 1)
                            nc.tensor.matmul(psUG[0:FQ, n % 2, 1, :], gp[:, e, k * FQ:(k + 1) * FQ], xT[:], start=True, stop=True).then_inc(S["g_ready"], 1)

                    def down(e):
                        pe.wait_ge(S["hs_ready"], b * 32 + 4 * (e + 1) + 1)
                        if e >= 2:
                            pe.wait_ge(S["added"], b * 8 + e)
                        else:
                            pe.wait_ge(S["added"], b * 8 + 1)
                        for j in range(4):
                            o = psO[:, e % 2, j * P:(j + 1) * P]
                            for k in range(4):
                                r = FQ + (k == 3)
                                m = nc.tensor.matmul(o, hs[0:r, e % 2, k, j * P:(j + 1) * P], dn[0:r, e, k, :], start=(k == 0), stop=(k == 3))
                        m.then_inc(S["out_ready"], 1)

                    inner(0)
                    for e in range(1, E1):
                        inner(e)
                        down(e - 1)
                    down(E1 - 1)

            @block.scalar
            def _(act):
                with act.Fori(0, B) as b:
                    act.wait_ge(S["turned"], b + 1)
                    nc.scalar.activation(xb[:], XF[:, b, 1:5, :], ACT.Copy).then_inc(S["xb_ready"], 1)
                    act.wait_ge(S["r_sub"], b + 1)
                    nc.scalar.activation(lg[:], lg[:], ACT.Exp).then_inc(S["r_exp"], 1)
                    for n in range(32):
                        act.wait_ge(S["u_ready"], b * 32 + n + 1)
                        if n < 2:
                            act.wait_ge(S["hg_ready"], b * 32 + 1)
                        else:
                            act.wait_ge(S["hg_ready"], b * 32 + n)
                        nc.scalar.activation(us[:, n % 2, :], psUG[0:FQ, n % 2, 0, :], ACT.Identity, bias=ub[:, n // 4, n % 4:n % 4 + 1]).then_inc(S["us_ready"], 1)
                        act.wait_ge(S["hg_ready"], b * 32 + n + 2)
                        if n // 4 >= 2:
                            act.wait_ge(S["out_ready"], b * 8 + n // 4)
                        nc.scalar.activation(hs[0:FQ, (n // 4) % 2, n % 4, :], hg[:, n % 2, :], ACT.Silu).then_inc(S["hs_ready"], 1)

            @block.vector
            def _(v):
                Xv = X[:].rearrange("p (b j) c -> p b j c", b=B)
                with v.Fori(0, B) as b:
                    v.wait_ge(S["turned"], b + 2)
                    v.wait_ge(S["out_ready"], b * 8 + 1)
                    nc.vector.tensor_copy(xT[:], psT[:]).then_inc(S["xT_ready"], 1)
                    v.wait_ge(S["logits"], b + 1)
                    lp = psR[:, 0:32].rearrange("p (j e) -> p j e", j=4)
                    nc.vector.tensor_reduce(mx[:], lp, AX.X, ALU.max, negate=True).then_inc(S["r_max"], 1)
                    v.wait_ge(S["r_max"], b + 1)
                    nc.vector.tensor_tensor(lg[:], lp, bcast(mx[:], 2, E1), ALU.add).then_inc(S["r_sub"], 1)
                    v.wait_ge(S["r_exp"], b + 1)
                    nc.vector.tensor_reduce(sm[:], lg[:], AX.X, ALU.add).then_inc(S["r_sum"], 1)
                    v.wait_ge(S["r_sum"], b + 1)
                    nc.vector.reciprocal(sm[:], sm[:]).then_inc(S["r_rec"], 1)
                    v.wait_ge(S["r_rec"], b + 1)
                    nc.vector.tensor_tensor(sc[:], lg[:], bcast(sm[:], 2, E1), ALU.mult).then_inc(S["r_score"], 1)
                    v.wait_ge(S["r_score"], b + 1)
                    for j in range(4):
                        other, own = bcast(sc[:, j, :], 1, E1), bcast(sc[:, j, :], 2, E1)
                        nc.vector.tensor_tensor(gt[:, j], other, own, ALU.is_gt)
                        m = nc.vector.tensor_tensor(eq[:, j], other, own, ALU.is_equal)
                    m.then_inc(S["r_cmp"], 1)
                    v.wait_ge(S["r_cmp"], b + 1)
                    nc.vector.tensor_tensor(eq[:], eq[:], bcast(before[:], 1, 4), ALU.mult).then_inc(S["r_eqm"], 1)
                    v.wait_ge(S["r_eqm"], b + 1)
                    nc.vector.tensor_tensor(gt[:], gt[:], eq[:], ALU.add).then_inc(S["r_or"], 1)
                    v.wait_ge(S["r_or"], b + 1)
                    nc.vector.tensor_reduce(rk[:], gt[:], AX.X, ALU.add).then_inc(S["r_rank"], 1)
                    v.wait_ge(S["r_rank"], b + 1)
                    nc.vector.scalar_tensor_tensor(out=sc[:], in0=rk[:], scalar=K1 - 0.5, in1=sc[:], op0=ALU.is_lt, op1=ALU.mult).then_inc(S["r_sel"], 1)
                    v.wait_ge(S["r_sel"], b + 1)
                    nc.vector.tensor_reduce(sm[:], sc[:], AX.X, ALU.add).then_inc(S["r_tot"], 1)
                    v.wait_ge(S["r_tot"], b + 1)
                    nc.vector.tensor_scalar(sm[:], sm[:], 1e-20, None, ALU.add).then_inc(S["r_inv"], 1)
                    v.wait_ge(S["r_inv"], 2 * b + 1)
                    nc.vector.reciprocal(sm[:], sm[:]).then_inc(S["r_inv"], 1)
                    v.wait_ge(S["r_inv"], 2 * b + 2)
                    nc.vector.tensor_tensor(comb[:], sc[:], bcast(sm[:], 2, E1), ALU.mult).then_inc(S["comb_ready"], 1)

                    def add(e):
                        v.wait_ge(S["out_ready"], b * 8 + e + 2)
                        if e == 0:
                            v.wait_ge(S["comb_ready"], b + 1)
                        if e:
                            v.wait_ge(S["added"], b * 8 + e + 1)
                        for j in range(4):
                            m = nc.vector.scalar_tensor_tensor(out=Xv[:, b, j], in0=psO[:, e % 2, j * P:(j + 1) * P], scalar=comb[:, j, e:e + 1], in1=Xv[:, b, j], op0=ALU.mult, op1=ALU.add)
                        m.then_inc(S["added"], 1)

                    for n in range(32):
                        v.wait_ge(S["us_ready"], b * 32 + n + 1)
                        v.wait_ge(S["g_ready"], b * 32 + n + 1)
                        if n < 2:
                            v.wait_ge(S["hs_ready"], b * 32 + 1)
                        else:
                            v.wait_ge(S["hs_ready"], b * 32 + n)
                        nc.vector.scalar_tensor_tensor(out=hg[:, n % 2, :], in0=psUG[0:FQ, n % 2, 1, :], scalar=gb[:, n // 4, n % 4:n % 4 + 1], in1=us[:, n % 2, :], op0=ALU.add, op1=ALU.mult).then_inc(S["hg_ready"], 1)
                        if n >= 8 and n % 4 == 3:
                            add(n // 4 - 2)
                    add(E1 - 2)
                    add(E1 - 1)
        clear(nc, S.values())


def top2_consts():
    a = np.arange(E1)
    return {"c_before": np.broadcast_to((a[None, :] < a[:, None]).astype(np.float32), (128, 8, 8)).copy()}

def top2_layout(w):
    return {"gate_wT": np.ascontiguousarray(w["gate_w"].T),
            "up_wT": np.ascontiguousarray(w["up_w"].transpose(0, 2, 1)), "gp_wT": np.ascontiguousarray(w["gp_w"].transpose(0, 2, 1)),
            "down_wT": np.ascontiguousarray(w["down_w"].transpose(0, 2, 1)),
            "up_b4": np.ascontiguousarray(w["up_b"].reshape(8, 4, FQ).transpose(2, 0, 1)), "gp_b4": np.ascontiguousarray(w["gp_b"].reshape(8, 4, FQ).transpose(2, 0, 1))}


NH, ND, NPAD, NW = 16, 8, 32, 8
KS = P + 2 * NW
QS = P + 2 * NPAD

def banded_attention(nc, X, XF, c, w):
    with ExitStack() as ctx:
        sb = lambda n, s, d=F32: ctx.enter_context(nc.sbuf_tensor("N" + n, s, d))
        ps = lambda n, s, d=F32: ctx.enter_context(nc.psum_tensor("N" + n, s, d))
        sem = lambda n: ctx.enter_context(nc.semaphore("N" + n))
        wqkv = sb("wqkv", [P, 384]); wp = sb("wp", [P, D]); bp = sb("bp", [1, D]); ones1 = sb("ones1", [1, P])
        mq = sb("mq", [P, 3, 2 * KS], BF16); mk = sb("mk", [P, 2 * QS], BF16); identb = sb("identb", [P, P], BF16)
        xb = sb("xb", [P, 4, D]); xT = sb("xT", [P, 512])
        kp = sb("kp", [P, 4, NH, PADH], BF16); qp = sb("qp", [P, 4, NH, PADH], BF16); nm = sb("nm", [P, 4, NH])
        kq = sb("kq", [P, 4, 2 * NH, ND])
        kT = sb("kT", [P, 8, 512 + 2 * NPAD], BF16); qT = sb("qT", [P, 8, 512 + 2 * NPAD], BF16)
        Vp = sb("Vp", [P, 4, NH, VPAD]); OT = sb("OT", [P, 4, 512]); PT = sb("PT", [P, 2, 4, 2, QS])
        rd = sb("rd", [P, 4, NH]); on = sb("on", [P, 4, NH, ND]); oT = sb("oT", [P, 512])
        psA = ps("psA", [P, 6, 512]); psB = ps("psB", [P, 1024])
        ident = c["ident"]
        S = {n: sem(n) for n in """loaded zeroed xb_ready x_turned xT_ready qkv_ready kq_copied v_ready part_h rest_m part_m part_l repeated k_turned kT_ready
          q_turned qT_ready s_ready mx_done nm_h nm_m nm_parts q2_turned qT2_ready st_ready exp_done
          av_done o_kept ot_turned rd_ready on_ready o_turned oT_ready y_ready y_added""".split()}
        start_at_one(nc, S, "exp_done y_added mx_done x_turned av_done qkv_ready")
        with nc.Block() as block:
            @block.sync
            def _(sp):
                L = S["loaded"]
                sp.dma_start(wqkv[:], w["Wqkv"]).then_inc(L, 16)
                sp.dma_start(wp[:], w["Wproj"]).then_inc(L, 16)
                sp.dma_start(bp[:], w["bproj"].unsqueeze(0)).then_inc(L, 16)
                sp.dma_start(mq[:], w["c_bandq"]).then_inc(L, 16)
                sp.dma_start(mk[:], w["c_bandk"]).then_inc(L, 16)
                sp.dma_start(identb[:], w["c_identb"]).then_inc(L, 16)
                sp.wait_ge(L, 96)
            @block.vector
            def _(v):
                nc.vector.memset(kp[:], 0.0)
                nc.vector.memset(qp[:], 0.0)
                nc.vector.memset(kT[:], 0.0)
                nc.vector.memset(qT[:], 0.0)
                nc.vector.memset(ones1[:], 1.0)
                nc.vector.memset(Vp[:], 0.0).then_inc(S["zeroed"], 1)
                v.wait_ge(S["zeroed"], 1)
                nc.vector.memset(kp[:, :, :, PARTS:PARTS + 3], 1.0)
                nc.vector.memset(Vp[:, :, :, ND:ND + 1], 1.0)

        def pair(n):
            return n % 2 + 4 * (n // 2), n % 2 + 4 * (n // 2) + 2

        with nc.Block() as block:
            @block.tensor
            def _(pe):
                with pe.Fori(0, B) as b:
                    pe.wait_ge(S["xb_ready"], b + 1)
                    pe.wait_ge(S["exp_done"], b * 32 + 1)
                    for j in range(4):
                        m = nc.tensor.transpose(psA[:, 0, j * P:(j + 1) * P], xb[:, j, :], ident[:])
                    m.then_inc(S["x_turned"], 1)
                    pe.wait_ge(S["xT_ready"], b + 1)
                    for j in range(4):
                        m = nc.tensor.matmul(psA[:, j + 1, 0:384], xT[:, j * P:(j + 1) * P], wqkv[:], start=True, stop=True)
                    m.then_inc(S["qkv_ready"], 1)
                    pe.wait_ge(S["v_ready"], b + 1)
                    pe.wait_ge(S["y_added"], b + 1)
                    pe.wait_ge(S["part_l"], 2 * b + 2)
                    pe.wait_ge(S["repeated"], b + 1)

                    def turn(src, half, turned):
                        for g in range(4 * half, 4 * half + 4):
                            tgt = psA[:, g, :] if g < 6 else psB[:, (g - 6) * 512:(g - 5) * 512]
                            for j in range(4):
                                m = nc.tensor.matmul(tgt[:, j * P:(j + 1) * P], src[:, j, 2 * g:2 * g + 2, :], identb[:], start=True, stop=True)
                        m.then_inc(S[turned], 1)

                    turn(kp, 0, "k_turned")
                    turn(kp, 1, "k_turned")
                    pe.wait_ge(S["kT_ready"], 2 * b + 2)
                    turn(qp, 0, "q_turned")
                    turn(qp, 1, "q_turned")
                    pe.wait_ge(S["qT_ready"], 2 * b + 2)
                    for n in range(32):
                        j = n // 8
                        if n >= 6:
                            pe.wait_ge(S["mx_done"], b * 32 + n - 4)
                        bank = psA[:, n % 6, :]
                        nc.tensor.matmul(bank[:, 0:2 * KS], identb[:], mq[:, (0, 1, 1, 2)[j], :], start=True, stop=True)
                        for a, h in enumerate(pair(n % 8)):
                            r = slice(64 * (h % 2), 64 * (h % 2) + PARTS)
                            k0 = NPAD + j * P - NW
                            m = nc.tensor.matmul(bank[:, a * KS:(a + 1) * KS], qT[r, h // 2, NPAD + j * P:NPAD + (j + 1) * P], kT[r, h // 2, k0:k0 + KS],
                                                 start=False, stop=True, skip_group_check=True)
                        m.then_inc(S["s_ready"], 1)
                    pe.wait_ge(S["mx_done"], (b + 1) * 32 + 1)
                    pe.wait_ge(S["nm_parts"], b + 1)
                    turn(qp, 0, "q2_turned")
                    turn(qp, 1, "q2_turned")
                    pe.wait_ge(S["qT2_ready"], 2 * b + 2)

                    def st(n):
                        hp, kj = n // 4, n % 4
                        if n >= 6:
                            pe.wait_ge(S["exp_done"], b * 32 + n - 4)
                        bank = psA[:, n % 6, 0:2 * QS]
                        nc.tensor.matmul(bank, identb[:], mk[:], start=True, stop=True)
                        for a, h in enumerate(pair(hp)):
                            r = slice(64 * (h % 2), 64 * (h % 2) + PARTS + 3)
                            m = nc.tensor.matmul(bank[:, a * QS:(a + 1) * QS], kT[r, h // 2, NPAD + kj * P:NPAD + (kj + 1) * P], qT[r, h // 2, kj * P:kj * P + QS],
                                                 start=False, stop=True, skip_group_check=True)
                        m.then_inc(S["st_ready"], 1)

                    def av(hp):
                        g = hp // 2
                        pe.wait_ge(S["exp_done"], b * 32 + 4 * (hp + 1) + 1)
                        if hp % 2 == 0 and g >= 2:
                            pe.wait_ge(S["o_kept"], b * 4 + g - 1)
                        for a, h in enumerate(pair(hp)):
                            r = 32 * (h % 4)
                            for kj in range(4):
                                q0, q1 = max(kj * P - NPAD, 0), min(kj * P + P + NPAD, 512)
                                s0 = q0 - (kj * P - NPAD)
                                m = nc.tensor.matmul(psB[r:r + 32, (g % 2) * 512 + q0:(g % 2) * 512 + q1], Vp[:, kj, h, :], PT[:, hp % 2, kj, a, s0:s0 + q1 - q0],
                                                     start=(kj == 0), stop=True, skip_group_check=True, tile_position=(0, r))
                        m.then_inc(S["av_done"], 1)

                    for n in range(32):
                        st(n)
                        if n >= 7 and n % 4 == 3:
                            av(n // 4 - 1)
                    av(7)
                    pe.wait_ge(S["o_kept"], b * 4 + 4)
                    for j in range(4):
                        for g in range(4):
                            m = nc.tensor.transpose(psA[:, j, g * P:(g + 1) * P], OT[:, g, j * P:(j + 1) * P], ident[:])
                    m.then_inc(S["ot_turned"], 1)
                    pe.wait_ge(S["on_ready"], b + 1)
                    for j in range(4):
                        m = nc.tensor.transpose(psB[:, j * P:(j + 1) * P], on[:, j], ident[:])
                    m.then_inc(S["o_turned"], 1)
                    pe.wait_ge(S["oT_ready"], b + 1)
                    for j in range(4):
                        o = psB[:, 512 + j * P:512 + (j + 1) * P]
                        nc.tensor.matmul(o, ones1[:], bp[:], start=True, stop=False)
                        m = nc.tensor.matmul(o, oT[:, j * P:(j + 1) * P], wp[:], start=False, stop=True)
                    m.then_inc(S["y_ready"], 1)

            @block.scalar
            def _(act):
                with act.Fori(0, B) as b:
                    act.wait_ge(S["x_turned"], b + 1)
                    nc.scalar.activation(xb[:], XF[:, b, 1:5, :], ACT.Copy).then_inc(S["xb_ready"], 1)
                    act.wait_ge(S["kq_copied"], b + 1)
                    nc.scalar.activation(Vp[:, :, :, 0:ND], psA[:, 1:5, 256:384].rearrange("p j (h d) -> p j h d", h=NH), ACT.Copy).then_inc(S["v_ready"], 1)
                    for part in ("h", "m"):
                        act.wait_ge(S["part_" + part], 2 * b + 2)
                        for t, where in ((kp, K_PARTS), (qp, Q_PARTS)):
                            k0 = where[part][0] * ND
                            for k in where[part][1:]:
                                m = nc.scalar.activation(t[:, :, :, k * ND:k * ND + ND], t[:, :, :, k0:k0 + ND], ACT.Copy)
                    m.then_inc(S["repeated"], 1)
                    for dst, turned, ready in ((kT, "k_turned", "kT_ready"), (qT, "q_turned", "qT_ready"), (qT, "q2_turned", "qT2_ready")):
                        act.wait_ge(S[turned], 2 * b + 1)
                        nc.scalar.activation(dst[:, 0:4, NPAD:NPAD + 512], psA[:, 0:4, :], ACT.Copy).then_inc(S[ready], 1)
                    for n in range(32):
                        act.wait_ge(S["st_ready"], b * 32 + n + 1)
                        if n // 4 >= 2:
                            act.wait_ge(S["av_done"], b * 8 + n // 4)
                        nc.scalar.activation(PT[:, (n // 4) % 2, n % 4], psA[:, n % 6, 0:2 * QS].rearrange("p (h q) -> p h q", h=2), ACT.Exp).then_inc(S["exp_done"], 1)
                    act.wait_ge(S["o_turned"], b + 1)
                    nc.scalar.activation(oT[:], psB[:, 0:512], ACT.Copy).then_inc(S["oT_ready"], 1)

            @block.vector
            def _(v):
                with v.Fori(0, B) as b:
                    v.wait_ge(S["x_turned"], b + 2)
                    v.wait_ge(S["qkv_ready"], b + 1)
                    nc.vector.tensor_copy(xT[:], psA[:, 0, :]).then_inc(S["xT_ready"], 1)
                    v.wait_ge(S["qkv_ready"], b + 2)
                    nc.vector.tensor_scalar(kq[:, :, NH:2 * NH, :], psA[:, 1:5, 0:128].rearrange("p j (h d) -> p j h d", h=NH), float(ND) ** -0.5, None, ALU.mult)
                    nc.vector.tensor_copy(kq[:, :, 0:NH, :], psA[:, 1:5, 128:256].rearrange("p j (h d) -> p j h d", h=NH)).then_inc(S["kq_copied"], 1)
                    v.wait_ge(S["kq_copied"], b + 1)
                    sides = [(kq[:, :, 0:NH, :], kp, K_PARTS), (kq[:, :, NH:2 * NH, :], qp, Q_PARTS)]
                    block_of = lambda t, where, part: t[:, :, :, where[part][0] * ND:where[part][0] * ND + ND]
                    for k, (x, t, where) in enumerate(sides):
                        nc.vector.tensor_copy(block_of(t, where, "h"), x).then_inc(S["part_h"], 1)
                    for k, (x, t, where) in enumerate(sides):
                        v.wait_ge(S["part_h"], 2 * b + k + 1)
                        nc.vector.tensor_tensor(x, x, block_of(t, where, "h"), ALU.subtract).then_inc(S["rest_m"], 1)
                    for k, (x, t, where) in enumerate(sides):
                        v.wait_ge(S["rest_m"], 2 * b + k + 1)
                        nc.vector.tensor_copy(block_of(t, where, "m"), x).then_inc(S["part_m"], 1)
                    for k, (x, t, where) in enumerate(sides):
                        v.wait_ge(S["part_m"], 2 * b + k + 1)
                        nc.vector.tensor_tensor(block_of(t, where, "l"), x, block_of(t, where, "m"), ALU.subtract).then_inc(S["part_l"], 1)

                    def last_groups(dst, turned, ready):
                        v.wait_ge(S[turned], 2 * b + 2)
                        nc.vector.tensor_copy(dst[:, 4:6, NPAD:NPAD + 512], psA[:, 4:6, :])
                        nc.vector.tensor_copy(dst[:, 6:8, NPAD:NPAD + 512], psB[:].rearrange("p (g t) -> p g t", g=2)).then_inc(S[ready], 1)

                    last_groups(kT, "k_turned", "kT_ready")
                    last_groups(qT, "q_turned", "qT_ready")
                    for n in range(32):
                        j, h0 = n // 8, pair(n % 8)[0]
                        v.wait_ge(S["s_ready"], b * 32 + n + 1)
                        nc.vector.tensor_reduce(nm[:, j, h0:h0 + 3:2], psA[:, n % 6, 0:2 * KS].rearrange("p (h k) -> p h k", h=2), AX.X, ALU.max, negate=True).then_inc(S["mx_done"], 1)
                    v.wait_ge(S["mx_done"], (b + 1) * 32 + 1)
                    nc.vector.tensor_copy(qp[:, :, :, PARTS], nm[:]).then_inc(S["nm_h"], 1)
                    v.wait_ge(S["nm_h"], 2 * b + 1)
                    nc.vector.tensor_tensor(nm[:], nm[:], qp[:, :, :, PARTS], ALU.subtract).then_inc(S["nm_h"], 1)
                    v.wait_ge(S["nm_h"], 2 * b + 2)
                    nc.vector.tensor_copy(qp[:, :, :, PARTS + 1], nm[:]).then_inc(S["nm_m"], 1)
                    v.wait_ge(S["nm_m"], b + 1)
                    nc.vector.tensor_tensor(qp[:, :, :, PARTS + 2], nm[:], qp[:, :, :, PARTS + 1], ALU.subtract).then_inc(S["nm_parts"], 1)
                    last_groups(qT, "q2_turned", "qT2_ready")
                    for g in range(4):
                        v.wait_ge(S["av_done"], b * 8 + 2 * (g + 1) + 1)
                        nc.vector.tensor_copy(OT[:, g], psB[:, (g % 2) * 512:(g % 2) * 512 + 512]).then_inc(S["o_kept"], 1)
                    v.wait_ge(S["ot_turned"], b + 1)
                    ov = psA[:, 0:4, :].rearrange("p j (h d) -> p j h d", d=VPAD)
                    nc.vector.reciprocal(rd[:], ov[:, :, :, ND]).then_inc(S["rd_ready"], 1)
                    v.wait_ge(S["rd_ready"], b + 1)
                    nc.vector.tensor_tensor(on[:], ov[:, :, :, 0:ND], bcast(rd[:], 3, ND), ALU.mult).then_inc(S["on_ready"], 1)
                    v.wait_ge(S["y_ready"], b + 1)
                    xv = X[:].rearrange("p (b j) c -> p b j c", b=B)
                    nc.vector.tensor_tensor(xv[:, b], psB[:, 512:1024].rearrange("p (j c) -> p j c", j=4), xv[:, b], ALU.add).then_inc(S["y_added"], 1)
        clear(nc, S.values())


def banded_consts():
    q = np.arange(P)[:, None]
    kk = np.arange(KS)[None] - NW
    near = np.where(np.abs(kk - q) <= NW, 0, -1e30)
    a = np.zeros((P, 3, 2, KS), np.float32)
    for t in range(3):
        m = near.copy()
        if t == 0:
            m[:, :NW] = -1e30
        if t == 2:
            m[:, KS - NW:] = -1e30
        a[:, t] = m[:, None]
    qq = np.arange(QS)[None] - NPAD
    k = np.where(np.abs(qq - q) <= NW, 0, -1e30)
    return {"c_bandq": a.reshape(P, 3, 2 * KS).astype("bfloat16"), "c_bandk": np.tile(k, 2).astype("bfloat16")}


E2, K2, HP2, CAP = 32, 8, 16, 256
LIMIT, ROUTED = 7.0, 2.5

def capped_experts(nc, X, XF, c, w):
    with ExitStack() as ctx:
        sb = lambda n, s, d=F32: ctx.enter_context(nc.sbuf_tensor("C" + n, s, d))
        ps = lambda n, s, d=F32: ctx.enter_context(nc.psum_tensor("C" + n, s, d))
        sem = lambda n: ctx.enter_context(nc.semaphore("C" + n))
        NP = HP2 + 2
        gw = sb("gw", [P, NP, P]); uw = sb("uw", [P, NP, P]); dw = sb("dw", [P, NP, D])
        rw = sb("rw", [P, E2]); bias = sb("bias", [P, E2]); spread = sb("spread", [E2, HP2, P])
        tri = sb("tri", [P, P], BF16); ones = sb("ones", [P, P], BF16); cum = sb("cum", [P, E2], BF16)
        xb = sb("xb", [P, 4, D]); xT = sb("xT", [P, 512])
        sc = sb("sc", [P, 4, E2]); sel = sb("sel", [P, 4, E2]); top = sb("top", [P, 4, 8]); rep = sb("rep", [P, 4, E2])
        mask = sb("mask", [P, 4, E2]); maskb = sb("maskb", [P, 4, E2], BF16); csum = sb("csum", [P, E2]); kept = sb("kept", [P, 4, E2]); sw = sb("sw", [P, 4, E2])
        tot = sb("tot", [P, 4]); comb = sb("comb", [P, 4, E2]); wT = sb("wT", [E2, 512])
        gs = sb("gs", [P, 2, 512]); us = sb("us", [P, 2, 512]); gl = sb("gl", [P, 2, 512]); hs = sb("hs", [P, 2, 512])
        psG = ps("psG", [P, 2, 512]); psU = ps("psU", [P, 2, 512]); psW = ps("psW", [P, 2, 512]); psT = ps("psT", [P, 512]); psO = ps("psO", [P, 512])
        ident = c["ident"]
        S = {n: sem(n) for n in """loaded ones xb_ready turned xT_ready logits score r_sel r_top r_rep r_mask r_maskb pos r_kept r_sw r_tot r_eps r_inv
          r_scale comb_ready comb_turned wT_ready r_csum r_cum g_ready u_ready w_ready g_min u_clip silu mixed h_ready out_ready added""".split()}
        start_at_one(nc, S, "added h_ready turned mixed out_ready silu")
        with nc.Block() as block:
            @block.sync
            def _(sp):
                L = S["loaded"]
                for a, n in ((gw, "gate"), (uw, "up")):
                    sp.dma_start(a[:, 0:HP2, :], w[n + "_pairs"]).then_inc(L, 16)
                    sp.dma_start(a[:, HP2:NP, :], w["shared_" + n + "T"].rearrange("d (k p) -> d k p", k=2)).then_inc(L, 16)
                sp.dma_start(dw[:, 0:HP2, :], w["down_pairs"].rearrange("k p d -> p k d")).then_inc(L, 16)
                sp.dma_start(dw[:, HP2:NP, :], w["shared_downT"].rearrange("(k p) d -> p k d", k=2)).then_inc(L, 16)
                sp.dma_start(rw[:], w["router_weightT"]).then_inc(L, 16)
                sp.dma_start(bias[:], rows(w["e_score_correction_bias"])).then_inc(L, 16)
                sp.dma_start(spread[:], w["c_spread"]).then_inc(L, 16)
                sp.dma_start(tri[:], w["c_earlier"]).then_inc(L, 16)
                sp.wait_ge(L, 160)
            @block.vector
            def _(v):
                nc.vector.memset(ones[:], 1.0)
                nc.vector.memset(cum[:], 0.0)

        with nc.Block() as block:
            @block.tensor
            def _(pe):
                with pe.Fori(0, B) as b:
                    pe.wait_ge(S["xb_ready"], b + 1)
                    pe.wait_ge(S["added"], b + 1)
                    for j in range(4):
                        m = nc.tensor.transpose(psT[:, j * P:(j + 1) * P], xb[:, j, :], ident[:])
                    m.then_inc(S["turned"], 1)
                    pe.wait_ge(S["xT_ready"], b + 1)
                    for j in range(4):
                        m = nc.tensor.matmul(psT[:, E2 * j:E2 * j + E2], xT[:, j * P:(j + 1) * P], rw[:], start=True, stop=True)
                    m.then_inc(S["logits"], 1)
                    pe.wait_ge(S["r_maskb"], b + 1)
                    pe.wait_ge(S["score"], b + 1)
                    for j in range(4):
                        o = psO[:, E2 * j:E2 * j + E2]
                        nc.tensor.matmul(o, tri[:], maskb[:, j, :], start=True, stop=False)
                        for k in range(j):
                            nc.tensor.matmul(o, ones[:], maskb[:, k, :], start=False, stop=False)
                        m = nc.tensor.matmul(o, ones[:], cum[:], start=False, stop=True)
                    m.then_inc(S["pos"], 1)
                    pe.wait_ge(S["comb_ready"], b + 1)
                    for j in range(4):
                        m = nc.tensor.transpose(psT[0:E2, j * P:(j + 1) * P], comb[:, j, :], ident[:])
                    m.then_inc(S["comb_turned"], 1)
                    pe.wait_ge(S["wT_ready"], b + 1)

                    def inner(n):
                        q = n % 2
                        if n >= 2:
                            pe.wait_ge(S["h_ready"], b * NP + n)
                        else:
                            pe.wait_ge(S["h_ready"], b * NP + 1)
                        nc.tensor.matmul(psG[:, q, :], gw[:, n, :], xT[:], start=True, stop=True).then_inc(S["g_ready"], 1)
                        nc.tensor.matmul(psU[:, q, :], uw[:, n, :], xT[:], start=True, stop=True).then_inc(S["u_ready"], 1)
                        if n < HP2:
                            nc.tensor.matmul(psW[:, q, :], spread[:, n, :], wT[:], start=True, stop=True).then_inc(S["w_ready"], 1)

                    def down(n):
                        pe.wait_ge(S["h_ready"], b * NP + n + 2)
                        for j in range(4):
                            m = nc.tensor.matmul(psO[:, j * P:(j + 1) * P], hs[:, n % 2, j * P:(j + 1) * P], dw[:, n, :],
                                                 start=(n == 0 and j == 0), stop=True, skip_group_check=True)
                        m.then_inc(S["out_ready"], 1)

                    inner(0)
                    inner(1)
                    for n in range(2, NP):
                        inner(n)
                        down(n - 2)
                    down(NP - 2)
                    down(NP - 1)

            @block.scalar
            def _(act):
                with act.Fori(0, B) as b:
                    act.wait_ge(S["turned"], b + 1)
                    nc.scalar.activation(xb[:], XF[:, b, 1:5, :], ACT.Copy).then_inc(S["xb_ready"], 1)
                    act.wait_ge(S["logits"], b + 1)
                    nc.scalar.activation(sc[:], psT[:, 0:4 * E2].rearrange("p (j e) -> p j e", j=4), ACT.Sigmoid).then_inc(S["score"], 1)
                    act.wait_ge(S["comb_turned"], b + 1)
                    nc.scalar.activation(wT[:], psT[0:E2, :], ACT.Copy).then_inc(S["wT_ready"], 1)
                    for n in range(NP):
                        q = n % 2
                        if n < HP2:
                            act.wait_ge(S["g_min"], b * HP2 + n + 1)
                            if n >= 2:
                                act.wait_ge(S["mixed"], b * HP2 + n)
                            nc.scalar.activation(gl[:, q, :], gs[:, q, :], ACT.Silu).then_inc(S["silu"], 1)
                        else:
                            act.wait_ge(S["g_ready"], b * NP + n + 1)
                            act.wait_ge(S["mixed"], 1 + (b * HP2 + n - 1 if n == HP2 else b * HP2 + HP2))
                            nc.scalar.activation(gl[:, q, :], psG[:, q, :], ACT.Silu).then_inc(S["silu"], 1)

            @block.gpsimd
            def _(g):
                with g.Fori(0, B) as b:
                    for n in range(HP2):
                        g.wait_ge(S["silu"], b * NP + n + 2)
                        g.wait_ge(S["u_clip"], b * HP2 + n + 1)
                        nc.gpsimd.tensor_tensor(us[:, n % 2, :], us[:, n % 2, :], gl[:, n % 2, :], ALU.mult).then_inc(S["mixed"], 1)

            @block.vector
            def _(v):
                Xv = X[:].rearrange("p (b j) c -> p b j c", b=B)
                with v.Fori(0, B) as b:
                    v.wait_ge(S["turned"], b + 2)
                    nc.vector.tensor_copy(xT[:], psT[:]).then_inc(S["xT_ready"], 1)
                    v.wait_ge(S["score"], b + 1)
                    nc.vector.tensor_tensor(sel[:], sc[:], bcast(bias[:], 1, 4), ALU.add).then_inc(S["r_sel"], 1)
                    v.wait_ge(S["r_sel"], b + 1)
                    v.sem_inc(S["ones"], 1)
                    for j in range(4):
                        m = nc.vector.max(top[:, j, :], sel[:, j, :])
                    m.then_inc(S["r_top"], 1)
                    v.wait_ge(S["r_top"], b + 1)
                    v.sem_inc(S["ones"], 1)
                    for j in range(4):
                        m = nc.vector.match_replace(rep[:, j, :], top[:, j, :], sel[:, j, :], -3e38)
                    m.then_inc(S["r_rep"], 1)
                    v.wait_ge(S["r_rep"], b + 1)
                    nc.vector.tensor_tensor(mask[:], sel[:], rep[:], ALU.not_equal).then_inc(S["r_mask"], 1)
                    v.wait_ge(S["r_mask"], b + 1)
                    nc.vector.tensor_copy(maskb[:], mask[:]).then_inc(S["r_maskb"], 1)
                    nc.vector.tensor_tensor(sw[:], sc[:], mask[:], ALU.mult).then_inc(S["r_sw"], 1)
                    v.wait_ge(S["r_sw"], b + 1)
                    nc.vector.tensor_reduce(tot[:], sw[:], AX.X, ALU.add).then_inc(S["r_tot"], 1)
                    v.wait_ge(S["r_tot"], b + 1)
                    nc.vector.tensor_scalar(tot[:], tot[:], 1e-20, None, ALU.add).then_inc(S["r_eps"], 1)
                    v.wait_ge(S["r_eps"], b + 1)
                    nc.vector.reciprocal(tot[:], tot[:]).then_inc(S["r_inv"], 1)
                    v.wait_ge(S["r_inv"], b + 1)
                    nc.vector.tensor_tensor(sw[:], sw[:], bcast(tot[:], 2, E2), ALU.mult).then_inc(S["r_scale"], 1)
                    v.wait_ge(S["pos"], b + 1)
                    v.wait_ge(S["r_scale"], b + 1)
                    nc.vector.scalar_tensor_tensor(out=kept[:], in0=psO[:, 0:4 * E2].rearrange("p (j e) -> p j e", j=4), scalar=CAP - 0.5, in1=sw[:], op0=ALU.is_lt, op1=ALU.mult).then_inc(S["r_kept"], 1)
                    v.wait_ge(S["r_kept"], b + 1)
                    nc.vector.tensor_scalar(comb[:], kept[:], ROUTED, None, ALU.mult).then_inc(S["comb_ready"], 1)
                    nc.vector.tensor_reduce(csum[:], mask[:].rearrange("p j e -> p e j"), AX.X, ALU.add).then_inc(S["r_csum"], 1)
                    v.wait_ge(S["r_csum"], b + 1)
                    nc.vector.tensor_tensor(cum[:], cum[:], csum[:], ALU.add).then_inc(S["r_cum"], 1)
                    def mix(n):
                        q = n % 2
                        if n < HP2:
                            v.wait_ge(S["mixed"], b * HP2 + n + 2)
                            v.wait_ge(S["w_ready"], b * HP2 + n + 1)
                            if n >= 2:
                                v.wait_ge(S["out_ready"], b * NP + n)
                            nc.vector.tensor_tensor(hs[:, q, :], psW[:, q, :], us[:, q, :], ALU.mult).then_inc(S["h_ready"], 1)
                        else:
                            v.wait_ge(S["silu"], b * NP + n + 2)
                            v.wait_ge(S["u_ready"], b * NP + n + 1)
                            v.wait_ge(S["out_ready"], b * NP + n)
                            nc.vector.tensor_tensor(hs[:, q, :], psU[:, q, :], gl[:, q, :], ALU.mult).then_inc(S["h_ready"], 1)

                    for n in range(NP):
                        q = n % 2
                        if n < HP2:
                            v.wait_ge(S["g_ready"], b * NP + n + 1)
                            if n >= 2:
                                v.wait_ge(S["silu"], b * NP + n)
                            nc.vector.tensor_scalar(gs[:, q, :], psG[:, q, :], LIMIT, None, ALU.min).then_inc(S["g_min"], 1)
                            v.wait_ge(S["u_ready"], b * NP + n + 1)
                            v.wait_ge(S["h_ready"], 1 + (b * NP + (n - 1 if n >= 2 else 0)))
                            nc.vector.tensor_scalar(us[:, q, :], psU[:, q, :], LIMIT, -LIMIT, ALU.min, ALU.max).then_inc(S["u_clip"], 1)
                        if n >= 1:
                            mix(n - 1)
                    mix(NP - 1)
                    v.wait_ge(S["out_ready"], (b + 1) * NP + 1)
                    nc.vector.tensor_tensor(Xv[:, b], psO[:].rearrange("p (j c) -> p j c", j=4), Xv[:, b], ALU.add).then_inc(S["added"], 1)
        clear(nc, S.values())


def capped_consts():
    a = np.arange(P)
    s = np.zeros((E2, HP2, P), np.float32)
    for p in range(HP2):
        s[2 * p, p, 0:64] = 1
        s[2 * p + 1, p, 64:] = 1
    return {"c_spread": s, "c_earlier": (a[:, None] < a[None, :]).astype("bfloat16")}

def capped_layout(w):
    gu, t = w["gate_up_proj"], np.ascontiguousarray
    pairs = lambda x: t(x.reshape(HP2, 2, 64, 128).transpose(3, 0, 1, 2).reshape(128, HP2, 128))
    return {"gate_pairs": pairs(gu[:, :64]), "up_pairs": pairs(gu[:, 64:]),
            "down_pairs": t(w["down_proj"].transpose(0, 2, 1).reshape(HP2, 128, 128)),
            "shared_gateT": t(w["shared_gate"].T), "shared_upT": t(w["shared_up"].T), "shared_downT": t(w["shared_down"].T),
            "router_weightT": t(w["router_weight"].T)}


QI, QB = 352, 16
ROWS4 = 88
QSTEPS = 12
DOWN = ((0, 128), (128, 128), (256, 96))

def fp4(nc, v, step, src, out, t, signs_of, signs_ready):
    p, nb = src.shape[0], src.shape[1]
    am, xn, ab, hi, lo = (t[k][0:p, 0:nb] for k in ("am", "xn", "ab", "hi", "lo"))
    rc = t["rc"][0:p, 0:nb]
    step(nc.vector.tensor_reduce(am, src, AX.X, ALU.max, apply_absolute_value=True))
    step(nc.vector.tensor_scalar(am, am, 1.0 / 6.0, 1e-12, ALU.mult, ALU.max))
    step(nc.vector.reciprocal(rc, am))
    step(nc.vector.tensor_tensor(xn, src, bcast(rc, 2, QB), ALU.mult))
    signs_of()
    step(nc.vector.scalar_tensor_tensor(out=ab, in0=xn, scalar=-1.0, in1=xn, op0=ALU.mult, op1=ALU.max))
    nc.vector.tensor_scalar(hi, ab, 5.0, 2.0, ALU.is_gt, ALU.mult)
    step(nc.vector.tensor_scalar(lo, ab, 0.25, None, ALU.is_gt))
    nc.vector.scalar_tensor_tensor(out=hi, in0=ab, scalar=3.5, in1=hi, op0=ALU.is_gt, op1=ALU.add)
    step(nc.vector.scalar_tensor_tensor(out=lo, in0=ab, scalar=0.75, in1=lo, op0=ALU.is_gt, op1=ALU.add))
    nc.vector.scalar_tensor_tensor(out=hi, in0=ab, scalar=2.5, in1=hi, op0=ALU.is_gt, op1=ALU.add)
    step(nc.vector.scalar_tensor_tensor(out=lo, in0=ab, scalar=1.25, in1=lo, op0=ALU.is_gt, op1=ALU.add))
    step(nc.vector.scalar_tensor_tensor(out=lo, in0=ab, scalar=1.75, in1=lo, op0=ALU.is_gt, op1=ALU.add))
    step(nc.vector.scalar_tensor_tensor(out=lo, in0=lo, scalar=0.5, in1=hi, op0=ALU.mult, op1=ALU.add))
    signs_ready()
    step(nc.vector.tensor_tensor(lo, lo, t["sg"][0:p, 0:nb], ALU.mult))
    step(nc.vector.tensor_tensor(out, lo, bcast(am, 2, QB), ALU.mult))

def fp4_ffn(nc, X, XF, c, w):
    with ExitStack() as ctx:
        sb = lambda n, s, d=F32: ctx.enter_context(nc.sbuf_tensor("F" + n, s, d))
        ps = lambda n, s, d=F32: ctx.enter_context(nc.psum_tensor("F" + n, s, d))
        sem = lambda n: ctx.enter_context(nc.semaphore("F" + n))
        raw = sb("raw", [P, 3, 32, QB])
        wq = sb("wq", [P, 3, 32, QB])
        gT = sb("gT", [P, QI]); uT = sb("uT", [P, QI]); dT = sb("dT", [P, 3, D])
        t = {k: sb(k, [P, 44, QB]) for k in ("xn", "ab", "hi", "lo", "sg")}
        t.update({k: sb(k, [P, 44]) for k in ("am", "rc")})
        xq = sb("xq", [P, 32, QB]); xqT = sb("xqT", [P, 512])
        sl = sb("sl", [P, 2, QI]); h = sb("h", [P, 44, QB]); hq = sb("hq", [P, 44, QB]); hT = sb("hT", [P, 2, 3, P])
        psT = ps("psT", [P, 512]); psG = ps("psG", [P, 2, 512]); psU = ps("psU", [P, 2, 512]); psH = ps("psH", [P, 2, 512]); psO = ps("psO", [P, 512])
        ident = c["ident"]
        S = {n: sem(n) for n in """loaded wsteps wxn wsign wquant wturned wcopied steps xn sign xq_ready x_turned xT_ready g_ready u_ready
          silu h_ready hq_ready h_turned hT_ready out added""".split()}
        start_at_one(nc, S, "wcopied h_ready added out x_turned u_ready h_turned")
        NBW = (32, 32, 22)

        def wsrc(k): return raw[0:ROWS4, k] if k < 2 else raw[:, 2, 0:22]
        def wdst(k): return wq[0:ROWS4, k] if k < 2 else wq[:, 2, 0:22]
        with nc.Block() as block:
            @block.sync
            def _(sp):
                L = S["loaded"]
                for k, n in enumerate(("w_gate", "w_up")):
                    sp.dma_start(raw[0:ROWS4, k].rearrange("p (a b) c -> p a (b c)", a=4), w[n].rearrange("(a p) c -> p a c", p=ROWS4)).then_inc(L, 16)
                sp.dma_start(raw[:, 2, 0:22].rearrange("p b c -> p (b c)"), w["w_down"]).then_inc(L, 16)
                sp.wait_ge(L, 48)
            @block.vector
            def _(v):
                v.wait_ge(S["loaded"], 48)
                step = Steps(v, S["wsteps"], 0)
                for k in range(3):
                    fp4(nc, v, step, wsrc(k), wdst(k), t, lambda: v.sem_inc(S["wxn"], 1), lambda: v.wait_ge(S["wsign"], k + 1))
                v.sem_inc(S["wquant"], 1)
                for k in range(3):
                    v.wait_ge(S["wturned"], k + 1)
                    if k < 2:
                        nc.vector.tensor_copy((gT, uT)[k][:], psT[:, 0:QI]).then_inc(S["wcopied"], 1)
                    else:
                        nc.vector.tensor_copy(dT[:, 0:2, :], psT[:, 0:256].rearrange("p (a b) -> p a b", a=2))
                        nc.vector.tensor_copy(dT[0:96, 2, :], psT[0:96, 256:384]).then_inc(S["wcopied"], 1)
            @block.scalar
            def _(act):
                for k in range(3):
                    act.wait_ge(S["wxn"], k + 1)
                    nb = NBW[k]
                    p = ROWS4 if k < 2 else P
                    nc.scalar.activation(t["sg"][0:p, 0:nb], t["xn"][0:p, 0:nb], ACT.Sign).then_inc(S["wsign"], 1)
            @block.tensor
            def _(pe):
                pe.wait_ge(S["wquant"], 1)
                for k in range(3):
                    if k:
                        pe.wait_ge(S["wcopied"], k + 1)
                    if k < 2:
                        for a in range(4):
                            m = nc.tensor.transpose(psT[:, a * ROWS4:(a + 1) * ROWS4], wq[0:ROWS4, k, 8 * a:8 * a + 8, :], ident[0:ROWS4, 0:ROWS4])
                    else:
                        flat = wq[:, 2].rearrange("p b c -> p (b c)")
                        for a, (f0, nf) in enumerate(DOWN):
                            m = nc.tensor.transpose(psT[0:nf, a * P:(a + 1) * P], flat[:, f0:f0 + nf], ident[:])
                    m.then_inc(S["wturned"], 1)

        with nc.Block() as block:
            @block.tensor
            def _(pe):
                with pe.Fori(0, B) as b:
                    pe.wait_ge(S["xq_ready"], b + 1)
                    for j in range(4):
                        m = nc.tensor.transpose(psT[:, j * P:(j + 1) * P], xq[:, 8 * j:8 * j + 8, :], ident[:])
                    m.then_inc(S["x_turned"], 1)
                    pe.wait_ge(S["xT_ready"], b + 1)

                    def inner(p):
                        pe.wait_ge(S["h_ready"], b * 2 + p + 1)
                        for psX, wT, ready in ((psG, gT, "g_ready"), (psU, uT, "u_ready")):
                            for q in range(2):
                                j = 2 * p + q
                                m = nc.tensor.matmul(psX[:, q, 0:QI], xqT[:, j * P:(j + 1) * P], wT[:], start=True, stop=True)
                            m.then_inc(S[ready], 1)

                    inner(0)
                    for p in range(2):
                        if p == 0:
                            inner(1)
                        pe.wait_ge(S["hq_ready"], b * 2 + p + 1)
                        for q in range(2):
                            flat = hq[:, 22 * q:22 * q + 22].rearrange("p b c -> p (b c)")
                            for a, (f0, nf) in enumerate(DOWN):
                                m = nc.tensor.transpose(psH[0:nf, q, a * P:(a + 1) * P], flat[:, f0:f0 + nf], ident[:])
                        m.then_inc(S["h_turned"], 1)
                        pe.wait_ge(S["hT_ready"], b * 2 + p + 1)
                        if p == 0:
                            pe.wait_ge(S["added"], b + 1)
                        for q in range(2):
                            j = 2 * p + q
                            for a, (f0, nf) in enumerate(DOWN):
                                m = nc.tensor.matmul(psO[:, j * P:(j + 1) * P], hT[0:nf, q, a, :], dT[0:nf, a, :], start=(a == 0), stop=(a == 2))
                        m.then_inc(S["out"], 1)
            @block.scalar
            def _(act):
                with act.Fori(0, B) as b:
                    act.wait_ge(S["xn"], b * 3 + 1)
                    nc.scalar.activation(t["sg"][:, 0:32], t["xn"][:, 0:32], ACT.Sign).then_inc(S["sign"], 1)
                    for p in range(2):
                        act.wait_ge(S["g_ready"], b * 2 + p + 1)
                        act.wait_ge(S["h_ready"], b * 2 + p + 1)
                        nc.scalar.activation(sl[:], psG[:, :, 0:QI], ACT.Silu).then_inc(S["silu"], 1)
                        act.wait_ge(S["xn"], b * 3 + p + 2)
                        nc.scalar.activation(t["sg"][:], t["xn"][:], ACT.Sign).then_inc(S["sign"], 1)
                        act.wait_ge(S["h_turned"], b * 2 + p + 2)
                        act.wait_ge(S["out"], b * 2 + p + 1)
                        nc.scalar.activation(hT[:, :, 0:2, :], psH[:, :, 0:256].rearrange("p q (a t) -> p q a t", a=2), ACT.Copy)
                        nc.scalar.activation(hT[0:96, :, 2, :], psH[0:96, :, 256:384], ACT.Copy).then_inc(S["hT_ready"], 1)
            @block.vector
            def _(v):
                Xv = X[:].rearrange("p (b j) c -> p b j c", b=B)
                with v.Fori(0, B) as b:
                    step = Steps(v, S["steps"], b * (QSTEPS * 3))
                    v.wait_ge(S["x_turned"], b + 1)
                    src = XF[:, b, 1:5, :].rearrange("p j (n q) -> p (j n) q", q=QB)
                    fp4(nc, v, step, src, xq[:], t, lambda: v.sem_inc(S["xn"], 1), lambda: v.wait_ge(S["sign"], b * 3 + 1))
                    v.sem_inc(S["xq_ready"], 1)
                    v.wait_ge(S["x_turned"], b + 2)
                    v.wait_ge(S["u_ready"], 2 * b + 1)
                    nc.vector.tensor_copy(xqT[:], psT[:]).then_inc(S["xT_ready"], 1)
                    for p in range(2):
                        v.wait_ge(S["silu"], b * 2 + p + 1)
                        v.wait_ge(S["u_ready"], b * 2 + p + 2)
                        nc.vector.tensor_tensor(h[:].rearrange("p (q a) b -> p q (a b)", q=2), psU[:, :, 0:QI], sl[:], ALU.mult).then_inc(S["h_ready"], 1)
                        v.wait_ge(S["h_ready"], b * 2 + p + 2)
                        v.wait_ge(S["h_turned"], b * 2 + p + 1)
                        fp4(nc, v, step, h[:], hq[:], t, lambda: v.sem_inc(S["xn"], 1), lambda: v.wait_ge(S["sign"], b * 3 + p + 2))
                        v.sem_inc(S["hq_ready"], 1)
                    v.wait_ge(S["out"], (b + 1) * 2 + 1)
                    nc.vector.tensor_tensor(Xv[:, b], psO[:].rearrange("p (j c) -> p j c", j=4), Xv[:, b], ALU.add).then_inc(S["added"], 1)
        clear(nc, S.values())


MD, CH, NC, G = 32, 64, 8, 2

def neural_memory(nc, X, XF, c, w):
    with ExitStack() as ctx:
        sb = lambda n, s, d=F32: ctx.enter_context(nc.sbuf_tensor("M" + n, s, d))
        ps = lambda n, s, d=F32: ctx.enter_context(nc.psum_tensor("M" + n, s, d))
        sem = lambda n: ctx.enter_context(nc.semaphore("M" + n))
        wp = sb("wp", [P, 6, MD]); cw = sb("cw", [P, 3, 4]); cb = sb("cb", [P, 6])
        mean = sb("mean", [P, P]); pick = sb("pick", [P, 4, CH]); pick1 = sb("pick1", [P, 4]); bd = sb("bd", [P, P])
        start = sb("start", [P, 2, 512]); inj = sb("inj", [CH, 512])
        half = sb("half", [CH, 4]); mhalf = sb("mhalf", [P, 4])
        woT = sb("woT", [P, D]); gwT = sb("gwT", [P, D]); gb = sb("gb", [1, D]); ones1 = sb("ones1", [1, P]); ng = sb("ng", [P, D])
        xb = sb("xb", [P, 4, D]); xT = sb("xT", [P, B, 512])
        T = {k: sb(k, [P, G, 512]) for k in ("K", "V", "Q", "QW", "QS", "AW", "AS", "AS0", "RET")}
        mw = sb("mw", [CH, G, 4, 512]); mse = sb("mse", [CH, G, NC, 4]); th = sb("th", [CH, G, NC, 4]); k2 = sb("k2", [CH, G, NC, 4])
        kqm = sb("kqm", [CH, G, NC, 4 * CH])
        kw = sb("kw", [CH, G, NC, P]); ks = sb("ks", [CH, G, NC, P])
        W3 = sb("W3", [P, G, 3, P]); S3 = sb("S3", [P, G, 3, P])
        ident = c["ident"]
        S = {n: sem(n) for n in """loaded zeroed xb_ready turned xT_ready projected conv gates signs sexp slog splus a_mean om_ready e_mean et_ready
          scans sel_a sel_e m64_ready theta th_copied qbd_ready kq_ready kqm_ready ktok_ready kw_ready chain x_kept""".split()}
        start_at_one(nc, S, "kqm_ready kw_ready th_copied m64_ready theta projected x_kept")
        kinds = ("k", "v", "q", "a", "e", "t")
        with nc.Block() as block:
            @block.sync
            def _(sp):
                L = S["loaded"]
                for k, n in enumerate(("WkT", "WvT", "WqT", "aWT", "eWT", "tWT")):
                    sp.dma_start(wp[:, k, :], w[n]).then_inc(L, 16)
                for r in range(4):
                    q = slice(32 * r, 32 * r + 32)
                    for k, n in enumerate(("ck", "cv", "cq")):
                        sp.dma_start(cw[q, k, :], w[n + "w"]).then_inc(L, 16)
                        sp.dma_start(cb[q, k:k + 1], w[n + "b"].unsqueeze(1)).then_inc(L, 16)
                    for k, n in enumerate(("ab", "eb", "tb")):
                        sp.dma_start(cb[q, 3 + k:4 + k], w[n].unsqueeze(1)).then_inc(L, 16)
                    sp.dma_start(woT[q], w["WoT"]).then_inc(L, 16)
                for a, n in ((mean, "c_mean"), (pick, "c_pick"), (pick1, "c_pick1"), (bd, "c_bd"), (start, "c_start"), (inj, "c_inj"), (gwT, "gWT"), (gb, None), (ng, None)):
                    src = w[n] if n else (w["gb"].unsqueeze(0) if a is gb else rows(w["norm_g"]))
                    sp.dma_start(a[:], src).then_inc(L, 16)
                sp.wait_ge(S["zeroed"], 1)
                for g in range(G):
                    for r in range(4):
                        q = slice(32 * r, 32 * r + 32)
                        for k, n in enumerate(("mW1T", "mW2T", "mW2")):
                            sp.dma_start(W3[q, g, k, q], w[n]).then_inc(L, 16)
                sp.wait_ge(L, 16 * (6 + 40 + 9 + 24))
            @block.vector
            def _(v):
                nc.vector.memset(W3[:], 0.0).then_inc(S["zeroed"], 1)
                nc.vector.memset(S3[:], 0.0)
                nc.vector.memset(half[:], 0.5)
                nc.vector.memset(mhalf[:], -0.5)
                nc.vector.memset(ones1[:], 1.0)

        with ExitStack() as inner:
            isb = lambda n, s: inner.enter_context(nc.sbuf_tensor("M" + n, s, F32))
            xs4 = isb("xs4", [P, 4, 512])
            sg = isb("sg", [P, 3, 512]); rl = isb("rl", [P, 512]); om = isb("om", [P, 512]); et = isb("et", [P, 512]); dn = isb("dn", [P, 2, 512])
            m64 = isb("m64", [CH, 2, 512]); s64 = isb("s64", [CH, 512])
            qbd = isb("qbd", [P, NC, 4, CH]); ksq = isb("ksq", [CH, NC, P])
            psP = inner.enter_context(nc.psum_tensor("MpsP", [P, 6, 512], F32)); psT = inner.enter_context(nc.psum_tensor("MpsT", [P, 512], F32)); psM = inner.enter_context(nc.psum_tensor("MpsM", [P, 512], F32))
            kstage = rl
            with nc.Block() as block:
                @block.tensor
                def _(pe):
                    with pe.Fori(0, G) as g:
                        for r in range(4):
                            n = g * 4 + r
                            pe.wait_ge(S["xb_ready"], n + 1)
                            pe.wait_ge(S["xT_ready"], n)
                            for j in range(4):
                                m = nc.tensor.transpose(psT[:, j * P:(j + 1) * P], xb[:, j, :], ident[:])
                            m.then_inc(S["turned"], 1)
                        pe.wait_ge(S["xT_ready"], g * 4 + 4)
                        pe.wait_ge(S["kqm_ready"], g + 1)
                        pe.wait_ge(S["kw_ready"], g + 1)
                        for k in range(6):
                            for r in range(4):
                                m = nc.tensor.matmul(psP[32 * r:32 * r + 32, k, :], wp[:, k, :], xs4[:, r, :], start=True, stop=True, tile_position=(0, 32 * r))
                        m.then_inc(S["projected"], 1)
                        pe.wait_ge(S["signs"], g + 1)
                        pe.wait_ge(S["th_copied"], g + 1)
                        nc.tensor.matmul(psM[:], mean[:], sg[:, 0, :], start=True, stop=True).then_inc(S["a_mean"], 1)
                        pe.wait_ge(S["om_ready"], g + 1)
                        nc.tensor.matmul(psM[:], mean[:], sg[:, 1, :], start=True, stop=True).then_inc(S["e_mean"], 1)
                        pe.wait_ge(S["et_ready"], g + 1)
                        for r in range(4):
                            pe.wait_ge(S["m64_ready"], 2 * (g * 4 + r) + 1)
                            nc.tensor.matmul(psM[0:CH, :], pick[:, r, :], sg[:, 0, :], start=True, stop=True).then_inc(S["sel_a"], 1)
                            pe.wait_ge(S["m64_ready"], 2 * (g * 4 + r) + 2)
                            nc.tensor.matmul(psM[0:CH, :], pick[:, r, :], sg[:, 1, :], start=True, stop=True).then_inc(S["sel_e"], 1)
                        pe.wait_ge(S["m64_ready"], 2 * (g * 4 + 4) + 1)
                        pe.wait_ge(S["splus"], g + 1)
                        for k in range(NC):
                            m = nc.tensor.matmul(psM[0:CH, 4 * k:4 * k + 4], sg[:, 2, k * CH:(k + 1) * CH], pick1[:], start=True, stop=True)
                        m.then_inc(S["theta"], 1)
                        pe.wait_ge(S["qbd_ready"], g + 1)
                        for k in range(NC):
                            o = psP[0:CH, k // 2, (k % 2) * 256:(k % 2) * 256 + 256]
                            m = nc.tensor.matmul(o, kstage[:, k * CH:(k + 1) * CH], qbd[:, k], start=True, stop=True)
                        m.then_inc(S["kq_ready"], 1)
                        for k in range(NC):
                            m = nc.tensor.transpose(psP[0:CH, 4 + k // 4, (k % 4) * P:(k % 4 + 1) * P], kstage[:, k * CH:(k + 1) * CH], ident[:])
                        m.then_inc(S["ktok_ready"], 1)

                @block.scalar
                def _(act):
                    with act.Fori(0, G) as g:
                        for r in range(4):
                            n = g * 4 + r
                            act.wait_ge(S["turned"], n)
                            nc.scalar.activation(xb[:], XF[:, n, 1:5, :], ACT.Copy).then_inc(S["xb_ready"], 1)
                        act.wait_ge(S["xT_ready"], g * 4 + 4)
                        nc.scalar.activation(xT[:, bass.ds(g * 4, 4), :], xs4[:], ACT.Copy).then_inc(S["x_kept"], 1)
                        act.wait_ge(S["projected"], g + 2)
                        act.wait_ge(S["theta"], g + 1)
                        for k in range(2):
                            nc.scalar.activation(sg[:, k, :], psP[:, 3 + k, :], ACT.Sigmoid, bias=cb[:, 3 + k:4 + k])
                        nc.scalar.activation(sg[:, 2, :], psP[:, 5, :], ACT.Abs, bias=cb[:, 5:6]).then_inc(S["signs"], 1)
                        act.wait_ge(S["signs"], g + 1)
                        nc.scalar.activation(sg[:, 2, :], sg[:, 2, :], ACT.Exp, scale=-1.0).then_inc(S["sexp"], 1)
                        act.wait_ge(S["sexp"], g + 1)
                        nc.scalar.activation(sg[:, 2, :], sg[:, 2, :], ACT.Ln, bias=1.0).then_inc(S["slog"], 1)

                @block.vector
                def _(v):
                    nc.vector.memset(qbd[:], 0.0).then_inc(S["zeroed"], 1)
                    with v.Fori(0, G) as g:
                        step = Steps(v, S["chain"], g * 27)
                        for r in range(4):
                            n = g * 4 + r
                            v.wait_ge(S["turned"], n + 1)
                            v.wait_ge(S["projected"], g + 1)
                            v.wait_ge(S["x_kept"], g + 1)
                            nc.vector.tensor_copy(xs4[:, r, :], psT[:]).then_inc(S["xT_ready"], 1)
                        v.wait_ge(S["projected"], g + 2)
                        outs = [T[k][:, g, :] for k in "KVQ"]
                        for k in range(3):
                            m = nc.vector.tensor_scalar(outs[k], psP[:, k, :], cw[:, k, 3:4], cb[:, k:k + 1], ALU.mult, ALU.add)
                        step(m)
                        for back in (1, 2, 3):
                            for k in range(3):
                                m = nc.vector.scalar_tensor_tensor(out=outs[k][:, back:512], in0=psP[:, k, 0:512 - back], scalar=cw[:, k, 3 - back:4 - back], in1=outs[k][:, back:512], op0=ALU.mult, op1=ALU.add)
                            step(m)
                        v.wait_ge(S["signs"], g + 1)
                        step(nc.vector.tensor_scalar(rl[:], psP[:, 5, :], cb[:, 5:6], 0.0, ALU.add, ALU.max))
                        v.wait_ge(S["slog"], g + 1)
                        nc.vector.tensor_tensor(sg[:, 2, :], sg[:, 2, :], rl[:], ALU.add).then_inc(S["splus"], 1)
                        v.wait_ge(S["a_mean"], g + 1)
                        nc.vector.tensor_scalar(om[:], psM[:], -0.1, 1.0, ALU.mult, ALU.add).then_inc(S["om_ready"], 1)
                        v.wait_ge(S["e_mean"], g + 1)
                        nc.vector.tensor_scalar(et[:], psM[:], 0.9, 0.05, ALU.mult, ALU.add).then_inc(S["et_ready"], 1)
                        v.wait_ge(S["et_ready"], g + 1)
                        notfirst, first = start[:, 0, :], start[:, 1, :]
                        aw, as_, as0 = T["AW"][:, g, :], T["AS"][:, g, :], T["AS0"][:, g, :]
                        nc.vector.tensor_tensor(dn[:, 0], om[:], notfirst, ALU.mult)
                        step(nc.vector.tensor_tensor(dn[:, 1], om[:], first, ALU.mult))
                        step(nc.vector.tensor_tensor_scan(aw, dn[:, 0], dn[:, 1], 0.0, ALU.mult, ALU.add))
                        nc.vector.tensor_tensor(dn[:, 1], et[:], first, ALU.mult)
                        step(nc.vector.tensor_tensor(om[:], et[:], notfirst, ALU.mult))
                        step(nc.vector.tensor_tensor_scan(as0, om[:], dn[:, 1], 0.0, ALU.mult, ALU.add))
                        step(nc.vector.tensor_tensor_scan(as_, dn[:, 0], as0, 0.0, ALU.mult, ALU.add))
                        nc.vector.tensor_tensor(T["QW"][:, g, :], T["Q"][:, g, :], aw, ALU.mult)
                        step(nc.vector.tensor_tensor(T["QS"][:, g, :], T["Q"][:, g, :], as_, ALU.mult))
                        for r in range(4):
                            n = g * 4 + r
                            v.wait_ge(S["sel_a"], n + 1)
                            nc.vector.tensor_scalar(m64[:, 0], psM[0:CH, :], -0.1, 1.0, ALU.mult, ALU.add).then_inc(S["m64_ready"], 1)
                            v.wait_ge(S["sel_e"], n + 1)
                            nc.vector.tensor_scalar(m64[:, 1], psM[0:CH, :], 0.9, 0.05, ALU.mult, ALU.add).then_inc(S["m64_ready"], 1)
                            v.wait_ge(S["m64_ready"], 2 * n + 3)
                            step(nc.vector.tensor_tensor(m64[:], m64[:], bcast(start[0:CH, 0, :], 1, 2), ALU.mult))
                            step(nc.vector.tensor_tensor_scan(s64[:], m64[:, 1], inj[:], 0.0, ALU.mult, ALU.add))
                            nc.vector.tensor_copy(mse[:, g, :, r], s64[:].rearrange("p (c t) -> p c t", c=NC)[:, :, CH - 1])
                            step(nc.vector.tensor_tensor_scan(mw[:, g, r, :], m64[:, 0], s64[:], 0.0, ALU.mult, ALU.add))
                        v.wait_ge(S["theta"], g + 2)
                        nc.vector.tensor_copy(th[:, g], psM[0:CH, 0:32].rearrange("p (c r) -> p c r", c=NC)).then_inc(S["th_copied"], 1)
                        v.wait_ge(S["splus"], g + 1)
                        nc.vector.tensor_scalar(rl[:], T["K"][:, g, :], 1.0, None, ALU.mult)
                        for r in range(4):
                            q = slice(32 * r, 32 * r + 32)
                            m = nc.vector.tensor_copy(qbd[q, :, r, :], T["Q"][q, g, :].rearrange("p (c t) -> p c t", c=NC))
                        m.then_inc(S["qbd_ready"], 1)
                        v.wait_ge(S["kq_ready"], g + 1)
                        kqv = psP[0:CH, 0:4, :].rearrange("p a (b x) -> p (a b) x", b=2).rearrange("p c (r t) -> p c r t", r=4)
                        mwv = mw[:, g].rearrange("p r (c t) -> p c r t", c=NC)
                        nc.vector.tensor_tensor(kqm[:, g].rearrange("p c (r t) -> p c r t", r=4), kqv, mwv, ALU.mult).then_inc(S["kqm_ready"], 1)
                        v.wait_ge(S["ktok_ready"], g + 1)
                        ktk = psP[0:CH, 4:6, :].rearrange("p a (b x) -> p (a b) x", b=4).rearrange("p c (r d) -> p c r d", r=4)
                        last = mwv[:, :, :, CH - 1]
                        step(nc.vector.tensor_tensor(kw[:, g].rearrange("p c (r d) -> p c r d", r=4), ktk, bcast(last, 3, MD), ALU.mult))
                        step(nc.vector.tensor_tensor(ks[:, g].rearrange("p c (r d) -> p c r d", r=4), ktk, bcast(mse[:, g], 3, MD), ALU.mult))
                        step(nc.vector.tensor_copy(ksq[:].rearrange("p c (r d) -> p c r d", r=4), ktk))
                        step(nc.vector.tensor_tensor(ksq[:], ksq[:], ksq[:], ALU.mult))
                        nc.vector.tensor_reduce(k2[:, g], ksq[:].rearrange("p c (r d) -> p c r d", r=4), AX.X, ALU.add).then_inc(S["kw_ready"], 1)

        with ExitStack() as inner:
            isb = lambda n, s: inner.enter_context(nc.sbuf_tensor("M" + n, s, F32))
            psZ = inner.enter_context(nc.psum_tensor("MpsZ", [P, 2, 512], F32)); psR = inner.enter_context(nc.psum_tensor("MpsR", [P, 2, 512], F32))
            psK = inner.enter_context(nc.psum_tensor("MpsK", [P, 2, 512], F32)); psW = inner.enter_context(nc.psum_tensor("MpsW", [P, 2, 512], F32))
            sig = isb("sig", [P, G, CH]); hT = isb("hT", [P, G, CH]); om1 = isb("om1", [P, G, CH]); eT = isb("eT", [P, G, CH]); dz = isb("dz", [P, G, CH])
            tok = isb("tok", [CH, G, 3, P]); sqr = isb("sqr", [CH, G, 3, P]); n2 = isb("n2", [CH, G, 3, 4]); nn = isb("nn", [CH, G, 2, 4]); ce = isb("ce", [CH, G, 4])
            src = isb("src", [CH, G, 2, P]); hw = isb("hw", [CH, G, 2, P])
            sq = isb("sq", [P, G, CH]); h2 = isb("h2", [P, G, CH]); h2w = isb("h2w", [P, G, 2, CH]); h2bd = isb("h2bd", [P, G, 4, CH]); hhm = isb("hhm", [CH, G, 4 * CH])
            upd = isb("upd", [P, G, 6, P]); t3 = isb("t3", [P, G, 3, P])
            stg = isb("stg", [P, G, 3, CH]); stt = isb("stt", [CH, G, 2, P])
            R = {n: sem("r_" + n) for n in """staged z sig h om1 ds pred e dh dz turned tok sqr n2 pow ce src zq sq h2 h2w hh hhm out ret hw upd masked t3 w3 chain zero clear""".split()}
            start_at_one(nc, R, "w3 ret masked upd")
            kqs = isb("kqs", [CH, G, 4 * CH])
            with nc.Block() as block:
                @block.tensor
                def _(pe):
                    with pe.Fori(0, NC) as k:
                        t0 = k * CH
                        n = [k * G + g for g in range(G)]
                        for g in range(G):
                            pe.wait_ge(R["w3"], k * G + 1)
                            pe.wait_ge(R["ret"], k * G + 1)
                            nc.tensor.matmul(psZ[:, g, 0:CH], W3[:, g, 0, :], T["K"][:, g, bass.ds(t0, CH)], start=True, stop=True).then_inc(R["z"], 1)
                            pe.wait_ge(R["h"], n[g] + 1)
                            nc.tensor.matmul(psZ[:, g, CH:2 * CH], W3[:, g, 1, :], hT[:, g, :], start=True, stop=True).then_inc(R["pred"], 1)
                            pe.wait_ge(R["e"], n[g] + 1)
                            nc.tensor.matmul(psZ[:, g, 2 * CH:3 * CH], W3[:, g, 2, :], eT[:, g, :], start=True, stop=True).then_inc(R["dh"], 1)
                            pe.wait_ge(R["dz"], n[g] + 1)
                            pe.sem_inc(R["clear"], 1)
                            for a, x in enumerate((hT, eT, dz)):
                                m = nc.tensor.transpose(psK[0:CH, g, a * P:(a + 1) * P], x[:, g, :], ident[:])
                            m.then_inc(R["turned"], 1)
                        for g in range(G):
                            pe.wait_ge(R["src"], n[g] + 1)
                            o = psR[:, g, 0:CH]
                            nc.tensor.matmul(o, W3[:, g, 0, :], T["QW"][:, g, bass.ds(t0, CH)], start=True, stop=True)
                            nc.tensor.matmul(o, S3[:, g, 0, :], T["QS"][:, g, bass.ds(t0, CH)], start=False, stop=True, skip_group_check=True)
                            for r in range(4):
                                q = slice(32 * r, 32 * r + 32)
                                m = nc.tensor.matmul(psR[q, g, 0:CH], src[:, g, 1, q], kqs[:, g, r * CH:(r + 1) * CH], start=False, stop=True, skip_group_check=True, tile_position=(0, 32 * r))
                            m.then_inc(R["zq"], 1)
                            pe.wait_ge(R["h2w"], n[g] + 1)
                            nc.tensor.matmul(psR[0:CH, g, 128:128 + 4 * CH], hT[:, g, :], h2bd[:, g], start=True, stop=True).then_inc(R["hh"], 1)
                            pe.wait_ge(R["hhm"], n[g] + 1)
                            o = psR[:, g, 0:CH]
                            nc.tensor.matmul(o, W3[:, g, 1, :], h2w[:, g, 0, :], start=True, stop=True)
                            nc.tensor.matmul(o, S3[:, g, 1, :], h2w[:, g, 1, :], start=False, stop=True, skip_group_check=True)
                            for r in range(4):
                                q = slice(32 * r, 32 * r + 32)
                                m = nc.tensor.matmul(psR[q, g, 0:CH], src[:, g, 0, q], hhm[:, g, r * CH:(r + 1) * CH], start=False, stop=True, skip_group_check=True, tile_position=(0, 32 * r))
                            m.then_inc(R["out"], 1)
                        for g in range(G):
                            pe.wait_ge(R["hw"], n[g] + 1)
                            pe.wait_ge(R["masked"], k * G + g + 1)
                            for a in range(2):
                                o = lambda s: psW[:, a, s * P:(s + 1) * P]
                                nc.tensor.matmul(o(0), stt[:, g, a, :], src[:, g, 1, :], start=True, stop=True)
                                nc.tensor.matmul(o(1), hw[:, g, a, :], src[:, g, 0, :], start=True, stop=True)
                                m = nc.tensor.matmul(o(2), src[:, g, 0, :], hw[:, g, a, :], start=True, stop=True)
                            m.then_inc(R["upd"], 1)

                @block.scalar
                def _(act):
                    with act.Fori(0, NC) as k:
                        t0 = k * CH
                        n = [k * G + g for g in range(G)]
                        for g in range(G):
                            act.wait_ge(R["upd"], k * G + 1)
                            nc.scalar.activation(kqs[:, g, :], kqm[:, g, k, :], ACT.Copy)
                            nc.scalar.activation(stt[:, g, 0, :], kw[:, g, k, :], ACT.Copy)
                            nc.scalar.activation(stt[:, g, 1, :], ks[:, g, k, :], ACT.Copy).then_inc(R["staged"], 1)
                        for g in range(G):
                            act.wait_ge(R["z"], n[g] + 1)
                            nc.scalar.activation(sig[:, g, :], psZ[:, g, 0:CH], ACT.Sigmoid).then_inc(R["sig"], 1)
                            act.wait_ge(R["turned"], n[g] + 1)
                            nc.scalar.activation(tok[:, g].rearrange("p a b -> p (a b)"), psK[0:CH, g, 0:3 * P], ACT.Copy).then_inc(R["tok"], 1)
                        for g in range(G):
                            act.wait_ge(R["zq"], n[g] + 1)
                            nc.scalar.activation(sq[:, g, :], psR[:, g, 0:CH], ACT.Sigmoid).then_inc(R["sq"], 1)
                            act.wait_ge(R["out"], n[g] + 1)
                            nc.scalar.activation(T["RET"][:, g, bass.ds(t0, CH)], psR[:, g, 0:CH], ACT.Copy).then_inc(R["ret"], 1)

                @block.gpsimd
                def _(g_):
                    with g_.Fori(0, NC) as k:
                        for g in range(G):
                            n = k * G + g
                            g_.wait_ge(R["n2"], n + 1)
                            nc.gpsimd.tensor_tensor(nn[:, g, 0, :], nn[:, g, 0, :], half[:], ALU.pow).then_inc(R["pow"], 1)

                @block.vector
                def _(v):
                    nc.vector.memset(h2bd[:], 0.0).then_inc(R["zero"], 1)
                    v.wait_ge(R["zero"], 1)
                    with v.Fori(0, NC) as k:
                        t0 = k * CH
                        step = Steps(v, R["chain"], k * 24)
                        n = [k * G + g for g in range(G)]
                        for g in range(G):
                            v.wait_ge(R["sig"], n[g] + 1)
                            z = psZ[:, g, 0:CH]
                            nc.vector.tensor_tensor(hT[:, g, :], z, sig[:, g, :], ALU.mult).then_inc(R["h"], 1)
                            step(nc.vector.tensor_scalar(om1[:, g, :], sig[:, g, :], -1.0, 1.0, ALU.mult, ALU.add))
                            v.wait_ge(R["h"], n[g] + 1)
                            step(nc.vector.tensor_tensor(om1[:, g, :], om1[:, g, :], hT[:, g, :], ALU.mult))
                            step(nc.vector.tensor_tensor(om1[:, g, :], om1[:, g, :], sig[:, g, :], ALU.add))
                            v.wait_ge(R["pred"], n[g] + 1)
                            nc.vector.tensor_tensor(eT[:, g, :], psZ[:, g, CH:2 * CH], T["V"][:, g, bass.ds(t0, CH)], ALU.subtract).then_inc(R["e"], 1)
                            v.wait_ge(R["dh"], n[g] + 1)
                            nc.vector.tensor_tensor(dz[:, g, :], psZ[:, g, 2 * CH:3 * CH], om1[:, g, :], ALU.mult).then_inc(R["dz"], 1)
                        for g in range(G):
                            v.wait_ge(R["tok"], n[g] + 1)
                            step(nc.vector.tensor_tensor(sqr[:, g], tok[:, g], tok[:, g], ALU.mult))
                            step(nc.vector.tensor_reduce(n2[:, g], sqr[:, g].rearrange("p a (r d) -> p a r d", r=4), AX.X, ALU.add))
                            nc.vector.tensor_tensor(nn[:, g, 0, :], n2[:, g, 0, :], n2[:, g, 1, :], ALU.mult)
                            step(nc.vector.tensor_tensor(nn[:, g, 1, :], n2[:, g, 2, :], k2[:, g, k, :], ALU.mult))
                            nc.vector.tensor_tensor(nn[:, g, 0, :], nn[:, g, 0, :], nn[:, g, 1, :], ALU.add).then_inc(R["n2"], 1)
                        for g in range(G):
                            v.wait_ge(R["pow"], n[g] + 1)
                            step(nc.vector.tensor_scalar(ce[:, g, :], nn[:, g, 0, :], 0.2, 1e-6, ALU.mult, ALU.max))
                            step(nc.vector.reciprocal(ce[:, g, :], ce[:, g, :]))
                            step(nc.vector.tensor_scalar(ce[:, g, :], ce[:, g, :], 1.0, 0.2, ALU.min, ALU.mult))
                            step(nc.vector.tensor_tensor(ce[:, g, :], ce[:, g, :], th[:, g, k, :], ALU.mult))
                            v.wait_ge(R["staged"], n[g] + 1)
                            nc.vector.tensor_tensor(src[:, g].rearrange("p a (r d) -> p a r d", r=4), tok[:, g, 1:3].rearrange("p a (r d) -> p a r d", r=4),
                                                    bcast(bcast(ce[:, g, :], 2, MD), 1, 2), ALU.mult).then_inc(R["src"], 1)
                            ht = tok[:, g, 0].rearrange("p (r d) -> p r d", r=4)
                            mwv = mw[:, g].rearrange("p r (c t) -> p c r t", c=NC)
                            nc.vector.tensor_tensor(hw[:, g, 0].rearrange("p (r d) -> p r d", r=4), ht, bcast(mwv[:, k, :, CH - 1], 2, MD), ALU.mult)
                            nc.vector.tensor_tensor(hw[:, g, 1].rearrange("p (r d) -> p r d", r=4), ht, bcast(mse[:, g, k, :], 2, MD), ALU.mult).then_inc(R["hw"], 1)
                        for g in range(G):
                            v.wait_ge(R["sq"], n[g] + 1)
                            step(nc.vector.tensor_tensor(h2[:, g, :], psR[:, g, 0:CH], sq[:, g, :], ALU.mult))
                            nc.vector.tensor_tensor(h2w[:, g, 0, :], h2[:, g, :], T["AW"][:, g, bass.ds(t0, CH)], ALU.mult)
                            nc.vector.tensor_tensor(h2w[:, g, 1, :], h2[:, g, :], T["AS"][:, g, bass.ds(t0, CH)], ALU.mult)
                            for r in range(4):
                                q = slice(32 * r, 32 * r + 32)
                                m = nc.vector.tensor_copy(h2bd[q, g, r, :], h2[q, g, :])
                            m.then_inc(R["h2w"], 1)
                            v.wait_ge(R["hh"], n[g] + 1)
                            mwc = mw[:, g].rearrange("p r (c t) -> p c r t", c=NC)[:, k]
                            nc.vector.tensor_tensor(hhm[:, g].rearrange("p (r t) -> p r t", r=4), psR[0:CH, g, 128:128 + 4 * CH].rearrange("p (r t) -> p r t", r=4), mwc, ALU.mult).then_inc(R["hhm"], 1)
                        for g in range(G):
                            v.wait_ge(R["upd"], n[g] + 2)
                            m = nc.vector.tensor_tensor(upd[:, g].rearrange("p (a s) x -> p a s x", a=2), psW[:, :, 0:3 * P].rearrange("p a (s x) -> p a s x", s=3), bcast(bcast(bd[:], 1, 3), 1, 2), ALU.mult)
                            m.then_inc(R["masked"], 1)
                            v.wait_ge(R["masked"], n[g] + 2)
                            v.wait_ge(R["out"], n[g] + 1)
                            at = bass.ds(t0 + CH - 1, 1)
                            step(nc.vector.scalar_tensor_tensor(out=t3[:, g], in0=S3[:, g], scalar=T["AS"][:, g, at], in1=upd[:, g, 0:3], op0=ALU.mult, op1=ALU.add))
                            nc.vector.scalar_tensor_tensor(out=S3[:, g], in0=S3[:, g], scalar=T["AS0"][:, g, at], in1=upd[:, g, 3:6], op0=ALU.mult, op1=ALU.add)
                            nc.vector.scalar_tensor_tensor(out=W3[:, g], in0=W3[:, g], scalar=T["AW"][:, g, at], in1=t3[:, g], op0=ALU.mult, op1=ALU.add).then_inc(R["w3"], 1)

        clear(nc, S.values())
        clear(nc, R.values())

        with ExitStack() as inner:
            isb = lambda n, s: inner.enter_context(nc.sbuf_tensor("M" + n, s, F32))
            psY = inner.enter_context(nc.psum_tensor("MpsY", [P, 2, 512], F32)); psG = inner.enter_context(nc.psum_tensor("MpsG", [P, 2, 512], F32))
            rg = isb("rg", [P, 512]); xg = isb("xg", [P, 2, 512]); ysq = isb("ysq", [P, 4, D]); ss = isb("ss", [P, 4]); y = isb("y", [P, 4, D])
            R = {n: sem("o_" + n) for n in "rg xg y gate sq ss eps rstd yn chain added".split()}
            start_at_one(nc, R, "y gate ss added")
            with nc.Block() as block:
                @block.scalar
                def _(act):
                    with act.Fori(0, G) as g:
                        act.wait_ge(R["y"], g * 4 + 1)
                        nc.scalar.activation(rg[:], T["RET"][:, g, :], ACT.Copy).then_inc(R["rg"], 1)
                        for r in range(4):
                            act.wait_ge(R["gate"], 1 + (g * 4 + (r - 1 if r >= 2 else 0)))
                            nc.scalar.activation(xg[:, r % 2, :], xT[:, g * 4 + r, :], ACT.Copy).then_inc(R["xg"], 1)
                            act.wait_ge(R["y"], g * 4 + r + 2)
                            act.wait_ge(R["ss"], g * 4 + r + 1)
                            nc.scalar.activation(ysq[:].rearrange("p a b -> p (a b)"), psY[:, r % 2, :], ACT.Square).then_inc(R["sq"], 1)
                @block.tensor
                def _(pe):
                    with pe.Fori(0, G) as g:
                        for r in range(4):
                            n = g * 4 + r
                            q = slice(32 * r, 32 * r + 32)
                            pe.wait_ge(R["rg"], g + 1)
                            pe.wait_ge(R["added"], 1 + (g * 4 + (r - 1 if r >= 2 else 0)))
                            for j in range(4):
                                m = nc.tensor.matmul(psY[:, r % 2, j * P:(j + 1) * P], rg[q, j * P:(j + 1) * P], woT[q, :], start=True, stop=True)
                            m.then_inc(R["y"], 1)
                            pe.wait_ge(R["xg"], n + 1)
                            for j in range(4):
                                o = psG[:, r % 2, j * P:(j + 1) * P]
                                nc.tensor.matmul(o, ones1[:], gb[:], start=True, stop=False)
                                m = nc.tensor.matmul(o, xg[:, r % 2, j * P:(j + 1) * P], gwT[:], start=False, stop=True)
                            m.then_inc(R["gate"], 1)
                @block.gpsimd
                def _(g_):
                    with g_.Fori(0, B) as n:
                        g_.wait_ge(R["eps"], n + 1)
                        nc.gpsimd.tensor_tensor(ss[:], ss[:], mhalf[:], ALU.pow).then_inc(R["rstd"], 1)
                @block.vector
                def _(v):
                    Xv = X[:].rearrange("p (b j) c -> p b j c", b=B)
                    with v.Fori(0, G) as g:
                        step = Steps(v, R["chain"], g * 16)
                        for r in range(4):
                            n = g * 4 + r
                            v.wait_ge(R["sq"], n + 1)
                            nc.vector.tensor_reduce(ss[:], ysq[:], AX.X, ALU.add).then_inc(R["ss"], 1)
                            v.wait_ge(R["ss"], n + 2)
                            nc.vector.tensor_scalar(ss[:], ss[:], 1.0 / D, 1e-6, ALU.mult, ALU.add).then_inc(R["eps"], 1)
                            v.wait_ge(R["rstd"], n + 1)
                            step(nc.vector.tensor_tensor(y[:], psY[:, r % 2, :].rearrange("p (j c) -> p j c", j=4), bcast(ss[:], 2, D), ALU.mult))
                            step(nc.vector.tensor_tensor(y[:], y[:], bcast(ng[:], 1, 4), ALU.mult))
                            v.wait_ge(R["gate"], n + 2)
                            step(nc.vector.tensor_tensor(y[:], psG[:, r % 2, :].rearrange("p (j c) -> p j c", j=4), y[:], ALU.mult))
                            step(nc.vector.tensor_tensor(Xv[:, n], y[:], Xv[:, n], ALU.add))
                            v.sem_inc(R["added"], 1)
        clear(nc, R.values())


def memory_consts():
    bd = np.kron(np.eye(4), np.ones((32, 32))).astype(np.float32)
    pick = np.zeros((P, 4, CH), np.float32)
    pick1 = np.zeros((P, 4), np.float32)
    for r in range(4):
        pick[32 * r:32 * r + 32, r] = 1 / 32
        pick1[32 * r:32 * r + 32, r] = -0.1 / 32
    t = np.arange(512)
    first = np.broadcast_to((t % CH == 0).astype(np.float32), (P, 512))
    start = np.stack([1 - first, first], 1).copy()
    inj = (t[None] % CH == np.arange(CH)[:, None]).astype(np.float32)
    return {"c_mean": bd / 32, "c_bd": bd, "c_pick": pick, "c_pick1": pick1, "c_start": start, "c_inj": inj}

def memory_layout(w):
    t = np.ascontiguousarray
    return {**{n + "T": t(w[n].T) for n in ("Wk", "Wv", "Wq", "aW", "eW", "tW", "Wo", "gW", "mW1", "mW2")}}


def network(nc, x, ident_in, w, out):
    with ExitStack() as ctx:
        X = ctx.enter_context(nc.sbuf_tensor("X", [P, 32, D], F32))
        XF = ctx.enter_context(nc.sbuf_tensor("XF", [P, B, 5, D], F32))
        ident = ctx.enter_context(nc.sbuf_tensor("ident", [P, P], F32))
        io = ctx.enter_context(nc.semaphore("io")); summed = ctx.enter_context(nc.semaphore("summed"))
        c = {"ident": ident}
        xt, ot = (a.rearrange("b (j p) c -> p (b j) c", p=P) for a in (x, out))
        with nc.Block() as block:
            @block.sync
            def _(sp):
                sp.dma_start(X[:], xt).then_inc(io, 16)
                sp.dma_start(ident[:], ident_in).then_inc(io, 16)
                sp.wait_ge(io, 32)
            @block.vector
            def _(v):
                nc.vector.memset(XF[:, :, 0, :], 0.0)

        layer_norm(nc, X, XF, "n0")
        with ExitStack() as building:
            K = kernel_buffers(nc, building, w["L1_attn"])
            causal_attention(nc, X, XF, c, w["L0_attn"], K)
            clear(nc, [K[n] for n in ("loaded", "steps", "built", "stored")])
        local_layers(nc, XF, c, w["L0_ffn"])
        with nc.Block() as block:
            @block.vector
            def _(v):
                xv = X[:].rearrange("p (b j) c -> p b (j c)", b=B)
                nc.vector.tensor_tensor(xv, XF[:, :, 1:5, :].rearrange("p b j c -> p b (j c)"), xv, ALU.add).then_inc(summed, 1)
        layer_norm(nc, X, XF, "n1")
        state_space(nc, X, XF, c, w["L1_attn"], K["scratch"])
        top2_experts(nc, X, XF, c, w["L1_ffn"])
        layer_norm(nc, X, XF, "n2")
        banded_attention(nc, X, XF, c, w["L2_attn"])
        capped_experts(nc, X, XF, c, w["L2_ffn"])
        layer_norm(nc, X, XF, "n3")
        neural_memory(nc, X, XF, c, w["L3_attn"])
        fp4_ffn(nc, X, XF, c, w["L3_ffn"])
        with nc.Block() as block:
            @block.sync
            def _(sp):
                sp.dma_start(ot, X[:]).then_inc(io, 16)
                sp.wait_ge(io, 48)


def kernel(**inputs):
    import numpy as _np
    import concourse.bacc as _bacc
    from concourse import mybir as _mybir
    from concourse.bass_utils import run_bass_kernel_spmd as _run

    inputs = {k: _np.asarray(v) for k, v in inputs.items()}
    sub = lambda p: {k[len(p) + 1:]: v for k, v in inputs.items() if k.startswith(p + "_")}
    t = _np.ascontiguousarray
    identb = {"c_identb": _np.eye(P).astype("bfloat16")}
    stages = {p: sub(p) for p in ("L0_attn", "L0_ffn", "L1_attn", "L1_ffn", "L2_attn", "L2_ffn", "L3_attn", "L3_ffn")}
    s = stages["L0_attn"]
    s.update({n + "T": t(s[n].T) for n in ("Wk", "Wq", "Wv", "Wu")}, **attention_consts(), **identb)
    x = s.pop("x")
    s = stages["L0_ffn"]
    s.update(local_layout(s), **identb)
    s.update(local_consts())
    s = stages["L1_attn"]
    s.update({"W_outT": t(s["W_out"].T), "c_flip": t(_np.eye(P, dtype=_np.float32)[::-1])})
    s = stages["L1_ffn"]
    s.update(top2_consts(), **top2_layout(s))
    stages["L2_attn"].update(banded_consts(), **identb)
    s = stages["L2_ffn"]
    s.update(capped_consts(), **capped_layout(s))
    s = stages["L3_attn"]
    s.update(memory_consts(), **memory_layout(s))

    nc = _bacc.Bacc("TRN2", target_bir_lowering=False, num_devices=1)
    arrays = {}

    def given(name, a):
        arrays[name] = t(a)
        return nc.dram_tensor(name, a.shape, _mybir.dt.from_np(a.dtype), kind="ExternalInput").ap()

    xin, ident_in = given("x", x), given("identity", _np.eye(P, dtype=_np.float32))
    w = {p: {n: given(p + "_" + n, a) for n, a in d.items() if n not in HOST_ONLY} for p, d in stages.items()}
    out = nc.dram_tensor("out_0", x.shape, F32, kind="ExternalOutput").ap()
    network(nc, xin, ident_in, w, out)
    r = _run(nc, [arrays], core_ids=[0])
    return r.results[0]["out_0"]
```
